# Optimizing a Trainium2 kernel written in Bass

```python
import numpy as np
import jax
import jax.numpy as jnp

def _softmax(x, axis=-1):
    return jax.nn.softmax(x, axis=axis)

def _gelu(x):
    return jax.nn.gelu(x, approximate=True)

def _silu(x):
    return jax.nn.silu(x)

def _sigmoid(x):
    return jax.nn.sigmoid(x)

def _layernorm(x, axis=-1, eps=1e-05):
    m = jnp.mean(x, axis=axis, keepdims=True)
    v = jnp.var(x, axis=axis, keepdims=True)
    return (x - m) / jnp.sqrt(v + eps)

def _scatter_add(tgt, idx, src, axis=0):
    return tgt.at[idx].add(src)

def _segment_sum(src, seg, n):
    return jax.ops.segment_sum(src, seg, n)
kernel_name = 'mk_xattn_ffn_d4_seqx_r4_f731e7'

def setup_inputs(seed: int=0):
    np.random.seed(seed)
    _w = jnp.asarray

    def _rec_inputs():
        import jax
        import jax.numpy as jnp
        _rk = jax.random.key(seed)
        x = -0.0003929 + 0.9999 * jax.random.normal(jax.random.fold_in(_rk, 1), (2, 1024, 256), jnp.float32)
        _lenS = 1024 - jax.random.randint(jax.random.fold_in(_rk, 7), (2,), 0, max(1, 1024 // 4) + 1, jnp.int32)
        _lenS2 = 64 - jax.random.randint(jax.random.fold_in(_rk, 8), (2,), 0, max(1, 64 // 4) + 1, jnp.int32)
        _ctx_1024P = jax.random.normal(jax.random.fold_in(_rk, 11), (2, 16, 256), jnp.float32)
        _ctx_1024c = jax.random.dirichlet(jax.random.fold_in(_rk, 511), 0.3 * jnp.ones((16,), jnp.float32), (2, 64))
        _ctx_1024t = jnp.einsum('bsk,bkd->bsd', _ctx_1024c, _ctx_1024P)
        _ctx_1024t = _ctx_1024t * jax.lax.rsqrt(jnp.mean(jnp.square(_ctx_1024t)) + 1e-12) * 0.953939
        ctx_1024 = -1.39393e-06 + 0.999914 * (_ctx_1024t + 0.3 * jax.random.normal(jax.random.fold_in(_rk, 611), (2, 64, 256), jnp.float32))
        itok_BxS_8_8191 = jax.random.randint(jax.random.fold_in(_rk, 12), (2, 1024), 8, 2048, jnp.int32)
        itok_BxS2_1_8191 = jax.random.randint(jax.random.fold_in(_rk, 13), (2, 64), 1, 2048, jnp.int32)
        _validS = jnp.arange(1024)[None, :] < _lenS[:, None]
        _validS2 = jnp.arange(64)[None, :] < _lenS2[:, None]
        _causal = jnp.tril(jnp.ones((1024, 1024), dtype=bool))
        mask_BxSxS2_if1 = jnp.where(jnp.ones((2, 1024, 64), dtype=bool), 1, 0).astype(jnp.int32)
        return (x, ctx_1024, itok_BxS_8_8191, itok_BxS2_1_8191, mask_BxSxS2_if1)
    x, ctx_1024, itok_BxS_8_8191, itok_BxS2_1_8191, mask_BxSxS2_if1 = _rec_inputs()

    def _L0_xattn_setup():
        import jax, jax.numpy as jnp
        import numpy as np
        B, C_LEN, Q_LEN, D = (8, 512, 128, 256)
        key = jax.random.key(seed)
        ks = jax.random.split(key, 10)
        scale = 1.0 / np.sqrt(D)
        return {'c': jax.random.normal(ks[0], (B, C_LEN, D), dtype=jnp.float32), 'q': jax.random.normal(ks[1], (B, Q_LEN, D), dtype=jnp.float32), 'w_cq': jax.random.normal(ks[2], (D,), dtype=jnp.float32) * scale, 'b_cq': jax.random.normal(ks[3], (), dtype=jnp.float32) * scale, 'w_c': jax.random.normal(ks[4], (D,), dtype=jnp.float32) * scale, 'b_c': jax.random.normal(ks[5], (), dtype=jnp.float32) * scale, 'w_q': jax.random.normal(ks[6], (D,), dtype=jnp.float32) * scale, 'b_q': jax.random.normal(ks[7], (), dtype=jnp.float32) * scale, 'W_l': jax.random.normal(ks[8], (D, 4 * D), dtype=jnp.float32) * (1.0 / np.sqrt(4 * D)), 'b_l': jax.random.normal(ks[9], (D,), dtype=jnp.float32) * (1.0 / np.sqrt(4 * D))}
    _L0_xattn_all = _L0_xattn_setup()
    _L0_xattn_in = {k: v for k, v in _L0_xattn_all.items() if k in ('w_cq', 'b_cq', 'w_c', 'b_c', 'w_q', 'b_q', 'W_l', 'b_l')}
    del _L0_xattn_all

    def _L0_ffn_setup():
        import jax, jax.numpy as jnp
        import numpy as np
        DIM = 256
        DEPTH = 2
        HEADS = 8
        DIM_HEAD = 64
        WINDOW = 128
        INNER = HEADS * DIM_HEAD
        HID = int(DIM * 4 * 2 / 3)
        B, N = (2, 2048)
        QK_SCALE = 8.0

        def shift_token(t):
            t1, t2 = jnp.split(t, 2, axis=-1)
            t2 = jnp.pad(t2, ((0, 0), (1, 0), (0, 0)))[:, :-1]
            return jnp.concatenate([t1, t2], axis=-1)

        def l2norm(t):
            return t / jnp.clip(jnp.linalg.norm(t, axis=-1, keepdims=True), 1e-12)

        def rotate_half(x):
            x1, x2 = jnp.split(x, 2, axis=-1)
            return jnp.concatenate([-x2, x1], axis=-1)

        def rotary_xpos(q, k):
            n = q.shape[-2]
            half_idx = jnp.arange(0, DIM_HEAD, 2, dtype=jnp.float32)
            inv_freq = 1.0 / 10000.0 ** (half_idx / DIM_HEAD)
            t = jnp.arange(n, dtype=jnp.float32)
            freqs = t[:, None] * inv_freq[None, :]
            freqs = jnp.concatenate([freqs, freqs], axis=-1)
            base = (half_idx + 0.4 * DIM_HEAD) / (1.4 * DIM_HEAD)
            power = (t - n // 2) / float(WINDOW // 2)
            scale = base[None, :] ** power[:, None]
            scale = jnp.concatenate([scale, scale], axis=-1)
            cos, sin = (jnp.cos(freqs), jnp.sin(freqs))
            q = q * cos * scale + rotate_half(q) * sin * scale
            k = k * cos / scale + rotate_half(k) * sin / scale
            return (q, k)

        def local_attention(q, k, v):
            b, h, n, d = q.shape
            w = n // WINDOW
            bq = q.reshape(b, h, w, WINDOW, d) * QK_SCALE
            bk = k.reshape(b, h, w, WINDOW, d)
            bv = v.reshape(b, h, w, WINDOW, d)

            def look_around(t):
                p = jnp.pad(t, ((0, 0), (0, 0), (1, 0), (0, 0), (0, 0)))
                return jnp.concatenate([p[:, :, :w], p[:, :, 1:]], axis=3)
            bk, bv = (look_around(bk), look_around(bv))
            bt = jnp.arange(n).reshape(w, WINDOW)
            btp = jnp.pad(bt, ((1, 0), (0, 0)), constant_values=-1)
            btk = jnp.concatenate([btp[:w], btp[1:]], axis=1)
            sim = jnp.einsum('bhwid,bhwjd->bhwij', bq, bk)
            i = bt[:, :, None]
            j = btk[:, None, :]
            mask = (i < j) | (i > j + WINDOW) | (j == -1)
            sim = jnp.where(mask, -jnp.finfo(sim.dtype).max, sim)
            attn = jax.nn.softmax(sim, axis=-1)
            out = jnp.einsum('bhwij,bhwjd->bhwid', attn, bv)
            return out.reshape(b, h, n, d)

        def _layer(x, wqkv, qs, ksc, wo, lg, lb, w1, b1, w2, b2):
            b, n, _ = x.shape
            h = shift_token(x)
            qkv = h @ wqkv
            q, k, v = jnp.split(qkv, 3, axis=-1)
            to_heads = lambda t: t.reshape(b, n, HEADS, DIM_HEAD).transpose(0, 2, 1, 3)
            q, k, v = (to_heads(q), to_heads(k), to_heads(v))
            q = l2norm(q) * qs
            k = l2norm(k) * ksc
            q, k = rotary_xpos(q, k)
            o = local_attention(q, k, v)
            o = o.transpose(0, 2, 1, 3).reshape(b, n, INNER)
            x = x + o @ wo
            h = shift_token(x)
            mu = h.mean(-1, keepdims=True)
            var = h.var(-1, keepdims=True)
            h = (h - mu) / jnp.sqrt(var + 1e-05) * lg + lb
            h = h @ w1 + b1
            a, g = jnp.split(h, 2, axis=-1)
            h = a * jax.nn.gelu(g, approximate=False)
            x = x + h @ w2 + b2
            return x
        key = jax.random.key(seed)
        ks = jax.random.split(key, 6)
        return {'x': jax.random.normal(ks[0], (B, N, DIM), jnp.float32), 'wqkv': jax.random.normal(ks[1], (DEPTH, DIM, 3 * INNER), jnp.float32) * 0.02, 'q_scale': jnp.ones((DEPTH, DIM_HEAD), jnp.float32), 'k_scale': jnp.ones((DEPTH, DIM_HEAD), jnp.float32), 'wo': jax.random.normal(ks[2], (DEPTH, INNER, DIM), jnp.float32) * 0.02, 'ln_g': jnp.ones((DEPTH, DIM), jnp.float32), 'ln_b': jnp.zeros((DEPTH, DIM), jnp.float32), 'w1': jax.random.normal(ks[3], (DEPTH, DIM, 2 * HID), jnp.float32) * 0.02, 'b1': jnp.zeros((DEPTH, 2 * HID), jnp.float32), 'w2': jax.random.normal(ks[4], (DEPTH, HID, DIM), jnp.float32) * 0.02, 'b2': jnp.zeros((DEPTH, DIM), jnp.float32)}
    _L0_ffn_all = _L0_ffn_setup()
    _L0_ffn_in = {k: v for k, v in _L0_ffn_all.items() if k in ('wqkv', 'q_scale', 'k_scale', 'wo', 'ln_g', 'ln_b', 'w1', 'b1', 'w2', 'b2')}
    del _L0_ffn_all

    def _L1_xattn_setup():
        import jax, jax.numpy as jnp
        import numpy as np
        NEG_INF = 1000000000.0
        key = jax.random.key(seed)
        kq, kv = jax.random.split(key)
        B, T, D = (4, 512, 256)
        query = jax.random.normal(kq, (B, T, D), dtype=jnp.float32)
        value = jax.random.normal(kv, (B, T, D), dtype=jnp.float32)
        return {'query': query, 'value': value}
    _L1_xattn_all = _L1_xattn_setup()
    _L1_xattn_in = {k: v for k, v in _L1_xattn_all.items() if k in ()}
    del _L1_xattn_all

    def _L1_ffn_setup():
        import math
        import jax, jax.numpy as jnp
        import numpy as np
        D_MODEL = 256
        D_HIDDEN = 512
        N_EXPERTS = 8
        TOP_K = 2
        CAPACITY_FACTOR = 1.25

        def _moe_forward(x, w_router, w_gate, w_down):
            B, T, D = x.shape
            N = B * T
            xf = x.reshape(N, D)
            logits = xf.astype(jnp.float32) @ w_router.T
            gates = jax.nn.softmax(logits, axis=-1)
            topk_gates, topk_idx = jax.lax.top_k(gates, TOP_K)
            expert_mask = jax.nn.one_hot(topk_idx, N_EXPERTS, dtype=jnp.int32).sum(axis=1)
            capacity = math.ceil(N / N_EXPERTS * CAPACITY_FACTOR)
            position_in_expert = jnp.cumsum(expert_mask, axis=0) - 1
            expert_mask = expert_mask * (position_in_expert < capacity)
            keep = jnp.take_along_axis(expert_mask, topk_idx, axis=1) > 0
            topk_gates = topk_gates * keep
            topk_gates = topk_gates / (topk_gates.sum(axis=-1, keepdims=True) + 1e-06)
            hidden = jax.nn.silu(xf @ w_gate.T)
            combine = (topk_gates[:, :, None] * jax.nn.one_hot(topk_idx, N_EXPERTS, dtype=topk_gates.dtype)).sum(axis=1)
            y = jnp.zeros((N, D), dtype=x.dtype)
            for e in range(N_EXPERTS):
                y = y + combine[:, e:e + 1] * (hidden @ w_down[e].T)
            return y.reshape(B, T, D)
        key = jax.random.key(seed)
        k0, k1, k2, k3 = jax.random.split(key, 4)
        B, T = (2, 512)
        x = jax.random.normal(k0, (B, T, D_MODEL), dtype=jnp.float32)
        w_router = jax.random.normal(k1, (N_EXPERTS, D_MODEL), dtype=jnp.float32) * 0.02
        w_gate = jax.random.normal(k2, (D_HIDDEN, D_MODEL), dtype=jnp.float32) * 0.02
        w_down = jax.random.normal(k3, (N_EXPERTS, D_MODEL, D_HIDDEN), dtype=jnp.float32) * 0.02
        return {'x': x, 'w_router': w_router, 'w_gate': w_gate, 'w_down': w_down}
    _L1_ffn_all = _L1_ffn_setup()
    _L1_ffn_in = {k: v for k, v in _L1_ffn_all.items() if k in ('w_router', 'w_gate', 'w_down')}
    del _L1_ffn_all

    def _L2_xattn_setup():
        import jax, jax.numpy as jnp
        import numpy as np
        D_MODEL = 256
        H = 16
        HEAD_DIM = D_MODEL // H
        key = jax.random.key(seed)
        ks = jax.random.split(key, 11)
        B, S, D = (1, 1024, D_MODEL)
        scale = 1.0 / np.sqrt(D)
        inp = {'q': jax.random.normal(ks[0], (B, S, D), jnp.float32), 'k': jax.random.normal(ks[1], (B, S, D), jnp.float32), 'v': jax.random.normal(ks[2], (B, S, D), jnp.float32), 'w_q': jax.random.normal(ks[3], (D, D), jnp.float32) * scale, 'b_q': jnp.zeros((D,), jnp.float32), 'w_k': jax.random.normal(ks[4], (D, D), jnp.float32) * scale, 'b_k': jnp.zeros((D,), jnp.float32), 'w_v': jax.random.normal(ks[5], (D, D), jnp.float32) * scale, 'b_v': jnp.zeros((D,), jnp.float32), 'w_o': jax.random.normal(ks[6], (D, D), jnp.float32) * scale, 'b_o': jnp.zeros((D,), jnp.float32)}
        return inp
    _L2_xattn_all = _L2_xattn_setup()
    _L2_xattn_in = {k: v for k, v in _L2_xattn_all.items() if k in ('w_q', 'b_q', 'w_k', 'b_k', 'w_v', 'b_v', 'w_o', 'b_o')}
    del _L2_xattn_all

    def _L2_ffn_setup():
        import jax, jax.numpy as jnp
        import numpy as np
        QMAX = 127.0

        def _ste_round(v):
            return v + jax.lax.stop_gradient(jnp.round(v) - v)

        def _act_fake_quant(x, clip_factor):
            scale = jax.nn.sigmoid(clip_factor) * jnp.max(jnp.abs(x)) / QMAX
            return jnp.clip(_ste_round(x / scale), -QMAX - 1.0, QMAX) * scale

        def _weight_fake_quant(w):
            scale = jnp.max(jnp.abs(w), axis=1, keepdims=True) / QMAX
            return jnp.clip(_ste_round(w / scale), -QMAX - 1.0, QMAX) * scale
        key = jax.random.key(seed)
        k1, k2, k3, k4 = jax.random.split(key, 4)
        B, S, H, I = (8, 2048, 256, 704)
        return {'x': jax.random.normal(k1, (B, S, H), dtype=jnp.float32), 'clip_x': jnp.full((1,), 4.0, dtype=jnp.float32), 'clip_down': jnp.full((1,), 4.0, dtype=jnp.float32), 'w_gate': jax.random.normal(k2, (I, H), dtype=jnp.float32) * 0.02, 'w_up': jax.random.normal(k3, (I, H), dtype=jnp.float32) * 0.02, 'w_down': jax.random.normal(k4, (H, I), dtype=jnp.float32) * 0.02}
    _L2_ffn_all = _L2_ffn_setup()
    _L2_ffn_in = {k: v for k, v in _L2_ffn_all.items() if k in ('clip_x', 'clip_down', 'w_gate', 'w_up', 'w_down')}
    del _L2_ffn_all

    def _L3_xattn_setup():
        import jax, jax.numpy as jnp
        import numpy as np
        DIM = 256
        NUM_HEADS = 16
        HEAD_DIM = DIM // NUM_HEADS

        def _slopes(num_heads):
            ratio = 2.0 ** (-8.0 / num_heads)
            return jnp.asarray([ratio ** i for i in range(1, num_heads + 1)], dtype=jnp.float32)
        key = jax.random.key(seed)
        ks = jax.random.split(key, 10)
        b, q_len, k_len = (2, 512, 1024)
        query = jax.random.normal(ks[0], (b, q_len, DIM), dtype=jnp.float32)
        keys = jax.random.normal(ks[1], (b, k_len, DIM), dtype=jnp.float32)
        values = jax.random.normal(ks[2], (b, k_len, DIM), dtype=jnp.float32)
        query_pos = jnp.sort(jax.random.randint(ks[3], (b, q_len), 0, 2048), axis=-1)
        key_pos = jnp.sort(jax.random.randint(ks[4], (b, k_len), 0, 2048), axis=-1)
        mask = jnp.ones((b, q_len, k_len), dtype=jnp.int32)
        lim = float(np.sqrt(6.0 / (DIM + DIM)))
        W_q = jax.random.uniform(ks[5], (DIM, DIM), minval=-lim, maxval=lim, dtype=jnp.float32)
        W_k = jax.random.uniform(ks[6], (DIM, DIM), minval=-lim, maxval=lim, dtype=jnp.float32)
        W_v = jax.random.uniform(ks[7], (DIM, DIM), minval=-lim, maxval=lim, dtype=jnp.float32)
        W_o = jax.random.uniform(ks[8], (DIM, DIM), minval=-lim, maxval=lim, dtype=jnp.float32)
        return {'query': query, 'keys': keys, 'values': values, 'W_q': W_q, 'W_k': W_k, 'W_v': W_v, 'W_o': W_o, 'query_pos': query_pos, 'key_pos': key_pos, 'mask': mask}
    _L3_xattn_all = _L3_xattn_setup()
    _L3_xattn_in = {k: v for k, v in _L3_xattn_all.items() if k in ('W_q', 'W_k', 'W_v', 'W_o')}
    del _L3_xattn_all

    def _L3_ffn_setup():
        import jax, jax.numpy as jnp
        import numpy as np
        D_MODEL, D_FF, N_EXPERTS, TOP_K = (256, 512, 8, 2)
        B, S = (2, 512)
        key = jax.random.key(seed)
        k1, k2, k3, k4 = jax.random.split(key, 4)
        scale = 0.02
        return {'x': jax.random.normal(k1, (B, S, D_MODEL), dtype=jnp.float32), 'gate_w': jax.random.normal(k2, (D_MODEL, N_EXPERTS), dtype=jnp.float32) * scale, 'w1': jax.random.normal(k3, (N_EXPERTS, D_MODEL, D_FF), dtype=jnp.float32) * scale, 'w2': jax.random.normal(k4, (N_EXPERTS, D_FF, D_MODEL), dtype=jnp.float32) * scale}
    _L3_ffn_all = _L3_ffn_setup()
    _L3_ffn_in = {k: v for k, v in _L3_ffn_all.items() if k in ('gate_w', 'w1', 'w2')}
    del _L3_ffn_all
    return {'x': x, 'ctx_1024': ctx_1024, 'itok_BxS_8_8191': itok_BxS_8_8191, 'itok_BxS2_1_8191': itok_BxS2_1_8191, 'mask_BxSxS2_if1': mask_BxSxS2_if1, 'L0_xattn_w_cq': _L0_xattn_in['w_cq'], 'L0_xattn_b_cq': _L0_xattn_in['b_cq'], 'L0_xattn_w_c': _L0_xattn_in['w_c'], 'L0_xattn_b_c': _L0_xattn_in['b_c'], 'L0_xattn_w_q': _L0_xattn_in['w_q'], 'L0_xattn_b_q': _L0_xattn_in['b_q'], 'L0_xattn_W_l': _L0_xattn_in['W_l'], 'L0_xattn_b_l': _L0_xattn_in['b_l'], 'L0_ffn_wqkv': _L0_ffn_in['wqkv'], 'L0_ffn_q_scale': _L0_ffn_in['q_scale'], 'L0_ffn_k_scale': _L0_ffn_in['k_scale'], 'L0_ffn_wo': _L0_ffn_in['wo'], 'L0_ffn_ln_g': _L0_ffn_in['ln_g'], 'L0_ffn_ln_b': _L0_ffn_in['ln_b'], 'L0_ffn_w1': _L0_ffn_in['w1'], 'L0_ffn_b1': _L0_ffn_in['b1'], 'L0_ffn_w2': _L0_ffn_in['w2'], 'L0_ffn_b2': _L0_ffn_in['b2'], 'L1_ffn_w_router': _L1_ffn_in['w_router'], 'L1_ffn_w_gate': _L1_ffn_in['w_gate'], 'L1_ffn_w_down': _L1_ffn_in['w_down'], 'L2_xattn_w_q': _L2_xattn_in['w_q'], 'L2_xattn_b_q': _L2_xattn_in['b_q'], 'L2_xattn_w_k': _L2_xattn_in['w_k'], 'L2_xattn_b_k': _L2_xattn_in['b_k'], 'L2_xattn_w_v': _L2_xattn_in['w_v'], 'L2_xattn_b_v': _L2_xattn_in['b_v'], 'L2_xattn_w_o': _L2_xattn_in['w_o'], 'L2_xattn_b_o': _L2_xattn_in['b_o'], 'L2_ffn_clip_x': _L2_ffn_in['clip_x'], 'L2_ffn_clip_down': _L2_ffn_in['clip_down'], 'L2_ffn_w_gate': _L2_ffn_in['w_gate'], 'L2_ffn_w_up': _L2_ffn_in['w_up'], 'L2_ffn_w_down': _L2_ffn_in['w_down'], 'L3_xattn_W_q': _L3_xattn_in['W_q'], 'L3_xattn_W_k': _L3_xattn_in['W_k'], 'L3_xattn_W_v': _L3_xattn_in['W_v'], 'L3_xattn_W_o': _L3_xattn_in['W_o'], 'L3_ffn_gate_w': _L3_ffn_in['gate_w'], 'L3_ffn_w1': _L3_ffn_in['w1'], 'L3_ffn_w2': _L3_ffn_in['w2']}

def reference(x, ctx_1024, itok_BxS_8_8191, itok_BxS2_1_8191, mask_BxSxS2_if1, L0_xattn_w_cq, L0_xattn_b_cq, L0_xattn_w_c, L0_xattn_b_c, L0_xattn_w_q, L0_xattn_b_q, L0_xattn_W_l, L0_xattn_b_l, L0_ffn_wqkv, L0_ffn_q_scale, L0_ffn_k_scale, L0_ffn_wo, L0_ffn_ln_g, L0_ffn_ln_b, L0_ffn_w1, L0_ffn_b1, L0_ffn_w2, L0_ffn_b2, L1_ffn_w_router, L1_ffn_w_gate, L1_ffn_w_down, L2_xattn_w_q, L2_xattn_b_q, L2_xattn_w_k, L2_xattn_b_k, L2_xattn_w_v, L2_xattn_b_v, L2_xattn_w_o, L2_xattn_b_o, L2_ffn_clip_x, L2_ffn_clip_down, L2_ffn_w_gate, L2_ffn_w_up, L2_ffn_w_down, L3_xattn_W_q, L3_xattn_W_k, L3_xattn_W_v, L3_xattn_W_o, L3_ffn_gate_w, L3_ffn_w1, L3_ffn_w2):
    import jax
    import jax.numpy as jnp

    def _L0_xattn_ref(c, q, w_cq, b_cq, w_c, b_c, w_q, b_q, W_l, b_l):
        import jax, jax.numpy as jnp
        import numpy as np
        B, C_LEN, Q_LEN, D = (8, 512, 128, 256)
        cq = jnp.einsum('bcd,bqd,d->bcq', c, q, w_cq) + b_cq
        s = (c @ w_c + b_c)[:, :, None] + (q @ w_q + b_q)[:, None, :] + cq
        a = jax.nn.softmax(s, axis=2)
        c2q_att = jnp.einsum('bcq,bqd->bcd', a, q)
        b_att = jax.nn.softmax(jnp.max(s, axis=2), axis=1)
        q2c_att = jnp.einsum('bc,bcd->bd', b_att, c)[:, None, :]
        x = jnp.concatenate([c, c2q_att, c * c2q_att, c * q2c_att], axis=-1)
        z = x @ W_l.T + b_l
        return z

    def _L0_ffn_ref(x, wqkv, q_scale, k_scale, wo, ln_g, ln_b, w1, b1, w2, b2):
        import jax, jax.numpy as jnp
        import numpy as np
        DIM = 256
        DEPTH = 2
        HEADS = 8
        DIM_HEAD = 64
        WINDOW = 128
        INNER = HEADS * DIM_HEAD
        HID = int(DIM * 4 * 2 / 3)
        B, N = (2, 2048)
        QK_SCALE = 8.0

        def shift_token(t):
            t1, t2 = jnp.split(t, 2, axis=-1)
            t2 = jnp.pad(t2, ((0, 0), (1, 0), (0, 0)))[:, :-1]
            return jnp.concatenate([t1, t2], axis=-1)

        def l2norm(t):
            return t / jnp.clip(jnp.linalg.norm(t, axis=-1, keepdims=True), 1e-12)

        def rotate_half(x):
            x1, x2 = jnp.split(x, 2, axis=-1)
            return jnp.concatenate([-x2, x1], axis=-1)

        def rotary_xpos(q, k):
            n = q.shape[-2]
            half_idx = jnp.arange(0, DIM_HEAD, 2, dtype=jnp.float32)
            inv_freq = 1.0 / 10000.0 ** (half_idx / DIM_HEAD)
            t = jnp.arange(n, dtype=jnp.float32)
            freqs = t[:, None] * inv_freq[None, :]
            freqs = jnp.concatenate([freqs, freqs], axis=-1)
            base = (half_idx + 0.4 * DIM_HEAD) / (1.4 * DIM_HEAD)
            power = (t - n // 2) / float(WINDOW // 2)
            scale = base[None, :] ** power[:, None]
            scale = jnp.concatenate([scale, scale], axis=-1)
            cos, sin = (jnp.cos(freqs), jnp.sin(freqs))
            q = q * cos * scale + rotate_half(q) * sin * scale
            k = k * cos / scale + rotate_half(k) * sin / scale
            return (q, k)

        def local_attention(q, k, v):
            b, h, n, d = q.shape
            w = n // WINDOW
            bq = q.reshape(b, h, w, WINDOW, d) * QK_SCALE
            bk = k.reshape(b, h, w, WINDOW, d)
            bv = v.reshape(b, h, w, WINDOW, d)

            def look_around(t):
                p = jnp.pad(t, ((0, 0), (0, 0), (1, 0), (0, 0), (0, 0)))
                return jnp.concatenate([p[:, :, :w], p[:, :, 1:]], axis=3)
            bk, bv = (look_around(bk), look_around(bv))
            bt = jnp.arange(n).reshape(w, WINDOW)
            btp = jnp.pad(bt, ((1, 0), (0, 0)), constant_values=-1)
            btk = jnp.concatenate([btp[:w], btp[1:]], axis=1)
            sim = jnp.einsum('bhwid,bhwjd->bhwij', bq, bk)
            i = bt[:, :, None]
            j = btk[:, None, :]
            mask = (i < j) | (i > j + WINDOW) | (j == -1)
            sim = jnp.where(mask, -jnp.finfo(sim.dtype).max, sim)
            attn = jax.nn.softmax(sim, axis=-1)
            out = jnp.einsum('bhwij,bhwjd->bhwid', attn, bv)
            return out.reshape(b, h, n, d)

        def _layer(x, wqkv, qs, ksc, wo, lg, lb, w1, b1, w2, b2):
            b, n, _ = x.shape
            h = shift_token(x)
            qkv = h @ wqkv
            q, k, v = jnp.split(qkv, 3, axis=-1)
            to_heads = lambda t: t.reshape(b, n, HEADS, DIM_HEAD).transpose(0, 2, 1, 3)
            q, k, v = (to_heads(q), to_heads(k), to_heads(v))
            q = l2norm(q) * qs
            k = l2norm(k) * ksc
            q, k = rotary_xpos(q, k)
            o = local_attention(q, k, v)
            o = o.transpose(0, 2, 1, 3).reshape(b, n, INNER)
            x = x + o @ wo
            h = shift_token(x)
            mu = h.mean(-1, keepdims=True)
            var = h.var(-1, keepdims=True)
            h = (h - mu) / jnp.sqrt(var + 1e-05) * lg + lb
            h = h @ w1 + b1
            a, g = jnp.split(h, 2, axis=-1)
            h = a * jax.nn.gelu(g, approximate=False)
            x = x + h @ w2 + b2
            return x
        for l in range(DEPTH):
            x = _layer(x, wqkv[l], q_scale[l], k_scale[l], wo[l], ln_g[l], ln_b[l], w1[l], b1[l], w2[l], b2[l])
        return x

    def _L1_xattn_ref(query, value):
        import jax, jax.numpy as jnp
        import numpy as np
        NEG_INF = 1000000000.0
        k = value
        scores = jnp.einsum('bqd,bkd->bqk', query, k)
        Tq, Tv = (scores.shape[-2], scores.shape[-1])
        causal_mask = jnp.tril(jnp.ones((Tq, Tv), dtype=bool))
        scores = scores - NEG_INF * (~causal_mask).astype(scores.dtype)
        weights = jax.nn.softmax(scores, axis=-1)
        result = jnp.einsum('bqv,bvd->bqd', weights, value)
        return result

    def _L1_ffn_ref(x, w_router, w_gate, w_down):
        import math
        import jax, jax.numpy as jnp
        import numpy as np
        D_MODEL = 256
        D_HIDDEN = 512
        N_EXPERTS = 8
        TOP_K = 2
        CAPACITY_FACTOR = 1.25

        def _moe_forward(x, w_router, w_gate, w_down):
            B, T, D = x.shape
            N = B * T
            xf = x.reshape(N, D)
            logits = xf.astype(jnp.float32) @ w_router.T
            gates = jax.nn.softmax(logits, axis=-1)
            topk_gates, topk_idx = jax.lax.top_k(gates, TOP_K)
            expert_mask = jax.nn.one_hot(topk_idx, N_EXPERTS, dtype=jnp.int32).sum(axis=1)
            capacity = math.ceil(N / N_EXPERTS * CAPACITY_FACTOR)
            position_in_expert = jnp.cumsum(expert_mask, axis=0) - 1
            expert_mask = expert_mask * (position_in_expert < capacity)
            keep = jnp.take_along_axis(expert_mask, topk_idx, axis=1) > 0
            topk_gates = topk_gates * keep
            topk_gates = topk_gates / (topk_gates.sum(axis=-1, keepdims=True) + 1e-06)
            hidden = jax.nn.silu(xf @ w_gate.T)
            combine = (topk_gates[:, :, None] * jax.nn.one_hot(topk_idx, N_EXPERTS, dtype=topk_gates.dtype)).sum(axis=1)
            y = jnp.zeros((N, D), dtype=x.dtype)
            for e in range(N_EXPERTS):
                y = y + combine[:, e:e + 1] * (hidden @ w_down[e].T)
            return y.reshape(B, T, D)
        return _moe_forward(x, w_router, w_gate, w_down)

    def _L2_xattn_ref(q, k, v, w_q, b_q, w_k, b_k, w_v, b_v, w_o, b_o):
        import jax, jax.numpy as jnp
        import numpy as np
        D_MODEL = 256
        H = 16
        HEAD_DIM = D_MODEL // H
        B, Sq, D = q.shape
        Sk = k.shape[1]
        Q = (q @ w_q.T + b_q).reshape(B, Sq, H, HEAD_DIM).transpose(0, 2, 1, 3)
        K = (k @ w_k.T + b_k).reshape(B, Sk, H, HEAD_DIM).transpose(0, 2, 1, 3)
        V = (v @ w_v.T + b_v).reshape(B, Sk, H, HEAD_DIM).transpose(0, 2, 1, 3)
        scores = jnp.einsum('bhqd,bhkd->bhqk', Q, K) / jnp.sqrt(jnp.float32(HEAD_DIM))
        attn = jax.nn.softmax(scores, axis=-1)
        ctx = jnp.einsum('bhqk,bhkd->bhqd', attn, V)
        concat = ctx.transpose(0, 2, 1, 3).reshape(B, Sq, D)
        return concat @ w_o.T + b_o

    def _L2_ffn_ref(x, clip_x, clip_down, w_gate, w_up, w_down):
        import jax, jax.numpy as jnp
        import numpy as np
        QMAX = 127.0

        def _ste_round(v):
            return v + jax.lax.stop_gradient(jnp.round(v) - v)

        def _act_fake_quant(x, clip_factor):
            scale = jax.nn.sigmoid(clip_factor) * jnp.max(jnp.abs(x)) / QMAX
            return jnp.clip(_ste_round(x / scale), -QMAX - 1.0, QMAX) * scale

        def _weight_fake_quant(w):
            scale = jnp.max(jnp.abs(w), axis=1, keepdims=True) / QMAX
            return jnp.clip(_ste_round(w / scale), -QMAX - 1.0, QMAX) * scale
        xq = _act_fake_quant(x, clip_x[0])
        gate = jnp.einsum('bsh,ih->bsi', xq, _weight_fake_quant(w_gate))
        up = jnp.einsum('bsh,ih->bsi', xq, _weight_fake_quant(w_up))
        h = _act_fake_quant(jax.nn.silu(gate) * up, clip_down[0])
        return jnp.einsum('bsi,hi->bsh', h, _weight_fake_quant(w_down))

    def _L3_xattn_ref(query, keys, values, W_q, W_k, W_v, W_o, query_pos, key_pos, mask):
        import jax, jax.numpy as jnp
        import numpy as np
        DIM = 256
        NUM_HEADS = 16
        HEAD_DIM = DIM // NUM_HEADS

        def _slopes(num_heads):
            ratio = 2.0 ** (-8.0 / num_heads)
            return jnp.asarray([ratio ** i for i in range(1, num_heads + 1)], dtype=jnp.float32)
        b, q_len, _ = query.shape
        k_len = keys.shape[1]
        scale = 1.0 / np.sqrt(HEAD_DIM)
        Q = (query @ W_q.T).reshape(b, q_len, NUM_HEADS, HEAD_DIM).transpose(0, 2, 1, 3)
        K = (keys @ W_k.T).reshape(b, k_len, NUM_HEADS, HEAD_DIM).transpose(0, 2, 1, 3)
        V = (values @ W_v.T).reshape(b, k_len, NUM_HEADS, HEAD_DIM).transpose(0, 2, 1, 3)
        scores = jnp.einsum('bhqd,bhkd->bhqk', Q, K) * scale
        dist = (query_pos[:, :, None] - key_pos[:, None, :]).astype(scores.dtype)
        bias = -_slopes(NUM_HEADS)[None, :, None, None] * dist[:, None, :, :]
        scores = scores + bias
        scores = jnp.where(mask[:, None, :, :] == 0, -jnp.inf, scores)
        m = jnp.max(scores, axis=-1, keepdims=True)
        e = jnp.exp(scores - m)
        attn = e / (1.0 + jnp.sum(e, axis=-1, keepdims=True))
        out = jnp.einsum('bhqk,bhkd->bhqd', attn, V)
        out = out.transpose(0, 2, 1, 3).reshape(b, q_len, DIM)
        return out @ W_o.T

    def _L3_ffn_ref(x, gate_w, w1, w2):
        import jax, jax.numpy as jnp
        import numpy as np
        D_MODEL, D_FF, N_EXPERTS, TOP_K = (256, 512, 8, 2)
        B, S = (2, 512)
        router_logits = jnp.einsum('bsd,de->bse', x, gate_w)
        top_logits, top_idx = jax.lax.top_k(router_logits, TOP_K)
        top_w = jax.nn.softmax(top_logits, axis=-1)
        combine = jnp.sum(jax.nn.one_hot(top_idx, N_EXPERTS, dtype=x.dtype) * top_w[..., None], axis=-2)
        h = jax.nn.silu(jnp.einsum('bsd,edf->ebsf', x, w1))
        y = jnp.einsum('ebsf,efd->ebsd', h, w2)
        out = jnp.einsum('ebsd,bse->bsd', y, combine)
        return out
    x = x + _L0_xattn_ref(_layernorm(x, axis=-1), ctx_1024, L0_xattn_w_cq, L0_xattn_b_cq, L0_xattn_w_c, L0_xattn_b_c, L0_xattn_w_q, L0_xattn_b_q, L0_xattn_W_l, L0_xattn_b_l)
    x = x + _L0_ffn_ref(_layernorm(x, axis=-1), L0_ffn_wqkv, L0_ffn_q_scale, L0_ffn_k_scale, L0_ffn_wo, L0_ffn_ln_g, L0_ffn_ln_b, L0_ffn_w1, L0_ffn_b1, L0_ffn_w2, L0_ffn_b2)
    x = x + _L1_xattn_ref(_layernorm(x, axis=-1), ctx_1024)
    x = x + _L1_ffn_ref(_layernorm(x, axis=-1), L1_ffn_w_router, L1_ffn_w_gate, L1_ffn_w_down)
    x = x + _L2_xattn_ref(_layernorm(x, axis=-1), ctx_1024, ctx_1024, L2_xattn_w_q, L2_xattn_b_q, L2_xattn_w_k, L2_xattn_b_k, L2_xattn_w_v, L2_xattn_b_v, L2_xattn_w_o, L2_xattn_b_o)
    x = x + _L2_ffn_ref(_layernorm(x, axis=-1), L2_ffn_clip_x, L2_ffn_clip_down, L2_ffn_w_gate, L2_ffn_w_up, L2_ffn_w_down)
    x = x + _L3_xattn_ref(_layernorm(x, axis=-1), ctx_1024, ctx_1024, L3_xattn_W_q, L3_xattn_W_k, L3_xattn_W_v, L3_xattn_W_o, itok_BxS_8_8191, itok_BxS2_1_8191, mask_BxSxS2_if1)
    x = x + _L3_ffn_ref(_layernorm(x, axis=-1), L3_ffn_gate_w, L3_ffn_w1, L3_ffn_w2)
    return x

_drawn_inputs = setup_inputs


def setup_inputs(seed=0):
    import zlib

    import numpy as np

    out = dict(_drawn_inputs(seed))
    spreads = {'L0_ffn_q_scale': (1.0, 0.6),
     'L0_ffn_k_scale': (1.0, 0.6),
     'L0_ffn_ln_g': (1.0, 0.6),
     'L0_ffn_ln_b': (0.0, 0.8),
     'L0_ffn_b1': (0.0, 0.644),
     'L0_ffn_b2': (0.0, 0.1),
     'L2_xattn_b_q': (0.0, 0.8),
     'L2_xattn_b_k': (0.0, 0.8),
     'L2_xattn_b_v': (0.0, 0.1),
     'L2_xattn_b_o': (0.0, 0.1)}
    factors = {'L1_ffn_w_router': 3.305,
     'L1_ffn_w_gate': 3.137,
     'L1_ffn_w_down': 3.094,
     'L2_ffn_w_gate': 5.091,
     'L2_ffn_w_up': 4.844,
     'L2_ffn_w_down': 4.805,
     'L3_ffn_gate_w': 3.272,
     'L3_ffn_w1': 2.881,
     'L3_ffn_w2': 2.853}
    for name, (base, spread) in spreads.items():
        noise = np.random.default_rng([zlib.crc32(name.encode()), seed]).standard_normal(out[name].shape)
        drawn = base * np.exp(spread * noise) if base else spread * noise
        out[name] = jnp.asarray(drawn.astype(out[name].dtype))
    for name, factor in factors.items():
        out[name] = (out[name] * factor).astype(out[name].dtype)
    return out
```

```python
from contextlib import ExitStack

import numpy as np

import concourse.bass as bass
from concourse import mybir

ALU = mybir.AluOpType
ACT = mybir.ActivationFunctionType
AX = mybir.AxisListType
F32 = mybir.dt.float32
BF16 = mybir.dt.bfloat16
I32 = mybir.dt.int32
U32 = mybir.dt.uint32

P = 128
BATCH, SEQ, D = 2, 1024, 256
CTX = 64
DCH = D // P
TILES = SEQ // P
ALL_TILES = BATCH * TILES
EPS = 1e-5
MASKED = -1e30
LIFT = 16


class Signal:

    def __init__(self, sem):
        self.sem, self.base, self.per = sem, LIFT, 0

    def each(self, per):
        assert per <= LIFT
        self.per = per

    def at(self, turn, k=1):
        return turn * self.per + (self.base + k)

    def before(self, turn, k=1):
        return turn * self.per + (self.base + k - self.per)

    def close(self, turns=1):
        self.base += self.per * turns


class Chain:

    def __init__(self, sem):
        self.sem = sem

    def begin(self, engine):
        self.engine, self.n = engine, 0
        engine.sem_clear(self.sem)

    def link(self, instruction):
        self.n += 1
        instruction.then_inc(self.sem, 1)
        self.engine.wait_ge(self.sem, self.n)


def memory(e, ctx, stage):
    return lambda name, shape, dt=F32: ctx.enter_context(e.nc.sbuf_tensor(f"{stage}_{name}", shape, dt))


def flat(ap):
    return ap.rearrange("p a b -> p (a b)")


def tile_of(buf, it, b):
    return flat(buf[:, bass.ds(it + b * TILES, 1), :])


class Signals:

    def __init__(self, new):
        self.ln_var = new("ln_var")
        self.ln_rstd = new("ln_rstd")
        self.cT_psum = new("cT_psum")
        self.c_ready = new("c_ready")
        self.cT_ready = new("cT_ready")
        self.prep_psum = new("prep_psum")
        self.c_kept = new("c_kept")
        self.scores_psum = new("scores_psum")
        self.max_ready = new("max_ready")
        self.probs_ready = new("probs_ready")
        self.probsT_psum = new("probsT_psum")
        self.probsT_ready = new("probsT_ready")
        self.mix_psum = new("mix_psum")
        self.mix_ready = new("mix_ready")
        self.mixT_psum = new("mixT_psum")
        self.mixT_ready = new("mixT_ready")
        self.out_psum = new("out_psum")
        self.x_done = new("x_done")
        self.allreduce = new("allreduce")
        self.sums_psum = new("sums_psum")
        self.ys_ready = new("ys_ready")
        self.yT_psum = new("yT_psum")
        self.hT_ready = new("hT_ready")
        self.qkv_psum = new("qkv_psum")
        self.sq_ready = new("sq_ready")
        self.v_ready = new("v_ready")
        self.ss_ready = new("ss_ready")
        self.norm_ready = new("norm_ready")
        self.q_norm_ready = new("q_norm_ready")
        self.rot_ready = new("rot_ready")
        self.qkT_psum = new("qkT_psum")
        self.qT_ready = new("qT_ready")
        self.kT_ready = new("kT_ready")
        self.bias_ready = new("bias_ready")
        self.mixed_psum = new("mixed_psum")
        self.y1_ready = new("y1_ready")
        self.shift_psum = new("shift_psum")
        self.shift_var = new("shift_var")
        self.shift_rstd = new("shift_rstd")
        self.h2_ready = new("h2_ready")
        self.h2T_psum = new("h2T_psum")
        self.h2T_ready = new("h2T_ready")
        self.y1b_ready = new("y1b_ready")
        self.ffn_out = new("ffn_out")
        self.y_done = new("y_done")
        self.pT_act = new("pT_act")
        self.pT_dve = new("pT_dve")
        self.hid_psum = new("hid_psum")
        self.gate_ready = new("gate_ready")
        self.ff_ready = new("ff_ready")
        self.mask_ready = new("mask_ready")
        self.logits_psum = new("logits_psum")
        self.routed = new("routed")
        self.hidden_psum = new("hidden_psum")
        self.hidden_ready = new("hidden_ready")
        self.expert_psum = new("expert_psum")
        self.expert_added = new("expert_added")
        self.prep_ready = new("prep_ready")
        self.prep_last = new("prep_last")
        self.probsT_ready2 = new("probsT_ready2")
        self.row_ready = new("row_ready")
        self.gate_done = new("gate_done")


class Env:

    def __init__(self, nc, dram, out):
        self.nc, self.dram, self.out = nc, dram, out


def build(nc, dram, out):
    with ExitStack() as ctx:
        def sem(name):
            return ctx.enter_context(nc.semaphore(name))

        e = Env(nc, dram, out)
        sb = lambda name, shape, dt=F32: ctx.enter_context(nc.sbuf_tensor(name, shape, dt))
        e.psum = ctx.enter_context(nc.psum_tensor("banks", [P, 8, 512], F32))
        e.ps = [e.psum[:, i, :] for i in range(8)]
        e.x = sb("x_res", [P, ALL_TILES, D])
        e.cs = sb("c_tile", [P, BATCH, D])
        e.cT = sb("cT", [P, BATCH, DCH, P])
        e.ident = sb("ident", [P, P])
        e.ident_bf = sb("ident_bf", [P, P], BF16)
        e.ones = sb("ones", [P, P])
        e.neg_half = sb("neg_half", [P, 16])
        e.ctxT = sb("ctxT", [P, DCH, BATCH, CTX])
        e.ctxT2 = sb("ctxT2", [P, DCH, BATCH, 2, CTX])
        e.ctx_tok = sb("ctx_tok", [P, BATCH, D])
        e.bn = sb("bn", [P, BATCH, 6])
        e.mv = sb("mv", [P, BATCH, 2])
        e.zero_eps = sb("zero_eps", [P, 2])
        e.mean_var = sb("mean_var", [P, ALL_TILES, 2])
        e.rstd = sb("rstd", [P, ALL_TILES])
        e.signals = []

        def new(name):
            e.signals.append(Signal(sem(name)))
            return e.signals[-1]

        e.s, e.dma_sem = Signals(new), sem
        e.chain = {n: Chain(sem(f"{n}_order")) for n in ("dve", "act", "pool", "pe")}
        e.loaded = sem("loaded")
        e.stored = sem("stored")
        e.loads = 0

        prologue(e)
        for stage in (l0_xattn, l0_ffn, l1_xattn, l1_ffn, l2_xattn, l2_ffn, l3_xattn, l3_ffn):
            stage(e)
        finish(e)


def begin(per, *signals):
    for n in signals:
        n.each(per)


def end(turns, *signals):
    for n in signals:
        n.close(turns)


def stats_dve(e, v, it, b):
    s, dve, row = e.s, e.chain["dve"], tile_of(e.x, it, b)
    dve.link(v.bn_stats(e.bn[:, b, :], row))
    dve.link(v.bn_aggr(e.mv[:, b, :], e.bn[:, b, :]))
    v.tensor_tensor(flat(e.mean_var[:, bass.ds(it + b * TILES, 1), :]), e.mv[:, b, :], e.zero_eps[:], ALU.add)\
     .then_inc(s.ln_var.sem, 1)


def stats_pool(e, p, it, b):
    s, k = e.s, it + b * TILES
    p.wait_ge(s.ln_var.sem, s.ln_var.at(it, b + 1))
    p.tensor_tensor(e.rstd[:, bass.ds(k, 1)], flat(e.mean_var[:, bass.ds(k, 1), 1:2]), e.neg_half[:, 0:1], ALU.pow)\
     .then_inc(s.ln_rstd.sem, 1)


def normalise(e, v, it, b):
    s, k = e.s, it + b * TILES
    v.wait_ge(s.cT_psum.sem, s.cT_psum.before(it, b + 1))
    v.tensor_scalar(e.cs[:, b, :], tile_of(e.x, it, b), flat(e.mean_var[:, bass.ds(k, 1), 0:1]), e.rstd[:, bass.ds(k, 1)],
                    ALU.subtract, ALU.mult).then_inc(s.c_ready.sem, 1)


def transpose_c(e, pe, it, b, bank):
    s = e.s
    pe.wait_ge(s.c_ready.sem, s.c_ready.at(it, b + 1))
    pe.wait_ge(s.cT_ready.sem, s.cT_ready.before(it, b + 1))
    for ch in range(DCH):
        mm = pe.transpose(e.ps[bank][:, ch * P:(ch + 1) * P], e.cs[:, b, ch * P:(ch + 1) * P], e.ident[:])
    mm.then_inc(s.cT_psum.sem, 1)


def copy_cT(e, act, it, b, bank, used):
    s = e.s
    act.wait_ge(s.cT_psum.sem, s.cT_psum.at(it, b + 1))
    act.wait_ge(used.sem, used.before(it, b + 1))
    e.nc.scalar.copy(flat(e.cT[:, b, :, :]), e.ps[bank][:, 0:D]).then_inc(s.cT_ready.sem, 1)


def prologue(e):
    nc, s, d = e.nc, e.s, e.dram
    for n in (s.ln_var, s.ln_rstd):
        n.each(2)
    with nc.Block() as block:
        @block.sync
        def _(sp):
            for one in e.signals:
                sp.sem_inc(one.sem, LIFT)
    with nc.Block() as block:
        @block.sync
        def _(sp):
            for to, of in ((e.x, "x"), (e.ident, "ident"), (e.ctxT, "ctxT"), (e.ctxT2, "ctxT2"), (e.ctx_tok, "ctx_tok")):
                sp.dma_start(to[:], d[of]).then_inc(e.loaded, 16)
                e.loads += 16

        @block.gpsimd
        def _(p):
            chain = e.chain["pool"]
            chain.begin(p)
            chain.link(p.memset(e.neg_half[:], -0.5))
            p.memset(e.ones[:], 1.0)
            with p.Fori(0, TILES) as it:
                for b in range(BATCH):
                    stats_pool(e, p, it, b)

        @block.vector
        def _(v):
            dve = e.chain["dve"]
            dve.begin(v)
            v.memset(e.zero_eps[:, 0:1], 0.0)
            dve.link(v.memset(e.zero_eps[:, 1:2], EPS))
            v.wait_ge(e.loaded, e.loads)
            v.tensor_copy(e.ident_bf[:], e.ident[:])
            with v.Fori(0, TILES) as it:
                e.chain["dve"].begin(v)
                for b in range(BATCH):
                    stats_dve(e, v, it, b)
    for n in (s.ln_var, s.ln_rstd):
        n.close(TILES)


def l0_xattn(e):
    nc, s, d, ps = e.nc, e.s, e.dram, e.ps
    with ExitStack() as ctx:
        sb = memory(e, ctx, "l0_xattn")
        w_l = sb("w_l", [P, 8, D])
        wcol = sb("wcol", [P, DCH, 3])
        b3 = sb("b3", [P, 3])
        b_l = sb("b_l", [1, D])
        qcat = sb("qcat", [P, DCH, BATCH, CTX])
        b_sum = sb("b_sum", [1, 1])
        q_bias = sb("q_bias", [1, BATCH * CTX])
        c_all = sb("c_all", [P, ALL_TILES, D])
        nmax = sb("nmax", [P, ALL_TILES])
        a = sb("a", [P, 2, CTX])
        a_sum = sb("a_sum", [P, 2])
        a_rec = sb("a_rec", [P, 2])
        aT = sb("aT", [P, P])
        uv = sb("uv", [P, 2, 2, D])
        uvT = sb("uvT", [P, 2, 4, P])
        top = sb("top", [P, BATCH])
        gtop = sb("gtop", [P, BATCH])
        ngtop = sb("ngtop", [P, BATCH])
        b_att = sb("b_att", [P, ALL_TILES])
        b_att_sum = sb("b_att_sum", [P, BATCH])
        rden = sb("rden", [P, BATCH])
        q2c = sb("q2c", [P, BATCH, DCH])
        w_c = sb("w_c", [P, BATCH, DCH, D])
        dve, act, pool = (e.chain[n] for n in ("dve", "act", "pool"))

        with nc.Block() as block:
            @block.sync
            def _(sp):
                for to, of in ((w_l, "L0_W_l"), (wcol, "L0_w3"), (b3, "L0_b3"), (b_l, "L0_b_l")):
                    sp.dma_start(to[:], d[of]).then_inc(e.loaded, 16)
                    e.loads += 16

            s.prep_psum.each(1)

            @block.tensor
            def _(pe):
                pe.wait_ge(e.loaded, e.loads)
                for ch in range(DCH):
                    mm = pe.matmul(ps[0][0:1, 0:BATCH * CTX], wcol[:, ch, 2:3], e.ctxT[:, ch, :, :],
                                   start=ch == 0, stop=ch == DCH - 1)
                mm.then_inc(s.prep_psum.sem, 1)

            @block.vector
            def _(v):
                v.wait_ge(e.loaded, e.loads)
                for ch in range(DCH):
                    v.tensor_scalar(qcat[:, ch, :, :], e.ctxT[:, ch, :, :], wcol[:, ch, 0:1],
                                    wcol[:, ch, 1:2], ALU.mult, ALU.add)
                dve.begin(v)
                dve.link(v.tensor_reduce(b_sum[:], b3[0:1, :], AX.X, ALU.add))
                v.wait_ge(s.prep_psum.sem, s.prep_psum.at(0))
                v.tensor_scalar(q_bias[:], ps[0][0:1, 0:BATCH * CTX], b_sum[0:1, 0:1], None, ALU.add)
        s.prep_psum.close()

        two = (s.c_ready, s.c_kept, s.cT_psum, s.cT_ready, s.scores_psum, s.max_ready, s.probs_ready, s.probsT_psum,
               s.probsT_ready, s.mix_psum, s.mix_ready, s.mixT_psum, s.mixT_ready, s.out_psum, s.x_done)
        for n in two:
            n.each(2)
        s.probsT_psum.each(1)
        s.probsT_ready.each(1)
        with nc.Block() as block:
            @block.tensor
            def _(pe):
                with pe.Fori(0, TILES) as it:
                    for b in range(BATCH):
                        transpose_c(e, pe, it, b, b)
                    for b in range(BATCH):
                        pe.wait_ge(s.cT_ready.sem, s.cT_ready.at(it, b + 1))
                        pe.wait_ge(s.x_done.sem, s.x_done.before(it, b + 1))
                        for ch in range(DCH):
                            pe.matmul(ps[2 + b][:, 0:CTX], e.cT[:, b, ch, :], qcat[:, ch, b, :], start=ch == 0, stop=False)
                        pe.matmul(ps[2 + b][:, 0:CTX], e.ones[0:1, :], q_bias[0:1, b * CTX:(b + 1) * CTX],
                                  start=False, stop=True).then_inc(s.scores_psum.sem, 1)
                    pe.wait_ge(s.probs_ready.sem, s.probs_ready.at(it, 2))
                    pe.wait_ge(s.mixT_ready.sem, s.mixT_ready.before(it, 1))
                    pe.transpose(ps[4][:, 0:P], flat(a[:]), e.ident[:]).then_inc(s.probsT_psum.sem, 1)
                    pe.wait_ge(s.probsT_ready.sem, s.probsT_ready.at(it))
                    for b in range(BATCH):
                        pe.wait_ge(s.mix_ready.sem, s.mix_ready.before(it, b + 1))
                        own = slice(b * CTX, (b + 1) * CTX)
                        pe.matmul(ps[6 + b][:, 0:D], aT[own, :], e.ctx_tok[own, b, :], start=True, stop=True)\
                          .then_inc(s.mix_psum.sem, 1)
                    for b in range(BATCH):
                        pe.wait_ge(s.mix_ready.sem, s.mix_ready.at(it, b + 1))
                        pe.wait_ge(s.mixT_ready.sem, s.mixT_ready.before(it, b + 1))
                        for k in range(4):
                            mm = pe.transpose(ps[4 + b][:, k * P:(k + 1) * P],
                                              uv[:, b, k // 2, (k % 2) * P:(k % 2 + 1) * P], e.ident[:])
                        mm.then_inc(s.mixT_psum.sem, 1)
                    for b in range(BATCH):
                        pe.wait_ge(s.mixT_ready.sem, s.mixT_ready.at(it, b + 1))
                        for k in range(4):
                            pe.matmul(ps[2 + b][:, 0:D], uvT[:, b, k, :], w_l[:, 2 + k, :], start=k == 0, stop=False)
                        pe.matmul(ps[2 + b][:, 0:D], e.ones[0:1, :], b_l[0:1, :], start=False, stop=True)\
                          .then_inc(s.out_psum.sem, 1)

            @block.scalar
            def _(act_):
                with act_.Fori(0, TILES) as it:
                    for b in range(BATCH):
                        copy_cT(e, act_, it, b, b, s.scores_psum)
                    for b in range(BATCH):
                        act_.wait_ge(s.max_ready.sem, s.max_ready.at(it, b + 1))
                        act_.wait_ge(s.probsT_psum.sem, s.probsT_psum.before(it))
                        act_.wait_ge(s.mix_ready.sem, s.mix_ready.before(it, b + 1))
                        nc.scalar.activation(a[:, b, :], ps[2 + b][:, 0:CTX], ACT.Exp,
                                             bias=nmax[:, bass.ds(it + b * TILES, 1)],
                                             accum_out=a_sum[:, b:b + 1]).then_inc(s.probs_ready.sem, 1)
                    act_.wait_ge(s.probsT_psum.sem, s.probsT_psum.at(it))
                    act_.wait_ge(s.mix_psum.sem, s.mix_psum.before(it, 2))
                    nc.scalar.copy(aT[:], ps[4][:, 0:P]).then_inc(s.probsT_ready.sem, 1)
                    for b in range(BATCH):
                        act_.wait_ge(s.mixT_psum.sem, s.mixT_psum.at(it, b + 1))
                        act_.wait_ge(s.out_psum.sem, s.out_psum.before(it, b + 1))
                        nc.scalar.copy(flat(uvT[:, b, :, :]), ps[4 + b][:, :]).then_inc(s.mixT_ready.sem, 1)

            @block.vector
            def _(v):
                with v.Fori(0, TILES) as it:
                    dve.begin(v)
                    for b in range(BATCH):
                        v.wait_ge(s.c_kept.sem, s.c_kept.before(it, b + 1))
                        normalise(e, v, it, b)
                    for b in range(BATCH):
                        v.wait_ge(s.scores_psum.sem, s.scores_psum.at(it, b + 1))
                        v.tensor_reduce(nmax[:, bass.ds(it + b * TILES, 1)], ps[2 + b][:, 0:CTX], AX.X, ALU.max,
                                        negate=True).then_inc(s.max_ready.sem, 1)
                    for b in range(BATCH):
                        v.wait_ge(s.probs_ready.sem, s.probs_ready.at(it, b + 1))
                        dve.link(v.reciprocal(a_rec[:, b:b + 1], a_sum[:, b:b + 1]))
                        v.wait_ge(s.mix_psum.sem, s.mix_psum.at(it, b + 1))
                        v.wait_ge(s.mixT_psum.sem, s.mixT_psum.before(it, b + 1))
                        dve.link(v.tensor_scalar(uv[:, b, 0, :], ps[6 + b][:, 0:D], a_rec[:, b:b + 1], None, ALU.mult))
                        v.tensor_tensor(uv[:, b, 1, :], uv[:, b, 0, :], e.cs[:, b, :], ALU.mult)\
                         .then_inc(s.mix_ready.sem, 1)
                    for b in range(BATCH):
                        v.wait_ge(s.out_psum.sem, s.out_psum.at(it, b + 1))
                        v.tensor_tensor(tile_of(e.x, it, b), ps[2 + b][:, 0:D], tile_of(e.x, it, b), ALU.add)\
                         .then_inc(s.x_done.sem, 1)

            @block.gpsimd
            def _(p):
                with p.Fori(0, TILES) as it:
                    for b in range(BATCH):
                        p.wait_ge(s.c_ready.sem, s.c_ready.at(it, b + 1))
                        p.tensor_copy(tile_of(c_all, it, b), e.cs[:, b, :]).then_inc(s.c_kept.sem, 1)
        for n in two:
            n.close(TILES)

        s.max_ready.each(2)
        for n in (s.allreduce, s.probs_ready, s.sums_psum):
            n.each(1)
        with nc.Block() as block:
            @block.vector
            def _(v):
                dve.begin(v)
                v.tensor_reduce(top[:], nmax[:].rearrange("p (b t) -> p b t", b=BATCH), AX.X, ALU.min, negate=True)\
                 .then_inc(s.max_ready.sem, 1)
                v.wait_ge(s.allreduce.sem, s.allreduce.at(0))
                v.tensor_scalar(ngtop[:], gtop[:], -1.0, None, ALU.mult).then_inc(s.max_ready.sem, 1)
                v.wait_ge(s.sums_psum.sem, s.sums_psum.at(0))
                dve.link(v.reciprocal(rden[:], ps[0][:, 0:BATCH]))
                for b in range(BATCH):
                    dve.link(v.tensor_scalar(q2c[:, b, :], ps[1][:, b * DCH:(b + 1) * DCH], rden[:, b:b + 1], None, ALU.mult))
                for b in range(BATCH):
                    for ch in range(DCH):
                        v.scalar_tensor_tensor(w_c[:, b, ch, :], w_l[:, 6 + ch, :], q2c[:, b, ch:ch + 1],
                                               w_l[:, ch, :], ALU.mult, ALU.add)

            @block.gpsimd
            def _(p):
                p.wait_ge(s.max_ready.sem, s.max_ready.at(0, 1))
                p.partition_all_reduce(gtop[:], top[:], P, bass.bass_isa.ReduceOp.max).then_inc(s.allreduce.sem, 1)

            @block.scalar
            def _(act_):
                act_.wait_ge(s.max_ready.sem, s.max_ready.at(0, 2))
                for b in range(BATCH):
                    ex = nc.scalar.activation(b_att[:, b * TILES:(b + 1) * TILES], nmax[:, b * TILES:(b + 1) * TILES], ACT.Exp,
                                              bias=ngtop[:, b:b + 1], scale=-1.0, accum_out=b_att_sum[:, b:b + 1])
                ex.then_inc(s.probs_ready.sem, 1)

            @block.tensor
            def _(pe):
                pe.wait_ge(s.probs_ready.sem, s.probs_ready.at(0))
                pe.matmul(ps[0][:, 0:BATCH], e.ones[:], b_att_sum[:], start=True, stop=True)
                for b in range(BATCH):
                    for ch in range(DCH):
                        for t in range(TILES):
                            k = b * TILES + t
                            mm = pe.matmul(ps[1][:, b * DCH + ch:b * DCH + ch + 1], c_all[:, k, ch * P:(ch + 1) * P],
                                           b_att[:, k:k + 1], start=(b, ch, t) == (0, 0, 0), stop=t == TILES - 1,
                                           skip_group_check=True)
                mm.then_inc(s.sums_psum.sem, 1)
        for n in (s.allreduce, s.probs_ready, s.sums_psum, s.max_ready):
            n.close()

        two = (s.c_ready, s.cT_psum, s.cT_ready, s.out_psum, s.ln_var, s.ln_rstd)
        for n in two:
            n.each(2)
        with nc.Block() as block:
            @block.tensor
            def _(pe):
                with pe.Fori(0, TILES) as it:
                    for b in range(BATCH):
                        transpose_c(e, pe, it, b, b)
                    for b in range(BATCH):
                        pe.wait_ge(s.cT_ready.sem, s.cT_ready.at(it, b + 1))
                        pe.wait_ge(s.ln_var.sem, s.ln_var.before(it, b + 1))
                        for ch in range(DCH):
                            mm = pe.matmul(ps[2 + b][:, 0:D], e.cT[:, b, ch, :], w_c[:, b, ch, :], start=ch == 0, stop=ch == DCH - 1)
                        mm.then_inc(s.out_psum.sem, 1)

            @block.scalar
            def _(act_):
                with act_.Fori(0, TILES) as it:
                    for b in range(BATCH):
                        copy_cT(e, act_, it, b, b, s.out_psum)

            @block.vector
            def _(v):
                with v.Fori(0, TILES) as it:
                    dve.begin(v)
                    for b in range(BATCH):
                        v.wait_ge(s.out_psum.sem, s.out_psum.at(it, b + 1))
                        dve.link(v.tensor_tensor(tile_of(e.x, it, b), ps[2 + b][:, 0:D], tile_of(e.x, it, b), ALU.add))
                        stats_dve(e, v, it, b)

            @block.gpsimd
            def _(p):
                with p.Fori(0, TILES) as it:
                    for b in range(BATCH):
                        p.wait_ge(s.cT_psum.sem, s.cT_psum.before(it, b + 1))
                        p.tensor_copy(e.cs[:, b, :], tile_of(c_all, it, b)).then_inc(s.c_ready.sem, 1)
                    for b in range(BATCH):
                        stats_pool(e, p, it, b)
        for n in two:
            n.close(TILES)


HEADS, DH = 8, 64
INNER = HEADS * DH
HID = int(D * 4 * 2 / 3)
FCH = -(-HID // P)
FPAIRS = FCH // 2
FW = [min(P, HID - j * P) for j in range(FCH)]
LAYERS = 2
HALF = TILES // 2


def l0_ffn(e):
    nc, s, d, ps = e.nc, e.s, e.dram, e.psum
    dve, act, pool = (e.chain[n] for n in ("dve", "act", "pool"))
    with ExitStack() as ctx:
        sb = memory(e, ctx, "l0_ffn")
        y = sb("y", [P, ALL_TILES, D])
        wqkv = sb("wqkv", [P, LAYERS, DCH, 3 * INNER])
        wo = sb("wo", [P, LAYERS, INNER // P, D])
        w1 = sb("w1", [P, DCH, 2 * HID])
        w2 = sb("w2", [P, LAYERS, FCH, D])
        all_cols = sb("ffn_cols", [P, LAYERS, 2 * DCH + 2 * FCH])
        cols = sb("layer_cols", [P, 2 * DCH + 2 * FCH])
        all_b2 = sb("b2", [P, LAYERS, D])
        b2 = sb("layer_b2", [P, D])
        qk_scale = sb("qk_scale", [P, LAYERS, 2, 2, DH])
        rot = sb("rot", [P, 2, TILES, 2, DH])
        shift = sb("shift", [P, 2, P])
        mask32 = sb("mask32", [P, 3, 2 * P])
        mask_even = sb("mask_even", [P, HALF, 2 * P], BF16)
        mask_odd = sb("mask_odd", [P, 2 * P], BF16)
        zero = sb("zero", [P, 1])
        unused = sb("unused", [P, 1])
        ys = sb("ys", [P, BATCH, D])
        hT = sb("hT", [P, BATCH, 2, DCH, P + 1])
        work = sb("work", [P, BATCH, HEADS, 2 * P])
        pT = sb("pT", [P, BATCH, 2 * HEADS, P])
        ss = sb("ss", [P, BATCH, 2 * HEADS])
        rn = sb("rn", [P, BATCH, 2 * HEADS])
        qT = sb("qT", [P, BATCH, 4, P])
        kT = sb("kT", [P, BATCH, 4, 2, 2, P])
        vv = sb("vv", [P, BATCH, 2, INNER])
        top = sb("att_top", [P, BATCH, HEADS])
        scale = sb("att_scale", [P, BATCH, HEADS])
        bias = sb("att_bias", [P, BATCH, HEADS])
        den = sb("att_den", [P, BATCH, HEADS])
        rden = sb("att_rden", [P, BATCH, HEADS])
        o = sb("o", [P, BATCH, INNER])
        oT = sb("oT", [P, BATCH, 4, P])
        y1 = sb("y1", [P, BATCH, 2, D])
        y1b = sb("y1b", [P, BATCH, D])
        bn2 = sb("bn2", [P, BATCH, 2, 6])
        mv2 = sb("mv2", [P, BATCH, 2])
        ve2 = sb("ve2", [P, BATCH])
        rstd2 = sb("rstd2", [P, BATCH])
        h2 = sb("h2", [P, BATCH, D])
        h2T = sb("h2T", [P, DCH, BATCH, P])
        gate = sb("gate", [P, FCH, P])
        ff = sb("ff", [P, FCH, P])

        with nc.Block() as block:
            @block.sync
            def _(sp):
                for to, of in ((all_cols, "L0_cols"), (all_b2, "L0_b2"), (qk_scale, "L0_qk_scale"), (shift, "shift"),
                               (mask32, "mask"), (wqkv, "L0_wqkv"), (wo, "L0_wo"), (w2, "L0_w2")):
                    sp.dma_start(to[:], d[of]).then_inc(e.loaded, 16)
                    e.loads += 16

            @block.gpsimd
            def _(p):
                p.memset(zero[:], 0.0)
                p.memset(kT[:], 0.0)
                p.memset(vv[:], 0.0)

            @block.vector
            def _(v):
                with v.Fori(0, TILES) as it:
                    for b in range(BATCH):
                        k = it + b * TILES
                        v.tensor_scalar(tile_of(y, it, b), tile_of(e.x, it, b), flat(e.mean_var[:, bass.ds(k, 1), 0:1]),
                                        e.rstd[:, bass.ds(k, 1)], ALU.subtract, ALU.mult)
                v.wait_ge(e.loaded, e.loads)
                v.tensor_copy(mask_odd[:], mask32[:, 2, :])
                for i in range(HALF):
                    v.tensor_copy(mask_even[:, i, :], mask32[:, min(i, 1), :])

        turns = LAYERS * HALF
        four = (s.ys_ready, s.yT_psum, s.hT_ready, s.qkv_psum, s.sq_ready, s.v_ready, s.ss_ready, s.norm_ready, s.q_norm_ready,
                s.rot_ready, s.qkT_psum, s.qT_ready, s.kT_ready, s.mixed_psum, s.mix_ready, s.mixT_psum,
                s.mixT_ready, s.out_psum, s.y1_ready, s.shift_psum, s.shift_var, s.shift_rstd, s.h2_ready, s.h2T_psum,
                s.h2T_ready, s.y1b_ready, s.ffn_out, s.y_done)
        begin(4, *four)
        begin(16, s.scores_psum, s.probs_ready, s.probsT_psum)
        begin(8, s.bias_ready, s.pT_act, s.pT_dve)
        begin(4 * FPAIRS, s.hid_psum, s.gate_ready, s.ff_ready)
        w1_loaded, rot_loaded = e.dma_sem("w1_loaded"), e.dma_sem("rot_loaded")

        class Item:

            def __init__(self, layer, i, q):
                self.layer, self.i, self.turn = layer, i, layer * HALF + i
                self.odd, self.b, self.k = q // 2, q % 2, q + 1
                self.t = i * 2 + self.odd
                self.bank = 4 * self.b

        def layers(engine, order, start, first, step):
            with engine.Fori(0, LAYERS) as layer:
                order.begin(engine)
                start(layer)
                with engine.Fori(0, 1) as i:
                    first(Item(layer, i, 0), Item(layer, i, 1))

                def turn(i, last):
                    order.begin(engine)
                    for q in range(4):
                        new, after = (None if last and q + n > 3 else Item(layer, i + (q + n) // 4, (q + n) % 4) for n in (1, 2))
                        step(Item(layer, i, q), new, after)

                with engine.Fori(0, HALF - 1) as i:
                    turn(i, False)
                with engine.Fori(HALF - 1, HALF) as i:
                    turn(i, True)

        with nc.Block() as block:
            @block.sync
            def _(sp):
                with sp.Fori(0, LAYERS) as layer:
                    first = layer * HALF
                    sp.wait_ge(s.rot_ready.sem, s.rot_ready.at(first, 0))
                    sp.dma_start(rot[:], d["rotary"]).then_inc(rot_loaded, 16)
                    sp.wait_ge(s.hid_psum.sem, s.hid_psum.at(first, 0))
                    sp.dma_start(w1[:], d["L0_w1"][bass.ds(layer, 1)].rearrange("l p c n -> (l p) c n"))\
                      .then_inc(w1_loaded, 16)

            @block.gpsimd
            def _(p):
                def norms(m):
                    p.wait_ge(s.ss_ready.sem, s.ss_ready.at(m.turn, m.k))
                    p.wait_ge(s.rot_ready.sem, s.rot_ready.at(m.turn, m.k - 2))
                    p.tensor_tensor(rn[:, m.b, HEADS:], ss[:, m.b, HEADS:], e.neg_half[:, 0:HEADS], ALU.pow).then_inc(s.norm_ready.sem, 1)
                    p.wait_ge(s.bias_ready.sem, s.bias_ready.at(m.turn, 2 * (m.k - 2)))
                    p.tensor_tensor(rn[:, m.b, 0:HEADS], ss[:, m.b, 0:HEADS], e.neg_half[:, 0:HEADS], ALU.pow)\
                     .then_inc(s.q_norm_ready.sem, 1)

                def first(new, after):
                    norms(new)

                def step(now, new, after):
                    p.wait_ge(s.shift_var.sem, s.shift_var.at(now.turn, now.k))
                    p.tensor_tensor(rstd2[:, now.b:now.b + 1], ve2[:, now.b:now.b + 1], e.neg_half[:, 0:1], ALU.pow)\
                     .then_inc(s.shift_rstd.sem, 1)
                    if new:
                        norms(new)
                    p.wait_ge(s.y_done.sem, s.y_done.at(now.turn, now.k - 2))
                    p.tensor_tensor(y1b[:, now.b, :], y1[:, now.b, now.odd, :], b2[:], ALU.add).then_inc(s.y1b_ready.sem, 1)

                layers(p, pool, lambda layer: None, first, step)

            @block.tensor
            def _(pe):
                pe.wait_ge(e.loaded, e.loads)

                def y_transposed(m):
                    pe.wait_ge(s.ff_ready.sem, s.ff_ready.at(m.turn, FPAIRS * (m.k - 3) + 1))
                    pe.wait_ge(s.ys_ready.sem, s.ys_ready.at(m.turn, m.k))
                    for ch in range(DCH):
                        mm = pe.transpose(ps[:, m.bank, ch * P:(ch + 1) * P], ys[:, m.b, ch * P:(ch + 1) * P], e.ident[:])
                    mm.then_inc(s.yT_psum.sem, 1)

                def qkv(m, n, chunks=range(DCH)):
                    if n == 0:
                        pe.wait_ge(s.hT_ready.sem, s.hT_ready.at(m.turn, m.k))
                    if n == 2:
                        pe.wait_ge(s.y_done.sem, s.y_done.at(m.turn, m.k - 2))
                    for ch in chunks:
                        mm = pe.matmul(ps[:, m.bank + 1 + n, :], hT[:, m.b, m.odd, ch, 1 - ch:P + 1 - ch],
                                       wqkv[:, bass.ds(m.layer, 1), ch, n * INNER:(n + 1) * INNER].rearrange("p l n -> p (l n)"),
                                       start=ch == 0, stop=ch == DCH - 1)
                    if n == 2:
                        mm.then_inc(s.qkv_psum.sem, 1)

                def qk_transposed(m):
                    pe.wait_ge(s.rot_ready.sem, s.rot_ready.at(m.turn, m.k))
                    for n in range(2):
                        for j in range(4):
                            mm = pe.transpose(ps[:, m.bank + n, j * P:(j + 1) * P],
                                              work[:, m.b, 2 * n + j // 2, (j % 2) * P:(j % 2 + 1) * P], e.ident[:])
                    mm.then_inc(s.qkT_psum.sem, 1)

                def scores(m):
                    pe.wait_ge(s.v_ready.sem, s.v_ready.at(m.turn, m.k))
                    pe.wait_ge(s.qT_ready.sem, s.qT_ready.at(m.turn, m.k))
                    pe.wait_ge(s.kT_ready.sem, s.kT_ready.at(m.turn, m.k))
                    for j in range(4):
                        bank = ps[:, m.bank + j, :]
                        mask = (mask_odd[:].unsqueeze(1) if m.odd else mask_even[:, bass.ds(m.i, 1), :]).broadcast_to((P, 2, 2 * P))
                        pe.matmul(bank, e.ident_bf[:], mask, start=True, stop=False)
                        pe.matmul(bank, qT[:, m.b, j, :], kT[:, m.b, j, :, :, :].rearrange("p h w n -> p (h w n)"),
                                  start=False, stop=True).then_inc(s.scores_psum.sem, 1)

                def probs_transposed(m):
                    for j in range(4):
                        pe.wait_ge(s.probs_ready.sem, s.probs_ready.at(m.turn, 4 * (m.k - 1) + j + 1))
                        for n in range(4):
                            mm = pe.transpose(ps[:, m.bank + j, n * P:(n + 1) * P],
                                              work[:, m.b, 2 * j + n // 2, (n % 2) * P:(n % 2 + 1) * P], e.ident[:])
                        mm.then_inc(s.probsT_psum.sem, 1)

                def mixed(m):
                    pe.wait_ge(s.pT_act.sem, s.pT_act.at(m.turn, 2 * m.k))
                    pe.wait_ge(s.pT_dve.sem, s.pT_dve.at(m.turn, 2 * m.k))
                    for h in range(HEADS):
                        for c in range(2):
                            mm = pe.matmul(ps[:, m.bank, h * DH:(h + 1) * DH], pT[:, m.b, 2 * h + c, :],
                                           vv[:, m.b, c, h * DH:(h + 1) * DH], start=(h, c) == (0, 0), stop=c == 1,
                                           skip_group_check=True)
                    mm.then_inc(s.mixed_psum.sem, 1)

                def mix_transposed(m):
                    pe.wait_ge(s.mix_ready.sem, s.mix_ready.at(m.turn, m.k))
                    for j in range(4):
                        mm = pe.transpose(ps[:, m.bank + 1, j * P:(j + 1) * P], o[:, m.b, j * P:(j + 1) * P], e.ident[:])
                    mm.then_inc(s.mixT_psum.sem, 1)

                def attention_out(m):
                    pe.wait_ge(s.mixT_ready.sem, s.mixT_ready.at(m.turn, m.k))
                    for j in range(4):
                        mm = pe.matmul(ps[:, m.bank + 2, 0:D], oT[:, m.b, j, :],
                                       wo[:, bass.ds(m.layer, 1), j, :].rearrange("p l n -> p (l n)"), start=j == 0, stop=j == 3)
                    mm.then_inc(s.out_psum.sem, 1)

                def shifted(m):
                    pe.wait_ge(s.y1_ready.sem, s.y1_ready.at(m.turn, m.k))
                    pe.matmul(ps[:, m.bank + 3, 0:P], shift[:, 0, :], y1[:, m.b, m.odd, P:D], start=True, stop=False)
                    pe.matmul(ps[:, m.bank + 3, 0:P], shift[:, 1, :], y1[:, m.b, 1 - m.odd, P:D], start=False, stop=True)\
                      .then_inc(s.shift_psum.sem, 1)

                def h2_transposed(m):
                    pe.wait_ge(s.h2_ready.sem, s.h2_ready.at(m.turn, m.k))
                    for ch in range(DCH):
                        mm = pe.transpose(ps[:, m.bank, ch * P:(ch + 1) * P], h2[:, m.b, ch * P:(ch + 1) * P], e.ident[:])
                    mm.then_inc(s.h2T_psum.sem, 1)

                def ffn_up(m):
                    pe.wait_ge(w1_loaded, m.layer * 16 + 16)
                    pe.wait_ge(s.h2T_ready.sem, s.h2T_ready.at(m.turn, m.k))
                    for j in range(FCH):
                        for n in range(2):
                            at, to = n * HID + j * P, (2 * (j % 2) + n) * P
                            for ch in range(DCH):
                                mm = pe.matmul(ps[0:FW[j], m.bank + j // 2, to:to + P], w1[:, ch, at:at + FW[j]],
                                               h2T[:, ch, m.b, :], start=(j % 2, n, ch) == (0, 0, 0), stop=ch == DCH - 1,
                                               skip_group_check=True)
                        if j % 2:
                            mm.then_inc(s.hid_psum.sem, 1)

                def ffn_down(m, pair):
                    pe.wait_ge(s.ff_ready.sem, s.ff_ready.at(m.turn, FPAIRS * (m.k - 1) + pair + 1))
                    for j in (2 * pair, 2 * pair + 1):
                        mm = pe.matmul(ps[:, m.bank + 3, 0:D], ff[0:FW[j], j, :],
                                       w2[0:FW[j], bass.ds(m.layer, 1), j, :].rearrange("p l n -> p (l n)"),
                                       start=j == 0, stop=j == FCH - 1, skip_group_check=True)
                    if pair == FPAIRS - 1:
                        mm.then_inc(s.ffn_out.sem, 1)

                def first(new, after):
                    y_transposed(new)
                    for n in range(3):
                        qkv(new, n)
                    qk_transposed(new)
                    y_transposed(after)
                    scores(new)
                    qkv(after, 0)

                def step(now, new, after):
                    probs_transposed(now)
                    if new:
                        qkv(new, 1, (0,))
                    mixed(now)
                    if new:
                        qkv(new, 1, (1,))
                    mix_transposed(now)
                    attention_out(now)
                    shifted(now)
                    if new:
                        qkv(new, 2)
                    h2_transposed(now)
                    ffn_up(now)
                    if new:
                        qk_transposed(new)
                    if after:
                        y_transposed(after)
                    ffn_down(now, 0)
                    ffn_down(now, 1)
                    if new:
                        scores(new)
                    ffn_down(now, 2)
                    if after:
                        qkv(after, 0)

                layers(pe, e.chain["pe"], lambda layer: None, first, step)

            @block.scalar
            def _(a):
                def start(layer):
                    at = layer * HALF
                    a.wait_ge(s.hT_ready.sem, s.hT_ready.at(at, 0))
                    a.wait_ge(s.qkv_psum.sem, s.qkv_psum.at(at, 0))
                    for b in range(BATCH):
                        z = nc.scalar.copy(hT[:, b, 0, 1, 0:1], zero[:])
                    act.link(z)
                    a.wait_ge(s.ff_ready.sem, s.ff_ready.at(at, 0))
                    act.link(nc.scalar.copy(cols[:], flat(all_cols[:, bass.ds(layer, 1), :])))
                    a.wait_ge(s.y1b_ready.sem, s.y1b_ready.at(at, 0))
                    act.link(nc.scalar.copy(b2[:], flat(all_b2[:, bass.ds(layer, 1), :])))

                def copy_hT(m):
                    a.wait_ge(s.yT_psum.sem, s.yT_psum.at(m.turn, m.k))
                    a.wait_ge(s.qkv_psum.sem, s.qkv_psum.at(m.turn, m.k - 2))
                    nc.scalar.copy(hT[:, m.b, m.odd, :, 1:P + 1], ps[:, m.bank, 0:D].rearrange("p (c n) -> p c n", c=DCH))
                    nc.scalar.copy(hT[:, m.b, 1 - m.odd, 1, 0:1], ps[:, m.bank, D - 1:D]).then_inc(s.hT_ready.sem, 1)

                def squares(m):
                    a.wait_ge(s.qkv_psum.sem, s.qkv_psum.at(m.turn, m.k))
                    a.wait_ge(s.mixed_psum.sem, s.mixed_psum.at(m.turn, m.k - 2))
                    nc.scalar.activation(flat(pT[:, m.b, 0:HEADS, :]), flat(ps[:, m.bank + 1:m.bank + 3, :]), ACT.Square)\
                      .then_inc(s.sq_ready.sem, 1)
                    nc.scalar.copy(vv[:, m.b, m.odd, :], ps[:, m.bank + 3, :]).then_inc(s.v_ready.sem, 1)

                def copy_qT(m):
                    a.wait_ge(s.qkT_psum.sem, s.qkT_psum.at(m.turn, m.k))
                    a.wait_ge(s.scores_psum.sem, s.scores_psum.at(m.turn, 4 * (m.k - 2)))
                    nc.scalar.copy(flat(qT[:, m.b, :, :]), ps[:, m.bank, :]).then_inc(s.qT_ready.sem, 1)

                def probs(m):
                    for slot in range(HEADS):
                        if slot % 4 == 0:
                            a.wait_ge(s.bias_ready.sem, s.bias_ready.at(m.turn, 2 * (m.k - 1) + slot // 4 + 1))
                        ex = nc.scalar.activation(work[:, m.b, slot, :], ps[:, m.bank + slot // 2, (slot % 2) * 2 * P:(slot % 2 + 1) * 2 * P],
                                                  ACT.Exp, bias=bias[:, m.b, slot:slot + 1], scale=scale[:, m.b, slot:slot + 1],
                                                  accum_out=den[:, m.b, slot:slot + 1])
                        if slot % 2:
                            ex.then_inc(s.probs_ready.sem, 1)

                def copy_pT(m):
                    for j in range(2):
                        a.wait_ge(s.probsT_psum.sem, s.probsT_psum.at(m.turn, 4 * (m.k - 1) + j + 1))
                        nc.scalar.copy(flat(pT[:, m.b, 4 * j:4 * j + 4, :]), ps[:, m.bank + j, :]).then_inc(s.pT_act.sem, 1)

                def copy_oT(m):
                    a.wait_ge(s.mixT_psum.sem, s.mixT_psum.at(m.turn, m.k))
                    a.wait_ge(s.out_psum.sem, s.out_psum.at(m.turn, m.k - 2))
                    nc.scalar.copy(flat(oT[:, m.b, :, :]), ps[:, m.bank + 1, :]).then_inc(s.mixT_ready.sem, 1)

                def affine_h2T(m):
                    a.wait_ge(s.h2T_psum.sem, s.h2T_psum.at(m.turn, m.k))
                    a.wait_ge(s.hid_psum.sem, s.hid_psum.at(m.turn, FPAIRS * (m.k - 2)))
                    for ch in range(DCH):
                        cp = nc.scalar.activation(h2T[:, ch, m.b, :], ps[:, m.bank, ch * P:(ch + 1) * P], ACT.Identity,
                                                  scale=cols[:, ch:ch + 1], bias=cols[:, DCH + ch:DCH + ch + 1])
                    cp.then_inc(s.h2T_ready.sem, 1)

                def gates(m):
                    for j in range(FCH):
                        if j % 2 == 0:
                            a.wait_ge(s.hid_psum.sem, s.hid_psum.at(m.turn, FPAIRS * (m.k - 1) + j // 2 + 1))
                            a.wait_ge(s.ff_ready.sem, s.ff_ready.at(m.turn, FPAIRS * (m.k - 2) + j // 2 + 1))
                        col, of = 2 * DCH + FCH + j, (2 * (j % 2) + 1) * P
                        g = nc.scalar.activation(gate[0:FW[j], j, :], ps[0:FW[j], m.bank + j // 2, of:of + P],
                                                 ACT.Gelu, bias=cols[0:FW[j], col:col + 1])
                        if j % 2:
                            g.then_inc(s.gate_ready.sem, 1)

                def load_table(func):
                    act.link(nc.scalar.activation(unused[:], zero[:], func))

                def first(new, after):
                    copy_hT(new)
                    squares(new)
                    copy_qT(new)
                    copy_hT(after)
                    probs(new)

                def step(now, new, after):
                    copy_pT(now)
                    copy_oT(now)
                    load_table(ACT.Gelu)
                    affine_h2T(now)
                    if new:
                        squares(new)
                    gates(now)
                    if new:
                        copy_qT(new)
                    if after:
                        copy_hT(after)
                    if new:
                        load_table(ACT.Exp)
                        probs(new)

                layers(a, act, start, first, step)

            @block.vector
            def _(v):
                def start(layer):
                    v.wait_ge(rot_loaded, layer * 16 + 16)
                    for part in range(2):
                        for n in range(2):
                            last = v.tensor_tensor(rot[:, part, :, n, :], rot[:, part, :, n, :],
                                                   qk_scale[:, bass.ds(layer, 1), part, n, :].broadcast_to((P, TILES, DH)), ALU.mult)
                    dve.link(last)
                    v.wait_ge(s.shift_psum.sem, s.shift_psum.at(layer * HALF, 0))
                    v.wait_ge(s.y1b_ready.sem, s.y1b_ready.at(layer * HALF, 0))
                    for b in range(BATCH):
                        z = v.memset(y1[:, b, 1, :], 0.0)
                    dve.link(z)

                def take_y(m):
                    v.wait_ge(s.y_done.sem, s.y_done.at(m.turn, m.k - 16))
                    v.wait_ge(s.y1_ready.sem, s.y1_ready.at(m.turn, m.k - 2))
                    v.tensor_copy(ys[:, m.b, :], tile_of(y, m.t, m.b)).then_inc(s.ys_ready.sem, 1)

                def rotary_parts(m):
                    qk = ps[:, m.bank + 1:m.bank + 3, :].rearrange("p n (h x) -> p n h x", x=DH)
                    w = [work[:, m.b, 4 * n:4 * n + 4, :].rearrange("p a f -> p (a f)").rearrange("p (n h x) -> p n h x", n=2, x=DH)
                         for n in range(2)]
                    table = [rot[:, part, bass.ds(m.t, 1), :, :].rearrange("p t n x -> p (t n) x").unsqueeze(2)
                             .broadcast_to((P, 2, HEADS, DH)) for part in range(2)]
                    return qk, w, table

                def norms(m):
                    v.wait_ge(s.sq_ready.sem, s.sq_ready.at(m.turn, m.k))
                    v.wait_ge(s.q_norm_ready.sem, s.q_norm_ready.at(m.turn, m.k - 2))
                    dve.link(v.tensor_reduce(ss[:, m.b, :], flat(pT[:, m.b, 0:HEADS, :]).rearrange("p (h x) -> p h x", x=DH), AX.X, ALU.add))
                    v.tensor_scalar(ss[:, m.b, :], ss[:, m.b, :], 1e-24, None, ALU.max).then_inc(s.ss_ready.sem, 1)

                def rotate_cos(m):
                    qk, w, table = rotary_parts(m)
                    v.wait_ge(s.probsT_psum.sem, s.probsT_psum.at(m.turn, 4 * (m.k - 2)))
                    v.tensor_tensor(w[0], qk, table[0], ALU.mult)

                def rotate_sin(m):
                    qk, w, table = rotary_parts(m)
                    hx = DH // 2
                    v.tensor_tensor(w[1][:, :, :, 0:hx], qk[:, :, :, hx:DH], table[1][:, :, :, 0:hx], ALU.mult)
                    dve.link(v.tensor_tensor(w[1][:, :, :, hx:DH], qk[:, :, :, 0:hx], table[1][:, :, :, hx:DH], ALU.mult))

                def rotate_sum(m):
                    _, w, _ = rotary_parts(m)
                    dve.link(v.tensor_tensor(w[0], w[0], w[1], ALU.add))

                def scale_k(m):
                    kr = work[:, m.b, 2:4, :].rearrange("p a f -> p (a f)").rearrange("p (h x) -> p h x", x=DH)
                    v.wait_ge(s.norm_ready.sem, s.norm_ready.at(m.turn, m.k))
                    v.tensor_tensor(kr, kr, rn[:, m.b, HEADS:].unsqueeze(2).broadcast_to((P, HEADS, DH)), ALU.mult)\
                     .then_inc(s.rot_ready.sem, 1)

                def copy_kT(m):
                    v.wait_ge(s.qkT_psum.sem, s.qkT_psum.at(m.turn, m.k))
                    v.wait_ge(s.scores_psum.sem, s.scores_psum.at(m.turn, 4 * (m.k - 2)))
                    for n in range(2):
                        own = slice(n * DH, (n + 1) * DH)
                        cp = v.tensor_copy(kT[own, m.b, :, n, m.odd, :], ps[own, m.bank + 1, :].rearrange("p (j n) -> p j n", j=4))
                    cp.then_inc(s.kT_ready.sem, 1)

                def maxima(m):
                    v.wait_ge(s.q_norm_ready.sem, s.q_norm_ready.at(m.turn, m.k))
                    v.wait_ge(s.probs_ready.sem, s.probs_ready.at(m.turn, 4 * (m.k - 2)))
                    v.tensor_scalar(scale[:, m.b, :], rn[:, m.b, 0:HEADS], float(DH) ** 0.5, None, ALU.mult)
                    for j in range(4):
                        v.wait_ge(s.scores_psum.sem, s.scores_psum.at(m.turn, 4 * (m.k - 1) + j + 1))
                        last = v.tensor_reduce(top[:, m.b, 2 * j:2 * j + 2], ps[:, m.bank + j, :].rearrange("p (n x) -> p n x", n=2),
                                               AX.X, ALU.max)
                        if j % 2:
                            dve.link(last)
                            four_heads = slice(2 * j - 2, 2 * j + 2)
                            v.scalar_tensor_tensor(bias[:, m.b, four_heads], top[:, m.b, four_heads], -1.0, scale[:, m.b, four_heads],
                                                   ALU.mult, ALU.mult).then_inc(s.bias_ready.sem, 1)

                def copy_pT(m):
                    for j in range(2, 4):
                        v.wait_ge(s.probsT_psum.sem, s.probsT_psum.at(m.turn, 4 * (m.k - 1) + j + 1))
                        v.tensor_copy(flat(pT[:, m.b, 4 * j:4 * j + 4, :]), ps[:, m.bank + j, :]).then_inc(s.pT_dve.sem, 1)

                def mix(m):
                    v.wait_ge(s.probs_ready.sem, s.probs_ready.at(m.turn, 4 * m.k))
                    dve.link(v.reciprocal(rden[:, m.b, :], den[:, m.b, :]))
                    v.wait_ge(s.mixed_psum.sem, s.mixed_psum.at(m.turn, m.k))
                    v.wait_ge(s.mixT_psum.sem, s.mixT_psum.at(m.turn, m.k - 2))
                    v.tensor_tensor(o[:, m.b, :].rearrange("p (h x) -> p h x", x=DH), ps[:, m.bank, :].rearrange("p (h x) -> p h x", x=DH),
                                    rden[:, m.b, :].unsqueeze(2).broadcast_to((P, HEADS, DH)), ALU.mult).then_inc(s.mix_ready.sem, 1)

                def add_attention(m):
                    v.wait_ge(s.out_psum.sem, s.out_psum.at(m.turn, m.k))
                    v.wait_ge(s.shift_psum.sem, s.shift_psum.at(m.turn, m.k - 2))
                    v.wait_ge(s.y1b_ready.sem, s.y1b_ready.at(m.turn, m.k - 2))
                    v.tensor_tensor(y1[:, m.b, m.odd, :], ps[:, m.bank + 2, 0:D], ys[:, m.b, :], ALU.add).then_inc(s.y1_ready.sem, 1)

                def shifted_stats(m):
                    v.wait_ge(s.y1_ready.sem, s.y1_ready.at(m.turn, m.k))
                    v.bn_stats(bn2[:, m.b, 0, :], y1[:, m.b, m.odd, 0:P])
                    v.wait_ge(s.shift_psum.sem, s.shift_psum.at(m.turn, m.k))
                    dve.link(v.bn_stats(bn2[:, m.b, 1, :], ps[:, m.bank + 3, 0:P]))
                    dve.link(v.bn_aggr(mv2[:, m.b, :], flat(bn2[:, m.b, :, :])))
                    v.tensor_scalar(ve2[:, m.b:m.b + 1], mv2[:, m.b, 1:2], EPS, None, ALU.add).then_inc(s.shift_var.sem, 1)

                def normalise_h2(m):
                    v.wait_ge(s.shift_rstd.sem, s.shift_rstd.at(m.turn, m.k))
                    v.wait_ge(s.h2T_psum.sem, s.h2T_psum.at(m.turn, m.k - 2))
                    v.tensor_scalar(h2[:, m.b, 0:P], y1[:, m.b, m.odd, 0:P], mv2[:, m.b, 0:1], rstd2[:, m.b:m.b + 1], ALU.subtract, ALU.mult)
                    v.tensor_scalar(h2[:, m.b, P:D], ps[:, m.bank + 3, 0:P], mv2[:, m.b, 0:1], rstd2[:, m.b:m.b + 1], ALU.subtract, ALU.mult)\
                     .then_inc(s.h2_ready.sem, 1)

                def gated(m, pair):
                    v.wait_ge(s.gate_ready.sem, s.gate_ready.at(m.turn, FPAIRS * (m.k - 1) + pair + 1))
                    if pair == 0:
                        v.wait_ge(s.ffn_out.sem, s.ffn_out.at(m.turn, m.k - 1))
                    for j in (2 * pair, 2 * pair + 1):
                        col, of = 2 * DCH + j, 2 * (j % 2) * P
                        ins = v.scalar_tensor_tensor(ff[0:FW[j], j, :], ps[0:FW[j], m.bank + pair, of:of + P], cols[0:FW[j], col:col + 1],
                                                     gate[0:FW[j], j, :], ALU.add, ALU.mult)
                    ins.then_inc(s.ff_ready.sem, 1)

                def add_ffn(m):
                    v.wait_ge(s.ffn_out.sem, s.ffn_out.at(m.turn, m.k))
                    v.wait_ge(s.y1b_ready.sem, s.y1b_ready.at(m.turn, m.k))
                    v.tensor_tensor(tile_of(y, m.t, m.b), ps[:, m.bank + 3, 0:D], y1b[:, m.b, :], ALU.add).then_inc(s.y_done.sem, 1)

                def first(new, after):
                    take_y(new)
                    take_y(after)
                    norms(new)
                    rotate_cos(new)
                    rotate_sin(new)
                    rotate_sum(new)
                    scale_k(new)
                    copy_kT(new)
                    maxima(new)

                def step(now, new, after):
                    copy_pT(now)
                    mix(now)
                    add_attention(now)
                    shifted_stats(now)
                    normalise_h2(now)
                    if new:
                        norms(new)
                        rotate_cos(new)
                        rotate_sin(new)
                        rotate_sum(new)
                    gated(now, 0)
                    if new:
                        scale_k(new)
                    gated(now, 1)
                    if after:
                        take_y(after)
                    gated(now, 2)
                    if new:
                        copy_kT(new)
                        maxima(new)
                    add_ffn(now)

                layers(v, dve, start, first, step)
        end(turns, *four, s.scores_psum, s.probs_ready, s.probsT_psum, s.bias_ready, s.pT_act, s.pT_dve, s.hid_psum, s.gate_ready, s.ff_ready)

        for n in (s.ln_var, s.ln_rstd):
            n.each(2)
        with nc.Block() as block:
            @block.vector
            def _(v):
                with v.Fori(0, TILES) as it:
                    dve.begin(v)
                    for b in range(BATCH):
                        dve.link(v.tensor_tensor(tile_of(e.x, it, b), tile_of(e.x, it, b), tile_of(y, it, b), ALU.add))
                        stats_dve(e, v, it, b)

            @block.gpsimd
            def _(p):
                with p.Fori(0, TILES) as it:
                    for b in range(BATCH):
                        stats_pool(e, p, it, b)
        for n in (s.ln_var, s.ln_rstd):
            n.close(TILES)


class Tile:

    def __init__(self, it, b):
        self.it, self.b, self.k = it, b, b + 1


def tiles(engine, order, first, step):
    def turn(it, last):
        order.begin(engine)
        for b in range(BATCH):
            step(Tile(it, b), *(None if last and b + n >= BATCH else Tile(it + (b + n) // BATCH, (b + n) % BATCH) for n in (1, 2)))

    with engine.Fori(0, 1) as it:
        order.begin(engine)
        first(Tile(it, 0), Tile(it, 1))
    with engine.Fori(0, TILES - 1) as it:
        turn(it, False)
    with engine.Fori(TILES - 1, TILES) as it:
        turn(it, True)


def load(e, sp, *pairs):
    for to, of in pairs:
        sp.dma_start(to[:], e.dram[of]).then_inc(e.loaded, 16)
        e.loads += 16


def add_to_x(e, v, it, b, out):
    e.chain["dve"].link(v.tensor_tensor(tile_of(e.x, it, b), out, tile_of(e.x, it, b), ALU.add))
    stats_dve(e, v, it, b)


def l1_xattn(e):
    nc, s, ps = e.nc, e.s, e.ps
    dve = e.chain["dve"]
    with ExitStack() as ctx:
        sb = memory(e, ctx, "l1_xattn")
        first_mask = sb("first_mask", [P, CTX])
        mask = sb("causal", [P, TILES, CTX], BF16)
        a = sb("a", [P, BATCH, CTX])
        den = sb("a_den", [P, BATCH])
        rec = sb("a_rec", [P, BATCH])
        nmax = sb("nmax", [P, BATCH])
        aT = sb("aT", [P, P])
        two = (s.c_ready, s.cT_psum, s.cT_ready, s.scores_psum, s.max_ready, s.probs_ready, s.mix_psum, s.ln_var, s.ln_rstd)
        begin(2, *two)
        begin(1, s.probsT_psum, s.probsT_ready, s.mask_ready)
        with nc.Block() as block:
            @block.sync
            def _(sp):
                load(e, sp, (first_mask, "causal"))

            @block.tensor
            def _(pe):
                pe.wait_ge(s.mask_ready.sem, s.mask_ready.at(0))
                with pe.Fori(0, TILES) as it:
                    for b in range(BATCH):
                        transpose_c(e, pe, it, b, b)
                    for b in range(BATCH):
                        pe.wait_ge(s.cT_ready.sem, s.cT_ready.at(it, b + 1))
                        pe.wait_ge(s.probs_ready.sem, s.probs_ready.before(it, b + 1))
                        pe.matmul(ps[2 + b][:, 0:CTX], e.ident_bf[:], flat(mask[:, bass.ds(it, 1), :]), start=True, stop=False)
                        for ch in range(DCH):
                            mm = pe.matmul(ps[2 + b][:, 0:CTX], e.cT[:, b, ch, :], e.ctxT[:, ch, b, :], start=False, stop=ch == DCH - 1)
                        mm.then_inc(s.scores_psum.sem, 1)
                    pe.wait_ge(s.probs_ready.sem, s.probs_ready.at(it, 2))
                    pe.wait_ge(s.probsT_ready.sem, s.probsT_ready.before(it))
                    pe.transpose(ps[4][:, 0:P], flat(a[:]), e.ident[:]).then_inc(s.probsT_psum.sem, 1)
                    pe.wait_ge(s.probsT_ready.sem, s.probsT_ready.at(it))
                    for b in range(BATCH):
                        own = slice(b * CTX, (b + 1) * CTX)
                        pe.wait_ge(s.ln_var.sem, s.ln_var.before(it, b + 1))
                        pe.matmul(ps[6 + b][:, 0:D], aT[own, :], e.ctx_tok[own, b, :], start=True, stop=True)\
                          .then_inc(s.mix_psum.sem, 1)

            @block.scalar
            def _(act_):
                with act_.Fori(0, TILES) as it:
                    for b in range(BATCH):
                        copy_cT(e, act_, it, b, b, s.scores_psum)
                    for b in range(BATCH):
                        act_.wait_ge(s.max_ready.sem, s.max_ready.at(it, b + 1))
                        act_.wait_ge(s.probsT_psum.sem, s.probsT_psum.before(it))
                        act_.wait_ge(s.ln_var.sem, s.ln_var.before(it, b + 1))
                        nc.scalar.activation(a[:, b, :], ps[2 + b][:, 0:CTX], ACT.Exp, bias=nmax[:, b:b + 1],
                                             accum_out=den[:, b:b + 1]).then_inc(s.probs_ready.sem, 1)
                    act_.wait_ge(s.probsT_psum.sem, s.probsT_psum.at(it))
                    act_.wait_ge(s.mix_psum.sem, s.mix_psum.before(it, 2))
                    nc.scalar.copy(aT[:], ps[4][:, 0:P]).then_inc(s.probsT_ready.sem, 1)

            @block.vector
            def _(v):
                dve.begin(v)
                dve.link(v.memset(mask[:], 0.0))
                v.wait_ge(e.loaded, e.loads)
                v.tensor_copy(mask[:, 0, :], first_mask[:]).then_inc(s.mask_ready.sem, 1)
                with v.Fori(0, TILES) as it:
                    dve.begin(v)
                    for b in range(BATCH):
                        normalise(e, v, it, b)
                    for b in range(BATCH):
                        v.wait_ge(s.scores_psum.sem, s.scores_psum.at(it, b + 1))
                        v.wait_ge(s.probs_ready.sem, s.probs_ready.before(it, b + 1))
                        v.tensor_reduce(nmax[:, b:b + 1], ps[2 + b][:, 0:CTX], AX.X, ALU.max, negate=True)\
                         .then_inc(s.max_ready.sem, 1)
                    for b in range(BATCH):
                        v.wait_ge(s.probs_ready.sem, s.probs_ready.at(it, b + 1))
                        dve.link(v.reciprocal(rec[:, b:b + 1], den[:, b:b + 1]))
                        v.wait_ge(s.mix_psum.sem, s.mix_psum.at(it, b + 1))
                        dve.link(v.scalar_tensor_tensor(tile_of(e.x, it, b), ps[6 + b][:, 0:D], rec[:, b:b + 1],
                                                        tile_of(e.x, it, b), ALU.mult, ALU.add))
                        stats_dve(e, v, it, b)

            @block.gpsimd
            def _(p):
                with p.Fori(0, TILES) as it:
                    for b in range(BATCH):
                        stats_pool(e, p, it, b)
        end(TILES, *two, s.probsT_psum, s.probsT_ready)
        end(1, s.mask_ready)


EXPERTS = 8
MOE_HID = 512
MCH = MOE_HID // P
CAPACITY = -(-BATCH * SEQ * 5 // (EXPERTS * 4))


def route(e, ctx, stage, w_router, gates_are_softmax):
    nc, s, ps = e.nc, e.s, e.ps
    dve = e.chain["dve"]
    sb = memory(e, ctx, stage)
    E8 = EXPERTS
    chosen = sb("chosen", [P, ALL_TILES, E8], BF16)
    comb = sb("comb", [P, ALL_TILES, E8])
    number = sb("expert_number", [P, E8])
    score = sb("score", [P, BATCH, E8])
    ntop = sb("ntop", [P, BATCH])
    ex = sb("gate_exp", [P, BATCH, E8])
    den = sb("gate_den", [P, BATCH])
    rec = sb("gate_rec", [P, BATCH])
    top8 = sb("top8", [P, BATCH, E8])
    idx8 = sb("idx8", [P, BATCH, E8], U32)
    idx = sb("idx", [P, BATCH, 2])
    hot = sb("hot", [P, BATCH, 2, E8])
    gap = sb("gap", [P, BATCH])
    pair = sb("pair_weights", [P, BATCH, 2])
    two = (s.c_ready, s.cT_psum, s.cT_ready, s.logits_psum, s.max_ready, s.probs_ready, s.routed)
    begin(2, *two)
    with nc.Block() as block:
        @block.sync
        def _(sp):
            load(e, sp, w_router, (number, "expert_number"))

        @block.tensor
        def _(pe):
            pe.wait_ge(e.loaded, e.loads)
            with pe.Fori(0, TILES) as it:
                for b in range(BATCH):
                    transpose_c(e, pe, it, b, b)
                for b in range(BATCH):
                    pe.wait_ge(s.cT_ready.sem, s.cT_ready.at(it, b + 1))
                    pe.wait_ge(s.routed.sem, s.routed.before(it, b + 1))
                    for ch in range(DCH):
                        mm = pe.matmul(ps[2 + b][:, 0:E8], e.cT[:, b, ch, :], w_router[0][:, ch, :], start=ch == 0, stop=ch == DCH - 1)
                    mm.then_inc(s.logits_psum.sem, 1)

        @block.scalar
        def _(act_):
            with act_.Fori(0, TILES) as it:
                for b in range(BATCH):
                    copy_cT(e, act_, it, b, b, s.logits_psum)
                for b in range(BATCH):
                    act_.wait_ge(s.max_ready.sem, s.max_ready.at(it, b + 1))
                    if gates_are_softmax:
                        nc.scalar.activation(ex[:, b, :], score[:, b, :], ACT.Exp, bias=ntop[:, b:b + 1],
                                             accum_out=den[:, b:b + 1]).then_inc(s.probs_ready.sem, 1)
                    else:
                        nc.scalar.activation(ex[:, b, 0:1], gap[:, b:b + 1], ACT.Exp).then_inc(s.probs_ready.sem, 1)

        def choose(v, b, values):
            dve.link(v.max(top8[:, b, :], values))
            dve.link(v.max_index(idx8[:, b, :], top8[:, b, :], values))
            dve.link(v.tensor_copy(idx[:, b, :], idx8[:, b, 0:2]))
            for n in range(2):
                last = v.tensor_scalar(hot[:, b, n, :], number[:], idx[:, b, n:n + 1], None, ALU.is_equal)
            dve.link(last)

        @block.vector
        def _(v):
            v.wait_ge(e.loaded, e.loads)
            with v.Fori(0, TILES) as it:
                dve.begin(v)
                for b in range(BATCH):
                    normalise(e, v, it, b)
                for b in range(BATCH):
                    k = it + b * TILES
                    v.wait_ge(s.logits_psum.sem, s.logits_psum.at(it, b + 1))
                    dve.link(v.tensor_copy(score[:, b, :], ps[2 + b][:, 0:E8]))
                    if gates_are_softmax:
                        v.tensor_reduce(ntop[:, b:b + 1], score[:, b, :], AX.X, ALU.max, negate=True).then_inc(s.max_ready.sem, 1)
                    else:
                        choose(v, b, score[:, b, :])
                        v.tensor_tensor(gap[:, b:b + 1], top8[:, b, 1:2], top8[:, b, 0:1], ALU.subtract).then_inc(s.max_ready.sem, 1)
                for b in range(BATCH):
                    k = it + b * TILES
                    v.wait_ge(s.probs_ready.sem, s.probs_ready.at(it, b + 1))
                    if gates_are_softmax:
                        dve.link(v.reciprocal(rec[:, b:b + 1], den[:, b:b + 1]))
                        dve.link(v.tensor_scalar(score[:, b, :], ex[:, b, :], rec[:, b:b + 1], None, ALU.mult))
                        choose(v, b, score[:, b, :])
                        dve.link(v.tensor_tensor(hot[:, b, 0, :], hot[:, b, 0, :], hot[:, b, 1, :], ALU.add))
                        v.tensor_copy(flat(chosen[:, bass.ds(k, 1), :]), hot[:, b, 0, :])
                        v.tensor_tensor(flat(comb[:, bass.ds(k, 1), :]), score[:, b, :], hot[:, b, 0, :], ALU.mult)\
                         .then_inc(s.routed.sem, 1)
                    else:
                        dve.link(v.tensor_scalar(gap[:, b:b + 1], ex[:, b, 0:1], 1.0, None, ALU.add))
                        dve.link(v.reciprocal(pair[:, b, 0:1], gap[:, b:b + 1]))
                        dve.link(v.tensor_tensor(pair[:, b, 1:2], pair[:, b, 0:1], ex[:, b, 0:1], ALU.mult))
                        dve.link(v.tensor_scalar(hot[:, b, 0, :], hot[:, b, 0, :], pair[:, b, 0:1], None, ALU.mult))
                        v.scalar_tensor_tensor(flat(comb[:, bass.ds(k, 1), :]), hot[:, b, 1, :], pair[:, b, 1:2], hot[:, b, 0, :],
                                               ALU.mult, ALU.add).then_inc(s.routed.sem, 1)
    end(TILES, *two)
    return chosen, comb


def l1_ffn(e):
    nc, s, ps = e.nc, e.s, e.ps
    dve = e.chain["dve"]
    E8 = EXPERTS
    with ExitStack() as ctx:
        sb = memory(e, ctx, "l1_ffn")
        w_router = sb("w_router", [P, DCH, E8])
        w_gate = sb("w_gate", [P, DCH, MOE_HID])
        w_down = sb("w_down", [P, MCH, E8, D])
        tri32 = sb("tri32", [P, P])
        tri = sb("tri", [P, P], BF16)
        ones_bf = sb("ones_bf", [P, P], BF16)
        with nc.Block() as block:
            @block.sync
            def _(sp):
                load(e, sp, (tri32, "tri"), (w_gate, "L1_gate"), (w_down, "L1_down"))

            @block.vector
            def _(v):
                v.wait_ge(e.loaded, e.loads)
                v.tensor_copy(tri[:], tri32[:])
                v.memset(ones_bf[:], 1.0)
        chosen, comb = route(e, ctx, "l1_route", (w_router, "L1_router"), True)

        totals = sb("totals", [P, ALL_TILES, E8])
        scan = sb("scan", [P, 2, ALL_TILES, E8])
        keep = sb("keep", [P, ALL_TILES, E8])
        weight = sb("weight", [P, ALL_TILES])
        begin(1, s.sums_psum)
        n8 = ALL_TILES * E8
        with nc.Block() as block:
            @block.tensor
            def _(pe):
                pe.matmul(ps[0][:, 0:n8], tri[:], flat(chosen[:]), start=True, stop=True)
                pe.matmul(ps[1][:, 0:n8], ones_bf[:], flat(chosen[:]), start=True, stop=True).then_inc(s.sums_psum.sem, 1)

            @block.vector
            def _(v):
                dve.begin(v)
                v.wait_ge(s.sums_psum.sem, s.sums_psum.at(0))
                v.tensor_copy(flat(totals[:]), ps[1][:, 0:n8])
                dve.link(v.tensor_copy(flat(scan[:, 0, :, :]), ps[1][:, 0:n8]))
                step, at = 1, 0
                while step < ALL_TILES:
                    v.tensor_copy(scan[:, 1 - at, 0:step, :], scan[:, at, 0:step, :])
                    dve.link(v.tensor_tensor(scan[:, 1 - at, step:, :], scan[:, at, step:, :], scan[:, at, 0:ALL_TILES - step, :], ALU.add))
                    step, at = 2 * step, 1 - at
                dve.link(v.tensor_tensor(keep[:], scan[:, at, :, :], totals[:], ALU.subtract))
                dve.link(v.tensor_tensor(flat(keep[:]), ps[0][:, 0:n8], flat(keep[:]), ALU.add))
                dve.link(v.scalar_tensor_tensor(comb[:], keep[:], float(CAPACITY), comb[:], ALU.is_le, ALU.mult))
                dve.link(v.tensor_reduce(weight[:], comb[:], AX.X, ALU.add))
                dve.link(v.tensor_scalar(weight[:], weight[:], 1e-6, None, ALU.add))
                dve.link(v.reciprocal(weight[:], weight[:]))
                v.tensor_tensor(comb[:], comb[:], weight[:].unsqueeze(2).broadcast_to((P, ALL_TILES, E8)), ALU.mult)
        end(1, s.sums_psum)

        hid = sb("hid", [P, MCH, BATCH, P])
        acc = sb("acc", [P, BATCH, D])
        two = (s.c_ready, s.cT_psum, s.cT_ready, s.hidden_psum, s.hidden_ready, s.ln_var, s.ln_rstd)
        begin(2, *two)
        begin(8, s.expert_psum, s.expert_added)
        with nc.Block() as block:
            @block.tensor
            def _(pe):
                with pe.Fori(0, TILES) as it:
                    for b in range(BATCH):
                        transpose_c(e, pe, it, b, b)
                    pe.wait_ge(s.cT_ready.sem, s.cT_ready.at(it, 2))
                    for n in range(2):
                        pe.wait_ge(s.hidden_ready.sem, s.hidden_ready.before(it, n + 1))
                        for m in range(2):
                            f = 2 * n + m
                            for ch in range(DCH):
                                mm = pe.matmul(ps[2 + n][:, m * 2 * P:(m + 1) * 2 * P], w_gate[:, ch, f * P:(f + 1) * P],
                                               e.cT[:, :, ch, :], start=(m, ch) == (0, 0), stop=ch == DCH - 1, skip_group_check=True)
                        mm.then_inc(s.hidden_psum.sem, 1)
                    pe.wait_ge(s.hidden_ready.sem, s.hidden_ready.at(it, 2))
                    for b in range(BATCH):
                        for n in range(E8 // 2):
                            pe.wait_ge(s.expert_added.sem, s.expert_added.at(it, 4 * b + n + 1 - 4))
                            for f in range(MCH):
                                mm = pe.matmul(ps[4 + n], hid[:, f, b, :], flat(w_down[:, f, 2 * n:2 * n + 2, :]),
                                               start=f == 0, stop=f == MCH - 1)
                            mm.then_inc(s.expert_psum.sem, 1)

            @block.scalar
            def _(act_):
                with act_.Fori(0, TILES) as it:
                    for b in range(BATCH):
                        copy_cT(e, act_, it, b, b, s.hidden_psum)
                    for n in range(2):
                        act_.wait_ge(s.hidden_psum.sem, s.hidden_psum.at(it, n + 1))
                        act_.wait_ge(s.expert_psum.sem, s.expert_psum.at(it, 0))
                        nc.scalar.activation(hid[:, 2 * n:2 * n + 2, :, :].rearrange("p f b n -> p (f b n)"), ps[2 + n], ACT.Silu)\
                          .then_inc(s.hidden_ready.sem, 1)

            @block.vector
            def _(v):
                with v.Fori(0, TILES) as it:
                    dve.begin(v)
                    for b in range(BATCH):
                        v.wait_ge(s.hidden_psum.sem, s.hidden_psum.before(it, 2))
                        normalise(e, v, it, b)
                    for b in range(BATCH):
                        k = it + b * TILES
                        for n in range(E8 // 2):
                            v.wait_ge(s.expert_psum.sem, s.expert_psum.at(it, 4 * b + n + 1))
                            for m in range(2):
                                x = 2 * n + m
                                add = v.scalar_tensor_tensor(
                                    tile_of(e.x, it, b) if x == E8 - 1 else acc[:, b, :], ps[4 + n][:, m * D:(m + 1) * D],
                                    flat(comb[:, bass.ds(k, 1), x:x + 1]), tile_of(e.x, it, b) if x == 0 else acc[:, b, :], ALU.mult, ALU.add)
                                dve.link(add)
                            v.sem_inc(s.expert_added.sem, 1)
                        stats_dve(e, v, it, b)

            @block.gpsimd
            def _(p):
                with p.Fori(0, TILES) as it:
                    for b in range(BATCH):
                        stats_pool(e, p, it, b)
        end(TILES, *two, s.expert_psum, s.expert_added)


XH, XD = 16, 16


def cross_attention(e, name, biased, sink):
    nc, s, ps = e.nc, e.s, e.ps
    dve = e.chain["dve"]
    with ExitStack() as ctx:
        sb = memory(e, ctx, name)
        wq = sb("wq", [XD, XH, D])
        wk = sb("wk", [P, DCH, D])
        wv = sb("wv", [P, DCH, D])
        wo = sb("wo", [P, DCH, D])
        keysT = sb("keysT", [XD, XH, BATCH, CTX])
        A = sb("A", [P, DCH, BATCH, XH, CTX])
        V = sb("V", [P, BATCH, XH // 2, 2, XD])
        rows = 1 if biased else 2
        add_rows = sb("add_rows", [rows, BATCH, XH, CTX])
        probs = sb("probs", [P, BATCH, XH, CTX])
        probsT = sb("probsT", [P, BATCH, XH // 2, P])
        top = sb("top", [P, BATCH, XH])
        den = sb("den", [P, BATCH, XH])
        rec = sb("rec", [P, BATCH, XH])
        o = sb("o", [P, BATCH, D])
        oT = sb("oT", [P, BATCH, DCH, P])
        if biased:
            bq = sb("bq", [XD, XH])
            bk = sb("bk", [XD, XH])
            bv = sb("bv", [P, D])
            bo = sb("bo", [1, D])
            given = ((bq, name + "bq"), (bk, name + "bk"), (bv, name + "bv"), (bo, name + "bo"))
        else:
            slopes = sb("slopes", [2, XH])
            key_pos = sb("key_pos", [2, BATCH, CTX], I32)
            key_posf = sb("key_posf", [2, BATCH, CTX])
            query_pos = sb("query_pos", [2, ALL_TILES, P], I32)
            query_row = sb("query_row", [2, BATCH, P])
            mask_i = sb("mask_i", [P, ALL_TILES, CTX], I32)
            mask = sb("mask", [P, ALL_TILES, CTX], BF16)
            given = ((slopes, "slopes"), (key_pos, "key_pos"), (query_pos, "query_pos"), (mask_i, "mask_if1"))
        begin(1, s.prep_psum, s.prep_ready)
        with nc.Block() as block:
            @block.sync
            def _(sp):
                load(e, sp, (wq, name + "wq"), (wk, name + "wk"), (wv, name + "wv"), (wo, name + "wo"), *given)

            @block.tensor
            def _(pe):
                pe.wait_ge(e.loaded, e.loads)
                for h in range(XH):
                    for ch in range(DCH):
                        mm = pe.matmul(ps[h // 4][0:XD, (h % 4) * P:(h % 4 + 1) * P], wk[:, ch, h * XD:(h + 1) * XD],
                                       e.ctxT[:, ch, :, :], start=(h % 4, ch) == (0, 0), stop=ch == DCH - 1, skip_group_check=True)
                for b in range(BATCH):
                    for ch in range(DCH):
                        mm = pe.matmul(ps[4][:, b * D:(b + 1) * D], e.ctxT2[:, ch, b, :, :], wv[:, ch, :],
                                       start=(b, ch) == (0, 0), stop=ch == DCH - 1, skip_group_check=True)
                mm.then_inc(s.prep_psum.sem, 1)

            @block.vector
            def _(v):
                dve.begin(v)
                dve.link(v.memset(V[:], 0.0))
                v.wait_ge(e.loaded, e.loads)
                v.wait_ge(s.prep_psum.sem, s.prep_psum.at(0))
                kt = keysT[:].rearrange("p h b n -> p h (b n)")
                kp = e.psum[0:XD, 0:4, :].rearrange("p a (h n) -> p (a h) n", n=P)
                if biased:
                    v.tensor_tensor(kt, kp, bk[:].unsqueeze(2).broadcast_to((XD, XH, P)), ALU.add)
                else:
                    v.tensor_copy(kt, kp)
                    dve.link(v.tensor_copy(key_posf[:], key_pos[:]))
                    for b in range(BATCH):
                        v.tensor_tensor(add_rows[:, b, :, :], slopes[:].unsqueeze(2).broadcast_to((2, XH, CTX)),
                                        key_posf[:, b, :].unsqueeze(1).broadcast_to((2, XH, CTX)), ALU.mult)
                    v.tensor_scalar(mask[:], mask_i[:], 0.0, MASKED, ALU.is_equal, ALU.mult)
                for b in range(BATCH):
                    for half in range(2):
                        r = slice(half * CTX, (half + 1) * CTX)
                        of = ps[4][r, b * D:(b + 1) * D].rearrange("p (h two x) -> p h two x", two=2, x=XD)[:, :, half, :]
                        to = V[r, b, :, half, :]
                        if biased:
                            v.tensor_tensor(to, of, bv[r, :].rearrange("p (h two x) -> p h two x", two=2, x=XD)[:, :, half, :], ALU.add)
                        else:
                            v.tensor_copy(to, of)
        end(1, s.prep_psum)
        begin(8, s.prep_psum)
        begin(8, s.prep_ready)
        with nc.Block() as block:
            @block.tensor
            def _(pe):
                for ch in range(DCH):
                    for g in range(4):
                        for m in range(4):
                            h = 4 * g + m
                            mm = pe.matmul(ps[4 * ch + g][:, m * P:(m + 1) * P], wq[:, h, ch * P:(ch + 1) * P],
                                           keysT[:, h, :, :], start=m == 0, stop=True, skip_group_check=True)
                        mm.then_inc(s.prep_psum.sem, 1)
                if biased:
                    pe.wait_ge(s.prep_ready.sem, s.prep_ready.at(0, 4))
                    for h in range(XH):
                        mm = pe.matmul(ps[h // 4][0:1, (h % 4) * P:(h % 4 + 1) * P], bq[:, h:h + 1], keysT[:, h, :, :],
                                       start=h % 4 == 0, stop=True, skip_group_check=True)
                    mm.then_inc(s.prep_last.sem, 1)

            @block.vector
            def _(v):
                for ch in range(DCH):
                    for g in range(4):
                        v.wait_ge(s.prep_psum.sem, s.prep_psum.at(0, 4 * ch + g + 1))
                        v.tensor_copy(A[:, ch, :, 4 * g:4 * g + 4, :], ps[4 * ch + g].rearrange("p (h b n) -> p b h n", b=BATCH, h=4))\
                         .then_inc(s.prep_ready.sem, 1)
                if biased:
                    v.wait_ge(s.prep_last.sem, s.prep_last.at(0))
                    for b in range(BATCH):
                        v.tensor_copy(add_rows[:, b, :, :], e.psum[0:1, 0:4, :].rearrange("p a (h b n) -> p (a h) b n", b=BATCH, h=4)[:, :, b, :])
        end(1, s.prep_psum, s.prep_ready)
        if biased:
            s.prep_last.base += 1

        two = (s.c_ready, s.cT_psum, s.cT_ready, s.scores_psum, s.max_ready, s.probs_ready, s.probsT_psum, s.probsT_ready,
               s.probsT_ready2, s.mix_psum, s.mix_ready, s.mixT_psum, s.mixT_ready, s.out_psum, s.ln_var, s.ln_rstd)\
            + (() if biased else (s.row_ready,))
        begin(2, *two)
        BANKS = 4
        with nc.Block() as block:
            @block.tensor
            def _(pe):
                def scores(m):
                    pe.wait_ge(s.cT_ready.sem, s.cT_ready.at(m.it, m.k))
                    pe.wait_ge(s.probsT_ready.sem, s.probsT_ready.before(m.it, m.k))
                    pe.wait_ge(s.probsT_ready2.sem, s.probsT_ready2.before(m.it, m.k))
                    if not biased:
                        pe.wait_ge(s.row_ready.sem, s.row_ready.at(m.it, m.k))
                    for half in range(2):
                        bank = ps[BANKS * m.b + 2 + half]
                        hs = slice(half * XH // 2, (half + 1) * XH // 2)
                        for ch in range(DCH):
                            pe.matmul(bank, e.cT[:, m.b, ch, :], A[:, ch, m.b, hs, :].rearrange("p h n -> p (h n)"), start=ch == 0, stop=False)
                        if not biased:
                            pe.matmul(bank, e.ident_bf[:], mask[:, bass.ds(m.it + m.b * TILES, 1), :].broadcast_to((P, XH // 2, CTX)),
                                      start=False, stop=False)
                        mm = pe.matmul(bank, e.ones[0:1, :] if biased else query_row[:, m.b, :],
                                       add_rows[:, m.b, hs, :].rearrange("p h n -> p (h n)"), start=False, stop=True)
                    mm.then_inc(s.scores_psum.sem, 1)

                def probs_transposed(m):
                    pe.wait_ge(s.probs_ready.sem, s.probs_ready.at(m.it, m.k))
                    for j in range(XH // 2):
                        mm = pe.transpose(ps[BANKS * m.b + 2 + j // 4][:, (j % 4) * P:(j % 4 + 1) * P],
                                          probs[:, m.b, 2 * j:2 * j + 2, :].rearrange("p h n -> p (h n)"), e.ident[:])
                    mm.then_inc(s.probsT_psum.sem, 1)

                def mix(m):
                    pe.wait_ge(s.probsT_ready.sem, s.probsT_ready.at(m.it, m.k))
                    pe.wait_ge(s.probsT_ready2.sem, s.probsT_ready2.at(m.it, m.k))
                    pe.wait_ge(s.ln_var.sem, s.ln_var.before(m.it, m.k))
                    for j in range(XH // 2):
                        mm = pe.matmul(ps[BANKS * m.b + 1][:, j * 2 * XD:(j + 1) * 2 * XD], probsT[:, m.b, j, :], flat(V[:, m.b, j, :, :]),
                                       start=j == 0, stop=True, skip_group_check=True)
                    mm.then_inc(s.mix_psum.sem, 1)

                def mix_transposed(m):
                    pe.wait_ge(s.mix_ready.sem, s.mix_ready.at(m.it, m.k))
                    for ch in range(DCH):
                        mm = pe.transpose(ps[BANKS * m.b + 1][:, D + ch * P:D + (ch + 1) * P], o[:, m.b, ch * P:(ch + 1) * P], e.ident[:])
                    mm.then_inc(s.mixT_psum.sem, 1)

                def projected(m):
                    pe.wait_ge(s.mixT_ready.sem, s.mixT_ready.at(m.it, m.k))
                    bank = ps[BANKS * m.b + 1][:, 0:D]
                    if biased:
                        pe.matmul(bank, e.ones[0:1, :], bo[:], start=True, stop=False)
                    for ch in range(DCH):
                        mm = pe.matmul(bank, oT[:, m.b, ch, :], wo[:, ch, :], start=ch == 0 and not biased, stop=ch == DCH - 1)
                    mm.then_inc(s.out_psum.sem, 1)

                def first(new, after):
                    transpose_c(e, pe, new.it, new.b, BANKS * new.b)
                    transpose_c(e, pe, after.it, after.b, BANKS * after.b)
                    scores(new)

                def step(now, new, after):
                    probs_transposed(now)
                    if new:
                        scores(new)
                    mix(now)
                    if after:
                        transpose_c(e, pe, after.it, after.b, BANKS * after.b)
                    mix_transposed(now)
                    projected(now)

                tiles(pe, e.chain["pe"], first, step)

            @block.scalar
            def _(act_):
                def exp(m):
                    act_.wait_ge(s.max_ready.sem, s.max_ready.at(m.it, m.k))
                    nc.scalar.activation(flat(probs[:, m.b, :, :]), flat(probs[:, m.b, :, :]), ACT.Exp, scale=float(XD) ** -0.5)\
                      .then_inc(s.probs_ready.sem, 1)

                def copy_probsT(m):
                    act_.wait_ge(s.probsT_psum.sem, s.probsT_psum.at(m.it, m.k))
                    act_.wait_ge(s.mix_psum.sem, s.mix_psum.before(m.it, m.k))
                    nc.scalar.copy(flat(probsT[:, m.b, 0:4, :]), ps[BANKS * m.b + 2]).then_inc(s.probsT_ready.sem, 1)

                def copy_oT(m):
                    act_.wait_ge(s.mixT_psum.sem, s.mixT_psum.at(m.it, m.k))
                    act_.wait_ge(s.out_psum.sem, s.out_psum.before(m.it, m.k))
                    nc.scalar.copy(flat(oT[:, m.b, :, :]), ps[BANKS * m.b + 1][:, D:2 * D]).then_inc(s.mixT_ready.sem, 1)

                def first(new, after):
                    copy_cT(e, act_, new.it, new.b, BANKS * new.b, s.scores_psum)
                    copy_cT(e, act_, after.it, after.b, BANKS * after.b, s.scores_psum)
                    exp(new)

                def step(now, new, after):
                    copy_probsT(now)
                    if after:
                        copy_cT(e, act_, after.it, after.b, BANKS * after.b, s.scores_psum)
                    copy_oT(now)
                    if new:
                        exp(new)

                tiles(act_, e.chain["act"], first, step)

            @block.vector
            def _(v):
                def scores_of(m):
                    return e.psum[:, BANKS * m.b + 2:BANKS * m.b + 4, :].rearrange("p a (h n) -> p (a h) n", n=CTX)

                def tile_in(m):
                    normalise(e, v, m.it, m.b)
                    if not biased:
                        v.wait_ge(s.scores_psum.sem, s.scores_psum.before(m.it, m.k))
                        v.tensor_copy(query_row[:, m.b, :], flat(query_pos[:, bass.ds(m.it + m.b * TILES, 1), :])).then_inc(s.row_ready.sem, 1)

                def maxima(m):
                    v.wait_ge(s.scores_psum.sem, s.scores_psum.at(m.it, m.k))
                    dve.link(v.tensor_reduce(top[:, m.b, :], scores_of(m), AX.X, ALU.max))

                def subtract(m):
                    v.wait_ge(s.probsT_psum.sem, s.probsT_psum.before(m.it, m.k))
                    v.tensor_tensor(probs[:, m.b, :, :], scores_of(m), top[:, m.b, :].unsqueeze(2).broadcast_to((P, XH, CTX)), ALU.subtract)\
                     .then_inc(s.max_ready.sem, 1)

                def copy_probsT(m):
                    v.wait_ge(s.probsT_psum.sem, s.probsT_psum.at(m.it, m.k))
                    v.wait_ge(s.mix_psum.sem, s.mix_psum.before(m.it, m.k))
                    v.tensor_copy(flat(probsT[:, m.b, 4:8, :]), ps[BANKS * m.b + 3]).then_inc(s.probsT_ready2.sem, 1)

                def denominators(m):
                    v.wait_ge(s.probs_ready.sem, s.probs_ready.at(m.it, m.k))
                    dve.link(v.tensor_reduce(den[:, m.b, :], probs[:, m.b, :, :], AX.X, ALU.add))
                    if sink:
                        dve.link(v.tensor_scalar(den[:, m.b, :], den[:, m.b, :], 1.0, None, ALU.add))
                    dve.link(v.reciprocal(rec[:, m.b, :], den[:, m.b, :]))

                def weighted(m):
                    v.wait_ge(s.mix_psum.sem, s.mix_psum.at(m.it, m.k))
                    v.wait_ge(s.mixT_psum.sem, s.mixT_psum.before(m.it, m.k))
                    v.tensor_tensor(o[:, m.b, :].rearrange("p (h x) -> p h x", x=XD),
                                    ps[BANKS * m.b + 1][:, 0:D].rearrange("p (h x) -> p h x", x=XD),
                                    rec[:, m.b, :].unsqueeze(2).broadcast_to((P, XH, XD)), ALU.mult).then_inc(s.mix_ready.sem, 1)

                def first(new, after):
                    tile_in(new)
                    tile_in(after)
                    maxima(new)
                    subtract(new)

                def step(now, new, after):
                    copy_probsT(now)
                    denominators(now)
                    if after:
                        tile_in(after)
                    if new:
                        maxima(new)
                    weighted(now)
                    if new:
                        subtract(new)
                    v.wait_ge(s.out_psum.sem, s.out_psum.at(now.it, now.k))
                    add_to_x(e, v, now.it, now.b, ps[BANKS * now.b + 1][:, 0:D])

                tiles(v, dve, first, step)

            @block.gpsimd
            def _(p):
                with p.Fori(0, TILES) as it:
                    for b in range(BATCH):
                        stats_pool(e, p, it, b)
        end(TILES, *two)


def l2_xattn(e):
    cross_attention(e, "L2_", True, False)


def l3_xattn(e):
    cross_attention(e, "L3_", False, True)


QI = 704
QCH = -(-QI // P)
QW = [min(P, QI - j * P) for j in range(QCH)]
QMAX = 127.0
MAGIC = 1.5 * 2.0 ** 23


def quantise(v, dve, to, tmp, of, inverse):
    dve.link(v.tensor_scalar(tmp, of, inverse, -QMAX - 1.0, ALU.mult, ALU.max))
    dve.link(v.tensor_scalar(tmp, tmp, QMAX, MAGIC, ALU.min, ALU.add))
    return v.tensor_scalar(to, tmp, -MAGIC, None, ALU.add)


def l2_ffn(e):
    nc, s, ps = e.nc, e.s, e.ps
    dve = e.chain["dve"]
    with ExitStack() as ctx:
        sb = memory(e, ctx, "l2_ffn")
        clips = sb("clips", [P, 2])
        sig = sb("sig", [P, 2])
        gu_scale = sb("gu_scale", [P, 2, QCH])
        d_scale = sb("d_scale", [P, DCH])
        d_row = sb("d_row", [P, D])
        w_guT = sb("w_guT", [P, DCH, 2, QI], BF16)
        w_dT = sb("w_dT", [P, QCH, D], BF16)
        h = sb("h", [P, QCH, ALL_TILES, P])
        amax = sb("amax", [P, ALL_TILES])
        one = sb("one_max", [P, 1])
        allmax = sb("allmax", [P, 1])
        xs = sb("xs", [P, 2])
        hmax = sb("hmax", [P, TILES, QCH])
        with ExitStack() as inner:
            sbi = lambda n, shape, dt=F32: inner.enter_context(nc.sbuf_tensor(n, shape, dt))
            w_gu = sbi("w_gu", [P, 2, QCH, D])
            w_d = sbi("w_d", [P, DCH, QI])
            tmp = sbi("q_tmp", [P, QCH * D])
            q_gu = sbi("q_gu", [P, 2, QCH, D], BF16)
            q_d = sbi("q_d", [P, DCH, QI], BF16)
            inv = sbi("inv", [P, 2 * QCH + DCH])
            diag = sbi("diag", [P, DCH, P])
            begin(1, s.probs_ready)
            with nc.Block() as block:
                @block.sync
                def _(sp):
                    load(e, sp, (w_gu, "L2_gu"), (w_d, "L2_d"), (clips, "L2_clips"))

                @block.scalar
                def _(act_):
                    act_.wait_ge(e.loaded, e.loads)
                    nc.scalar.activation(sig[:], clips[:], ACT.Exp, scale=-1.0).then_inc(s.probs_ready.sem, 1)

                @block.vector
                def _(v):
                    dve.begin(v)
                    v.memset(hmax[:], 0.0)
                    v.wait_ge(e.loaded, e.loads)
                    dve.link(v.memset(gu_scale[:], 0.0))
                    for n in range(2):
                        v.tensor_reduce(gu_scale[:, n, 0:QCH - 1], w_gu[:, n, 0:QCH - 1, :], AX.X, ALU.max, apply_absolute_value=True)
                        v.tensor_reduce(gu_scale[0:QW[-1], n, QCH - 1:QCH], w_gu[0:QW[-1], n, QCH - 1, :], AX.X, ALU.max, apply_absolute_value=True)
                    dve.link(v.tensor_reduce(d_scale[:], w_d[:], AX.X, ALU.max, apply_absolute_value=True))
                    v.tensor_scalar(gu_scale[:], gu_scale[:], 1.0 / QMAX, None, ALU.mult)
                    dve.link(v.tensor_scalar(d_scale[:], d_scale[:], 1.0 / QMAX, None, ALU.mult))
                    for n in range(2):
                        v.reciprocal(inv[:, n * QCH:n * QCH + QCH - 1], gu_scale[:, n, 0:QCH - 1])
                        v.reciprocal(inv[0:QW[-1], n * QCH + QCH - 1:(n + 1) * QCH], gu_scale[0:QW[-1], n, QCH - 1:QCH])
                    dve.link(v.reciprocal(inv[:, 2 * QCH:], d_scale[:]))
                    for n in range(2):
                        for j in range(QCH):
                            r = slice(0, QW[j])
                            dve.link(quantise(v, dve, q_gu[r, n, j, :], tmp[r, 0:D], w_gu[r, n, j, :], inv[r, n * QCH + j:n * QCH + j + 1]))
                    for ch in range(DCH):
                        dve.link(quantise(v, dve, q_d[:, ch, :], tmp[:, 0:QI], w_d[:, ch, :], inv[:, 2 * QCH + ch:2 * QCH + ch + 1]))
                        dve.link(v.tensor_scalar(diag[:, ch, :], e.ident[:], d_scale[:, ch:ch + 1], None, ALU.mult))
                    v.wait_ge(s.probs_ready.sem, s.probs_ready.at(0))
                    dve.link(v.tensor_scalar(sig[:], sig[:], 1.0, None, ALU.add))
                    dve.link(v.reciprocal(sig[:], sig[:]))
                    v.tensor_scalar(sig[:], sig[:], 1.0 / QMAX, None, ALU.mult)
            end(1, s.probs_ready)
            begin(8, s.prep_psum, s.prep_ready)
            with nc.Block() as block:
                @block.tensor
                def _(pe):
                    for n in range(2):
                        for ch in range(DCH):
                            for j in range(QCH):
                                bank = ps[2 * (2 * n + ch) + j // 4]
                                mm = pe.matmul(bank[:, (j % 4) * P:(j % 4) * P + QW[j]], q_gu[0:QW[j], n, j, ch * P:(ch + 1) * P],
                                               e.ident_bf[0:QW[j], 0:QW[j]], start=j % 4 == 0, stop=True, skip_group_check=True)
                            mm.then_inc(s.prep_psum.sem, 1)
                    pe.wait_ge(s.prep_ready.sem, s.prep_ready.at(0, 4))
                    for j in range(QCH):
                        for ch in range(DCH):
                            mm = pe.matmul(ps[j // 2][0:QW[j], (j % 2) * D + ch * P:(j % 2) * D + (ch + 1) * P], q_d[:, ch, j * P:j * P + QW[j]],
                                           e.ident_bf[:], start=(j % 2, ch) == (0, 0), stop=True, skip_group_check=True)
                    mm.then_inc(s.prep_psum.sem, 1)
                    for ch in range(DCH):
                        mm = pe.matmul(ps[4][:, ch * P:(ch + 1) * P], e.ones[:], diag[:, ch, :], start=ch == 0, stop=True, skip_group_check=True)
                    mm.then_inc(s.prep_psum.sem, 1)

                @block.vector
                def _(v):
                    for n in range(2):
                        for ch in range(DCH):
                            k = 2 * n + ch
                            v.wait_ge(s.prep_psum.sem, s.prep_psum.at(0, k + 1))
                            v.tensor_copy(w_guT[:, ch, n, :], e.psum[:, 2 * k:2 * k + 2, :].rearrange("p a n -> p (a n)")[:, 0:QI])\
                             .then_inc(s.prep_ready.sem, 1)
                    v.wait_ge(s.prep_psum.sem, s.prep_psum.at(0, 5))
                    for j in range(QCH):
                        v.tensor_copy(w_dT[0:QW[j], j, :], ps[j // 2][0:QW[j], (j % 2) * D:(j % 2 + 1) * D])
                    v.wait_ge(s.prep_psum.sem, s.prep_psum.at(0, 6))
                    v.tensor_copy(d_row[:], ps[4][:, 0:D])
            s.prep_psum.base += 6
            s.prep_ready.base += 4

        def all_max(of):
            begin(1, s.max_ready, s.allreduce)
            with nc.Block() as block:
                @block.vector
                def _(v):
                    v.tensor_reduce(one[:], of, AX.X, ALU.max).then_inc(s.max_ready.sem, 1)

                @block.gpsimd
                def _(p):
                    p.wait_ge(s.max_ready.sem, s.max_ready.at(0))
                    p.partition_all_reduce(allmax[:], one[:], P, bass.bass_isa.ReduceOp.max).then_inc(s.allreduce.sem, 1)

        cs2 = sb("cs2", [P, BATCH, D])
        begin(2, s.c_ready, s.max_ready)
        with nc.Block() as block:
            @block.vector
            def _(v):
                with v.Fori(0, TILES) as it:
                    dve.begin(v)
                    for b in range(BATCH):
                        k = it + b * TILES
                        dve.link(v.tensor_scalar(cs2[:, b, :], tile_of(e.x, it, b), flat(e.mean_var[:, bass.ds(k, 1), 0:1]),
                                                 e.rstd[:, bass.ds(k, 1)], ALU.subtract, ALU.mult))
                        v.tensor_reduce(amax[:, bass.ds(k, 1)], cs2[:, b, :], AX.X, ALU.max, apply_absolute_value=True)
        all_max(amax[:])
        gsc = sb("gsc", [P, 2, QCH])
        with nc.Block() as block:
            @block.vector
            def _(v):
                dve.begin(v)
                v.wait_ge(s.allreduce.sem, s.allreduce.at(0))
                dve.link(v.tensor_scalar(xs[:, 0:1], allmax[:], sig[:, 0:1], None, ALU.mult))
                v.reciprocal(xs[:, 1:2], xs[:, 0:1])
                v.tensor_scalar(gsc[:], gu_scale[:], xs[:, 0:1], None, ALU.mult)
        end(1, s.max_ready, s.allreduce)

        q_tmp = sb("q_tmp2", [P, BATCH, QCH, P])
        xq = sb("xq", [P, BATCH, D], BF16)
        xqT = sb("xqT", [P, BATCH, DCH, P], BF16)
        gate = sb("q_gate", [P, QCH, BATCH * P])
        two = (s.c_ready, s.cT_psum, s.cT_ready)
        begin(2, *two)
        begin(QCH, s.hidden_psum, s.gate_done, s.hidden_ready)
        with nc.Block() as block:
            @block.tensor
            def _(pe):
                with pe.Fori(0, TILES) as it:
                    for b in range(BATCH):
                        pe.wait_ge(s.c_ready.sem, s.c_ready.at(it, b + 1))
                        pe.wait_ge(s.cT_ready.sem, s.cT_ready.before(it, b + 1))
                        for ch in range(DCH):
                            mm = pe.matmul(ps[b][:, ch * P:(ch + 1) * P], xq[:, b, ch * P:(ch + 1) * P], e.ident_bf[:],
                                           start=ch == 0, stop=True, skip_group_check=True)
                        mm.then_inc(s.cT_psum.sem, 1)
                    pe.wait_ge(s.cT_ready.sem, s.cT_ready.at(it, 2))
                    for j in range(QCH):
                        pe.wait_ge(s.hidden_ready.sem, s.hidden_ready.before(it, j + 1))
                        for n in range(2):
                            for ch in range(DCH):
                                mm = pe.matmul(ps[2 + j][0:QW[j], n * 2 * P:(n + 1) * 2 * P], w_guT[:, ch, n, j * P:j * P + QW[j]],
                                               xqT[:, :, ch, :], start=(n, ch) == (0, 0), stop=ch == DCH - 1, skip_group_check=True)
                        mm.then_inc(s.hidden_psum.sem, 1)

            @block.scalar
            def _(act_):
                with act_.Fori(0, TILES) as it:
                    for b in range(BATCH):
                        act_.wait_ge(s.cT_psum.sem, s.cT_psum.at(it, b + 1))
                        act_.wait_ge(s.hidden_psum.sem, s.hidden_psum.before(it, QCH))
                        nc.scalar.copy(flat(xqT[:, b, :, :]), ps[b][:, 0:D]).then_inc(s.cT_ready.sem, 1)
                    for j in range(QCH):
                        act_.wait_ge(s.hidden_psum.sem, s.hidden_psum.at(it, j + 1))
                        act_.wait_ge(s.hidden_ready.sem, s.hidden_ready.before(it, j + 1))
                        nc.scalar.activation(gate[0:QW[j], j, :], ps[2 + j][0:QW[j], 0:2 * P], ACT.Silu, scale=gsc[0:QW[j], 0, j:j + 1])\
                          .then_inc(s.gate_done.sem, 1)

            @block.vector
            def _(v):
                with v.Fori(0, TILES) as it:
                    dve.begin(v)
                    for b in range(BATCH):
                        k = it + b * TILES
                        dve.link(v.tensor_scalar(e.cs[:, b, :], tile_of(e.x, it, b), flat(e.mean_var[:, bass.ds(k, 1), 0:1]),
                                                 e.rstd[:, bass.ds(k, 1)], ALU.subtract, ALU.mult))
                        v.wait_ge(s.cT_psum.sem, s.cT_psum.before(it, b + 1))
                        quantise(v, dve, xq[:, b, :], e.cs[:, b, :], e.cs[:, b, :], xs[:, 1:2]).then_inc(s.c_ready.sem, 1)
                    for j in range(QCH):
                        r = slice(0, QW[j])
                        to = h[r, j, :, :].rearrange("p (b t) n -> p b t n", b=BATCH)[:, :, bass.ds(it, 1), :].rearrange("p b t n -> p b (t n)")
                        v.wait_ge(s.gate_done.sem, s.gate_done.at(it, j + 1))
                        dve.link(v.scalar_tensor_tensor(to, ps[2 + j][r, 2 * P:4 * P].rearrange("p (b n) -> p b n", b=BATCH), gsc[r, 1, j:j + 1],
                                                        gate[r, j, :].rearrange("p (b n) -> p b n", b=BATCH), ALU.mult, ALU.mult))
                        v.tensor_reduce(flat(hmax[r, bass.ds(it, 1), j:j + 1]), to, AX.XY, ALU.max, apply_absolute_value=True)\
                         .then_inc(s.hidden_ready.sem, 1)
        end(TILES, *two, s.hidden_psum, s.gate_done, s.hidden_ready)

        all_max(flat(hmax[:]))
        with nc.Block() as block:
            @block.vector
            def _(v):
                dve.begin(v)
                v.wait_ge(s.allreduce.sem, s.allreduce.at(0))
                dve.link(v.tensor_scalar(xs[:, 0:1], allmax[:], sig[:, 1:2], None, ALU.mult))
                v.reciprocal(xs[:, 1:2], xs[:, 0:1])
                v.tensor_scalar(d_row[:], d_row[:], xs[:, 0:1], None, ALU.mult)
        end(1, s.max_ready, s.allreduce)

        hq = sb("hq", [P, BATCH, QCH, P], BF16)
        out = sb("q_out", [P, BATCH, D])
        two = (s.hidden_ready, s.out_psum, s.ln_var, s.ln_rstd)
        begin(2, *two)
        with nc.Block() as block:
            @block.tensor
            def _(pe):
                with pe.Fori(0, TILES) as it:
                    for b in range(BATCH):
                        pe.wait_ge(s.hidden_ready.sem, s.hidden_ready.at(it, b + 1))
                        pe.wait_ge(s.ln_var.sem, s.ln_var.before(it, b + 1))
                        for j in range(QCH):
                            mm = pe.matmul(ps[b][:, 0:D], hq[0:QW[j], b, j, :], w_dT[0:QW[j], j, :], start=j == 0, stop=j == QCH - 1)
                        mm.then_inc(s.out_psum.sem, 1)

            @block.vector
            def _(v):
                with v.Fori(0, TILES) as it:
                    dve.begin(v)
                    for b in range(BATCH):
                        k = it + b * TILES
                        v.wait_ge(s.out_psum.sem, s.out_psum.before(it, b + 1))
                        full = slice(0, QCH - 1)
                        dve.link(quantise(v, dve, hq[:, b, full, :], q_tmp[:, b, full, :],
                                          h[:, full, bass.ds(k, 1), :].rearrange("p j t n -> p j (t n)"), xs[:, 1:2]))
                        r = slice(0, QW[-1])
                        quantise(v, dve, hq[r, b, QCH - 1, :], q_tmp[r, b, QCH - 1, :], flat(h[r, QCH - 1, bass.ds(k, 1), :]), xs[r, 1:2])\
                            .then_inc(s.hidden_ready.sem, 1)
                    for b in range(BATCH):
                        v.wait_ge(s.out_psum.sem, s.out_psum.at(it, b + 1))
                        dve.link(v.tensor_tensor(out[:, b, :], ps[b][:, 0:D], d_row[:], ALU.mult))
                        add_to_x(e, v, it, b, out[:, b, :])

            @block.gpsimd
            def _(p):
                with p.Fori(0, TILES) as it:
                    for b in range(BATCH):
                        stats_pool(e, p, it, b)
        end(TILES, *two)


def l3_ffn(e):
    nc, s, ps = e.nc, e.s, e.ps
    dve = e.chain["dve"]
    E8 = EXPERTS
    with ExitStack() as ctx:
        sb = memory(e, ctx, "l3_ffn")
        gate_w = sb("gate_w", [P, DCH, E8])
        w1 = sb("ew1", [P, E8, DCH, MOE_HID])
        w2 = sb("ew2", [P, E8, MCH, D])
        with nc.Block() as block:
            @block.sync
            def _(sp):
                load(e, sp, (w1, "L3_w1"), (w2, "L3_w2"))
        _, comb = route(e, ctx, "l3_route", (gate_w, "L3_gate"), False)
        hid = sb("hid", [P, 2, MCH, BATCH, P])
        acc = sb("acc", [P, BATCH, D])
        two = (s.c_ready, s.cT_psum, s.cT_ready)
        begin(2, *two)
        begin(16, s.hidden_psum, s.hidden_ready)
        begin(8, s.expert_psum, s.expert_added)
        with nc.Block() as block:
            @block.tensor
            def _(pe):
                with pe.Fori(0, TILES) as it:
                    for b in range(BATCH):
                        transpose_c(e, pe, it, b, b)
                    pe.wait_ge(s.cT_ready.sem, s.cT_ready.at(it, 2))

                    def up(x):
                        for n in range(2):
                            bank = ps[2 + 2 * (x % 2) + n]
                            pe.wait_ge(s.hidden_ready.sem, s.hidden_ready.at(it, 2 * x + n + 1 - 4))
                            for m in range(2):
                                f = 2 * n + m
                                for ch in range(DCH):
                                    mm = pe.matmul(bank[:, m * 2 * P:(m + 1) * 2 * P], w1[:, x, ch, f * P:(f + 1) * P], e.cT[:, :, ch, :],
                                                   start=(m, ch) == (0, 0), stop=ch == DCH - 1, skip_group_check=True)
                            mm.then_inc(s.hidden_psum.sem, 1)

                    def down(x):
                        pe.wait_ge(s.hidden_ready.sem, s.hidden_ready.at(it, 2 * x + 2))
                        pe.wait_ge(s.expert_added.sem, s.expert_added.at(it, x + 1 - 2))
                        for b in range(BATCH):
                            for f in range(MCH):
                                mm = pe.matmul(ps[6 + x % 2][:, b * D:(b + 1) * D], hid[:, x % 2, f, b, :], w2[:, x, f, :],
                                               start=(b, f) == (0, 0), stop=f == MCH - 1, skip_group_check=True)
                        mm.then_inc(s.expert_psum.sem, 1)

                    up(0)
                    for x in range(E8):
                        if x + 1 < E8:
                            up(x + 1)
                        down(x)

            @block.scalar
            def _(act_):
                with act_.Fori(0, TILES) as it:
                    for b in range(BATCH):
                        copy_cT(e, act_, it, b, b, s.expert_psum)
                    for x in range(E8):
                        act_.wait_ge(s.expert_psum.sem, s.expert_psum.at(it, x + 1 - 2))
                        for n in range(2):
                            act_.wait_ge(s.hidden_psum.sem, s.hidden_psum.at(it, 2 * x + n + 1))
                            nc.scalar.activation(hid[:, x % 2, 2 * n:2 * n + 2, :, :].rearrange("p f b n -> p (f b n)"),
                                                 ps[2 + 2 * (x % 2) + n], ACT.Silu).then_inc(s.hidden_ready.sem, 1)

            @block.vector
            def _(v):
                with v.Fori(0, TILES) as it:
                    dve.begin(v)
                    for b in range(BATCH):
                        normalise(e, v, it, b)
                    for x in range(E8):
                        v.wait_ge(s.expert_psum.sem, s.expert_psum.at(it, x + 1))
                        for b in range(BATCH):
                            k = it + b * TILES
                            add = v.scalar_tensor_tensor(
                                tile_of(e.x, it, b) if x == E8 - 1 else acc[:, b, :], ps[6 + x % 2][:, b * D:(b + 1) * D],
                                flat(comb[:, bass.ds(k, 1), x:x + 1]), tile_of(e.x, it, b) if x == 0 else acc[:, b, :], ALU.mult, ALU.add)
                        add.then_inc(s.expert_added.sem, 1)
                        v.wait_ge(s.expert_added.sem, s.expert_added.at(it, x + 1))
        end(TILES, *two, s.hidden_psum, s.hidden_ready, s.expert_psum, s.expert_added)


def finish(e):
    with e.nc.Block() as block:
        @block.sync
        def _(sp):
            sp.dma_start(e.out, e.x[:]).then_inc(e.stored, 16)
            sp.wait_ge(e.stored, 16)


def rotary():
    one = np.float32
    half = np.arange(0, DH, 2, dtype=one)
    t = np.arange(SEQ, dtype=one)
    freqs = t[:, None] * (one(1.0) / one(10000.0) ** (half / one(DH)))[None]
    base = (half + one(0.4 * DH)) / one(1.4 * DH)
    scale = base[None] ** ((t - SEQ // 2) / one(P // 2))[:, None]
    cos, sin = np.cos(freqs), np.sin(freqs)
    both = lambda w: np.stack([w * scale, w / scale], 1)
    c, n = both(cos), both(sin)
    parts = np.stack([np.concatenate([c, c], -1), np.concatenate([-n, n], -1)])
    return parts.reshape(2, TILES, P, 2, DH).transpose(2, 0, 1, 3, 4).astype(one)


def laid_out(inp):
    f = {k: np.asarray(v) for k, v in inp.items()}
    rows = lambda w: w.reshape(-1, P, w.shape[-1]).transpose(1, 0, 2)
    ctx = f["ctx_1024"]
    a = {}
    a["x"] = f["x"].reshape(ALL_TILES, P, D).transpose(1, 0, 2)
    a["ident"] = np.eye(P, dtype=np.float32)
    a["ctxT"] = ctx.transpose(2, 0, 1).reshape(DCH, P, BATCH, CTX).transpose(1, 0, 2, 3)
    a["ctx_tok"] = np.concatenate([ctx, ctx], 1).transpose(1, 0, 2)
    a["L0_W_l"] = rows(f["L0_xattn_W_l"].T)
    a["L0_w3"] = rows(np.stack([f["L0_xattn_w_cq"], f["L0_xattn_w_c"], f["L0_xattn_w_q"]], 1))
    a["L0_b3"] = np.tile(np.stack([f["L0_xattn_b_cq"], f["L0_xattn_b_c"], f["L0_xattn_b_q"]])[None], (P, 1))
    a["L0_b_l"] = f["L0_xattn_b_l"][None]
    every = lambda w: np.tile(w[None], (P,) + (1,) * w.ndim)
    per_layer = lambda w: np.stack([rows(w[l]) for l in range(LAYERS)], 1)
    padded = lambda w: np.pad(w, [(0, FCH * P - HID)] + [(0, 0)] * (w.ndim - 1))
    swap = lambda w: np.concatenate([w[..., DH // 2:], w[..., :DH // 2]], -1)
    a["L0_wqkv"] = per_layer(f["L0_ffn_wqkv"])
    a["L0_wo"] = per_layer(f["L0_ffn_wo"])
    a["L0_w1"] = per_layer(f["L0_ffn_w1"]).transpose(1, 0, 2, 3)
    a["L0_w2"] = per_layer(np.stack([padded(w) for w in f["L0_ffn_w2"]]))
    columns = lambda l: np.concatenate([f["L0_ffn_ln_g"][l], f["L0_ffn_ln_b"][l], padded(f["L0_ffn_b1"][l, :HID]),
                                        padded(f["L0_ffn_b1"][l, HID:])]).reshape(-1, P).T
    a["L0_cols"] = np.stack([columns(l) for l in range(LAYERS)], 1)
    a["L0_b2"] = every(f["L0_ffn_b2"])
    scales = np.stack([f["L0_ffn_q_scale"], f["L0_ffn_k_scale"]], 1)
    a["L0_qk_scale"] = every(np.stack([scales, swap(scales)], 1))
    a["rotary"] = rotary()
    a["shift"] = np.stack([np.eye(P, k=1), np.eye(P, k=1 - P)], 1).astype(np.float32)
    q, k = np.arange(P)[:, None], np.arange(P)[None]
    own, before, none = np.where(k <= q, 0, MASKED), np.where(k >= q, 0, MASKED), np.full((P, P), MASKED)
    a["mask"] = np.stack([np.concatenate(m, 1) for m in ((own, none), (own, before), (before, own))], 1).astype(np.float32)
    a["ctxT2"] = np.stack([a["ctxT"], a["ctxT"]], 3)
    a["causal"] = np.where(np.arange(CTX)[None] <= np.arange(P)[:, None], 0, MASKED).astype(np.float32)
    a["tri"] = np.triu(np.ones((P, P), np.float32))
    a["expert_number"] = every(np.arange(EXPERTS, dtype=np.float32))
    a["L1_router"] = rows(f["L1_ffn_w_router"].T)
    a["L1_gate"] = rows(f["L1_ffn_w_gate"].T)
    a["L1_down"] = f["L1_ffn_w_down"].transpose(2, 0, 1).reshape(MCH, P, EXPERTS, D).transpose(1, 0, 2, 3)
    for n, (q, k, v, o) in (("L2_", [f["L2_xattn_w_" + c] for c in "qkvo"]), ("L3_", [f["L3_xattn_W_" + c] for c in "qkvo"])):
        a[n + "wq"] = q.reshape(XH, XD, D).transpose(1, 0, 2)
        a[n + "wk"], a[n + "wv"], a[n + "wo"] = rows(k.T), rows(v.T), rows(o.T)
    a["L2_bq"] = f["L2_xattn_b_q"].reshape(XH, XD).T
    a["L2_bk"] = f["L2_xattn_b_k"].reshape(XH, XD).T
    a["L2_bv"] = every(f["L2_xattn_b_v"])
    a["L2_bo"] = f["L2_xattn_b_o"][None]
    to_chunks = lambda w: np.pad(w, [(0, QCH * P - QI), (0, 0)]).reshape(QCH, P, D).transpose(1, 0, 2)
    a["L2_gu"] = np.stack([to_chunks(f["L2_ffn_w_gate"]), to_chunks(f["L2_ffn_w_up"])], 1)
    a["L2_d"] = rows(f["L2_ffn_w_down"])
    a["L2_clips"] = every(np.concatenate([f["L2_ffn_clip_x"], f["L2_ffn_clip_down"]]))
    ratio = 2.0 ** (-8.0 / XH)
    slopes = np.asarray([ratio ** i for i in range(1, XH + 1)], np.float32) * np.float32(XD ** 0.5)
    a["slopes"] = np.stack([slopes, slopes])
    kp, qp = f["itok_BxS2_1_8191"], f["itok_BxS_8_8191"].reshape(ALL_TILES, P)
    a["key_pos"] = np.stack([np.full_like(kp, -1), kp])
    a["query_pos"] = np.stack([qp, np.ones_like(qp)])
    a["mask_if1"] = f["mask_BxSxS2_if1"].reshape(ALL_TILES, P, CTX).transpose(1, 0, 2)
    a["L3_gate"] = rows(f["L3_ffn_gate_w"])
    a["L3_w1"] = f["L3_ffn_w1"].reshape(EXPERTS, DCH, P, MOE_HID).transpose(2, 0, 1, 3)
    a["L3_w2"] = f["L3_ffn_w2"].reshape(EXPERTS, MCH, P, D).transpose(2, 0, 1, 3)
    return {k: np.ascontiguousarray(v) for k, v in a.items()}


def kernel(**inputs):
    import concourse.bacc as bacc
    from concourse.bass_utils import run_bass_kernel_spmd as run

    arrays = laid_out(inputs)
    nc = bacc.Bacc("TRN2", target_bir_lowering=False, num_devices=1)
    dram = {k: nc.dram_tensor(f"in_{k}", v.shape, mybir.dt.from_np(v.dtype), kind="ExternalInput").ap()
            for k, v in arrays.items()}
    out = nc.dram_tensor("out_x", (P, ALL_TILES, D), F32, kind="ExternalOutput").ap()
    build(nc, dram, out)
    r = run(nc, [{f"in_{k}": v for k, v in arrays.items()}], core_ids=[0])
    return r.results[0]["out_x"].transpose(1, 0, 2).reshape(BATCH, SEQ, D)
```

```python
from contextlib import ExitStack

import numpy as np

import concourse.bass as bass
from concourse import mybir

ALU = mybir.AluOpType
ACT = mybir.ActivationFunctionType
AX = mybir.AxisListType
F32 = mybir.dt.float32
BF16 = mybir.dt.bfloat16
I32 = mybir.dt.int32
U32 = mybir.dt.uint32

P = 128
BATCH, SEQ, D = 2, 1024, 256
CTX = 64
DCH = D // P
TILES = SEQ // P
ALL_TILES = BATCH * TILES
EPS = 1e-5
MASKED = -1e30
LIFT = 16


class Signal:

    def __init__(self, sem):
        self.sem, self.base, self.per = sem, LIFT, 0

    def each(self, per):
        assert per <= LIFT
        self.per = per

    def at(self, turn, k=1):
        return turn * self.per + (self.base + k)

    def before(self, turn, k=1):
        return turn * self.per + (self.base + k - self.per)

    def close(self, turns=1):
        self.base += self.per * turns


class Chain:

    def __init__(self, sem):
        self.sem = sem

    def begin(self, engine):
        self.engine, self.n = engine, 0
        engine.sem_clear(self.sem)

    def link(self, instruction):
        self.n += 1
        instruction.then_inc(self.sem, 1)
        self.engine.wait_ge(self.sem, self.n)


def memory(e, ctx, stage):
    return lambda name, shape, dt=F32: ctx.enter_context(e.nc.sbuf_tensor(f"{stage}_{name}", shape, dt))


def flat(ap):
    return ap.rearrange("p a b -> p (a b)")


def tile_of(buf, it, b):
    return flat(buf[:, bass.ds(it + b * TILES, 1), :])


class Signals:

    def __init__(self, new):
        self.ln_var = new("ln_var")
        self.ln_rstd = new("ln_rstd")
        self.cT_psum = new("cT_psum")
        self.c_ready = new("c_ready")
        self.cT_ready = new("cT_ready")
        self.prep_psum = new("prep_psum")
        self.c_kept = new("c_kept")
        self.scores_psum = new("scores_psum")
        self.max_ready = new("max_ready")
        self.probs_ready = new("probs_ready")
        self.probsT_psum = new("probsT_psum")
        self.probsT_ready = new("probsT_ready")
        self.mix_psum = new("mix_psum")
        self.mix_ready = new("mix_ready")
        self.mixT_psum = new("mixT_psum")
        self.mixT_ready = new("mixT_ready")
        self.out_psum = new("out_psum")
        self.x_done = new("x_done")
        self.allreduce = new("allreduce")
        self.sums_psum = new("sums_psum")
        self.ys_ready = new("ys_ready")
        self.yT_psum = new("yT_psum")
        self.hT_ready = new("hT_ready")
        self.qkv_psum = new("qkv_psum")
        self.sq_ready = new("sq_ready")
        self.v_ready = new("v_ready")
        self.ss_ready = new("ss_ready")
        self.norm_ready = new("norm_ready")
        self.q_norm_ready = new("q_norm_ready")
        self.rot_ready = new("rot_ready")
        self.qkT_psum = new("qkT_psum")
        self.qT_ready = new("qT_ready")
        self.kT_ready = new("kT_ready")
        self.mixed_psum = new("mixed_psum")
        self.y1_ready = new("y1_ready")
        self.shift_psum = new("shift_psum")
        self.shift_var = new("shift_var")
        self.shift_rstd = new("shift_rstd")
        self.h2_ready = new("h2_ready")
        self.h2T_psum = new("h2T_psum")
        self.h2T_ready = new("h2T_ready")
        self.y1b_ready = new("y1b_ready")
        self.ffn_out = new("ffn_out")
        self.y_done = new("y_done")
        self.bias_ready = new("bias_ready")
        self.pT_act = new("pT_act")
        self.pT_dve = new("pT_dve")
        self.hid_psum = new("hid_psum")
        self.gate_ready = new("gate_ready")
        self.ff_ready = new("ff_ready")
        self.mask_ready = new("mask_ready")
        self.logits_psum = new("logits_psum")
        self.routed = new("routed")
        self.placed = new("placed")
        self.row_copied = new("row_copied")
        self.rowT_psum = new("rowT_psum")
        self.rowT_ready = new("rowT_ready")
        self.up_psum = new("up_psum")
        self.up_ready = new("up_ready")
        self.upT_psum = new("upT_psum")
        self.upT_ready = new("upT_ready")
        self.down_psum = new("down_psum")
        self.y_copied = new("y_copied")
        self.y_stored0 = new("y_stored0")
        self.y_stored1 = new("y_stored1")
        self.y_stored2 = new("y_stored2")
        self.prep_ready = new("prep_ready")
        self.hidden_psum = new("hidden_psum")
        self.gate_done = new("gate_done")
        self.hidden_ready = new("hidden_ready")
        self.bias_added = new("bias_added")
        self.ones_set = new("ones_set")
        self.q_psum = new("q_psum")
        self.q_ready = new("q_ready")



class Env:

    def __init__(self, nc, dram, out):
        self.nc, self.dram, self.out = nc, dram, out


def build(nc, dram, out):
    with ExitStack() as ctx:
        def sem(name):
            return ctx.enter_context(nc.semaphore(name))

        e = Env(nc, dram, out)
        sb = lambda name, shape, dt=F32: ctx.enter_context(nc.sbuf_tensor(name, shape, dt))
        e.psum = ctx.enter_context(nc.psum_tensor("banks", [P, 8, 512], F32))
        e.ps = [e.psum[:, i, :] for i in range(8)]
        e.x = sb("x_res", [P, ALL_TILES, D])
        e.cs = sb("c_tile", [P, BATCH, D])
        e.cT = sb("cT", [P, BATCH, DCH, P])
        e.ident = sb("ident", [P, P])
        e.ident_bf = sb("ident_bf", [P, P], BF16)
        e.ones = sb("ones", [P, P])
        e.neg_half = sb("neg_half", [P, 16])
        e.ctxT = sb("ctxT", [P, DCH, BATCH, CTX])
        e.ctxT2 = sb("ctxT2", [P, DCH, BATCH, 2, CTX])
        e.ctx_tok = sb("ctx_tok", [P, BATCH, D])
        e.bn = sb("bn", [P, BATCH, 6])
        e.mv = sb("mv", [P, BATCH, 2])
        e.zero_eps = sb("zero_eps", [P, 2])
        e.mean_var = sb("mean_var", [P, ALL_TILES, 2])
        e.rstd = sb("rstd", [P, ALL_TILES])
        e.signals = []

        def new(name):
            e.signals.append(Signal(sem(name)))
            return e.signals[-1]

        e.s, e.dma_sem = Signals(new), sem
        e.chain = {n: Chain(sem(f"{n}_order")) for n in ("dve", "act", "pool", "pe")}
        e.loaded = sem("loaded")
        e.stored = sem("stored")
        e.loads = 0

        prologue(e)
        for stage in (l0_xattn, l0_ffn, l1_xattn, l1_ffn, l2_xattn, l2_ffn, l3_xattn, l3_ffn):
            stage(e)
        finish(e)


def begin(per, *signals):
    for n in signals:
        n.each(per)


def end(turns, *signals):
    for n in signals:
        n.close(turns)


def stats_dve(e, v, it, b):
    s, dve, row = e.s, e.chain["dve"], tile_of(e.x, it, b)
    dve.link(v.bn_stats(e.bn[:, b, :], row))
    dve.link(v.bn_aggr(e.mv[:, b, :], e.bn[:, b, :]))
    v.tensor_tensor(flat(e.mean_var[:, bass.ds(it + b * TILES, 1), :]), e.mv[:, b, :], e.zero_eps[:], ALU.add)\
     .then_inc(s.ln_var.sem, 1)


def stats_pool(e, p, it, b):
    s, k = e.s, it + b * TILES
    p.wait_ge(s.ln_var.sem, s.ln_var.at(it, b + 1))
    p.tensor_tensor(e.rstd[:, bass.ds(k, 1)], flat(e.mean_var[:, bass.ds(k, 1), 1:2]), e.neg_half[:, 0:1], ALU.pow)\
     .then_inc(s.ln_rstd.sem, 1)


def normalise(e, v, it, b):
    s, k = e.s, it + b * TILES
    v.wait_ge(s.cT_psum.sem, s.cT_psum.before(it, b + 1))
    v.tensor_scalar(e.cs[:, b, :], tile_of(e.x, it, b), flat(e.mean_var[:, bass.ds(k, 1), 0:1]), e.rstd[:, bass.ds(k, 1)],
                    ALU.subtract, ALU.mult).then_inc(s.c_ready.sem, 1)


def transpose_c(e, pe, it, b, bank):
    s = e.s
    pe.wait_ge(s.c_ready.sem, s.c_ready.at(it, b + 1))
    pe.wait_ge(s.cT_ready.sem, s.cT_ready.before(it, b + 1))
    for ch in range(DCH):
        mm = pe.transpose(e.ps[bank][:, ch * P:(ch + 1) * P], e.cs[:, b, ch * P:(ch + 1) * P], e.ident[:])
    mm.then_inc(s.cT_psum.sem, 1)


def copy_cT(e, act, it, b, bank, used):
    s = e.s
    act.wait_ge(s.cT_psum.sem, s.cT_psum.at(it, b + 1))
    act.wait_ge(used.sem, used.before(it, b + 1))
    e.nc.scalar.copy(flat(e.cT[:, b, :, :]), e.ps[bank][:, 0:D]).then_inc(s.cT_ready.sem, 1)


class Tile:

    def __init__(self, it, b):
        self.it, self.b, self.k = it, b, b + 1


def pipeline(engine, order, turns, width, item, first, step, cuts=None, wait=None, depth=3):
    ahead = -(-(depth - 1) // width)

    def turn(at, left):
        order.begin(engine)
        for n in range(width):
            step(item(at, n), *(item(at + (n + m) // width, (n + m) % width) if (n + m) // width <= left else None
                                for m in range(1, depth)))

    cuts = cuts or [0, turns - ahead]
    for n, (start, stop) in enumerate(zip(cuts[:-1], cuts[1:])):
        if wait:
            wait(n)
        if n == 0:
            with engine.Fori(0, 1) as at:
                order.begin(engine)
                first(*(item(at + m // width, m % width) for m in range(depth - 1)))
        with engine.Fori(start, stop) as at:
            turn(at, ahead)
    for left in reversed(range(ahead)):
        with engine.Fori(turns - 1 - left, turns - left) as at:
            turn(at, left)


def turns_of_tiles(engine, order, first, step):
    pipeline(engine, order, TILES, 1, lambda it, n: it, first, step)


def tiles(engine, order, first, step, depth=3):
    pipeline(engine, order, TILES, BATCH, Tile, first, step, depth=depth)


def prologue(e):
    nc, s, d = e.nc, e.s, e.dram
    for n in (s.ln_var, s.ln_rstd):
        n.each(2)
    with nc.Block() as block:
        @block.sync
        def _(sp):
            for one in e.signals:
                sp.sem_inc(one.sem, LIFT)
    with nc.Block() as block:
        @block.sync
        def _(sp):
            for to, of in ((e.x, "x"), (e.ident, "ident"), (e.ctxT, "ctxT"), (e.ctxT2, "ctxT2"), (e.ctx_tok, "ctx_tok")):
                sp.dma_start(to[:], d[of]).then_inc(e.loaded, 16)
                e.loads += 16

        @block.gpsimd
        def _(p):
            chain = e.chain["pool"]
            chain.begin(p)
            chain.link(p.memset(e.neg_half[:], -0.5))
            p.memset(e.ones[:], 1.0)
            with p.Fori(0, TILES) as it:
                for b in range(BATCH):
                    stats_pool(e, p, it, b)

        @block.vector
        def _(v):
            dve = e.chain["dve"]
            dve.begin(v)
            v.memset(e.zero_eps[:, 0:1], 0.0)
            dve.link(v.memset(e.zero_eps[:, 1:2], EPS))
            v.wait_ge(e.loaded, e.loads)
            v.tensor_copy(e.ident_bf[:], e.ident[:])
            with v.Fori(0, TILES) as it:
                e.chain["dve"].begin(v)
                for b in range(BATCH):
                    stats_dve(e, v, it, b)
    for n in (s.ln_var, s.ln_rstd):
        n.close(TILES)


def l0_xattn(e):
    nc, s, d, ps = e.nc, e.s, e.dram, e.ps
    with ExitStack() as ctx:
        sb = memory(e, ctx, "l0_xattn")
        w_l = sb("w_l", [P, 8, D])
        wcol = sb("wcol", [P, DCH, 3])
        b3 = sb("b3", [P, 3])
        b_l = sb("b_l", [1, D])
        qcat = sb("qcat", [P, DCH, BATCH, CTX])
        b_sum = sb("b_sum", [1, 1])
        q_bias = sb("q_bias", [1, BATCH * CTX])
        c_all = sb("c_all", [P, ALL_TILES, D])
        nmax = sb("nmax", [P, ALL_TILES])
        a = sb("a", [P, 2, CTX])
        a_sum = sb("a_sum", [P, 2])
        a_rec = sb("a_rec", [P, 2])
        aT = sb("aT", [P, P])
        uv = sb("uv", [P, 2, 2, D])
        uvT = sb("uvT", [P, 2, 4, P])
        top = sb("top", [P, BATCH])
        gtop = sb("gtop", [P, BATCH])
        ngtop = sb("ngtop", [P, BATCH])
        b_att = sb("b_att", [P, ALL_TILES])
        b_att_sum = sb("b_att_sum", [P, BATCH])
        rden = sb("rden", [P, BATCH])
        q2c = sb("q2c", [P, BATCH, DCH])
        w_c = sb("w_c", [P, BATCH, DCH, D])
        dve, act, pool = (e.chain[n] for n in ("dve", "act", "pool"))

        with nc.Block() as block:
            @block.sync
            def _(sp):
                for to, of in ((w_l, "L0_W_l"), (wcol, "L0_w3"), (b3, "L0_b3"), (b_l, "L0_b_l")):
                    sp.dma_start(to[:], d[of]).then_inc(e.loaded, 16)
                    e.loads += 16

            s.prep_psum.each(1)

            @block.tensor
            def _(pe):
                pe.wait_ge(e.loaded, e.loads)
                for ch in range(DCH):
                    mm = pe.matmul(ps[0][0:1, 0:BATCH * CTX], wcol[:, ch, 2:3], e.ctxT[:, ch, :, :],
                                   start=ch == 0, stop=ch == DCH - 1)
                mm.then_inc(s.prep_psum.sem, 1)

            @block.vector
            def _(v):
                v.wait_ge(e.loaded, e.loads)
                for ch in range(DCH):
                    v.tensor_scalar(qcat[:, ch, :, :], e.ctxT[:, ch, :, :], wcol[:, ch, 0:1],
                                    wcol[:, ch, 1:2], ALU.mult, ALU.add)
                dve.begin(v)
                dve.link(v.tensor_reduce(b_sum[:], b3[0:1, :], AX.X, ALU.add))
                v.wait_ge(s.prep_psum.sem, s.prep_psum.at(0))
                v.tensor_scalar(q_bias[:], ps[0][0:1, 0:BATCH * CTX], b_sum[0:1, 0:1], None, ALU.add)
        s.prep_psum.close()

        two = (s.c_ready, s.c_kept, s.cT_psum, s.cT_ready, s.scores_psum, s.max_ready, s.probs_ready, s.mix_psum, s.mix_ready,
               s.mixT_psum, s.mixT_ready, s.out_psum, s.x_done)
        one = (s.probsT_psum, s.probsT_ready)
        begin(2, *two)
        begin(1, *one)
        with nc.Block() as block:
            @block.tensor
            def _(pe):
                def transposes(it):
                    for b in range(BATCH):
                        transpose_c(e, pe, it, b, b)

                def scores(it):
                    for b in range(BATCH):
                        pe.wait_ge(s.cT_ready.sem, s.cT_ready.at(it, b + 1))
                        pe.wait_ge(s.probs_ready.sem, s.probs_ready.before(it, b + 1))
                        for ch in range(DCH):
                            pe.matmul(ps[2 + b][:, 0:CTX], e.cT[:, b, ch, :], qcat[:, ch, b, :], start=ch == 0, stop=False)
                        pe.matmul(ps[2 + b][:, 0:CTX], e.ones[0:1, :], q_bias[0:1, b * CTX:(b + 1) * CTX],
                                  start=False, stop=True).then_inc(s.scores_psum.sem, 1)

                def probs_transposed(it):
                    pe.wait_ge(s.probs_ready.sem, s.probs_ready.at(it, 2))
                    pe.wait_ge(s.mixT_ready.sem, s.mixT_ready.before(it, 1))
                    pe.transpose(ps[4][:, 0:P], flat(a[:]), e.ident[:]).then_inc(s.probsT_psum.sem, 1)

                def mix(it):
                    pe.wait_ge(s.probsT_ready.sem, s.probsT_ready.at(it))
                    for b in range(BATCH):
                        own = slice(b * CTX, (b + 1) * CTX)
                        pe.wait_ge(s.x_done.sem, s.x_done.before(it, b + 1))
                        pe.matmul(ps[6 + b][:, 0:D], aT[own, :], e.ctx_tok[own, b, :], start=True, stop=True)\
                          .then_inc(s.mix_psum.sem, 1)

                def mix_transposed(it):
                    for b in range(BATCH):
                        pe.wait_ge(s.mix_ready.sem, s.mix_ready.at(it, b + 1))
                        pe.wait_ge(s.mixT_ready.sem, s.mixT_ready.before(it, b + 1))
                        for k in range(4):
                            mm = pe.transpose(ps[4 + b][:, k * P:(k + 1) * P],
                                              uv[:, b, k // 2, (k % 2) * P:(k % 2 + 1) * P], e.ident[:])
                        mm.then_inc(s.mixT_psum.sem, 1)

                def project(it):
                    for b in range(BATCH):
                        pe.wait_ge(s.mixT_ready.sem, s.mixT_ready.at(it, b + 1))
                        for k in range(4):
                            pe.matmul(ps[6 + b][:, 0:D], uvT[:, b, k, :], w_l[:, 2 + k, :], start=k == 0, stop=False)
                        pe.matmul(ps[6 + b][:, 0:D], e.ones[0:1, :], b_l[0:1, :], start=False, stop=True)\
                          .then_inc(s.out_psum.sem, 1)

                def first(new, after):
                    transposes(new)
                    scores(new)
                    transposes(after)

                def step(now, new, after):
                    probs_transposed(now)
                    if new is not None:
                        scores(new)
                    mix(now)
                    if after is not None:
                        transposes(after)
                    mix_transposed(now)
                    project(now)

                turns_of_tiles(pe, e.chain["pe"], first, step)

            @block.scalar
            def _(act_):
                def copy(it):
                    for b in range(BATCH):
                        copy_cT(e, act_, it, b, b, s.scores_psum)

                def exp(it):
                    for b in range(BATCH):
                        act_.wait_ge(s.max_ready.sem, s.max_ready.at(it, b + 1))
                        act_.wait_ge(s.probsT_psum.sem, s.probsT_psum.before(it))
                        act_.wait_ge(s.mix_ready.sem, s.mix_ready.before(it, b + 1))
                        nc.scalar.activation(a[:, b, :], ps[2 + b][:, 0:CTX], ACT.Exp,
                                             bias=nmax[:, bass.ds(it + b * TILES, 1)],
                                             accum_out=a_sum[:, b:b + 1]).then_inc(s.probs_ready.sem, 1)

                def copy_aT(it):
                    act_.wait_ge(s.probsT_psum.sem, s.probsT_psum.at(it))
                    act_.wait_ge(s.mix_psum.sem, s.mix_psum.before(it, 2))
                    nc.scalar.copy(aT[:], ps[4][:, 0:P]).then_inc(s.probsT_ready.sem, 1)

                def copy_uvT(it):
                    for b in range(BATCH):
                        act_.wait_ge(s.mixT_psum.sem, s.mixT_psum.at(it, b + 1))
                        act_.wait_ge(s.out_psum.sem, s.out_psum.before(it, b + 1))
                        nc.scalar.copy(flat(uvT[:, b, :, :]), ps[4 + b][:, :]).then_inc(s.mixT_ready.sem, 1)

                def first(new, after):
                    copy(new)
                    exp(new)
                    copy(after)

                def step(now, new, after):
                    copy_aT(now)
                    if after is not None:
                        copy(after)
                    copy_uvT(now)
                    if new is not None:
                        exp(new)

                turns_of_tiles(act_, act, first, step)

            @block.vector
            def _(v):
                def normal(it):
                    for b in range(BATCH):
                        v.wait_ge(s.c_kept.sem, s.c_kept.before(it, b + 1))
                        normalise(e, v, it, b)

                def maxima(it):
                    for b in range(BATCH):
                        v.wait_ge(s.scores_psum.sem, s.scores_psum.at(it, b + 1))
                        v.tensor_reduce(nmax[:, bass.ds(it + b * TILES, 1)], ps[2 + b][:, 0:CTX], AX.X, ALU.max,
                                        negate=True).then_inc(s.max_ready.sem, 1)

                def mixed(it):
                    for b in range(BATCH):
                        v.wait_ge(s.probs_ready.sem, s.probs_ready.at(it, b + 1))
                        dve.link(v.reciprocal(a_rec[:, b:b + 1], a_sum[:, b:b + 1]))
                        v.wait_ge(s.mix_psum.sem, s.mix_psum.at(it, b + 1))
                        v.wait_ge(s.mixT_psum.sem, s.mixT_psum.before(it, b + 1))
                        dve.link(v.tensor_scalar(uv[:, b, 0, :], ps[6 + b][:, 0:D], a_rec[:, b:b + 1], None, ALU.mult))
                        v.wait_ge(s.c_kept.sem, s.c_kept.at(it, b + 1))
                        v.tensor_tensor(uv[:, b, 1, :], uv[:, b, 0, :], tile_of(c_all, it, b), ALU.mult)\
                         .then_inc(s.mix_ready.sem, 1)

                def add(it):
                    for b in range(BATCH):
                        v.wait_ge(s.out_psum.sem, s.out_psum.at(it, b + 1))
                        v.tensor_tensor(tile_of(e.x, it, b), ps[6 + b][:, 0:D], tile_of(e.x, it, b), ALU.add)\
                         .then_inc(s.x_done.sem, 1)

                def first(new, after):
                    normal(new)
                    normal(after)
                    maxima(new)

                def step(now, new, after):
                    if new is not None:
                        maxima(new)
                    mixed(now)
                    if after is not None:
                        normal(after)
                    add(now)

                turns_of_tiles(v, dve, first, step)

            @block.gpsimd
            def _(p):
                with p.Fori(0, TILES) as it:
                    for b in range(BATCH):
                        p.wait_ge(s.c_ready.sem, s.c_ready.at(it, b + 1))
                        p.tensor_copy(tile_of(c_all, it, b), e.cs[:, b, :]).then_inc(s.c_kept.sem, 1)
        end(TILES, *two, *one)

        s.max_ready.each(2)
        for n in (s.allreduce, s.probs_ready, s.sums_psum):
            n.each(1)
        with nc.Block() as block:
            @block.vector
            def _(v):
                dve.begin(v)
                v.tensor_reduce(top[:], nmax[:].rearrange("p (b t) -> p b t", b=BATCH), AX.X, ALU.min, negate=True)\
                 .then_inc(s.max_ready.sem, 1)
                v.wait_ge(s.allreduce.sem, s.allreduce.at(0))
                v.tensor_scalar(ngtop[:], gtop[:], -1.0, None, ALU.mult).then_inc(s.max_ready.sem, 1)
                v.wait_ge(s.sums_psum.sem, s.sums_psum.at(0))
                dve.link(v.reciprocal(rden[:], ps[0][:, 0:BATCH]))
                for b in range(BATCH):
                    dve.link(v.tensor_scalar(q2c[:, b, :], ps[1][:, b * DCH:(b + 1) * DCH], rden[:, b:b + 1], None, ALU.mult))
                for b in range(BATCH):
                    for ch in range(DCH):
                        v.scalar_tensor_tensor(w_c[:, b, ch, :], w_l[:, 6 + ch, :], q2c[:, b, ch:ch + 1],
                                               w_l[:, ch, :], ALU.mult, ALU.add)

            @block.gpsimd
            def _(p):
                p.wait_ge(s.max_ready.sem, s.max_ready.at(0, 1))
                p.partition_all_reduce(gtop[:], top[:], P, bass.bass_isa.ReduceOp.max).then_inc(s.allreduce.sem, 1)

            @block.scalar
            def _(act_):
                act_.wait_ge(s.max_ready.sem, s.max_ready.at(0, 2))
                for b in range(BATCH):
                    ex = nc.scalar.activation(b_att[:, b * TILES:(b + 1) * TILES], nmax[:, b * TILES:(b + 1) * TILES], ACT.Exp,
                                              bias=ngtop[:, b:b + 1], scale=-1.0, accum_out=b_att_sum[:, b:b + 1])
                ex.then_inc(s.probs_ready.sem, 1)

            @block.tensor
            def _(pe):
                pe.wait_ge(s.probs_ready.sem, s.probs_ready.at(0))
                pe.matmul(ps[0][:, 0:BATCH], e.ones[:], b_att_sum[:], start=True, stop=True)
                for b in range(BATCH):
                    for ch in range(DCH):
                        for t in range(TILES):
                            k = b * TILES + t
                            mm = pe.matmul(ps[1][:, b * DCH + ch:b * DCH + ch + 1], c_all[:, k, ch * P:(ch + 1) * P],
                                           b_att[:, k:k + 1], start=(b, ch, t) == (0, 0, 0), stop=t == TILES - 1,
                                           skip_group_check=True)
                mm.then_inc(s.sums_psum.sem, 1)
        for n in (s.allreduce, s.probs_ready, s.sums_psum, s.max_ready):
            n.close()

        two = (s.c_ready, s.cT_psum, s.cT_ready, s.out_psum, s.ln_var, s.ln_rstd)
        for n in two:
            n.each(2)
        with nc.Block() as block:
            @block.tensor
            def _(pe):
                with pe.Fori(0, TILES) as it:
                    for b in range(BATCH):
                        transpose_c(e, pe, it, b, b)
                    for b in range(BATCH):
                        pe.wait_ge(s.cT_ready.sem, s.cT_ready.at(it, b + 1))
                        pe.wait_ge(s.ln_var.sem, s.ln_var.before(it, b + 1))
                        for ch in range(DCH):
                            mm = pe.matmul(ps[2 + b][:, 0:D], e.cT[:, b, ch, :], w_c[:, b, ch, :], start=ch == 0, stop=ch == DCH - 1)
                        mm.then_inc(s.out_psum.sem, 1)

            @block.scalar
            def _(act_):
                with act_.Fori(0, TILES) as it:
                    for b in range(BATCH):
                        copy_cT(e, act_, it, b, b, s.out_psum)

            @block.vector
            def _(v):
                with v.Fori(0, TILES) as it:
                    dve.begin(v)
                    for b in range(BATCH):
                        v.wait_ge(s.out_psum.sem, s.out_psum.at(it, b + 1))
                        dve.link(v.tensor_tensor(tile_of(e.x, it, b), ps[2 + b][:, 0:D], tile_of(e.x, it, b), ALU.add))
                        stats_dve(e, v, it, b)

            @block.gpsimd
            def _(p):
                with p.Fori(0, TILES) as it:
                    for b in range(BATCH):
                        p.wait_ge(s.cT_psum.sem, s.cT_psum.before(it, b + 1))
                        p.tensor_copy(e.cs[:, b, :], tile_of(c_all, it, b)).then_inc(s.c_ready.sem, 1)
                    for b in range(BATCH):
                        stats_pool(e, p, it, b)
        for n in two:
            n.close(TILES)


HEADS, DH = 8, 64
INNER = HEADS * DH
HID = int(D * 4 * 2 / 3)
FCH = -(-HID // P)
FPAIRS = FCH // 2
FW = [min(P, HID - j * P) for j in range(FCH)]
LAYERS = 2
HALF = TILES // 2


def l0_ffn(e):
    nc, s, d, ps = e.nc, e.s, e.dram, e.psum
    dve, act, pool = (e.chain[n] for n in ("dve", "act", "pool"))
    with ExitStack() as ctx:
        sb = memory(e, ctx, "l0_ffn")
        y = sb("y", [P, ALL_TILES, D])
        wqkv = sb("wqkv", [P, LAYERS, DCH, 3 * INNER])
        wo = sb("wo", [P, LAYERS, INNER // P, D])
        w1 = sb("w1", [P, DCH, 2 * HID])
        w2 = sb("w2", [P, LAYERS, FCH, D])
        all_cols = sb("ffn_cols", [P, LAYERS, 2 * DCH + 2 * FCH])
        cols = sb("layer_cols", [P, 2 * DCH + 2 * FCH])
        all_b2 = sb("b2", [P, LAYERS, D])
        b2 = sb("layer_b2", [P, D])
        qk_scale = sb("qk_scale", [P, LAYERS, 2, 2, DH])
        rot = sb("rot", [P, 2, TILES, 2, DH])
        shift = sb("shift", [P, 2, P])
        mask32 = sb("mask32", [P, 3, 2 * P])
        mask_even = sb("mask_even", [P, HALF, 2 * P], BF16)
        mask_odd = sb("mask_odd", [P, 2 * P], BF16)
        zero = sb("zero", [P, 1])
        unused = sb("unused", [P, 1])
        ys = sb("ys", [P, BATCH, D])
        hT = sb("hT", [P, BATCH, 2, DCH, P + 1])
        work = sb("work", [P, BATCH, HEADS, 2 * P])
        pT = sb("pT", [P, BATCH, 2 * HEADS, P])
        ss = sb("ss", [P, BATCH, 2 * HEADS])
        rn = sb("rn", [P, BATCH, 2 * HEADS])
        qT = sb("qT", [P, BATCH, 4, P])
        kT = sb("kT", [P, BATCH, 4, 2, 2, P])
        vv = sb("vv", [P, BATCH, 2, INNER])
        top = sb("att_top", [P, BATCH, HEADS])
        scale = sb("att_scale", [P, BATCH, HEADS])
        bias = sb("att_bias", [P, BATCH, HEADS])
        den = sb("att_den", [P, BATCH, HEADS])
        rden = sb("att_rden", [P, BATCH, HEADS])
        o = sb("o", [P, BATCH, INNER])
        oT = sb("oT", [P, BATCH, 4, P])
        y1 = sb("y1", [P, BATCH, 2, D])
        y1b = sb("y1b", [P, BATCH, D])
        bn2 = sb("bn2", [P, BATCH, 2, 6])
        mv2 = sb("mv2", [P, BATCH, 2])
        ve2 = sb("ve2", [P, BATCH])
        rstd2 = sb("rstd2", [P, BATCH])
        h2 = sb("h2", [P, BATCH, D])
        h2T = sb("h2T", [P, DCH, BATCH, P])
        gate = sb("gate", [P, FCH, P])
        ff = sb("ff", [P, FCH, P])

        with nc.Block() as block:
            @block.sync
            def _(sp):
                for to, of in ((all_cols, "L0_cols"), (all_b2, "L0_b2"), (qk_scale, "L0_qk_scale"), (shift, "shift"),
                               (mask32, "mask"), (wqkv, "L0_wqkv"), (wo, "L0_wo"), (w2, "L0_w2")):
                    sp.dma_start(to[:], d[of]).then_inc(e.loaded, 16)
                    e.loads += 16

            @block.gpsimd
            def _(p):
                p.memset(zero[:], 0.0)
                p.memset(kT[:], 0.0)
                p.memset(vv[:], 0.0)

            @block.vector
            def _(v):
                with v.Fori(0, TILES) as it:
                    for b in range(BATCH):
                        k = it + b * TILES
                        v.tensor_scalar(tile_of(y, it, b), tile_of(e.x, it, b), flat(e.mean_var[:, bass.ds(k, 1), 0:1]),
                                        e.rstd[:, bass.ds(k, 1)], ALU.subtract, ALU.mult)
                v.wait_ge(e.loaded, e.loads)
                v.tensor_copy(mask_odd[:], mask32[:, 2, :])
                for i in range(HALF):
                    v.tensor_copy(mask_even[:, i, :], mask32[:, min(i, 1), :])

        turns = LAYERS * HALF
        four = (s.ys_ready, s.yT_psum, s.hT_ready, s.qkv_psum, s.sq_ready, s.v_ready, s.ss_ready, s.norm_ready, s.q_norm_ready,
                s.rot_ready, s.qkT_psum, s.qT_ready, s.kT_ready, s.mixed_psum, s.mix_ready, s.mixT_psum,
                s.mixT_ready, s.out_psum, s.y1_ready, s.shift_psum, s.shift_var, s.shift_rstd, s.h2_ready, s.h2T_psum,
                s.h2T_ready, s.y1b_ready, s.ffn_out, s.y_done)
        begin(4, *four)
        begin(16, s.scores_psum, s.probs_ready, s.probsT_psum)
        begin(8, s.bias_ready, s.pT_act, s.pT_dve)
        begin(4 * FPAIRS, s.hid_psum, s.gate_ready, s.ff_ready)
        w1_loaded, rot_loaded = e.dma_sem("w1_loaded"), e.dma_sem("rot_loaded")

        class Item:

            def __init__(self, layer, i, q):
                self.layer, self.i, self.turn = layer, i, layer * HALF + i
                self.odd, self.b, self.k = q // 2, q % 2, q + 1
                self.t = i * 2 + self.odd
                self.bank = 4 * self.b

        def layers(engine, order, start, first, step):
            with engine.Fori(0, LAYERS) as layer:
                order.begin(engine)
                start(layer)
                with engine.Fori(0, 1) as i:
                    first(Item(layer, i, 0), Item(layer, i, 1))

                def turn(i, last):
                    order.begin(engine)
                    for q in range(4):
                        new, after = (None if last and q + n > 3 else Item(layer, i + (q + n) // 4, (q + n) % 4) for n in (1, 2))
                        step(Item(layer, i, q), new, after)

                with engine.Fori(0, HALF - 1) as i:
                    turn(i, False)
                with engine.Fori(HALF - 1, HALF) as i:
                    turn(i, True)

        with nc.Block() as block:
            @block.sync
            def _(sp):
                with sp.Fori(0, LAYERS) as layer:
                    first = layer * HALF
                    sp.wait_ge(s.rot_ready.sem, s.rot_ready.at(first, 0))
                    sp.dma_start(rot[:], d["rotary"]).then_inc(rot_loaded, 16)
                    sp.wait_ge(s.hid_psum.sem, s.hid_psum.at(first, 0))
                    sp.dma_start(w1[:], d["L0_w1"][bass.ds(layer, 1)].rearrange("l p c n -> (l p) c n"))\
                      .then_inc(w1_loaded, 16)

            @block.gpsimd
            def _(p):
                def norms(m):
                    p.wait_ge(s.ss_ready.sem, s.ss_ready.at(m.turn, m.k))
                    p.wait_ge(s.rot_ready.sem, s.rot_ready.at(m.turn, m.k - 2))
                    p.tensor_tensor(rn[:, m.b, HEADS:], ss[:, m.b, HEADS:], e.neg_half[:, 0:HEADS], ALU.pow).then_inc(s.norm_ready.sem, 1)
                    p.wait_ge(s.bias_ready.sem, s.bias_ready.at(m.turn, 2 * (m.k - 2)))
                    p.tensor_tensor(rn[:, m.b, 0:HEADS], ss[:, m.b, 0:HEADS], e.neg_half[:, 0:HEADS], ALU.pow)\
                     .then_inc(s.q_norm_ready.sem, 1)

                def first(new, after):
                    norms(new)

                def step(now, new, after):
                    p.wait_ge(s.shift_var.sem, s.shift_var.at(now.turn, now.k))
                    p.tensor_tensor(rstd2[:, now.b:now.b + 1], ve2[:, now.b:now.b + 1], e.neg_half[:, 0:1], ALU.pow)\
                     .then_inc(s.shift_rstd.sem, 1)
                    if new:
                        norms(new)
                    p.wait_ge(s.y_done.sem, s.y_done.at(now.turn, now.k - 2))
                    p.tensor_tensor(y1b[:, now.b, :], y1[:, now.b, now.odd, :], b2[:], ALU.add).then_inc(s.y1b_ready.sem, 1)

                layers(p, pool, lambda layer: None, first, step)

            @block.tensor
            def _(pe):
                pe.wait_ge(e.loaded, e.loads)

                def y_transposed(m):
                    pe.wait_ge(s.ff_ready.sem, s.ff_ready.at(m.turn, FPAIRS * (m.k - 3) + 1))
                    pe.wait_ge(s.ys_ready.sem, s.ys_ready.at(m.turn, m.k))
                    for ch in range(DCH):
                        mm = pe.transpose(ps[:, m.bank, ch * P:(ch + 1) * P], ys[:, m.b, ch * P:(ch + 1) * P], e.ident[:])
                    mm.then_inc(s.yT_psum.sem, 1)

                def qkv(m, n, chunks=range(DCH)):
                    if n == 0:
                        pe.wait_ge(s.hT_ready.sem, s.hT_ready.at(m.turn, m.k))
                    if n == 2:
                        pe.wait_ge(s.y_done.sem, s.y_done.at(m.turn, m.k - 2))
                    for ch in chunks:
                        mm = pe.matmul(ps[:, m.bank + 1 + n, :], hT[:, m.b, m.odd, ch, 1 - ch:P + 1 - ch],
                                       wqkv[:, bass.ds(m.layer, 1), ch, n * INNER:(n + 1) * INNER].rearrange("p l n -> p (l n)"),
                                       start=ch == 0, stop=ch == DCH - 1)
                    if n == 2:
                        mm.then_inc(s.qkv_psum.sem, 1)

                def qk_transposed(m):
                    pe.wait_ge(s.rot_ready.sem, s.rot_ready.at(m.turn, m.k))
                    for n in range(2):
                        for j in range(4):
                            mm = pe.transpose(ps[:, m.bank + n, j * P:(j + 1) * P],
                                              work[:, m.b, 2 * n + j // 2, (j % 2) * P:(j % 2 + 1) * P], e.ident[:])
                    mm.then_inc(s.qkT_psum.sem, 1)

                def scores(m):
                    pe.wait_ge(s.v_ready.sem, s.v_ready.at(m.turn, m.k))
                    pe.wait_ge(s.qT_ready.sem, s.qT_ready.at(m.turn, m.k))
                    pe.wait_ge(s.kT_ready.sem, s.kT_ready.at(m.turn, m.k))
                    for j in range(4):
                        bank = ps[:, m.bank + j, :]
                        mask = (mask_odd[:].unsqueeze(1) if m.odd else mask_even[:, bass.ds(m.i, 1), :]).broadcast_to((P, 2, 2 * P))
                        pe.matmul(bank, e.ident_bf[:], mask, start=True, stop=False)
                        pe.matmul(bank, qT[:, m.b, j, :], kT[:, m.b, j, :, :, :].rearrange("p h w n -> p (h w n)"),
                                  start=False, stop=True).then_inc(s.scores_psum.sem, 1)

                def probs_transposed(m):
                    for j in range(4):
                        pe.wait_ge(s.probs_ready.sem, s.probs_ready.at(m.turn, 4 * (m.k - 1) + j + 1))
                        for n in range(4):
                            mm = pe.transpose(ps[:, m.bank + j, n * P:(n + 1) * P],
                                              work[:, m.b, 2 * j + n // 2, (n % 2) * P:(n % 2 + 1) * P], e.ident[:])
                        mm.then_inc(s.probsT_psum.sem, 1)

                def mixed(m):
                    pe.wait_ge(s.pT_act.sem, s.pT_act.at(m.turn, 2 * m.k))
                    pe.wait_ge(s.pT_dve.sem, s.pT_dve.at(m.turn, 2 * m.k))
                    for h in range(HEADS):
                        for c in range(2):
                            mm = pe.matmul(ps[:, m.bank, h * DH:(h + 1) * DH], pT[:, m.b, 2 * h + c, :],
                                           vv[:, m.b, c, h * DH:(h + 1) * DH], start=(h, c) == (0, 0), stop=c == 1,
                                           skip_group_check=True)
                    mm.then_inc(s.mixed_psum.sem, 1)

                def mix_transposed(m):
                    pe.wait_ge(s.mix_ready.sem, s.mix_ready.at(m.turn, m.k))
                    for j in range(4):
                        mm = pe.transpose(ps[:, m.bank + 1, j * P:(j + 1) * P], o[:, m.b, j * P:(j + 1) * P], e.ident[:])
                    mm.then_inc(s.mixT_psum.sem, 1)

                def attention_out(m):
                    pe.wait_ge(s.mixT_ready.sem, s.mixT_ready.at(m.turn, m.k))
                    for j in range(4):
                        mm = pe.matmul(ps[:, m.bank + 2, 0:D], oT[:, m.b, j, :],
                                       wo[:, bass.ds(m.layer, 1), j, :].rearrange("p l n -> p (l n)"), start=j == 0, stop=j == 3)
                    mm.then_inc(s.out_psum.sem, 1)

                def shifted(m):
                    pe.wait_ge(s.y1_ready.sem, s.y1_ready.at(m.turn, m.k))
                    pe.matmul(ps[:, m.bank + 3, 0:P], shift[:, 0, :], y1[:, m.b, m.odd, P:D], start=True, stop=False)
                    pe.matmul(ps[:, m.bank + 3, 0:P], shift[:, 1, :], y1[:, m.b, 1 - m.odd, P:D], start=False, stop=True)\
                      .then_inc(s.shift_psum.sem, 1)

                def h2_transposed(m):
                    pe.wait_ge(s.h2_ready.sem, s.h2_ready.at(m.turn, m.k))
                    for ch in range(DCH):
                        mm = pe.transpose(ps[:, m.bank, ch * P:(ch + 1) * P], h2[:, m.b, ch * P:(ch + 1) * P], e.ident[:])
                    mm.then_inc(s.h2T_psum.sem, 1)

                def ffn_up(m):
                    pe.wait_ge(w1_loaded, m.layer * 16 + 16)
                    pe.wait_ge(s.h2T_ready.sem, s.h2T_ready.at(m.turn, m.k))
                    for j in range(FCH):
                        for n in range(2):
                            at, to = n * HID + j * P, (2 * (j % 2) + n) * P
                            for ch in range(DCH):
                                mm = pe.matmul(ps[0:FW[j], m.bank + j // 2, to:to + P], w1[:, ch, at:at + FW[j]],
                                               h2T[:, ch, m.b, :], start=(j % 2, n, ch) == (0, 0, 0), stop=ch == DCH - 1,
                                               skip_group_check=True)
                        if j % 2:
                            mm.then_inc(s.hid_psum.sem, 1)

                def ffn_down(m, pair):
                    pe.wait_ge(s.ff_ready.sem, s.ff_ready.at(m.turn, FPAIRS * (m.k - 1) + pair + 1))
                    for j in (2 * pair, 2 * pair + 1):
                        mm = pe.matmul(ps[:, m.bank + 3, 0:D], ff[0:FW[j], j, :],
                                       w2[0:FW[j], bass.ds(m.layer, 1), j, :].rearrange("p l n -> p (l n)"),
                                       start=j == 0, stop=j == FCH - 1, skip_group_check=True)
                    if pair == FPAIRS - 1:
                        mm.then_inc(s.ffn_out.sem, 1)

                def first(new, after):
                    y_transposed(new)
                    for n in range(3):
                        qkv(new, n)
                    qk_transposed(new)
                    y_transposed(after)
                    scores(new)
                    qkv(after, 0)

                def step(now, new, after):
                    probs_transposed(now)
                    if new:
                        qkv(new, 1, (0,))
                    mixed(now)
                    if new:
                        qkv(new, 1, (1,))
                    mix_transposed(now)
                    attention_out(now)
                    shifted(now)
                    if new:
                        qkv(new, 2)
                    h2_transposed(now)
                    ffn_up(now)
                    if new:
                        qk_transposed(new)
                    if after:
                        y_transposed(after)
                    ffn_down(now, 0)
                    ffn_down(now, 1)
                    if new:
                        scores(new)
                    ffn_down(now, 2)
                    if after:
                        qkv(after, 0)

                layers(pe, e.chain["pe"], lambda layer: None, first, step)

            @block.scalar
            def _(a):
                def start(layer):
                    at = layer * HALF
                    a.wait_ge(s.hT_ready.sem, s.hT_ready.at(at, 0))
                    a.wait_ge(s.qkv_psum.sem, s.qkv_psum.at(at, 0))
                    for b in range(BATCH):
                        z = nc.scalar.copy(hT[:, b, 0, 1, 0:1], zero[:])
                    act.link(z)
                    a.wait_ge(s.ff_ready.sem, s.ff_ready.at(at, 0))
                    act.link(nc.scalar.copy(cols[:], flat(all_cols[:, bass.ds(layer, 1), :])))
                    a.wait_ge(s.y1b_ready.sem, s.y1b_ready.at(at, 0))
                    act.link(nc.scalar.copy(b2[:], flat(all_b2[:, bass.ds(layer, 1), :])))

                def copy_hT(m):
                    a.wait_ge(s.yT_psum.sem, s.yT_psum.at(m.turn, m.k))
                    a.wait_ge(s.qkv_psum.sem, s.qkv_psum.at(m.turn, m.k - 2))
                    nc.scalar.copy(hT[:, m.b, m.odd, :, 1:P + 1], ps[:, m.bank, 0:D].rearrange("p (c n) -> p c n", c=DCH))
                    nc.scalar.copy(hT[:, m.b, 1 - m.odd, 1, 0:1], ps[:, m.bank, D - 1:D]).then_inc(s.hT_ready.sem, 1)

                def squares(m):
                    a.wait_ge(s.qkv_psum.sem, s.qkv_psum.at(m.turn, m.k))
                    a.wait_ge(s.mixed_psum.sem, s.mixed_psum.at(m.turn, m.k - 2))
                    nc.scalar.activation(flat(pT[:, m.b, 0:HEADS, :]), flat(ps[:, m.bank + 1:m.bank + 3, :]), ACT.Square)\
                      .then_inc(s.sq_ready.sem, 1)
                    nc.scalar.copy(vv[:, m.b, m.odd, :], ps[:, m.bank + 3, :]).then_inc(s.v_ready.sem, 1)

                def copy_qT(m):
                    a.wait_ge(s.qkT_psum.sem, s.qkT_psum.at(m.turn, m.k))
                    a.wait_ge(s.scores_psum.sem, s.scores_psum.at(m.turn, 4 * (m.k - 2)))
                    nc.scalar.copy(flat(qT[:, m.b, :, :]), ps[:, m.bank, :]).then_inc(s.qT_ready.sem, 1)

                def probs(m):
                    for slot in range(HEADS):
                        if slot % 4 == 0:
                            a.wait_ge(s.bias_ready.sem, s.bias_ready.at(m.turn, 2 * (m.k - 1) + slot // 4 + 1))
                        ex = nc.scalar.activation(work[:, m.b, slot, :], ps[:, m.bank + slot // 2, (slot % 2) * 2 * P:(slot % 2 + 1) * 2 * P],
                                                  ACT.Exp, bias=bias[:, m.b, slot:slot + 1], scale=scale[:, m.b, slot:slot + 1],
                                                  accum_out=den[:, m.b, slot:slot + 1])
                        if slot % 2:
                            ex.then_inc(s.probs_ready.sem, 1)

                def copy_pT(m):
                    for j in range(2):
                        a.wait_ge(s.probsT_psum.sem, s.probsT_psum.at(m.turn, 4 * (m.k - 1) + j + 1))
                        nc.scalar.copy(flat(pT[:, m.b, 4 * j:4 * j + 4, :]), ps[:, m.bank + j, :]).then_inc(s.pT_act.sem, 1)

                def copy_oT(m):
                    a.wait_ge(s.mixT_psum.sem, s.mixT_psum.at(m.turn, m.k))
                    a.wait_ge(s.out_psum.sem, s.out_psum.at(m.turn, m.k - 2))
                    nc.scalar.copy(flat(oT[:, m.b, :, :]), ps[:, m.bank + 1, :]).then_inc(s.mixT_ready.sem, 1)

                def affine_h2T(m):
                    a.wait_ge(s.h2T_psum.sem, s.h2T_psum.at(m.turn, m.k))
                    a.wait_ge(s.hid_psum.sem, s.hid_psum.at(m.turn, FPAIRS * (m.k - 2)))
                    for ch in range(DCH):
                        cp = nc.scalar.activation(h2T[:, ch, m.b, :], ps[:, m.bank, ch * P:(ch + 1) * P], ACT.Identity,
                                                  scale=cols[:, ch:ch + 1], bias=cols[:, DCH + ch:DCH + ch + 1])
                    cp.then_inc(s.h2T_ready.sem, 1)

                def gates(m):
                    for j in range(FCH):
                        if j % 2 == 0:
                            a.wait_ge(s.hid_psum.sem, s.hid_psum.at(m.turn, FPAIRS * (m.k - 1) + j // 2 + 1))
                            a.wait_ge(s.ff_ready.sem, s.ff_ready.at(m.turn, FPAIRS * (m.k - 2) + j // 2 + 1))
                        col, of = 2 * DCH + FCH + j, (2 * (j % 2) + 1) * P
                        g = nc.scalar.activation(gate[0:FW[j], j, :], ps[0:FW[j], m.bank + j // 2, of:of + P],
                                                 ACT.Gelu, bias=cols[0:FW[j], col:col + 1])
                        if j % 2:
                            g.then_inc(s.gate_ready.sem, 1)

                def load_table(func):
                    act.link(nc.scalar.activation(unused[:], zero[:], func))

                def first(new, after):
                    copy_hT(new)
                    squares(new)
                    copy_qT(new)
                    copy_hT(after)
                    probs(new)

                def step(now, new, after):
                    copy_pT(now)
                    copy_oT(now)
                    load_table(ACT.Gelu)
                    affine_h2T(now)
                    if new:
                        squares(new)
                    gates(now)
                    if new:
                        copy_qT(new)
                    if after:
                        copy_hT(after)
                    if new:
                        load_table(ACT.Exp)
                        probs(new)

                layers(a, act, start, first, step)

            @block.vector
            def _(v):
                def start(layer):
                    v.wait_ge(rot_loaded, layer * 16 + 16)
                    for part in range(2):
                        for n in range(2):
                            last = v.tensor_tensor(rot[:, part, :, n, :], rot[:, part, :, n, :],
                                                   qk_scale[:, bass.ds(layer, 1), part, n, :].broadcast_to((P, TILES, DH)), ALU.mult)
                    dve.link(last)
                    v.wait_ge(s.shift_psum.sem, s.shift_psum.at(layer * HALF, 0))
                    v.wait_ge(s.y1b_ready.sem, s.y1b_ready.at(layer * HALF, 0))
                    for b in range(BATCH):
                        z = v.memset(y1[:, b, 1, :], 0.0)
                    dve.link(z)

                def take_y(m):
                    v.wait_ge(s.y_done.sem, s.y_done.at(m.turn, m.k - 16))
                    v.wait_ge(s.y1_ready.sem, s.y1_ready.at(m.turn, m.k - 2))
                    v.tensor_copy(ys[:, m.b, :], tile_of(y, m.t, m.b)).then_inc(s.ys_ready.sem, 1)

                def rotary_parts(m):
                    qk = ps[:, m.bank + 1:m.bank + 3, :].rearrange("p n (h x) -> p n h x", x=DH)
                    w = [work[:, m.b, 4 * n:4 * n + 4, :].rearrange("p a f -> p (a f)").rearrange("p (n h x) -> p n h x", n=2, x=DH)
                         for n in range(2)]
                    table = [rot[:, part, bass.ds(m.t, 1), :, :].rearrange("p t n x -> p (t n) x").unsqueeze(2)
                             .broadcast_to((P, 2, HEADS, DH)) for part in range(2)]
                    return qk, w, table

                def norms(m):
                    v.wait_ge(s.sq_ready.sem, s.sq_ready.at(m.turn, m.k))
                    v.wait_ge(s.q_norm_ready.sem, s.q_norm_ready.at(m.turn, m.k - 2))
                    dve.link(v.tensor_reduce(ss[:, m.b, :], flat(pT[:, m.b, 0:HEADS, :]).rearrange("p (h x) -> p h x", x=DH), AX.X, ALU.add))
                    v.tensor_scalar(ss[:, m.b, :], ss[:, m.b, :], 1e-24, None, ALU.max).then_inc(s.ss_ready.sem, 1)

                def rotate_cos(m):
                    qk, w, table = rotary_parts(m)
                    v.wait_ge(s.probsT_psum.sem, s.probsT_psum.at(m.turn, 4 * (m.k - 2)))
                    v.tensor_tensor(w[0], qk, table[0], ALU.mult)

                def rotate_sin(m):
                    qk, w, table = rotary_parts(m)
                    hx = DH // 2
                    v.tensor_tensor(w[1][:, :, :, 0:hx], qk[:, :, :, hx:DH], table[1][:, :, :, 0:hx], ALU.mult)
                    dve.link(v.tensor_tensor(w[1][:, :, :, hx:DH], qk[:, :, :, 0:hx], table[1][:, :, :, hx:DH], ALU.mult))

                def rotate_sum(m):
                    _, w, _ = rotary_parts(m)
                    dve.link(v.tensor_tensor(w[0], w[0], w[1], ALU.add))

                def scale_k(m):
                    kr = work[:, m.b, 2:4, :].rearrange("p a f -> p (a f)").rearrange("p (h x) -> p h x", x=DH)
                    v.wait_ge(s.norm_ready.sem, s.norm_ready.at(m.turn, m.k))
                    v.tensor_tensor(kr, kr, rn[:, m.b, HEADS:].unsqueeze(2).broadcast_to((P, HEADS, DH)), ALU.mult)\
                     .then_inc(s.rot_ready.sem, 1)

                def copy_kT(m):
                    v.wait_ge(s.qkT_psum.sem, s.qkT_psum.at(m.turn, m.k))
                    v.wait_ge(s.scores_psum.sem, s.scores_psum.at(m.turn, 4 * (m.k - 2)))
                    for n in range(2):
                        own = slice(n * DH, (n + 1) * DH)
                        cp = v.tensor_copy(kT[own, m.b, :, n, m.odd, :], ps[own, m.bank + 1, :].rearrange("p (j n) -> p j n", j=4))
                    cp.then_inc(s.kT_ready.sem, 1)

                def maxima(m):
                    v.wait_ge(s.q_norm_ready.sem, s.q_norm_ready.at(m.turn, m.k))
                    v.wait_ge(s.probs_ready.sem, s.probs_ready.at(m.turn, 4 * (m.k - 2)))
                    v.tensor_scalar(scale[:, m.b, :], rn[:, m.b, 0:HEADS], float(DH) ** 0.5, None, ALU.mult)
                    for j in range(4):
                        v.wait_ge(s.scores_psum.sem, s.scores_psum.at(m.turn, 4 * (m.k - 1) + j + 1))
                        last = v.tensor_reduce(top[:, m.b, 2 * j:2 * j + 2], ps[:, m.bank + j, :].rearrange("p (n x) -> p n x", n=2),
                                               AX.X, ALU.max)
                        if j % 2:
                            dve.link(last)
                            four_heads = slice(2 * j - 2, 2 * j + 2)
                            v.scalar_tensor_tensor(bias[:, m.b, four_heads], top[:, m.b, four_heads], -1.0, scale[:, m.b, four_heads],
                                                   ALU.mult, ALU.mult).then_inc(s.bias_ready.sem, 1)

                def copy_pT(m):
                    for j in range(2, 4):
                        v.wait_ge(s.probsT_psum.sem, s.probsT_psum.at(m.turn, 4 * (m.k - 1) + j + 1))
                        v.tensor_copy(flat(pT[:, m.b, 4 * j:4 * j + 4, :]), ps[:, m.bank + j, :]).then_inc(s.pT_dve.sem, 1)

                def mix(m):
                    v.wait_ge(s.probs_ready.sem, s.probs_ready.at(m.turn, 4 * m.k))
                    dve.link(v.reciprocal(rden[:, m.b, :], den[:, m.b, :]))
                    v.wait_ge(s.mixed_psum.sem, s.mixed_psum.at(m.turn, m.k))
                    v.wait_ge(s.mixT_psum.sem, s.mixT_psum.at(m.turn, m.k - 2))
                    v.tensor_tensor(o[:, m.b, :].rearrange("p (h x) -> p h x", x=DH), ps[:, m.bank, :].rearrange("p (h x) -> p h x", x=DH),
                                    rden[:, m.b, :].unsqueeze(2).broadcast_to((P, HEADS, DH)), ALU.mult).then_inc(s.mix_ready.sem, 1)

                def add_attention(m):
                    v.wait_ge(s.out_psum.sem, s.out_psum.at(m.turn, m.k))
                    v.wait_ge(s.shift_psum.sem, s.shift_psum.at(m.turn, m.k - 2))
                    v.wait_ge(s.y1b_ready.sem, s.y1b_ready.at(m.turn, m.k - 2))
                    v.tensor_tensor(y1[:, m.b, m.odd, :], ps[:, m.bank + 2, 0:D], ys[:, m.b, :], ALU.add).then_inc(s.y1_ready.sem, 1)

                def shifted_stats(m):
                    v.wait_ge(s.y1_ready.sem, s.y1_ready.at(m.turn, m.k))
                    v.bn_stats(bn2[:, m.b, 0, :], y1[:, m.b, m.odd, 0:P])
                    v.wait_ge(s.shift_psum.sem, s.shift_psum.at(m.turn, m.k))
                    dve.link(v.bn_stats(bn2[:, m.b, 1, :], ps[:, m.bank + 3, 0:P]))
                    dve.link(v.bn_aggr(mv2[:, m.b, :], flat(bn2[:, m.b, :, :])))
                    v.tensor_scalar(ve2[:, m.b:m.b + 1], mv2[:, m.b, 1:2], EPS, None, ALU.add).then_inc(s.shift_var.sem, 1)

                def normalise_h2(m):
                    v.wait_ge(s.shift_rstd.sem, s.shift_rstd.at(m.turn, m.k))
                    v.wait_ge(s.h2T_psum.sem, s.h2T_psum.at(m.turn, m.k - 2))
                    v.tensor_scalar(h2[:, m.b, 0:P], y1[:, m.b, m.odd, 0:P], mv2[:, m.b, 0:1], rstd2[:, m.b:m.b + 1], ALU.subtract, ALU.mult)
                    v.tensor_scalar(h2[:, m.b, P:D], ps[:, m.bank + 3, 0:P], mv2[:, m.b, 0:1], rstd2[:, m.b:m.b + 1], ALU.subtract, ALU.mult)\
                     .then_inc(s.h2_ready.sem, 1)

                def gated(m, pair):
                    v.wait_ge(s.gate_ready.sem, s.gate_ready.at(m.turn, FPAIRS * (m.k - 1) + pair + 1))
                    if pair == 0:
                        v.wait_ge(s.ffn_out.sem, s.ffn_out.at(m.turn, m.k - 1))
                    for j in (2 * pair, 2 * pair + 1):
                        col, of = 2 * DCH + j, 2 * (j % 2) * P
                        ins = v.scalar_tensor_tensor(ff[0:FW[j], j, :], ps[0:FW[j], m.bank + pair, of:of + P], cols[0:FW[j], col:col + 1],
                                                     gate[0:FW[j], j, :], ALU.add, ALU.mult)
                    ins.then_inc(s.ff_ready.sem, 1)

                def add_ffn(m):
                    v.wait_ge(s.ffn_out.sem, s.ffn_out.at(m.turn, m.k))
                    v.wait_ge(s.y1b_ready.sem, s.y1b_ready.at(m.turn, m.k))
                    v.tensor_tensor(tile_of(y, m.t, m.b), ps[:, m.bank + 3, 0:D], y1b[:, m.b, :], ALU.add).then_inc(s.y_done.sem, 1)

                def first(new, after):
                    take_y(new)
                    take_y(after)
                    norms(new)
                    rotate_cos(new)
                    rotate_sin(new)
                    rotate_sum(new)
                    scale_k(new)
                    copy_kT(new)
                    maxima(new)

                def step(now, new, after):
                    copy_pT(now)
                    mix(now)
                    add_attention(now)
                    shifted_stats(now)
                    normalise_h2(now)
                    if new:
                        norms(new)
                        rotate_cos(new)
                        rotate_sin(new)
                        rotate_sum(new)
                    gated(now, 0)
                    if new:
                        scale_k(new)
                    gated(now, 1)
                    if after:
                        take_y(after)
                    gated(now, 2)
                    if new:
                        copy_kT(new)
                        maxima(new)
                    add_ffn(now)

                layers(v, dve, start, first, step)
        end(turns, *four, s.scores_psum, s.probs_ready, s.probsT_psum, s.bias_ready, s.pT_act, s.pT_dve, s.hid_psum, s.gate_ready, s.ff_ready)

        for n in (s.ln_var, s.ln_rstd):
            n.each(2)
        with nc.Block() as block:
            @block.vector
            def _(v):
                with v.Fori(0, TILES) as it:
                    dve.begin(v)
                    for b in range(BATCH):
                        dve.link(v.tensor_tensor(tile_of(e.x, it, b), tile_of(e.x, it, b), tile_of(y, it, b), ALU.add))
                        stats_dve(e, v, it, b)

            @block.gpsimd
            def _(p):
                with p.Fori(0, TILES) as it:
                    for b in range(BATCH):
                        stats_pool(e, p, it, b)
        for n in (s.ln_var, s.ln_rstd):
            n.close(TILES)


def load(e, sp, *pairs):
    for to, of in pairs:
        sp.dma_start(to[:], e.dram[of]).then_inc(e.loaded, 16)
        e.loads += 16


def add_to_x(e, v, it, b, out):
    e.chain["dve"].link(v.tensor_tensor(tile_of(e.x, it, b), out, tile_of(e.x, it, b), ALU.add))
    stats_dve(e, v, it, b)


def l1_xattn(e):
    nc, s, ps = e.nc, e.s, e.ps
    dve = e.chain["dve"]
    with ExitStack() as ctx:
        sb = memory(e, ctx, "l1_xattn")
        first_mask = sb("first_mask", [P, CTX])
        mask = sb("causal", [P, TILES, CTX], BF16)
        a = sb("a", [P, BATCH, CTX])
        den = sb("a_den", [P, BATCH])
        rec = sb("a_rec", [P, BATCH])
        nmax = sb("nmax", [P, BATCH])
        aT = sb("aT", [P, P])
        two = (s.c_ready, s.cT_psum, s.cT_ready, s.scores_psum, s.max_ready, s.probs_ready, s.mix_psum, s.mix_ready, s.ln_var, s.ln_rstd)
        begin(2, *two)
        begin(1, s.probsT_psum, s.probsT_ready, s.mask_ready)
        with nc.Block() as block:
            @block.sync
            def _(sp):
                load(e, sp, (first_mask, "causal"))

            @block.tensor
            def _(pe):
                pe.wait_ge(s.mask_ready.sem, s.mask_ready.at(0))

                def transposes(it):
                    for b in range(BATCH):
                        transpose_c(e, pe, it, b, b)

                def scores(it):
                    for b in range(BATCH):
                        pe.wait_ge(s.cT_ready.sem, s.cT_ready.at(it, b + 1))
                        pe.wait_ge(s.probs_ready.sem, s.probs_ready.before(it, b + 1))
                        pe.matmul(ps[2 + b][:, 0:CTX], e.ident_bf[:], flat(mask[:, bass.ds(it, 1), :]), start=True, stop=False)
                        for ch in range(DCH):
                            mm = pe.matmul(ps[2 + b][:, 0:CTX], e.cT[:, b, ch, :], e.ctxT[:, ch, b, :], start=False, stop=ch == DCH - 1)
                        mm.then_inc(s.scores_psum.sem, 1)

                def probs_transposed(it):
                    pe.wait_ge(s.probs_ready.sem, s.probs_ready.at(it, 2))
                    pe.wait_ge(s.probsT_ready.sem, s.probsT_ready.before(it))
                    pe.transpose(ps[4][:, 0:P], flat(a[:]), e.ident[:]).then_inc(s.probsT_psum.sem, 1)

                def mix(it):
                    pe.wait_ge(s.probsT_ready.sem, s.probsT_ready.at(it))
                    for b in range(BATCH):
                        own = slice(b * CTX, (b + 1) * CTX)
                        pe.wait_ge(s.ln_var.sem, s.ln_var.before(it, b + 1))
                        pe.matmul(ps[6 + b][:, 0:D], aT[own, :], e.ctx_tok[own, b, :], start=True, stop=True)\
                          .then_inc(s.mix_psum.sem, 1)

                def first(new, after):
                    transposes(new)
                    scores(new)
                    transposes(after)

                def step(now, new, after):
                    probs_transposed(now)
                    if new is not None:
                        scores(new)
                    mix(now)
                    if after is not None:
                        transposes(after)

                turns_of_tiles(pe, e.chain["pe"], first, step)

            @block.scalar
            def _(act_):
                def copy(it):
                    for b in range(BATCH):
                        copy_cT(e, act_, it, b, b, s.scores_psum)

                def exp(it):
                    for b in range(BATCH):
                        act_.wait_ge(s.max_ready.sem, s.max_ready.at(it, b + 1))
                        act_.wait_ge(s.probsT_psum.sem, s.probsT_psum.before(it))
                        act_.wait_ge(s.mix_ready.sem, s.mix_ready.before(it, b + 1))
                        nc.scalar.activation(a[:, b, :], ps[2 + b][:, 0:CTX], ACT.Exp, bias=nmax[:, b:b + 1],
                                             accum_out=den[:, b:b + 1]).then_inc(s.probs_ready.sem, 1)

                def copy_aT(it):
                    act_.wait_ge(s.probsT_psum.sem, s.probsT_psum.at(it))
                    act_.wait_ge(s.mix_psum.sem, s.mix_psum.before(it, 2))
                    nc.scalar.copy(aT[:], ps[4][:, 0:P]).then_inc(s.probsT_ready.sem, 1)

                def first(new, after):
                    copy(new)
                    exp(new)
                    copy(after)

                def step(now, new, after):
                    copy_aT(now)
                    if new is not None:
                        exp(new)
                    if after is not None:
                        copy(after)

                turns_of_tiles(act_, e.chain["act"], first, step)

            @block.vector
            def _(v):
                dve.begin(v)
                dve.link(v.memset(mask[:], 0.0))
                v.wait_ge(e.loaded, e.loads)
                v.tensor_copy(mask[:, 0, :], first_mask[:]).then_inc(s.mask_ready.sem, 1)

                def normal(it):
                    for b in range(BATCH):
                        normalise(e, v, it, b)

                def maxima(it):
                    for b in range(BATCH):
                        v.wait_ge(s.scores_psum.sem, s.scores_psum.at(it, b + 1))
                        v.wait_ge(s.probs_ready.sem, s.probs_ready.before(it, b + 1))
                        v.tensor_reduce(nmax[:, b:b + 1], ps[2 + b][:, 0:CTX], AX.X, ALU.max, negate=True)\
                         .then_inc(s.max_ready.sem, 1)

                def reciprocals(it):
                    for b in range(BATCH):
                        v.wait_ge(s.probs_ready.sem, s.probs_ready.at(it, b + 1))
                        v.reciprocal(rec[:, b:b + 1], den[:, b:b + 1]).then_inc(s.mix_ready.sem, 1)

                def add(it):
                    for b in range(BATCH):
                        v.wait_ge(s.mix_ready.sem, s.mix_ready.at(it, b + 1))
                        v.wait_ge(s.mix_psum.sem, s.mix_psum.at(it, b + 1))
                        dve.link(v.scalar_tensor_tensor(tile_of(e.x, it, b), ps[6 + b][:, 0:D], rec[:, b:b + 1],
                                                        tile_of(e.x, it, b), ALU.mult, ALU.add))
                        stats_dve(e, v, it, b)

                def first(new, after):
                    normal(new)
                    normal(after)
                    maxima(new)

                def step(now, new, after):
                    reciprocals(now)
                    if new is not None:
                        maxima(new)
                    if after is not None:
                        normal(after)
                    add(now)

                turns_of_tiles(v, dve, first, step)

            @block.gpsimd
            def _(p):
                with p.Fori(0, TILES) as it:
                    for b in range(BATCH):
                        stats_pool(e, p, it, b)
        end(TILES, *two, s.probsT_psum, s.probsT_ready)
        end(1, s.mask_ready)


EXPERTS = 8
MOE_HID = 512
MCH = MOE_HID // P
CAPACITY = -(-BATCH * SEQ * 5 // (EXPERTS * 4))
CHOICES = 2
ITEMS = ALL_TILES * CHOICES
WIDTH = 3
CAPACITY_TILES = -(-CAPACITY // P)
DROPPING_TILES = EXPERTS * CAPACITY_TILES
KEEPING_TILES = (BATCH * SEQ * CHOICES + EXPERTS * (P - 1)) // P
assert DROPPING_TILES % WIDTH == 0 and KEEPING_TILES % WIDTH == 0 and CAPACITY_TILES == WIDTH
MAX_TILES = max(DROPPING_TILES, KEEPING_TILES)


def expert_constants():
    rows = [np.arange(MAX_TILES + 1) * P, np.arange(P), np.arange(ITEMS) // CHOICES, np.arange(EXPERTS) * CAPACITY_TILES * P]
    at = np.cumsum([0] + [len(r) for r in rows])
    return np.concatenate(rows), [slice(int(a), int(b)) for a, b in zip(at[:-1], at[1:])]


def route(e, ctx, stage, w_router, gates_are_softmax):
    nc, s, ps = e.nc, e.s, e.ps
    dve = e.chain["dve"]
    sb = memory(e, ctx, stage)
    E8 = EXPERTS
    every = (P, ALL_TILES, E8)
    chosen = sb("chosen", every, BF16)
    hots = sb("hots", [P, ALL_TILES, CHOICES, E8])
    comb = sb("comb", every)
    c_all = sb("c_all", [P, ALL_TILES, D])
    number = sb("expert_number", [P, E8])
    values = sb("values", [P, CHOICES, ALL_TILES, E8])
    equal = sb("equal", every)
    top = sb("top", [P, CHOICES, ALL_TILES])
    index = sb("index", [P, ALL_TILES])
    den = sb("gate_den", [P, ALL_TILES])
    pair = sb("pair_weights", [P, CHOICES, ALL_TILES])
    two = (s.c_ready, s.cT_psum, s.cT_ready, s.logits_psum, s.routed)
    begin(2, *two)
    with nc.Block() as block:
        @block.sync
        def _(sp):
            load(e, sp, w_router, (number, "expert_number"))

        @block.tensor
        def _(pe):
            pe.wait_ge(e.loaded, e.loads)

            def logits(m):
                pe.wait_ge(s.cT_ready.sem, s.cT_ready.at(m.it, m.k))
                pe.wait_ge(s.routed.sem, s.routed.before(m.it, m.k))
                for ch in range(DCH):
                    mm = pe.matmul(ps[2 + m.b][:, 0:E8], e.cT[:, m.b, ch, :], w_router[0][:, ch, :], start=ch == 0, stop=ch == DCH - 1)
                mm.then_inc(s.logits_psum.sem, 1)

            def first(new, after):
                transpose_c(e, pe, new.it, new.b, new.b)
                transpose_c(e, pe, after.it, after.b, after.b)

            def step(now, new, after):
                logits(now)
                if after:
                    transpose_c(e, pe, after.it, after.b, after.b)

            tiles(pe, e.chain["pe"], first, step)

        @block.scalar
        def _(act_):
            def copy(m):
                copy_cT(e, act_, m.it, m.b, m.b, s.logits_psum)

            def first(new, after):
                copy(new)
                copy(after)

            def step(now, new, after):
                if after:
                    copy(after)

            tiles(act_, e.chain["act"], first, step)

        @block.vector
        def _(v):
            def keep_c(m):
                k = m.it + m.b * TILES
                v.tensor_scalar(tile_of(c_all, m.it, m.b), tile_of(e.x, m.it, m.b), flat(e.mean_var[:, bass.ds(k, 1), 0:1]),
                                e.rstd[:, bass.ds(k, 1)], ALU.subtract, ALU.mult)

            def copy_logits(m):
                v.wait_ge(s.logits_psum.sem, s.logits_psum.at(m.it, m.k))
                v.tensor_copy(tile_of(values[:, 0, :, :], m.it, m.b), ps[2 + m.b][:, 0:E8]).then_inc(s.routed.sem, 1)

            def first(new, after):
                normalise(e, v, new.it, new.b)
                normalise(e, v, after.it, after.b)

            def step(now, new, after):
                keep_c(now)
                if after:
                    normalise(e, v, after.it, after.b)
                copy_logits(now)

            tiles(v, dve, first, step)
    end(TILES, *two)

    begin(1, s.max_ready, s.probs_ready)
    by_expert = lambda a: a.unsqueeze(2).broadcast_to(every)
    numbers = number[:].unsqueeze(1).broadcast_to(every)
    with nc.Block() as block:
        @block.scalar
        def _(act_):
            act_.wait_ge(s.max_ready.sem, s.max_ready.at(0))
            of = values[:, 0, :, :] if gates_are_softmax else pair[:, 1, :]
            nc.scalar.activation(of, of, ACT.Exp).then_inc(s.probs_ready.sem, 1)

        @block.vector
        def _(v):
            dve.begin(v)
            dve.link(v.tensor_scalar(number[:], number[:], -float(E8), None, ALU.add))
            if gates_are_softmax:
                dve.link(v.tensor_reduce(top[:, 0, :], values[:, 0, :, :], AX.X, ALU.max))
                v.tensor_tensor(values[:, 0, :, :], values[:, 0, :, :], by_expert(top[:, 0, :]), ALU.subtract).then_inc(s.max_ready.sem, 1)
                v.wait_ge(s.probs_ready.sem, s.probs_ready.at(0))
                dve.link(v.tensor_reduce(den[:], values[:, 0, :, :], AX.X, ALU.add))
                dve.link(v.reciprocal(den[:], den[:]))
                dve.link(v.tensor_tensor(values[:, 0, :, :], values[:, 0, :, :], by_expert(den[:]), ALU.mult))
            for c in range(CHOICES):
                dve.link(v.tensor_reduce(top[:, c, :], values[:, c, :, :], AX.X, ALU.max))
                dve.link(v.tensor_tensor(equal[:], values[:, c, :, :], by_expert(top[:, c, :]), ALU.is_equal))
                dve.link(v.tensor_tensor(equal[:], equal[:], numbers, ALU.mult))
                dve.link(v.tensor_reduce(index[:], equal[:], AX.X, ALU.min))
                dve.link(v.tensor_tensor(hots[:, :, c, :], numbers, by_expert(index[:]), ALU.is_equal))
                if c == 0:
                    dve.link(v.scalar_tensor_tensor(values[:, 1, :, :], hots[:, :, 0, :], MASKED, values[:, 0, :, :], ALU.mult, ALU.add))
            dve.link(v.tensor_tensor(chosen[:], hots[:, :, 0, :], hots[:, :, 1, :], ALU.add))
            if gates_are_softmax:
                v.tensor_tensor(comb[:], values[:, 0, :, :], chosen[:], ALU.mult)
            else:
                v.tensor_tensor(pair[:, 1, :], top[:, 1, :], top[:, 0, :], ALU.subtract).then_inc(s.max_ready.sem, 1)
                v.wait_ge(s.probs_ready.sem, s.probs_ready.at(0))
                dve.link(v.tensor_scalar(den[:], pair[:, 1, :], 1.0, None, ALU.add))
                dve.link(v.reciprocal(pair[:, 0, :], den[:]))
                dve.link(v.tensor_tensor(pair[:, 1, :], pair[:, 1, :], pair[:, 0, :], ALU.mult))
                dve.link(v.tensor_tensor(comb[:], hots[:, :, 0, :], by_expert(pair[:, 0, :]), ALU.mult))
                dve.link(v.tensor_tensor(equal[:], hots[:, :, 1, :], by_expert(pair[:, 1, :]), ALU.mult))
                v.tensor_tensor(comb[:], comb[:], equal[:], ALU.add)
    end(1, s.max_ready, s.probs_ready)
    return chosen, hots, comb, c_all


class Slots:

    def __init__(self, turn, j):
        self.turn, self.j, self.k = turn, j, j + 1


def experts(e, ctx, stage, routed, n_tiles, dropping, up_weight, down_weight, with_stats):
    nc, s, ps = e.nc, e.s, e.ps
    dve = e.chain["dve"]
    sb = memory(e, ctx, stage)
    E8, turns = EXPERTS, n_tiles // WIDTH
    chosen, hots, comb, c_all = routed
    c_rows = nc.dram_tensor(f"{stage}_c_rows", (ALL_TILES * P, D), F32).ap()
    y_rows = nc.dram_tensor(f"{stage}_y_rows", (n_tiles * P, D), F32).ap()
    values, (of_p, to_p, of_item, of_base) = expert_constants()
    const = sb("constants", [P, len(values)])
    p_col = sb("p_col", [P, 1])
    tri32 = sb("tri32", [P, P])
    tri = sb("tri", [P, P], BF16)
    ones_bf = sb("ones_bf", [P, P], BF16)
    scan = sb("scan", [P, 2, ALL_TILES, E8])
    rank = sb("rank", [P, ALL_TILES, E8])
    weight = sb("weight", [P, ALL_TILES])
    prod = sb("prod", [P, ALL_TILES, CHOICES, E8])
    weights = sb("weights", [P, ITEMS])
    slot = sb("slot", [P, ITEMS])
    above = sb("above", [P, ITEMS, n_tiles + 1])
    in_tile = sb("in_tile", [P, ITEMS, n_tiles])
    high = sb("high", [P, ITEMS])
    low = sb("low", [P, ITEMS])
    in_row = sb("in_row", [P, ITEMS, P], BF16)
    place = sb("place", [P, ITEMS, 2, n_tiles], BF16)
    token_f = sb("token_f", [P, n_tiles])
    token = sb("token", [P, n_tiles], U32)
    back = sb("back", [P, ITEMS], U32)
    rows = sb("rows", [P, max(n_tiles, ITEMS), D])
    row = sb("row", [P, WIDTH, D])
    rowT = sb("rowT", [P, WIDTH, DCH, P])
    up = sb("up", [P, WIDTH, MOE_HID])
    upT = sb("upT", [P, WIDTH, MCH, P])
    y = sb("y", [P, WIDTH, D])
    if not dropping:
        filled = sb("filled", [P, E8, ALL_TILES])
        ends = sb("ends", [P, 2, E8])
        base = sb("base", [P, E8])
        past = sb("past", [P, n_tiles, E8])
        expert_f = sb("expert_f", [P, n_tiles])
        expert_of = sb("expert_of", [P, n_tiles], I32)
    n8 = ALL_TILES * E8
    c_kept = e.dma_sem(f"{stage}_c_kept")
    gathered = [e.dma_sem(f"{stage}_gathered{g}") for g in range(3)]
    returned = [e.dma_sem(f"{stage}_returned{g}") for g in range(4)]
    cuts = [0, turns // 4, turns * 9 // 16, turns - 1]
    until = [WIDTH * (c + 1) for c in cuts]
    until[0] = 0
    begin(1, s.sums_psum, s.placed, s.prep_psum)
    with nc.Block() as block:
        @block.sync
        def _(sp):
            load(e, sp, (tri32, "tri"), (const, "expert_constants"), (p_col, "p_col"))
            sp.dma_start(c_rows.rearrange("(t p) d -> p t d", p=P), c_all[:]).then_inc(c_kept, 16)

        @block.tensor
        def _(pe):
            pe.wait_ge(s.placed.sem, s.placed.at(0, 1))
            pe.matmul(ps[0][:, 0:n8], tri[:], flat(chosen[:]), start=True, stop=True)
            pe.matmul(ps[1][:, 0:n8], ones_bf[:], flat(chosen[:]), start=True, stop=True).then_inc(s.sums_psum.sem, 1)
            pe.wait_ge(s.placed.sem, s.placed.at(0, 2))
            for i in range(ITEMS):
                mm = pe.matmul(ps[2][:, 0:2 * n_tiles], in_row[:, i, :], place[:, i, :, :].rearrange("p c n -> p (c n)"),
                               start=i == 0, stop=i == ITEMS - 1)
            mm.then_inc(s.prep_psum.sem, 1)

        @block.vector
        def _(v):
            dve.begin(v)
            v.wait_ge(e.loaded, e.loads)
            v.memset(ones_bf[:], 1.0)
            v.tensor_copy(tri[:], tri32[:]).then_inc(s.placed.sem, 1)
            v.wait_ge(s.sums_psum.sem, s.sums_psum.at(0))
            dve.link(v.tensor_copy(flat(scan[:, 0, :, :]), ps[1][:, 0:n8]))
            step, at = 1, 0
            while step < ALL_TILES:
                v.tensor_copy(scan[:, 1 - at, 0:step, :], scan[:, at, 0:step, :])
                dve.link(v.tensor_tensor(scan[:, 1 - at, step:, :], scan[:, at, step:, :], scan[:, at, 0:ALL_TILES - step, :], ALU.add))
                step, at = 2 * step, 1 - at
            count = scan[:, at, ALL_TILES - 1, :]
            dve.link(v.tensor_tensor(flat(rank[:]), flat(scan[:, at, :, :]), ps[1][:, 0:n8], ALU.subtract))
            dve.link(v.tensor_tensor(flat(rank[:]), ps[0][:, 0:n8], flat(rank[:]), ALU.add))
            by_item = lambda a: a.unsqueeze(2).broadcast_to((P, ALL_TILES, CHOICES, E8))
            if dropping:
                dve.link(v.scalar_tensor_tensor(comb[:], rank[:], float(CAPACITY), comb[:], ALU.is_le, ALU.mult))
                dve.link(v.tensor_reduce(weight[:], comb[:], AX.X, ALU.add))
                dve.link(v.tensor_scalar(weight[:], weight[:], 1e-6, None, ALU.add))
                dve.link(v.reciprocal(weight[:], weight[:]))
                dve.link(v.tensor_tensor(comb[:], comb[:], weight[:].unsqueeze(2).broadcast_to((P, ALL_TILES, E8)), ALU.mult))
                dve.link(v.tensor_tensor(scan[:, 0, :, :], rank[:], const[:, of_base].unsqueeze(1).broadcast_to((P, ALL_TILES, E8)), ALU.add))
                dve.link(v.scalar_tensor_tensor(rank[:], rank[:], float(CAPACITY), scan[:, 0, :, :], ALU.is_le, ALU.mult))
            else:
                dve.link(v.tensor_tensor(filled[:], count.unsqueeze(2).broadcast_to((P, E8, ALL_TILES)),
                                         const[:, of_p][:, 0:ALL_TILES].unsqueeze(1).broadcast_to((P, E8, ALL_TILES)), ALU.is_gt))
                dve.link(v.tensor_reduce(base[:], filled[:], AX.X, ALU.add))
                dve.link(v.tensor_copy(ends[:, 0, :], base[:]))
                step, at = 1, 0
                while step < E8:
                    v.tensor_copy(ends[:, 1 - at, 0:step], ends[:, at, 0:step])
                    dve.link(v.tensor_tensor(ends[:, 1 - at, step:], ends[:, at, step:], ends[:, at, 0:E8 - step], ALU.add))
                    step, at = 2 * step, 1 - at
                dve.link(v.tensor_tensor(base[:], ends[:, at, :], base[:], ALU.subtract))
                dve.link(v.tensor_scalar(base[:], base[:], float(P), None, ALU.mult))
                dve.link(v.tensor_tensor(rank[:], rank[:], base[:].unsqueeze(1).broadcast_to((P, ALL_TILES, E8)), ALU.add))
                dve.link(v.tensor_scalar(ends[:, 1 - at, :], ends[:, at, :], float(P), None, ALU.mult))
                dve.link(v.tensor_tensor(past[:], const[:, of_p][:, 0:n_tiles].unsqueeze(2).broadcast_to((P, n_tiles, E8)),
                                         ends[:, 1 - at, :].unsqueeze(1).broadcast_to((P, n_tiles, E8)), ALU.is_ge))
                dve.link(v.tensor_reduce(expert_f[:], past[:], AX.X, ALU.add))
                v.tensor_scalar(expert_of[:], expert_f[:], float(E8 - 1), None, ALU.min)
            dve.link(v.tensor_tensor(prod[:], hots[:], by_item(rank[:]), ALU.mult))
            dve.link(v.tensor_reduce(slot[:].rearrange("p (t c) -> p t c", c=CHOICES), prod[:], AX.X, ALU.add))
            dve.link(v.tensor_tensor(prod[:], hots[:], by_item(comb[:]), ALU.mult))
            v.tensor_reduce(weights[:].rearrange("p (t c) -> p t c", c=CHOICES), prod[:], AX.X, ALU.add)
            dve.link(v.tensor_tensor(above[:], slot[:].unsqueeze(2).broadcast_to((P, ITEMS, n_tiles + 1)),
                                     const[:, of_p][:, 0:n_tiles + 1].unsqueeze(1).broadcast_to((P, ITEMS, n_tiles + 1)), ALU.is_gt))
            v.tensor_tensor(in_tile[:], above[:, :, 0:n_tiles], above[:, :, 1:], ALU.subtract)
            dve.link(v.tensor_reduce(high[:], above[:], AX.X, ALU.add))
            dve.link(v.tensor_scalar(high[:], high[:], -float(P), float(P - 1), ALU.mult, ALU.add))
            dve.link(v.tensor_tensor(low[:], slot[:], high[:], ALU.add))
            v.tensor_tensor(in_row[:], low[:].unsqueeze(2).broadcast_to((P, ITEMS, P)),
                            const[:, to_p].unsqueeze(1).broadcast_to((P, ITEMS, P)), ALU.is_equal)
            v.tensor_scalar(place[:, :, 0, :], in_tile[:], p_col[:], None, ALU.mult)
            v.tensor_tensor(place[:, :, 1, :], in_tile[:], const[:, of_item].unsqueeze(2).broadcast_to((P, ITEMS, n_tiles)), ALU.mult)\
             .then_inc(s.placed.sem, 1)
            v.tensor_scalar(back[:], slot[:], -1.0, 0.0, ALU.add, ALU.max)
            v.wait_ge(s.prep_psum.sem, s.prep_psum.at(0))
            dve.link(v.tensor_copy(token_f[:], ps[2][:, 0:n_tiles]))
            v.scalar_tensor_tensor(token[:], ps[2][:, n_tiles:2 * n_tiles], float(P), token_f[:], ALU.mult, ALU.add)
    end(1, s.sums_psum, s.prep_psum)
    s.placed.base += 2

    three = (s.row_copied, s.rowT_psum, s.rowT_ready, s.up_psum, s.up_ready, s.upT_psum, s.upT_ready, s.down_psum, s.y_copied)
    begin(WIDTH, *three)
    stored = (s.y_stored0, s.y_stored1, s.y_stored2)
    begin(16, *stored)

    def expert(pe, m):
        if dropping:
            return m.turn
        return pe.value_load(expert_of[0:1, bass.ds(m.turn * WIDTH + m.j, 1)], min_val=0, max_val=E8 - 1)

    with nc.Block() as block:
        @block.gpsimd
        def _(p):
            p.wait_ge(c_kept, 16)
            for g in range(3):
                for t in range(until[g], until[g + 1]):
                    p.indirect_dma_start(rows[:, t, :], None, c_rows, bass.IndirectOffsetOnAxis(ap=token[:, t:t + 1], axis=0))\
                     .then_inc(gathered[g], 16)

        @block.sync
        def _(sp):
            with sp.Fori(0, turns) as turn:
                for j in range(WIDTH):
                    sp.wait_ge(s.y_copied.sem, s.y_copied.at(turn, j + 1))
                    sp.dma_start(y_rows.rearrange("(t p) d -> p t d", p=P)[:, bass.ds(turn * WIDTH + j, 1), :].rearrange("p t d -> p (t d)"),
                                 y[:, j, :]).then_inc(stored[j].sem, 16)

        @block.tensor
        def _(pe):
            def row_transposed(m):
                pe.wait_ge(s.row_copied.sem, s.row_copied.at(m.turn, m.k))
                pe.wait_ge(s.rowT_ready.sem, s.rowT_ready.at(m.turn, m.k - 1))
                for ch in range(DCH):
                    mm = pe.transpose(ps[6][:, ch * P:(ch + 1) * P], row[:, m.j, ch * P:(ch + 1) * P], e.ident[:])
                mm.then_inc(s.rowT_psum.sem, 1)

            def up_product(m):
                x = expert(pe, m)
                pe.wait_ge(s.upT_ready.sem, s.upT_ready.at(m.turn, m.k - WIDTH))
                pe.wait_ge(s.rowT_ready.sem, s.rowT_ready.at(m.turn, m.k))
                for ch in range(DCH):
                    mm = pe.matmul(ps[m.j], rowT[:, m.j, ch, :], up_weight(x, ch), start=ch == 0, stop=ch == DCH - 1)
                mm.then_inc(s.up_psum.sem, 1)

            def up_transposed(m):
                pe.wait_ge(s.up_ready.sem, s.up_ready.at(m.turn, m.k))
                for f in range(MCH):
                    mm = pe.transpose(ps[m.j][:, f * P:(f + 1) * P], up[:, m.j, f * P:(f + 1) * P], e.ident[:])
                mm.then_inc(s.upT_psum.sem, 1)

            def down_product(m):
                x = expert(pe, m)
                pe.wait_ge(s.y_copied.sem, s.y_copied.at(m.turn, m.k - WIDTH))
                pe.wait_ge(s.upT_ready.sem, s.upT_ready.at(m.turn, m.k))
                for f in range(MCH):
                    mm = pe.matmul(ps[3 + m.j][:, 0:D], upT[:, m.j, f, :], down_weight(x, f), start=f == 0, stop=f == MCH - 1)
                mm.then_inc(s.down_psum.sem, 1)

            def first(new, after):
                row_transposed(new)
                row_transposed(after)
                up_product(new)

            def step(now, new, after):
                up_transposed(now)
                if new:
                    up_product(new)
                if after:
                    row_transposed(after)
                down_product(now)

            pipeline(pe, e.chain["pe"], turns, WIDTH, Slots, first, step)

        @block.scalar
        def _(act_):
            def copy_rowT(m):
                act_.wait_ge(s.rowT_psum.sem, s.rowT_psum.at(m.turn, m.k))
                act_.wait_ge(s.up_psum.sem, s.up_psum.at(m.turn, m.k - WIDTH))
                nc.scalar.copy(flat(rowT[:, m.j, :, :]), ps[6][:, 0:D]).then_inc(s.rowT_ready.sem, 1)

            def silu(m):
                act_.wait_ge(s.up_psum.sem, s.up_psum.at(m.turn, m.k))
                act_.wait_ge(s.upT_psum.sem, s.upT_psum.at(m.turn, m.k - WIDTH))
                nc.scalar.activation(up[:, m.j, :], ps[m.j], ACT.Silu).then_inc(s.up_ready.sem, 1)

            def copy_y(m):
                act_.wait_ge(s.down_psum.sem, s.down_psum.at(m.turn, m.k))
                act_.wait_ge(stored[m.j].sem, stored[m.j].at(m.turn, 0))
                nc.scalar.copy(y[:, m.j, :], ps[3 + m.j][:, 0:D]).then_inc(s.y_copied.sem, 1)

            def first(new, after):
                copy_rowT(new)
                copy_rowT(after)
                silu(new)

            def step(now, new, after):
                if new:
                    silu(new)
                if after:
                    copy_rowT(after)
                copy_y(now)

            pipeline(act_, e.chain["act"], turns, WIDTH, Slots, first, step)

        @block.vector
        def _(v):
            def copy_row(m):
                v.wait_ge(s.rowT_psum.sem, s.rowT_psum.at(m.turn, m.k - WIDTH))
                v.tensor_copy(row[:, m.j, :], flat(rows[:, bass.ds(m.turn * WIDTH + m.j, 1), :])).then_inc(s.row_copied.sem, 1)

            def copy_upT(m):
                v.wait_ge(s.upT_psum.sem, s.upT_psum.at(m.turn, m.k))
                v.wait_ge(s.down_psum.sem, s.down_psum.at(m.turn, m.k - WIDTH))
                v.tensor_copy(flat(upT[:, m.j, :, :]), ps[m.j]).then_inc(s.upT_ready.sem, 1)

            def first(new, after):
                copy_row(new)
                copy_row(after)

            def step(now, new, after):
                if after:
                    copy_row(after)
                copy_upT(now)

            def wait_rows(g):
                v.wait_ge(gathered[g], 16 * (until[g + 1] - until[g]))

            pipeline(v, dve, turns, WIDTH, Slots, first, step, cuts, wait_rows)
    end(turns, *three, *stored)

    if with_stats:
        begin(2, s.ln_var, s.ln_rstd)
    per = TILES // len(returned)
    with nc.Block() as block:
        @block.gpsimd
        def _(p):
            for one in stored:
                p.wait_ge(one.sem, one.base)
            for g in range(len(returned)):
                for t in range(g * per, (g + 1) * per):
                    for b in range(BATCH):
                        for c in range(CHOICES):
                            i = (t + b * TILES) * CHOICES + c
                            p.indirect_dma_start(rows[:, i, :], None, y_rows, bass.IndirectOffsetOnAxis(ap=back[:, i:i + 1], axis=0))\
                             .then_inc(returned[g], 16)
            if with_stats:
                with p.Fori(0, TILES) as it:
                    for b in range(BATCH):
                        stats_pool(e, p, it, b)

        @block.vector
        def _(v):
            for g in range(len(returned)):
                v.wait_ge(returned[g], 16 * per * BATCH * CHOICES)
                with v.Fori(g * per, (g + 1) * per) as it:
                    dve.begin(v)
                    for b in range(BATCH):
                        for c in range(CHOICES):
                            i = (it + b * TILES) * CHOICES + c
                            dve.link(v.scalar_tensor_tensor(tile_of(e.x, it, b), flat(rows[:, bass.ds(i, 1), :]), weights[:, bass.ds(i, 1)],
                                                            tile_of(e.x, it, b), ALU.mult, ALU.add))
                        if with_stats:
                            stats_dve(e, v, it, b)
    if with_stats:
        end(TILES, s.ln_var, s.ln_rstd)


def l1_ffn(e):
    nc = e.nc
    with ExitStack() as ctx:
        sb = memory(e, ctx, "l1_ffn")
        w_router = sb("w_router", [P, DCH, EXPERTS])
        w_gate = sb("w_gate", [P, DCH, MOE_HID])
        w_down = sb("w_down", [P, MCH, EXPERTS, D])
        with nc.Block() as block:
            @block.sync
            def _(sp):
                load(e, sp, (w_gate, "L1_gate"), (w_down, "L1_down"))
        routed = route(e, ctx, "l1_route", (w_router, "L1_router"), True)
        experts(e, ctx, "l1_experts", routed, DROPPING_TILES, True, lambda x, ch: w_gate[:, ch, :],
                lambda x, f: flat(w_down[:, f, bass.ds(x, 1), :]), True)


PARTS = 3
XH, XD = 16, 16


def cross_attention(e, name, biased, sink):
    nc, s, ps = e.nc, e.s, e.ps
    dve = e.chain["dve"]
    with ExitStack() as ctx:
        sb = memory(e, ctx, name)
        HALF_XH = XH // 2
        wq, wk, wv, wo = (sb(n, [P, DCH, D]) for n in ("wq", "wk", "wv", "wo"))
        own_head = sb("own_head", [P, HALF_XH])
        keysT = sb("keysT", [P, DCH, BATCH, CTX])
        keys = sb("keys", [P, DCH, BATCH, HALF_XH, CTX])
        qT = sb("qT", [P, BATCH, DCH, P])
        V1 = sb("V1", [P, BATCH, HALF_XH, 2, XD + 1])
        MIX = XH * (XD + 1)
        probs = sb("probs", [P, BATCH, XH, CTX])
        probsT = sb("probsT", [P, BATCH, HALF_XH, P])
        top = sb("top", [P, BATCH, XH])
        den = sb("den", [P, BATCH, XH])
        rec = sb("rec", [P, BATCH, XH])
        o = sb("o", [P, BATCH, D])
        oT = sb("oT", [P, BATCH, DCH, P])
        if biased:
            bq = sb("bq", [P, DCH])
            bk = sb("bk", [P, DCH])
            bv = sb("bv", [P, D])
            bo = sb("bo", [P, D])
            given = ((bq, name + "bq"), (bk, name + "bk"), (bv, name + "bv"), (bo, name + "bo"))
        else:
            ROWS = PARTS * PARTS + PARTS
            BH = BATCH * XH
            slopes = sb("slopes", [BH, 1])
            key_pos = sb("key_pos", [BH, CTX], I32)
            query_pos = sb("query_pos", [ALL_TILES, P], I32)
            pos_f = sb("pos_f", [BH, P])
            rest = sb("rest", [BH, P])
            slope_f = sb("slope_f", [BH, CTX])
            query_parts = sb("query_parts", [ALL_TILES, PARTS, P], BF16)
            slope_parts = sb("slope_parts", [BH, PARTS, CTX], BF16)
            key_parts = sb("key_parts", [BH, PARTS, CTX], BF16)
            query_rows = sb("query_rows", [ROWS, ALL_TILES, P], BF16)
            key_rows = sb("key_rows", [ROWS, BATCH, XH, CTX], BF16)
            mask_i = sb("mask_i", [P, ALL_TILES, CTX], I32)
            mask = sb("mask", [P, ALL_TILES, CTX], BF16)
            of_query = nc.dram_tensor("query_parts", (PARTS, ALL_TILES, P), BF16).ap()
            of_slope = nc.dram_tensor("slope_parts", (PARTS, BH, CTX), BF16).ap()
            of_key = nc.dram_tensor("key_parts", (PARTS, BH, CTX), BF16).ap()
            pos_loaded, parts_stored, rows_loaded = (e.dma_sem(n) for n in ("pos_loaded", "parts_stored", "rows_loaded"))
            given = ((mask_i, "mask_if1"),)
        begin(1, s.prep_psum, s.prep_ready, s.ones_set)
        with nc.Block() as block:
            @block.sync
            def _(sp):
                if not biased:
                    for to, of in ((slopes, "slopes"), (key_pos, "key_pos"), (query_pos, "query_pos")):
                        sp.dma_start(to[:], e.dram[of]).then_inc(pos_loaded, 16)
                load(e, sp, (own_head, "own_head"), (wk, name + "wk"), (wv, name + "wv"), (wq, name + "wq"), (wo, name + "wo"), *given)
                if not biased:
                    sp.wait_ge(s.prep_ready.sem, s.prep_ready.at(0))
                    for to, of in ((of_query, query_parts), (of_slope, slope_parts), (of_key, key_parts)):
                        sp.dma_start(to.rearrange("i r n -> r i n"), of[:]).then_inc(parts_stored, 16)
                    sp.wait_ge(s.ones_set.sem, s.ones_set.at(0))
                    sp.wait_ge(parts_stored, 3 * 16)
                    for j in range(PARTS):
                        own = slice(PARTS * j, PARTS * (j + 1))
                        sp.dma_start(query_rows[own].rearrange("i t p -> i (t p)"), of_query.rearrange("i t p -> i (t p)"))\
                          .then_inc(rows_loaded, 16)
                        sp.dma_start(key_rows[own].rearrange("i b h n -> i (b h n)"),
                                     of_slope[j:j + 1].rearrange("i r n -> i (r n)").broadcast_to((PARTS, BH * CTX))).then_inc(rows_loaded, 16)
                    sp.dma_start(key_rows[PARTS * PARTS:ROWS].rearrange("i b h n -> i (b h n)"), of_key.rearrange("i r n -> i (r n)"))\
                      .then_inc(rows_loaded, 16)

            @block.gpsimd
            def _(p):
                if not biased:
                    p.memset(query_rows[:], 1.0).then_inc(s.ones_set.sem, 1)

            @block.tensor
            def _(pe):
                pe.wait_ge(e.loaded, e.loads)
                for half in range(2):
                    for ch in range(DCH):
                        pe.matmul(ps[0][:, half * P:(half + 1) * P], wk[:, ch, half * P:(half + 1) * P],
                                  e.ctxT[:, ch, :, :], start=(half, ch) == (0, 0), stop=ch == DCH - 1, skip_group_check=True)
                for b in range(BATCH):
                    for ch in range(DCH):
                        mm = pe.matmul(ps[4][:, b * D:(b + 1) * D], e.ctxT2[:, ch, b, :, :], wv[:, ch, :],
                                       start=(b, ch) == (0, 0), stop=ch == DCH - 1, skip_group_check=True)
                mm.then_inc(s.prep_psum.sem, 1)

            @block.vector
            def _(v):
                dve.begin(v)
                if not biased:
                    def in_parts(parts, of, left):
                        for i in range(PARTS):
                            dve.link(v.tensor_copy(parts[:, i, :], of))
                            if i < PARTS - 1:
                                dve.link(v.tensor_tensor(left, of, parts[:, i, :], ALU.subtract))
                                of = left

                    v.wait_ge(pos_loaded, 3 * 16)
                    dve.link(v.tensor_copy(pos_f[0:ALL_TILES, :], query_pos[:]))
                    in_parts(query_parts, pos_f[0:ALL_TILES, :], rest[0:ALL_TILES, :])
                    dve.link(v.tensor_scalar(slope_f[:], slopes[:].broadcast_to((BH, CTX)), -1.0, None, ALU.mult))
                    in_parts(slope_parts, slope_f[:], rest[:, 0:CTX])
                    dve.link(v.tensor_copy(pos_f[:, 0:CTX], key_pos[:]))
                    dve.link(v.tensor_scalar(pos_f[:, 0:CTX], pos_f[:, 0:CTX], slopes[:, 0:1], None, ALU.mult))
                    in_parts(key_parts, pos_f[:, 0:CTX], rest[:, 0:CTX])
                dve.link(v.memset(V1[:], 0.0))
                for half in range(2):
                    ones = v.memset(V1[half * CTX:(half + 1) * CTX, :, :, half, XD:], 1.0)
                ones.then_inc(s.prep_ready.sem, 1)
                v.wait_ge(s.prep_ready.sem, s.prep_ready.at(0))
                v.wait_ge(e.loaded, e.loads)
                if not biased:
                    v.tensor_scalar(mask[:], mask_i[:], 0.0, MASKED, ALU.is_equal, ALU.mult)
                v.wait_ge(s.prep_psum.sem, s.prep_psum.at(0))
                kp = ps[0][:, 0:D].rearrange("p (a n) -> p a n", n=P)
                kt = keysT[:].rearrange("p a b n -> p a (b n)")
                if biased:
                    dve.link(v.tensor_tensor(kt, kp, bk[:].unsqueeze(2).broadcast_to((P, DCH, P)), ALU.add))
                else:
                    dve.link(v.tensor_copy(kt, kp))
                for half in range(2):
                    for b in range(BATCH):
                        v.tensor_tensor(keys[:, half, b, :, :], keysT[:, half, b, :].unsqueeze(1).broadcast_to((P, HALF_XH, CTX)),
                                        own_head[:].unsqueeze(2).broadcast_to((P, HALF_XH, CTX)), ALU.mult)
                for b in range(BATCH):
                    for half in range(2):
                        r = slice(half * CTX, (half + 1) * CTX)
                        of = ps[4][r, b * D:(b + 1) * D].rearrange("p (h two x) -> p h two x", two=2, x=XD)[:, :, half, :]
                        to = V1[r, b, :, half, 0:XD]
                        if biased:
                            v.tensor_tensor(to, of, bv[r, :].rearrange("p (h two x) -> p h two x", two=2, x=XD)[:, :, half, :], ALU.add)
                        else:
                            v.tensor_copy(to, of)
        end(1, s.prep_psum, s.prep_ready)
        if not biased:
            end(1, s.ones_set)

        two = (s.c_ready, s.cT_psum, s.cT_ready, s.scores_psum, s.max_ready, s.probs_ready, s.probsT_psum, s.probsT_ready,
               s.mix_psum, s.mix_ready, s.mixT_psum, s.mixT_ready, s.out_psum, s.ln_var, s.ln_rstd,
               s.q_psum, s.q_ready) + ((s.bias_added,) if biased else ())
        begin(2, *two)

        BANKS = 4
        with nc.Block() as block:
            @block.tensor
            def _(pe):
                if not biased:
                    pe.wait_ge(rows_loaded, (2 * PARTS + 1) * 16)

                def transposed(m):
                    pe.wait_ge(s.q_ready.sem, s.q_ready.before(m.it, m.k))
                    transpose_c(e, pe, m.it, m.b, BANKS * m.b)

                def queries(m):
                    pe.wait_ge(s.cT_ready.sem, s.cT_ready.at(m.it, m.k))
                    for half in range(2):
                        for ch in range(DCH):
                            mm = pe.matmul(ps[BANKS * m.b][:, D + half * P:D + (half + 1) * P], wq[:, ch, half * P:(half + 1) * P], e.cT[:, m.b, ch, :],
                                           start=(half, ch) == (0, 0), stop=ch == DCH - 1, skip_group_check=True)
                    mm.then_inc(s.q_psum.sem, 1)

                def scores(m):
                    pe.wait_ge(s.q_ready.sem, s.q_ready.at(m.it, m.k))
                    pe.wait_ge(s.probsT_ready.sem, s.probsT_ready.before(m.it, m.k))
                    for half in range(2):
                        bank = ps[BANKS * m.b + 2 + half]
                        mm = pe.matmul(bank, qT[:, m.b, half, :], keys[:, half, m.b, :, :].rearrange("p h n -> p (h n)"), start=True, stop=biased)
                        if not biased:
                            tile = bass.ds(m.it + m.b * TILES, 1)
                            pe.matmul(bank, e.ident_bf[:], mask[:, tile, :].broadcast_to((P, HALF_XH, CTX)), start=False, stop=False)
                            mm = pe.matmul(bank, flat(query_rows[:, tile, :]),
                                           key_rows[:, m.b, half * HALF_XH:(half + 1) * HALF_XH, :].rearrange("p h n -> p (h n)"),
                                           start=False, stop=True)
                    mm.then_inc(s.scores_psum.sem, 1)

                def probs_transposed(m):
                    pe.wait_ge(s.probs_ready.sem, s.probs_ready.at(m.it, m.k))
                    for j in range(XH // 2):
                        mm = pe.transpose(ps[BANKS * m.b + 2 + j // 4][:, (j % 4) * P:(j % 4 + 1) * P],
                                          probs[:, m.b, 2 * j:2 * j + 2, :].rearrange("p h n -> p (h n)"), e.ident[:])
                    mm.then_inc(s.probsT_psum.sem, 1)

                def mix(m):
                    pe.wait_ge(s.probsT_ready.sem, s.probsT_ready.at(m.it, m.k))
                    pe.wait_ge(s.ln_var.sem, s.ln_var.before(m.it, m.k))
                    for j in range(XH // 2):
                        mm = pe.matmul(ps[BANKS * m.b + 1][:, j * 2 * (XD + 1):(j + 1) * 2 * (XD + 1)], probsT[:, m.b, j, :], flat(V1[:, m.b, j, :, :]),
                                       start=j == 0, stop=True, skip_group_check=True)
                    mm.then_inc(s.mix_psum.sem, 1)

                def mix_transposed(m):
                    pe.wait_ge(s.mix_ready.sem, s.mix_ready.at(m.it, m.k))
                    for ch in range(DCH):
                        mm = pe.transpose(ps[BANKS * m.b + 1][:, ch * P:(ch + 1) * P], o[:, m.b, ch * P:(ch + 1) * P], e.ident[:])
                    mm.then_inc(s.mixT_psum.sem, 1)

                def projected(m):
                    pe.wait_ge(s.mixT_ready.sem, s.mixT_ready.at(m.it, m.k))
                    bank = ps[BANKS * m.b + 1][:, D:2 * D]
                    for ch in range(DCH):
                        mm = pe.matmul(bank, oT[:, m.b, ch, :], wo[:, ch, :], start=ch == 0, stop=ch == DCH - 1)
                    mm.then_inc(s.out_psum.sem, 1)

                def first(one, two, three):
                    transposed(one)
                    transposed(two)
                    queries(one)
                    queries(two)
                    scores(one)
                    transposed(three)
                    scores(two)
                    probs_transposed(one)
                    queries(three)
                    mix(one)

                def step(one, two, three, four):
                    if three:
                        scores(three)
                    mix_transposed(one)
                    if four:
                        transposed(four)
                    projected(one)
                    if two:
                        probs_transposed(two)
                    if four:
                        queries(four)
                    if two:
                        mix(two)

                tiles(pe, e.chain["pe"], first, step, depth=4)

            @block.scalar
            def _(act_):
                def exp(m):
                    act_.wait_ge(s.max_ready.sem, s.max_ready.at(m.it, m.k))
                    nc.scalar.activation(flat(probs[:, m.b, :, :]), flat(probs[:, m.b, :, :]), ACT.Exp, scale=float(XD) ** -0.5)\
                      .then_inc(s.probs_ready.sem, 1)

                def copy_probsT(m):
                    act_.wait_ge(s.probsT_psum.sem, s.probsT_psum.at(m.it, m.k))
                    act_.wait_ge(s.mix_psum.sem, s.mix_psum.before(m.it, m.k))
                    nc.scalar.copy(flat(probsT[:, m.b, :, :]), flat(e.psum[:, BANKS * m.b + 2:BANKS * m.b + 4, :])).then_inc(s.probsT_ready.sem, 1)

                def copy_oT(m):
                    act_.wait_ge(s.mixT_psum.sem, s.mixT_psum.at(m.it, m.k))
                    act_.wait_ge(s.out_psum.sem, s.out_psum.before(m.it, m.k))
                    nc.scalar.copy(flat(oT[:, m.b, :, :]), ps[BANKS * m.b + 1][:, 0:D]).then_inc(s.mixT_ready.sem, 1)

                def copy_qT(m):
                    act_.wait_ge(s.q_psum.sem, s.q_psum.at(m.it, m.k))
                    act_.wait_ge(s.scores_psum.sem, s.scores_psum.before(m.it, m.k))
                    of = ps[BANKS * m.b][:, D:2 * D]
                    if biased:
                        nc.scalar.activation(qT[:, m.b, 0, :], of[:, 0:P], ACT.Identity, bias=bq[:, 0:1])
                        nc.scalar.activation(qT[:, m.b, 1, :], of[:, P:D], ACT.Identity, bias=bq[:, 1:2]).then_inc(s.q_ready.sem, 1)
                    else:
                        nc.scalar.copy(flat(qT[:, m.b, :, :]), of).then_inc(s.q_ready.sem, 1)

                def copy_c(m):
                    copy_cT(e, act_, m.it, m.b, BANKS * m.b, s.q_psum)

                def first(one, two, three):
                    copy_c(one)
                    copy_c(two)
                    copy_qT(one)
                    copy_qT(two)
                    copy_c(three)
                    exp(one)
                    copy_probsT(one)
                    copy_qT(three)
                    exp(two)

                def step(one, two, three, four):
                    copy_oT(one)
                    if four:
                        copy_c(four)
                    if two:
                        copy_probsT(two)
                    if four:
                        copy_qT(four)
                    if three:
                        exp(three)

                tiles(act_, e.chain["act"], first, step, depth=4)

            @block.vector
            def _(v):
                def scores_of(m):
                    return e.psum[:, BANKS * m.b + 2:BANKS * m.b + 4, :].rearrange("p a (h n) -> p (a h) n", n=CTX)

                def maxima(m):
                    v.wait_ge(s.scores_psum.sem, s.scores_psum.at(m.it, m.k))
                    dve.link(v.tensor_reduce(top[:, m.b, :], scores_of(m), AX.X, ALU.max))

                def subtract(m):
                    v.wait_ge(s.probsT_psum.sem, s.probsT_psum.before(m.it, m.k))
                    v.tensor_tensor(probs[:, m.b, :, :], scores_of(m), top[:, m.b, :].unsqueeze(2).broadcast_to((P, XH, CTX)), ALU.subtract)\
                     .then_inc(s.max_ready.sem, 1)

                def weighted(m):
                    mixed = ps[BANKS * m.b + 1][:, 0:MIX].rearrange("p (h x) -> p h x", x=XD + 1)
                    v.wait_ge(s.mix_psum.sem, s.mix_psum.at(m.it, m.k))
                    of = mixed[:, :, XD]
                    if sink:
                        dve.link(v.tensor_scalar(den[:, m.b, :], of, 1.0, None, ALU.add))
                        of = den[:, m.b, :]
                    dve.link(v.reciprocal(rec[:, m.b, :], of))
                    v.wait_ge(s.mixT_psum.sem, s.mixT_psum.before(m.it, m.k))
                    v.tensor_tensor(o[:, m.b, :].rearrange("p (h x) -> p h x", x=XD), mixed[:, :, 0:XD],
                                    rec[:, m.b, :].unsqueeze(2).broadcast_to((P, XH, XD)), ALU.mult).then_inc(s.mix_ready.sem, 1)

                def normal(m):
                    normalise(e, v, m.it, m.b)

                def softmax(m):
                    maxima(m)
                    subtract(m)

                def add(m):
                    v.wait_ge(s.out_psum.sem, s.out_psum.at(m.it, m.k))
                    if biased:
                        v.wait_ge(s.bias_added.sem, s.bias_added.at(m.it, m.k))
                    add_to_x(e, v, m.it, m.b, ps[BANKS * m.b + 1][:, D:2 * D])

                def first(one, two, three):
                    normal(one)
                    normal(two)
                    softmax(one)
                    normal(three)
                    softmax(two)

                def step(one, two, three, four):
                    weighted(one)
                    if four:
                        normal(four)
                    if three:
                        softmax(three)
                    add(one)

                tiles(v, e.chain["dve"], first, step, depth=4)

            @block.gpsimd
            def _(p):
                with p.Fori(0, TILES) as it:
                    if biased:
                        for b in range(BATCH):
                            p.wait_ge(s.c_ready.sem, s.c_ready.at(it, b + 1))
                            p.tensor_tensor(tile_of(e.x, it, b), tile_of(e.x, it, b), bo[:], ALU.add).then_inc(s.bias_added.sem, 1)
                    for b in range(BATCH):
                        stats_pool(e, p, it, b)
        end(TILES, *two)


def l2_xattn(e):
    cross_attention(e, "L2_", True, False)


def l3_xattn(e):
    cross_attention(e, "L3_", False, True)


QI = 704
QCH = -(-QI // P)
QW = [min(P, QI - j * P) for j in range(QCH)]
QMAX = 127.0
MAGIC = 1.5 * 2.0 ** 23


def quantise(v, dve, to, tmp, of, inverse):
    dve.link(v.tensor_scalar(tmp, of, inverse, -QMAX - 1.0, ALU.mult, ALU.max))
    dve.link(v.tensor_scalar(tmp, tmp, QMAX, MAGIC, ALU.min, ALU.add))
    return v.tensor_scalar(to, tmp, -MAGIC, None, ALU.add)


def l2_ffn(e):
    nc, s, ps = e.nc, e.s, e.ps
    dve = e.chain["dve"]
    with ExitStack() as ctx:
        sb = memory(e, ctx, "l2_ffn")
        clips = sb("clips", [P, 2])
        sig = sb("sig", [P, 2])
        gu_scale = sb("gu_scale", [P, 2, QCH])
        d_scale = sb("d_scale", [P, DCH])
        d_row = sb("d_row", [P, D])
        w_guT = sb("w_guT", [P, DCH, 2, QI], BF16)
        w_dT = sb("w_dT", [P, QCH, D], BF16)
        h = sb("h", [P, QCH, ALL_TILES, P])
        amax = sb("amax", [P, ALL_TILES])
        one = sb("one_max", [P, 1])
        allmax = sb("allmax", [P, 1])
        xs = sb("xs", [P, 2])
        hmax = sb("hmax", [P, TILES, QCH])
        with ExitStack() as inner:
            sbi = lambda n, shape, dt=F32: inner.enter_context(nc.sbuf_tensor(n, shape, dt))
            w_gu = sbi("w_gu", [P, 2, QCH, D])
            w_d = sbi("w_d", [P, DCH, QI])
            tmp = sbi("q_tmp", [P, QCH * D])
            q_gu = sbi("q_gu", [P, 2, QCH, D], BF16)
            q_d = sbi("q_d", [P, DCH, QI], BF16)
            inv = sbi("inv", [P, 2 * QCH + DCH])
            diag = sbi("diag", [P, DCH, P])
            begin(1, s.probs_ready)
            with nc.Block() as block:
                @block.sync
                def _(sp):
                    load(e, sp, (w_gu, "L2_gu"), (w_d, "L2_d"), (clips, "L2_clips"))

                @block.scalar
                def _(act_):
                    act_.wait_ge(e.loaded, e.loads)
                    nc.scalar.activation(sig[:], clips[:], ACT.Exp, scale=-1.0).then_inc(s.probs_ready.sem, 1)

                @block.vector
                def _(v):
                    dve.begin(v)
                    v.memset(hmax[:], 0.0)
                    v.wait_ge(e.loaded, e.loads)
                    dve.link(v.memset(gu_scale[:], 0.0))
                    for n in range(2):
                        v.tensor_reduce(gu_scale[:, n, 0:QCH - 1], w_gu[:, n, 0:QCH - 1, :], AX.X, ALU.max, apply_absolute_value=True)
                        v.tensor_reduce(gu_scale[0:QW[-1], n, QCH - 1:QCH], w_gu[0:QW[-1], n, QCH - 1, :], AX.X, ALU.max, apply_absolute_value=True)
                    dve.link(v.tensor_reduce(d_scale[:], w_d[:], AX.X, ALU.max, apply_absolute_value=True))
                    v.tensor_scalar(gu_scale[:], gu_scale[:], 1.0 / QMAX, None, ALU.mult)
                    dve.link(v.tensor_scalar(d_scale[:], d_scale[:], 1.0 / QMAX, None, ALU.mult))
                    for n in range(2):
                        v.reciprocal(inv[:, n * QCH:n * QCH + QCH - 1], gu_scale[:, n, 0:QCH - 1])
                        v.reciprocal(inv[0:QW[-1], n * QCH + QCH - 1:(n + 1) * QCH], gu_scale[0:QW[-1], n, QCH - 1:QCH])
                    dve.link(v.reciprocal(inv[:, 2 * QCH:], d_scale[:]))
                    for n in range(2):
                        for j in range(QCH):
                            r = slice(0, QW[j])
                            dve.link(quantise(v, dve, q_gu[r, n, j, :], tmp[r, 0:D], w_gu[r, n, j, :], inv[r, n * QCH + j:n * QCH + j + 1]))
                    for ch in range(DCH):
                        dve.link(quantise(v, dve, q_d[:, ch, :], tmp[:, 0:QI], w_d[:, ch, :], inv[:, 2 * QCH + ch:2 * QCH + ch + 1]))
                        dve.link(v.tensor_scalar(diag[:, ch, :], e.ident[:], d_scale[:, ch:ch + 1], None, ALU.mult))
                    v.wait_ge(s.probs_ready.sem, s.probs_ready.at(0))
                    dve.link(v.tensor_scalar(sig[:], sig[:], 1.0, None, ALU.add))
                    dve.link(v.reciprocal(sig[:], sig[:]))
                    v.tensor_scalar(sig[:], sig[:], 1.0 / QMAX, None, ALU.mult)
            end(1, s.probs_ready)
            begin(8, s.prep_psum, s.prep_ready)
            with nc.Block() as block:
                @block.tensor
                def _(pe):
                    for n in range(2):
                        for ch in range(DCH):
                            for j in range(QCH):
                                bank = ps[2 * (2 * n + ch) + j // 4]
                                mm = pe.matmul(bank[:, (j % 4) * P:(j % 4) * P + QW[j]], q_gu[0:QW[j], n, j, ch * P:(ch + 1) * P],
                                               e.ident_bf[0:QW[j], 0:QW[j]], start=j % 4 == 0, stop=True, skip_group_check=True)
                            mm.then_inc(s.prep_psum.sem, 1)
                    pe.wait_ge(s.prep_ready.sem, s.prep_ready.at(0, 4))
                    for j in range(QCH):
                        for ch in range(DCH):
                            mm = pe.matmul(ps[j // 2][0:QW[j], (j % 2) * D + ch * P:(j % 2) * D + (ch + 1) * P], q_d[:, ch, j * P:j * P + QW[j]],
                                           e.ident_bf[:], start=(j % 2, ch) == (0, 0), stop=True, skip_group_check=True)
                    mm.then_inc(s.prep_psum.sem, 1)
                    for ch in range(DCH):
                        mm = pe.matmul(ps[4][:, ch * P:(ch + 1) * P], e.ones[:], diag[:, ch, :], start=ch == 0, stop=True, skip_group_check=True)
                    mm.then_inc(s.prep_psum.sem, 1)

                @block.vector
                def _(v):
                    for n in range(2):
                        for ch in range(DCH):
                            k = 2 * n + ch
                            v.wait_ge(s.prep_psum.sem, s.prep_psum.at(0, k + 1))
                            v.tensor_copy(w_guT[:, ch, n, :], e.psum[:, 2 * k:2 * k + 2, :].rearrange("p a n -> p (a n)")[:, 0:QI])\
                             .then_inc(s.prep_ready.sem, 1)
                    v.wait_ge(s.prep_psum.sem, s.prep_psum.at(0, 5))
                    for j in range(QCH):
                        v.tensor_copy(w_dT[0:QW[j], j, :], ps[j // 2][0:QW[j], (j % 2) * D:(j % 2 + 1) * D])
                    v.wait_ge(s.prep_psum.sem, s.prep_psum.at(0, 6))
                    v.tensor_copy(d_row[:], ps[4][:, 0:D])
            s.prep_psum.base += 6
            s.prep_ready.base += 4

        def all_max(of):
            begin(1, s.max_ready, s.allreduce)
            with nc.Block() as block:
                @block.vector
                def _(v):
                    v.tensor_reduce(one[:], of, AX.X, ALU.max).then_inc(s.max_ready.sem, 1)

                @block.gpsimd
                def _(p):
                    p.wait_ge(s.max_ready.sem, s.max_ready.at(0))
                    p.partition_all_reduce(allmax[:], one[:], P, bass.bass_isa.ReduceOp.max).then_inc(s.allreduce.sem, 1)

        cs2 = sb("cs2", [P, BATCH, D])
        begin(2, s.c_ready, s.max_ready)
        with nc.Block() as block:
            @block.vector
            def _(v):
                with v.Fori(0, TILES) as it:
                    dve.begin(v)
                    for b in range(BATCH):
                        k = it + b * TILES
                        dve.link(v.tensor_scalar(cs2[:, b, :], tile_of(e.x, it, b), flat(e.mean_var[:, bass.ds(k, 1), 0:1]),
                                                 e.rstd[:, bass.ds(k, 1)], ALU.subtract, ALU.mult))
                        v.tensor_reduce(amax[:, bass.ds(k, 1)], cs2[:, b, :], AX.X, ALU.max, apply_absolute_value=True)
        all_max(amax[:])
        gsc = sb("gsc", [P, 2, QCH])
        with nc.Block() as block:
            @block.vector
            def _(v):
                dve.begin(v)
                v.wait_ge(s.allreduce.sem, s.allreduce.at(0))
                dve.link(v.tensor_scalar(xs[:, 0:1], allmax[:], sig[:, 0:1], None, ALU.mult))
                v.reciprocal(xs[:, 1:2], xs[:, 0:1])
                v.tensor_scalar(gsc[:], gu_scale[:], xs[:, 0:1], None, ALU.mult)
        end(1, s.max_ready, s.allreduce)

        q_tmp = sb("q_tmp2", [P, BATCH, QCH, P])
        xq = sb("xq", [P, BATCH, D], BF16)
        xqT = sb("xqT", [P, BATCH, DCH, P], BF16)
        gate = sb("q_gate", [P, QCH, BATCH * P])
        two = (s.c_ready, s.cT_psum, s.cT_ready)
        begin(2, *two)
        begin(QCH, s.hidden_psum, s.gate_done, s.hidden_ready)
        with nc.Block() as block:
            @block.tensor
            def _(pe):
                with pe.Fori(0, TILES) as it:
                    for b in range(BATCH):
                        pe.wait_ge(s.c_ready.sem, s.c_ready.at(it, b + 1))
                        pe.wait_ge(s.cT_ready.sem, s.cT_ready.before(it, b + 1))
                        for ch in range(DCH):
                            mm = pe.matmul(ps[b][:, ch * P:(ch + 1) * P], xq[:, b, ch * P:(ch + 1) * P], e.ident_bf[:],
                                           start=ch == 0, stop=True, skip_group_check=True)
                        mm.then_inc(s.cT_psum.sem, 1)
                    pe.wait_ge(s.cT_ready.sem, s.cT_ready.at(it, 2))
                    for j in range(QCH):
                        pe.wait_ge(s.hidden_ready.sem, s.hidden_ready.before(it, j + 1))
                        for n in range(2):
                            for ch in range(DCH):
                                mm = pe.matmul(ps[2 + j][0:QW[j], n * 2 * P:(n + 1) * 2 * P], w_guT[:, ch, n, j * P:j * P + QW[j]],
                                               xqT[:, :, ch, :], start=(n, ch) == (0, 0), stop=ch == DCH - 1, skip_group_check=True)
                        mm.then_inc(s.hidden_psum.sem, 1)

            @block.scalar
            def _(act_):
                with act_.Fori(0, TILES) as it:
                    for b in range(BATCH):
                        act_.wait_ge(s.cT_psum.sem, s.cT_psum.at(it, b + 1))
                        act_.wait_ge(s.hidden_psum.sem, s.hidden_psum.before(it, QCH))
                        nc.scalar.copy(flat(xqT[:, b, :, :]), ps[b][:, 0:D]).then_inc(s.cT_ready.sem, 1)
                    for j in range(QCH):
                        act_.wait_ge(s.hidden_psum.sem, s.hidden_psum.at(it, j + 1))
                        act_.wait_ge(s.hidden_ready.sem, s.hidden_ready.before(it, j + 1))
                        nc.scalar.activation(gate[0:QW[j], j, :], ps[2 + j][0:QW[j], 0:2 * P], ACT.Silu, scale=gsc[0:QW[j], 0, j:j + 1])\
                          .then_inc(s.gate_done.sem, 1)

            @block.vector
            def _(v):
                with v.Fori(0, TILES) as it:
                    dve.begin(v)
                    for b in range(BATCH):
                        k = it + b * TILES
                        dve.link(v.tensor_scalar(e.cs[:, b, :], tile_of(e.x, it, b), flat(e.mean_var[:, bass.ds(k, 1), 0:1]),
                                                 e.rstd[:, bass.ds(k, 1)], ALU.subtract, ALU.mult))
                        v.wait_ge(s.cT_psum.sem, s.cT_psum.before(it, b + 1))
                        quantise(v, dve, xq[:, b, :], e.cs[:, b, :], e.cs[:, b, :], xs[:, 1:2]).then_inc(s.c_ready.sem, 1)
                    for j in range(QCH):
                        r = slice(0, QW[j])
                        to = h[r, j, :, :].rearrange("p (b t) n -> p b t n", b=BATCH)[:, :, bass.ds(it, 1), :].rearrange("p b t n -> p b (t n)")
                        v.wait_ge(s.gate_done.sem, s.gate_done.at(it, j + 1))
                        dve.link(v.scalar_tensor_tensor(to, ps[2 + j][r, 2 * P:4 * P].rearrange("p (b n) -> p b n", b=BATCH), gsc[r, 1, j:j + 1],
                                                        gate[r, j, :].rearrange("p (b n) -> p b n", b=BATCH), ALU.mult, ALU.mult))
                        v.tensor_reduce(flat(hmax[r, bass.ds(it, 1), j:j + 1]), to, AX.XY, ALU.max, apply_absolute_value=True)\
                         .then_inc(s.hidden_ready.sem, 1)
        end(TILES, *two, s.hidden_psum, s.gate_done, s.hidden_ready)

        all_max(flat(hmax[:]))
        with nc.Block() as block:
            @block.vector
            def _(v):
                dve.begin(v)
                v.wait_ge(s.allreduce.sem, s.allreduce.at(0))
                dve.link(v.tensor_scalar(xs[:, 0:1], allmax[:], sig[:, 1:2], None, ALU.mult))
                v.reciprocal(xs[:, 1:2], xs[:, 0:1])
                v.tensor_scalar(d_row[:], d_row[:], xs[:, 0:1], None, ALU.mult)
        end(1, s.max_ready, s.allreduce)

        hq = sb("hq", [P, BATCH, QCH, P], BF16)
        out = sb("q_out", [P, BATCH, D])
        two = (s.hidden_ready, s.out_psum, s.ln_var, s.ln_rstd)
        begin(2, *two)
        with nc.Block() as block:
            @block.tensor
            def _(pe):
                with pe.Fori(0, TILES) as it:
                    for b in range(BATCH):
                        pe.wait_ge(s.hidden_ready.sem, s.hidden_ready.at(it, b + 1))
                        pe.wait_ge(s.ln_var.sem, s.ln_var.before(it, b + 1))
                        for j in range(QCH):
                            mm = pe.matmul(ps[b][:, 0:D], hq[0:QW[j], b, j, :], w_dT[0:QW[j], j, :], start=j == 0, stop=j == QCH - 1)
                        mm.then_inc(s.out_psum.sem, 1)

            @block.vector
            def _(v):
                with v.Fori(0, TILES) as it:
                    dve.begin(v)
                    for b in range(BATCH):
                        k = it + b * TILES
                        v.wait_ge(s.out_psum.sem, s.out_psum.before(it, b + 1))
                        full = slice(0, QCH - 1)
                        dve.link(quantise(v, dve, hq[:, b, full, :], q_tmp[:, b, full, :],
                                          h[:, full, bass.ds(k, 1), :].rearrange("p j t n -> p j (t n)"), xs[:, 1:2]))
                        r = slice(0, QW[-1])
                        quantise(v, dve, hq[r, b, QCH - 1, :], q_tmp[r, b, QCH - 1, :], flat(h[r, QCH - 1, bass.ds(k, 1), :]), xs[r, 1:2])\
                            .then_inc(s.hidden_ready.sem, 1)
                    for b in range(BATCH):
                        v.wait_ge(s.out_psum.sem, s.out_psum.at(it, b + 1))
                        dve.link(v.tensor_tensor(out[:, b, :], ps[b][:, 0:D], d_row[:], ALU.mult))
                        add_to_x(e, v, it, b, out[:, b, :])

            @block.gpsimd
            def _(p):
                with p.Fori(0, TILES) as it:
                    for b in range(BATCH):
                        stats_pool(e, p, it, b)
        end(TILES, *two)


def l3_ffn(e):
    nc = e.nc
    with ExitStack() as ctx:
        sb = memory(e, ctx, "l3_ffn")
        gate_w = sb("gate_w", [P, DCH, EXPERTS])
        w1 = sb("w1", [P, EXPERTS, DCH, MOE_HID])
        w2 = sb("w2", [P, EXPERTS, MCH, D])
        with nc.Block() as block:
            @block.sync
            def _(sp):
                load(e, sp, (w1, "L3_w1"), (w2, "L3_w2"))
        routed = route(e, ctx, "l3_route", (gate_w, "L3_gate"), False)
        experts(e, ctx, "l3_experts", routed, KEEPING_TILES, False, lambda x, ch: w1[:, bass.ds(x, 1), ch, :].rearrange("p x n -> p (x n)"),
                lambda x, f: w2[:, bass.ds(x, 1), f, :].rearrange("p x n -> p (x n)"), False)


def finish(e):
    with e.nc.Block() as block:
        @block.sync
        def _(sp):
            sp.dma_start(e.out, e.x[:]).then_inc(e.stored, 16)
            sp.wait_ge(e.stored, 16)


def rotary():
    one = np.float32
    half = np.arange(0, DH, 2, dtype=one)
    t = np.arange(SEQ, dtype=one)
    freqs = t[:, None] * (one(1.0) / one(10000.0) ** (half / one(DH)))[None]
    base = (half + one(0.4 * DH)) / one(1.4 * DH)
    scale = base[None] ** ((t - SEQ // 2) / one(P // 2))[:, None]
    cos, sin = np.cos(freqs), np.sin(freqs)
    both = lambda w: np.stack([w * scale, w / scale], 1)
    c, n = both(cos), both(sin)
    parts = np.stack([np.concatenate([c, c], -1), np.concatenate([-n, n], -1)])
    return parts.reshape(2, TILES, P, 2, DH).transpose(2, 0, 1, 3, 4).astype(one)


def laid_out(inp):
    f = {k: np.asarray(v) for k, v in inp.items()}
    rows = lambda w: w.reshape(-1, P, w.shape[-1]).transpose(1, 0, 2)
    ctx = f["ctx_1024"]
    a = {}
    a["x"] = f["x"].reshape(ALL_TILES, P, D).transpose(1, 0, 2)
    a["ident"] = np.eye(P, dtype=np.float32)
    a["ctxT"] = ctx.transpose(2, 0, 1).reshape(DCH, P, BATCH, CTX).transpose(1, 0, 2, 3)
    a["ctx_tok"] = np.concatenate([ctx, ctx], 1).transpose(1, 0, 2)
    a["L0_W_l"] = rows(f["L0_xattn_W_l"].T)
    a["L0_w3"] = rows(np.stack([f["L0_xattn_w_cq"], f["L0_xattn_w_c"], f["L0_xattn_w_q"]], 1))
    a["L0_b3"] = np.tile(np.stack([f["L0_xattn_b_cq"], f["L0_xattn_b_c"], f["L0_xattn_b_q"]])[None], (P, 1))
    a["L0_b_l"] = f["L0_xattn_b_l"][None]
    every = lambda w: np.tile(w[None], (P,) + (1,) * w.ndim)
    per_layer = lambda w: np.stack([rows(w[l]) for l in range(LAYERS)], 1)
    padded = lambda w: np.pad(w, [(0, FCH * P - HID)] + [(0, 0)] * (w.ndim - 1))
    swap = lambda w: np.concatenate([w[..., DH // 2:], w[..., :DH // 2]], -1)
    a["L0_wqkv"] = per_layer(f["L0_ffn_wqkv"])
    a["L0_wo"] = per_layer(f["L0_ffn_wo"])
    a["L0_w1"] = per_layer(f["L0_ffn_w1"]).transpose(1, 0, 2, 3)
    a["L0_w2"] = per_layer(np.stack([padded(w) for w in f["L0_ffn_w2"]]))
    columns = lambda l: np.concatenate([f["L0_ffn_ln_g"][l], f["L0_ffn_ln_b"][l], padded(f["L0_ffn_b1"][l, :HID]),
                                        padded(f["L0_ffn_b1"][l, HID:])]).reshape(-1, P).T
    a["L0_cols"] = np.stack([columns(l) for l in range(LAYERS)], 1)
    a["L0_b2"] = every(f["L0_ffn_b2"])
    scales = np.stack([f["L0_ffn_q_scale"], f["L0_ffn_k_scale"]], 1)
    a["L0_qk_scale"] = every(np.stack([scales, swap(scales)], 1))
    a["rotary"] = rotary()
    a["shift"] = np.stack([np.eye(P, k=1), np.eye(P, k=1 - P)], 1).astype(np.float32)
    q, k = np.arange(P)[:, None], np.arange(P)[None]
    own, before, none = np.where(k <= q, 0, MASKED), np.where(k >= q, 0, MASKED), np.full((P, P), MASKED)
    a["mask"] = np.stack([np.concatenate(m, 1) for m in ((own, none), (own, before), (before, own))], 1).astype(np.float32)
    a["ctxT2"] = np.stack([a["ctxT"], a["ctxT"]], 3)
    a["causal"] = np.where(np.arange(CTX)[None] <= np.arange(P)[:, None], 0, MASKED).astype(np.float32)
    a["tri"] = np.triu(np.ones((P, P), np.float32))
    a["expert_constants"] = every(expert_constants()[0].astype(np.float32))
    a["p_col"] = np.arange(P, dtype=np.float32)[:, None]
    a["expert_number"] = every(np.arange(EXPERTS, dtype=np.float32))
    a["L1_router"] = rows(f["L1_ffn_w_router"].T)
    a["L1_gate"] = rows(f["L1_ffn_w_gate"].T)
    a["L1_down"] = f["L1_ffn_w_down"].transpose(2, 0, 1).reshape(MCH, P, EXPERTS, D).transpose(1, 0, 2, 3)
    for n, (q, k, v, o) in (("L2_", [f["L2_xattn_w_" + c] for c in "qkvo"]), ("L3_", [f["L3_xattn_W_" + c] for c in "qkvo"])):
        for c, w in zip("qkvo", (q, k, v, o)):
            a[n + "w" + c] = rows(w.T)
    a["own_head"] = (np.arange(P)[:, None] // XD == np.arange(XH // 2)[None]).astype(np.float32)
    a["L2_bq"] = f["L2_xattn_b_q"].reshape(DCH, P).T
    a["L2_bk"] = f["L2_xattn_b_k"].reshape(DCH, P).T
    a["L2_bv"] = every(f["L2_xattn_b_v"])
    a["L2_bo"] = every(f["L2_xattn_b_o"])
    to_chunks = lambda w: np.pad(w, [(0, QCH * P - QI), (0, 0)]).reshape(QCH, P, D).transpose(1, 0, 2)
    a["L2_gu"] = np.stack([to_chunks(f["L2_ffn_w_gate"]), to_chunks(f["L2_ffn_w_up"])], 1)
    a["L2_d"] = rows(f["L2_ffn_w_down"])
    a["L2_clips"] = every(np.concatenate([f["L2_ffn_clip_x"], f["L2_ffn_clip_down"]]))
    ratio = 2.0 ** (-8.0 / XH)
    slopes = np.asarray([ratio ** i for i in range(1, XH + 1)], np.float32) * np.float32(XD ** 0.5)
    a["slopes"] = np.tile(slopes, BATCH)[:, None]
    kp, qp = f["itok_BxS2_1_8191"], f["itok_BxS_8_8191"].reshape(ALL_TILES, P)
    a["key_pos"], a["query_pos"] = np.repeat(kp, XH, 0), qp
    a["mask_if1"] = f["mask_BxSxS2_if1"].reshape(ALL_TILES, P, CTX).transpose(1, 0, 2)
    a["L3_gate"] = rows(f["L3_ffn_gate_w"])
    a["L3_w1"] = f["L3_ffn_w1"].reshape(EXPERTS, DCH, P, MOE_HID).transpose(2, 0, 1, 3)
    a["L3_w2"] = f["L3_ffn_w2"].reshape(EXPERTS, MCH, P, D).transpose(2, 0, 1, 3)
    return {k: np.ascontiguousarray(v) for k, v in a.items()}


def kernel(**inputs):
    import concourse.bacc as bacc
    from concourse.bass_utils import run_bass_kernel_spmd as run

    arrays = laid_out(inputs)
    nc = bacc.Bacc("TRN2", target_bir_lowering=False, num_devices=1)
    dram = {k: nc.dram_tensor(f"in_{k}", v.shape, mybir.dt.from_np(v.dtype), kind="ExternalInput").ap()
            for k, v in arrays.items()}
    out = nc.dram_tensor("out_x", (P, ALL_TILES, D), F32, kind="ExternalOutput").ap()
    build(nc, dram, out)
    r = run(nc, [{f"in_{k}": v for k, v in arrays.items()}], core_ids=[0])
    return r.results[0]["out_x"].transpose(1, 0, 2).reshape(BATCH, SEQ, D)
```

```python
from contextlib import ExitStack

import numpy as np

import concourse.bass as bass
from concourse import mybir

ALU = mybir.AluOpType
ACT = mybir.ActivationFunctionType
AX = mybir.AxisListType
F32 = mybir.dt.float32
BF16 = mybir.dt.bfloat16
I32 = mybir.dt.int32
U32 = mybir.dt.uint32

P = 128
BATCH, SEQ, D = 2, 1024, 256
CTX = 64
DCH = D // P
TILES = SEQ // P
ALL_TILES = BATCH * TILES
EPS = 1e-5
MASKED = -1e30
LIFT = 16


class Signal:

    def __init__(self, sem):
        self.sem, self.base, self.per = sem, LIFT, 0

    def each(self, per):
        assert per <= LIFT
        self.per = per

    def at(self, turn, k=1):
        return turn * self.per + (self.base + k)

    def before(self, turn, k=1):
        return turn * self.per + (self.base + k - self.per)

    def close(self, turns=1):
        self.base += self.per * turns


class Chain:

    def __init__(self, sem):
        self.sem = sem

    def begin(self, engine):
        self.engine, self.n = engine, 0
        engine.sem_clear(self.sem)

    def link(self, instruction):
        self.n += 1
        instruction.then_inc(self.sem, 1)
        self.engine.wait_ge(self.sem, self.n)


def memory(e, ctx, stage):
    return lambda name, shape, dt=F32: ctx.enter_context(e.nc.sbuf_tensor(f"{stage}_{name}", shape, dt))


def flat(ap):
    return ap.rearrange("p a b -> p (a b)")


def tile_of(buf, it, b):
    return flat(buf[:, bass.ds(it + b * TILES, 1), :])


class Signals:

    def __init__(self, new):
        self.ln_var = new("ln_var")
        self.ln_rstd = new("ln_rstd")
        self.cT_psum = new("cT_psum")
        self.c_ready = new("c_ready")
        self.cT_ready = new("cT_ready")
        self.prep_psum = new("prep_psum")
        self.c_kept = new("c_kept")
        self.scores_psum = new("scores_psum")
        self.max_ready = new("max_ready")
        self.probs_ready = new("probs_ready")
        self.probsT_psum = new("probsT_psum")
        self.probsT_ready = new("probsT_ready")
        self.mix_psum = new("mix_psum")
        self.mix_ready = new("mix_ready")
        self.mixT_psum = new("mixT_psum")
        self.mixT_ready = new("mixT_ready")
        self.out_psum = new("out_psum")
        self.x_done = new("x_done")
        self.allreduce = new("allreduce")
        self.sums_psum = new("sums_psum")
        self.ys_ready = new("ys_ready")
        self.yT_psum = new("yT_psum")
        self.hT_ready = new("hT_ready")
        self.sq_ready = new("sq_ready")
        self.v_ready = new("v_ready")
        self.ss_ready = new("ss_ready")
        self.norm_ready = new("norm_ready")
        self.q_norm_ready = new("q_norm_ready")
        self.rot_ready = new("rot_ready")
        self.qkT_psum = new("qkT_psum")
        self.qT_ready = new("qT_ready")
        self.kT_ready = new("kT_ready")
        self.mixed_psum = new("mixed_psum")
        self.y1_ready = new("y1_ready")
        self.shift_psum = new("shift_psum")
        self.shift_var = new("shift_var")
        self.shift_rstd = new("shift_rstd")
        self.h2_ready = new("h2_ready")
        self.h2T_psum = new("h2T_psum")
        self.h2T_ready = new("h2T_ready")
        self.y1b_ready = new("y1b_ready")
        self.ffn_out = new("ffn_out")
        self.y_done = new("y_done")
        self.bias_ready = new("bias_ready")
        self.pT_act = new("pT_act")
        self.pT_dve = new("pT_dve")
        self.hid_psum = new("hid_psum")
        self.gate_ready = new("gate_ready")
        self.ff_ready = new("ff_ready")
        self.mask_ready = new("mask_ready")
        self.logits_psum = new("logits_psum")
        self.routed = new("routed")
        self.placed = new("placed")
        self.row_copied = new("row_copied")
        self.rowT_psum = new("rowT_psum")
        self.rowT_ready = new("rowT_ready")
        self.up_psum = new("up_psum")
        self.upT_ready = new("upT_ready")
        self.down_psum = new("down_psum")
        self.y_copied = new("y_copied")
        self.y_stored0 = new("y_stored0")
        self.y_stored1 = new("y_stored1")
        self.y_stored2 = new("y_stored2")
        self.prep_ready = new("prep_ready")
        self.hidden_psum = new("hidden_psum")
        self.gate_done = new("gate_done")
        self.hidden_ready = new("hidden_ready")
        self.bias_added = new("bias_added")
        self.ones_set = new("ones_set")
        self.q_psum = new("q_psum")
        self.q_ready = new("q_ready")
        self.qk_psum = new("qk_psum")
        self.v_psum = new("v_psum")
        self.cT_kept = new("cT_kept")
        self.clipped = new("clipped")
        self.h_max = new("h_max")
        self.inv_ready = new("inv_ready")
        self.scaled = new("scaled")
        self.up_w_ready = new("up_w_ready")


class Env:

    def __init__(self, nc, dram, out):
        self.nc, self.dram, self.out = nc, dram, out


def build(nc, dram, out):
    with ExitStack() as ctx:
        def sem(name):
            return ctx.enter_context(nc.semaphore(name))

        e = Env(nc, dram, out)
        sb = lambda name, shape, dt=F32: ctx.enter_context(nc.sbuf_tensor(name, shape, dt))
        e.psum = ctx.enter_context(nc.psum_tensor("banks", [P, 8, 512], F32))
        e.ps = [e.psum[:, i, :] for i in range(8)]
        e.x = sb("x_res", [P, ALL_TILES, D])
        e.cs = sb("c_tile", [P, BATCH, D])
        e.cT = sb("cT", [P, BATCH, DCH, P])
        e.ident = sb("ident", [P, P])
        e.ident_bf = sb("ident_bf", [P, P], BF16)
        e.ones = sb("ones", [P, P])
        e.neg_half = sb("neg_half", [P, 16])
        e.ctxT = sb("ctxT", [P, DCH, BATCH, CTX])
        e.ctxT2 = sb("ctxT2", [P, DCH, BATCH, 2, CTX])
        e.ctx_tok = sb("ctx_tok", [P, BATCH, D])
        e.bn = sb("bn", [P, BATCH, 6])
        e.mv = sb("mv", [P, BATCH, 2])
        e.zero_eps = sb("zero_eps", [P, 2])
        e.mean_var = sb("mean_var", [P, ALL_TILES, 2])
        e.rstd = sb("rstd", [P, ALL_TILES])
        e.signals = []

        def new(name):
            e.signals.append(Signal(sem(name)))
            return e.signals[-1]

        e.s, e.dma_sem = Signals(new), sem
        e.chain = {n: Chain(sem(f"{n}_order")) for n in ("dve", "act", "pool", "pe")}
        e.loaded = sem("loaded")
        e.stored = sem("stored")
        e.loads = 0

        prologue(e)
        with ExitStack() as early:
            ffn = L0Ffn(e, early)
            l0_xattn(e, ffn)
            l0_ffn(e, ffn)
        with ExitStack() as later:
            x2 = Xattn(e, later, "L2_", True)
            with ExitStack() as early:
                moe = l1_ffn_ahead(e, early)
                l1_xattn(e, moe, x2)
                l1_ffn(e, moe)
            moe = l3_ffn_ahead(e, later)
            with ExitStack() as early:
                x3 = Xattn(e, early, "L3_", False, x2)
                with ExitStack() as earlier:
                    ffn = L2Ffn(e, earlier)
                    l2_xattn(e, x2, ffn, moe)
                    l2_ffn(e, ffn, x3)
                l3_xattn(e, x3)
            l3_ffn(e, moe)
        finish(e)


def begin(per, *signals):
    for n in signals:
        n.each(per)


def end(turns, *signals):
    for n in signals:
        n.close(turns)


def stats_dve(e, v, it, b):
    s, dve, row = e.s, e.chain["dve"], tile_of(e.x, it, b)
    dve.link(v.bn_stats(e.bn[:, b, :], row))
    dve.link(v.bn_aggr(e.mv[:, b, :], e.bn[:, b, :]))
    v.tensor_tensor(flat(e.mean_var[:, bass.ds(it + b * TILES, 1), :]), e.mv[:, b, :], e.zero_eps[:], ALU.add)\
     .then_inc(s.ln_var.sem, 1)


def stats_pool(e, p, it, b):
    s, k = e.s, it + b * TILES
    p.wait_ge(s.ln_var.sem, s.ln_var.at(it, b + 1))
    p.tensor_tensor(e.rstd[:, bass.ds(k, 1)], flat(e.mean_var[:, bass.ds(k, 1), 1:2]), e.neg_half[:, 0:1], ALU.pow)\
     .then_inc(s.ln_rstd.sem, 1)


def normalise(e, v, it, b):
    s, k = e.s, it + b * TILES
    v.wait_ge(s.cT_psum.sem, s.cT_psum.before(it, b + 1))
    v.tensor_scalar(e.cs[:, b, :], tile_of(e.x, it, b), flat(e.mean_var[:, bass.ds(k, 1), 0:1]), e.rstd[:, bass.ds(k, 1)],
                    ALU.subtract, ALU.mult).then_inc(s.c_ready.sem, 1)


def transpose_c(e, pe, it, b, bank):
    s = e.s
    pe.wait_ge(s.c_ready.sem, s.c_ready.at(it, b + 1))
    pe.wait_ge(s.cT_ready.sem, s.cT_ready.before(it, b + 1))
    for ch in range(DCH):
        mm = pe.transpose(e.ps[bank][:, ch * P:(ch + 1) * P], e.cs[:, b, ch * P:(ch + 1) * P], e.ident[:])
    mm.then_inc(s.cT_psum.sem, 1)


def copy_cT(e, act, it, b, bank, used):
    s = e.s
    act.wait_ge(s.cT_psum.sem, s.cT_psum.at(it, b + 1))
    act.wait_ge(used.sem, used.before(it, b + 1))
    e.nc.scalar.copy(flat(e.cT[:, b, :, :]), e.ps[bank][:, 0:D]).then_inc(s.cT_ready.sem, 1)


class Tile:

    def __init__(self, it, b):
        self.it, self.b, self.k = it, b, b + 1


def pipeline(engine, order, turns, width, item, first, step, cuts=None, wait=None, depth=3):
    ahead = -(-(depth - 1) // width)

    def turn(at, left):
        order.begin(engine)
        for n in range(width):
            step(item(at, n), *(item(at + (n + m) // width, (n + m) % width) if (n + m) // width <= left else None
                                for m in range(1, depth)))

    cuts = cuts or [0, turns - ahead]
    for n, (start, stop) in enumerate(zip(cuts[:-1], cuts[1:])):
        if wait:
            wait(n)
        if n == 0:
            with engine.Fori(0, 1) as at:
                order.begin(engine)
                first(*(item(at + m // width, m % width) for m in range(depth - 1)))
        with engine.Fori(start, stop) as at:
            turn(at, ahead)
    for left in reversed(range(ahead)):
        with engine.Fori(turns - 1 - left, turns - left) as at:
            turn(at, left)


def turns_of_tiles(engine, order, first, step):
    pipeline(engine, order, TILES, 1, lambda it, n: it, first, step)


def tiles(engine, order, first, step, depth=3):
    pipeline(engine, order, TILES, BATCH, Tile, first, step, depth=depth)


class Ahead:

    def __init__(self, e, stage, given):
        self.given, self.loaded, self.all = given, e.dma_sem(f"{stage}_loaded"), 16 * len(given)


def load_ahead(e, sp, *stages):
    for ahead in stages:
        for to, of in ahead.given:
            sp.dma_start(to[:], e.dram[of]).then_inc(ahead.loaded, 16)


class L0Ffn(Ahead):

    def __init__(self, e, ctx):
        sb = memory(e, ctx, "l0_ffn_in")
        self.wqkv = sb("wqkv", [P, LAYERS, DCH, 3 * INNER])
        self.wo = sb("wo", [P, LAYERS, INNER // P, D])
        self.w2 = sb("w2", [P, LAYERS, FCH, D])
        self.all_cols = sb("ffn_cols", [P, LAYERS, 2 * DCH + 2 * FCH])
        self.all_b2 = sb("b2", [P, LAYERS, D])
        self.qk_scale = sb("qk_scale", [P, LAYERS, 2, 2, DH])
        self.shift = sb("shift", [P, 2, P])
        self.mask32 = sb("mask32", [P, 3, 2 * P])
        super().__init__(e, "l0_ffn", ((self.all_cols, "L0_cols"), (self.all_b2, "L0_b2"), (self.qk_scale, "L0_qk_scale"),
                         (self.shift, "shift"), (self.mask32, "mask"), (self.wqkv, "L0_wqkv"), (self.wo, "L0_wo"), (self.w2, "L0_w2")))


def prologue(e):
    nc, s, d = e.nc, e.s, e.dram
    for n in (s.ln_var, s.ln_rstd):
        n.each(2)
    with nc.Block() as block:
        @block.sync
        def _(sp):
            for one in e.signals:
                sp.sem_inc(one.sem, LIFT)
    with nc.Block() as block:
        @block.sync
        def _(sp):
            for to, of in ((e.x, "x"), (e.ident, "ident"), (e.ctxT, "ctxT"), (e.ctxT2, "ctxT2"), (e.ctx_tok, "ctx_tok")):
                sp.dma_start(to[:], d[of]).then_inc(e.loaded, 16)
                e.loads += 16

        @block.gpsimd
        def _(p):
            chain = e.chain["pool"]
            chain.begin(p)
            chain.link(p.memset(e.neg_half[:], -0.5))
            p.memset(e.ones[:], 1.0)
            with p.Fori(0, TILES) as it:
                for b in range(BATCH):
                    stats_pool(e, p, it, b)

        @block.vector
        def _(v):
            dve = e.chain["dve"]
            dve.begin(v)
            v.memset(e.zero_eps[:, 0:1], 0.0)
            dve.link(v.memset(e.zero_eps[:, 1:2], EPS))
            v.wait_ge(e.loaded, e.loads)
            v.tensor_copy(e.ident_bf[:], e.ident[:])
            with v.Fori(0, TILES) as it:
                e.chain["dve"].begin(v)
                for b in range(BATCH):
                    stats_dve(e, v, it, b)
    for n in (s.ln_var, s.ln_rstd):
        n.close(TILES)


def l0_xattn(e, ffn):
    nc, s, d, ps = e.nc, e.s, e.dram, e.ps
    with ExitStack() as ctx:
        sb = memory(e, ctx, "l0_xattn")
        w_l = sb("w_l", [P, 8, D])
        wcol = sb("wcol", [P, DCH, 3])
        b3 = sb("b3", [P, 3])
        b_l = sb("b_l", [1, D])
        qcat = sb("qcat", [P, DCH, BATCH, CTX])
        b_sum = sb("b_sum", [1, 1])
        q_bias = sb("q_bias", [1, BATCH * CTX])
        c_all = sb("c_all", [P, ALL_TILES, D])
        cT_all = sb("cT_all", [P, ALL_TILES, D])
        nmax = sb("nmax", [P, ALL_TILES])
        a = sb("a", [P, 2, CTX])
        a_sum = sb("a_sum", [P, 2])
        a_rec = sb("a_rec", [P, 2])
        aT = sb("aT", [P, P])
        uv = sb("uv", [P, 2, 2, D])
        uvT = sb("uvT", [P, 2, 4, P])
        top = sb("top", [P, BATCH])
        gtop = sb("gtop", [P, BATCH])
        ngtop = sb("ngtop", [P, BATCH])
        b_att = sb("b_att", [P, ALL_TILES])
        b_att_sum = sb("b_att_sum", [P, BATCH])
        rden = sb("rden", [P, BATCH])
        q2c = sb("q2c", [P, BATCH, DCH])
        w_c = sb("w_c", [P, BATCH, DCH, D])
        dve, act, pool = (e.chain[n] for n in ("dve", "act", "pool"))

        with nc.Block() as block:
            @block.sync
            def _(sp):
                for to, of in ((w_l, "L0_W_l"), (wcol, "L0_w3"), (b3, "L0_b3"), (b_l, "L0_b_l")):
                    sp.dma_start(to[:], d[of]).then_inc(e.loaded, 16)
                    e.loads += 16
                load_ahead(e, sp, ffn)

            s.prep_psum.each(1)

            @block.tensor
            def _(pe):
                pe.wait_ge(e.loaded, e.loads)
                for ch in range(DCH):
                    mm = pe.matmul(ps[0][0:1, 0:BATCH * CTX], wcol[:, ch, 2:3], e.ctxT[:, ch, :, :],
                                   start=ch == 0, stop=ch == DCH - 1)
                mm.then_inc(s.prep_psum.sem, 1)

            @block.vector
            def _(v):
                v.wait_ge(e.loaded, e.loads)
                for ch in range(DCH):
                    v.tensor_scalar(qcat[:, ch, :, :], e.ctxT[:, ch, :, :], wcol[:, ch, 0:1],
                                    wcol[:, ch, 1:2], ALU.mult, ALU.add)
                dve.begin(v)
                dve.link(v.tensor_reduce(b_sum[:], b3[0:1, :], AX.X, ALU.add))
                v.wait_ge(s.prep_psum.sem, s.prep_psum.at(0))
                v.tensor_scalar(q_bias[:], ps[0][0:1, 0:BATCH * CTX], b_sum[0:1, 0:1], None, ALU.add)
        s.prep_psum.close()

        two = (s.c_ready, s.c_kept, s.cT_kept, s.cT_psum, s.cT_ready, s.scores_psum, s.max_ready, s.probs_ready, s.mix_psum, s.mix_ready,
               s.mixT_psum, s.mixT_ready, s.out_psum, s.x_done)
        one = (s.probsT_psum, s.probsT_ready)
        begin(2, *two)
        begin(1, *one)
        with nc.Block() as block:
            @block.tensor
            def _(pe):
                def transposes(it):
                    for b in range(BATCH):
                        transpose_c(e, pe, it, b, b)

                def scores(it):
                    for b in range(BATCH):
                        pe.wait_ge(s.cT_ready.sem, s.cT_ready.at(it, b + 1))
                        pe.wait_ge(s.probs_ready.sem, s.probs_ready.before(it, b + 1))
                        for ch in range(DCH):
                            pe.matmul(ps[2 + b][:, 0:CTX], e.cT[:, b, ch, :], qcat[:, ch, b, :], start=ch == 0, stop=False)
                        pe.matmul(ps[2 + b][:, 0:CTX], e.ones[0:1, :], q_bias[0:1, b * CTX:(b + 1) * CTX],
                                  start=False, stop=True).then_inc(s.scores_psum.sem, 1)

                def probs_transposed(it):
                    pe.wait_ge(s.probs_ready.sem, s.probs_ready.at(it, 2))
                    pe.wait_ge(s.mixT_ready.sem, s.mixT_ready.before(it, 1))
                    pe.transpose(ps[4][:, 0:P], flat(a[:]), e.ident[:]).then_inc(s.probsT_psum.sem, 1)

                def mix(it):
                    pe.wait_ge(s.probsT_ready.sem, s.probsT_ready.at(it))
                    for b in range(BATCH):
                        own = slice(b * CTX, (b + 1) * CTX)
                        pe.wait_ge(s.x_done.sem, s.x_done.before(it, b + 1))
                        pe.matmul(ps[6 + b][:, 0:D], aT[own, :], e.ctx_tok[own, b, :], start=True, stop=True)\
                          .then_inc(s.mix_psum.sem, 1)

                def mix_transposed(it):
                    for b in range(BATCH):
                        pe.wait_ge(s.mix_ready.sem, s.mix_ready.at(it, b + 1))
                        pe.wait_ge(s.mixT_ready.sem, s.mixT_ready.before(it, b + 1))
                        for k in range(4):
                            mm = pe.transpose(ps[4 + b][:, k * P:(k + 1) * P],
                                              uv[:, b, k // 2, (k % 2) * P:(k % 2 + 1) * P], e.ident[:])
                        mm.then_inc(s.mixT_psum.sem, 1)

                def project(it):
                    for b in range(BATCH):
                        pe.wait_ge(s.mixT_ready.sem, s.mixT_ready.at(it, b + 1))
                        for k in range(4):
                            pe.matmul(ps[6 + b][:, 0:D], uvT[:, b, k, :], w_l[:, 2 + k, :], start=k == 0, stop=False)
                        pe.matmul(ps[6 + b][:, 0:D], e.ones[0:1, :], b_l[0:1, :], start=False, stop=True)\
                          .then_inc(s.out_psum.sem, 1)

                def first(new, after):
                    transposes(new)
                    scores(new)
                    transposes(after)

                def step(now, new, after):
                    probs_transposed(now)
                    if new is not None:
                        scores(new)
                    mix(now)
                    if after is not None:
                        transposes(after)
                    mix_transposed(now)
                    project(now)

                turns_of_tiles(pe, e.chain["pe"], first, step)

            @block.scalar
            def _(act_):
                def copy(it):
                    for b in range(BATCH):
                        act_.wait_ge(s.cT_kept.sem, s.cT_kept.before(it, b + 1))
                        copy_cT(e, act_, it, b, b, s.scores_psum)

                def exp(it):
                    for b in range(BATCH):
                        act_.wait_ge(s.max_ready.sem, s.max_ready.at(it, b + 1))
                        act_.wait_ge(s.probsT_psum.sem, s.probsT_psum.before(it))
                        act_.wait_ge(s.mix_ready.sem, s.mix_ready.before(it, b + 1))
                        nc.scalar.activation(a[:, b, :], ps[2 + b][:, 0:CTX], ACT.Exp,
                                             bias=nmax[:, bass.ds(it + b * TILES, 1)],
                                             accum_out=a_sum[:, b:b + 1]).then_inc(s.probs_ready.sem, 1)

                def copy_aT(it):
                    act_.wait_ge(s.probsT_psum.sem, s.probsT_psum.at(it))
                    act_.wait_ge(s.mix_psum.sem, s.mix_psum.before(it, 2))
                    nc.scalar.copy(aT[:], ps[4][:, 0:P]).then_inc(s.probsT_ready.sem, 1)

                def copy_uvT(it):
                    for b in range(BATCH):
                        act_.wait_ge(s.mixT_psum.sem, s.mixT_psum.at(it, b + 1))
                        act_.wait_ge(s.out_psum.sem, s.out_psum.before(it, b + 1))
                        nc.scalar.copy(flat(uvT[:, b, :, :]), ps[4 + b][:, :]).then_inc(s.mixT_ready.sem, 1)

                def first(new, after):
                    copy(new)
                    exp(new)
                    copy(after)

                def step(now, new, after):
                    copy_aT(now)
                    if after is not None:
                        copy(after)
                    copy_uvT(now)
                    if new is not None:
                        exp(new)

                turns_of_tiles(act_, act, first, step)

            @block.vector
            def _(v):
                def normal(it):
                    for b in range(BATCH):
                        v.wait_ge(s.c_kept.sem, s.c_kept.before(it, b + 1))
                        normalise(e, v, it, b)

                def maxima(it):
                    for b in range(BATCH):
                        v.wait_ge(s.scores_psum.sem, s.scores_psum.at(it, b + 1))
                        v.tensor_reduce(nmax[:, bass.ds(it + b * TILES, 1)], ps[2 + b][:, 0:CTX], AX.X, ALU.max,
                                        negate=True).then_inc(s.max_ready.sem, 1)

                def mixed(it):
                    for b in range(BATCH):
                        v.wait_ge(s.probs_ready.sem, s.probs_ready.at(it, b + 1))
                        dve.link(v.reciprocal(a_rec[:, b:b + 1], a_sum[:, b:b + 1]))
                        v.wait_ge(s.mix_psum.sem, s.mix_psum.at(it, b + 1))
                        v.wait_ge(s.mixT_psum.sem, s.mixT_psum.before(it, b + 1))
                        dve.link(v.tensor_scalar(uv[:, b, 0, :], ps[6 + b][:, 0:D], a_rec[:, b:b + 1], None, ALU.mult))
                        v.wait_ge(s.c_kept.sem, s.c_kept.at(it, b + 1))
                        v.tensor_tensor(uv[:, b, 1, :], uv[:, b, 0, :], tile_of(c_all, it, b), ALU.mult)\
                         .then_inc(s.mix_ready.sem, 1)

                def add(it):
                    for b in range(BATCH):
                        v.wait_ge(s.out_psum.sem, s.out_psum.at(it, b + 1))
                        v.tensor_tensor(tile_of(e.x, it, b), ps[6 + b][:, 0:D], tile_of(e.x, it, b), ALU.add)\
                         .then_inc(s.x_done.sem, 1)

                def first(new, after):
                    normal(new)
                    normal(after)
                    maxima(new)

                def step(now, new, after):
                    if new is not None:
                        maxima(new)
                    mixed(now)
                    if after is not None:
                        normal(after)
                    add(now)

                turns_of_tiles(v, dve, first, step)

            @block.gpsimd
            def _(p):
                with p.Fori(0, TILES) as it:
                    for b in range(BATCH):
                        p.wait_ge(s.c_ready.sem, s.c_ready.at(it, b + 1))
                        p.tensor_copy(tile_of(c_all, it, b), e.cs[:, b, :]).then_inc(s.c_kept.sem, 1)
                    for b in range(BATCH):
                        p.wait_ge(s.cT_ready.sem, s.cT_ready.at(it, b + 1))
                        p.tensor_copy(tile_of(cT_all, it, b), flat(e.cT[:, b, :, :])).then_inc(s.cT_kept.sem, 1)
        end(TILES, *two, *one)

        s.max_ready.each(2)
        for n in (s.allreduce, s.probs_ready, s.sums_psum):
            n.each(1)
        with nc.Block() as block:
            @block.vector
            def _(v):
                dve.begin(v)
                v.tensor_reduce(top[:], nmax[:].rearrange("p (b t) -> p b t", b=BATCH), AX.X, ALU.min, negate=True)\
                 .then_inc(s.max_ready.sem, 1)
                v.wait_ge(s.allreduce.sem, s.allreduce.at(0))
                v.tensor_scalar(ngtop[:], gtop[:], -1.0, None, ALU.mult).then_inc(s.max_ready.sem, 1)
                v.wait_ge(s.sums_psum.sem, s.sums_psum.at(0))
                dve.link(v.reciprocal(rden[:], ps[0][:, 0:BATCH]))
                for b in range(BATCH):
                    dve.link(v.tensor_scalar(q2c[:, b, :], ps[1][:, b * DCH:(b + 1) * DCH], rden[:, b:b + 1], None, ALU.mult))
                for b in range(BATCH):
                    for ch in range(DCH):
                        v.scalar_tensor_tensor(w_c[:, b, ch, :], w_l[:, 6 + ch, :], q2c[:, b, ch:ch + 1],
                                               w_l[:, ch, :], ALU.mult, ALU.add)

            @block.gpsimd
            def _(p):
                p.wait_ge(s.max_ready.sem, s.max_ready.at(0, 1))
                p.partition_all_reduce(gtop[:], top[:], P, bass.bass_isa.ReduceOp.max).then_inc(s.allreduce.sem, 1)

            @block.scalar
            def _(act_):
                act_.wait_ge(s.max_ready.sem, s.max_ready.at(0, 2))
                for b in range(BATCH):
                    ex = nc.scalar.activation(b_att[:, b * TILES:(b + 1) * TILES], nmax[:, b * TILES:(b + 1) * TILES], ACT.Exp,
                                              bias=ngtop[:, b:b + 1], scale=-1.0, accum_out=b_att_sum[:, b:b + 1])
                ex.then_inc(s.probs_ready.sem, 1)

            @block.tensor
            def _(pe):
                pe.wait_ge(s.probs_ready.sem, s.probs_ready.at(0))
                pe.matmul(ps[0][:, 0:BATCH], e.ones[:], b_att_sum[:], start=True, stop=True)
                for b in range(BATCH):
                    for ch in range(DCH):
                        for t in range(TILES):
                            k = b * TILES + t
                            mm = pe.matmul(ps[1][:, b * DCH + ch:b * DCH + ch + 1], c_all[:, k, ch * P:(ch + 1) * P],
                                           b_att[:, k:k + 1], start=(b, ch, t) == (0, 0, 0), stop=t == TILES - 1,
                                           skip_group_check=True)
                mm.then_inc(s.sums_psum.sem, 1)
        for n in (s.allreduce, s.probs_ready, s.sums_psum, s.max_ready):
            n.close()

        two = (s.cT_ready, s.out_psum, s.ln_var, s.ln_rstd)
        begin(2, *two)
        with nc.Block() as block:
            @block.scalar
            def _(act_):
                with act_.Fori(0, TILES) as it:
                    for b in range(BATCH):
                        act_.wait_ge(s.out_psum.sem, s.out_psum.before(it, b + 1))
                        nc.scalar.copy(flat(e.cT[:, b, :, :]), tile_of(cT_all, it, b)).then_inc(s.cT_ready.sem, 1)

            @block.tensor
            def _(pe):
                with pe.Fori(0, TILES) as it:
                    for b in range(BATCH):
                        pe.wait_ge(s.cT_ready.sem, s.cT_ready.at(it, b + 1))
                        pe.wait_ge(s.ln_var.sem, s.ln_var.before(it, b + 1))
                        for ch in range(DCH):
                            mm = pe.matmul(ps[2 + b][:, 0:D], e.cT[:, b, ch, :], w_c[:, b, ch, :], start=ch == 0, stop=ch == DCH - 1)
                        mm.then_inc(s.out_psum.sem, 1)

            @block.vector
            def _(v):
                with v.Fori(0, TILES) as it:
                    dve.begin(v)
                    for b in range(BATCH):
                        v.wait_ge(s.out_psum.sem, s.out_psum.at(it, b + 1))
                        add_to_x(e, v, it, b, ps[2 + b][:, 0:D])

            @block.gpsimd
            def _(p):
                with p.Fori(0, TILES) as it:
                    for b in range(BATCH):
                        stats_pool(e, p, it, b)
        end(TILES, *two)


HEADS, DH = 8, 64
INNER = HEADS * DH
HID = int(D * 4 * 2 / 3)
FCH = -(-HID // P)
FPAIRS = FCH // 2
FW = [min(P, HID - j * P) for j in range(FCH)]
LAYERS = 2
HALF = TILES // 2


def l0_ffn(e, ffn):
    nc, s, d, ps = e.nc, e.s, e.dram, e.psum
    dve, act, pool = (e.chain[n] for n in ("dve", "act", "pool"))
    with ExitStack() as ctx:
        sb = memory(e, ctx, "l0_ffn")
        wqkv, wo, w2, all_cols, all_b2, qk_scale, shift, mask32 = (ffn.wqkv, ffn.wo, ffn.w2, ffn.all_cols, ffn.all_b2, ffn.qk_scale, ffn.shift, ffn.mask32)
        y = sb("y", [P, ALL_TILES, D])
        w1 = sb("w1", [P, DCH, 2 * HID])
        cols = sb("layer_cols", [P, 2 * DCH + 2 * FCH])
        b2 = sb("layer_b2", [P, D])
        rot = sb("rot", [P, 2, TILES, 2, DH])
        mask_even = sb("mask_even", [P, HALF, 2 * P], BF16)
        mask_odd = sb("mask_odd", [P, 2 * P], BF16)
        zero = sb("zero", [P, 1])
        unused = sb("unused", [P, 1])
        ys = sb("ys", [P, BATCH, D])
        hT = sb("hT", [P, BATCH, 2, DCH, P + 1])
        work = sb("work", [P, BATCH, HEADS, 2 * P])
        pT = sb("pT", [P, BATCH, 2 * HEADS, P])
        ss = sb("ss", [P, BATCH, 2 * HEADS])
        rn = sb("rn", [P, BATCH, 2 * HEADS])
        qT = sb("qT", [P, BATCH, 4, P])
        kT = sb("kT", [P, BATCH, 4, 2, 2, P])
        vv = sb("vv", [P, BATCH, 2, INNER])
        top = sb("att_top", [P, BATCH, HEADS])
        scale = sb("att_scale", [P, BATCH, HEADS])
        bias = sb("att_bias", [P, BATCH, HEADS])
        den = sb("att_den", [P, BATCH, HEADS])
        rden = sb("att_rden", [P, BATCH, HEADS])
        o = sb("o", [P, BATCH, INNER])
        oT = sb("oT", [P, BATCH, 4, P])
        y1 = sb("y1", [P, BATCH, 2, D])
        y1b = sb("y1b", [P, BATCH, D])
        bn2 = sb("bn2", [P, BATCH, 2, 6])
        mv2 = sb("mv2", [P, BATCH, 2])
        ve2 = sb("ve2", [P, BATCH])
        rstd2 = sb("rstd2", [P, BATCH])
        h2 = sb("h2", [P, BATCH, D])
        h2T = sb("h2T", [P, DCH, BATCH, P])
        gate = sb("gate", [P, FCH, P])
        ff = sb("ff", [P, FCH, P])

        with nc.Block() as block:
            @block.gpsimd
            def _(p):
                p.memset(zero[:], 0.0)
                p.memset(kT[:], 0.0)
                p.memset(vv[:], 0.0)

            @block.vector
            def _(v):
                with v.Fori(0, TILES) as it:
                    for b in range(BATCH):
                        k = it + b * TILES
                        v.tensor_scalar(tile_of(y, it, b), tile_of(e.x, it, b), flat(e.mean_var[:, bass.ds(k, 1), 0:1]),
                                        e.rstd[:, bass.ds(k, 1)], ALU.subtract, ALU.mult)
                v.wait_ge(ffn.loaded, ffn.all)
                v.tensor_copy(mask_odd[:], mask32[:, 2, :])
                for i in range(HALF):
                    v.tensor_copy(mask_even[:, i, :], mask32[:, min(i, 1), :])

        turns = LAYERS * HALF
        four = (s.ys_ready, s.yT_psum, s.hT_ready, s.qk_psum, s.v_psum, s.sq_ready, s.v_ready, s.ss_ready, s.norm_ready, s.q_norm_ready,
                s.rot_ready, s.qkT_psum, s.qT_ready, s.kT_ready, s.mixed_psum, s.mix_ready, s.mixT_psum,
                s.mixT_ready, s.out_psum, s.y1_ready, s.shift_psum, s.shift_var, s.shift_rstd, s.h2_ready, s.h2T_psum,
                s.h2T_ready, s.y1b_ready, s.ffn_out, s.y_done)
        begin(4, *four)
        begin(16, s.scores_psum, s.bias_ready, s.probs_ready, s.probsT_psum)
        begin(8, s.pT_act, s.pT_dve)
        begin(4 * FPAIRS, s.hid_psum, s.gate_ready, s.ff_ready)
        w1_loaded, rot_loaded = e.dma_sem("w1_loaded"), e.dma_sem("rot_loaded")

        class Item:

            def __init__(self, layer, i, q):
                self.layer, self.i, self.turn = layer, i, layer * HALF + i
                self.odd, self.b, self.k = q // 2, q % 2, q + 1
                self.t = i * 2 + self.odd
                self.bank = 4 * self.b

        def layers(engine, order, start, first, step):
            with engine.Fori(0, LAYERS) as layer:
                order.begin(engine)
                start(layer)
                with engine.Fori(0, 1) as i:
                    first(Item(layer, i, 0), Item(layer, i, 1))

                def turn(i, last):
                    order.begin(engine)
                    for q in range(4):
                        new, after = (None if last and q + n > 3 else Item(layer, i + (q + n) // 4, (q + n) % 4) for n in (1, 2))
                        step(Item(layer, i, q), new, after)

                with engine.Fori(0, HALF - 1) as i:
                    turn(i, False)
                with engine.Fori(HALF - 1, HALF) as i:
                    turn(i, True)

        with nc.Block() as block:
            @block.sync
            def _(sp):
                with sp.Fori(0, LAYERS) as layer:
                    first = layer * HALF
                    sp.wait_ge(s.rot_ready.sem, s.rot_ready.at(first, 0))
                    sp.dma_start(rot[:], d["rotary"]).then_inc(rot_loaded, 16)
                    sp.wait_ge(s.hid_psum.sem, s.hid_psum.at(first, 0))
                    sp.dma_start(w1[:], d["L0_w1"][bass.ds(layer, 1)].rearrange("l p c n -> (l p) c n"))\
                      .then_inc(w1_loaded, 16)

            @block.gpsimd
            def _(p):
                def norms(m):
                    p.wait_ge(s.ss_ready.sem, s.ss_ready.at(m.turn, m.k))
                    p.wait_ge(s.rot_ready.sem, s.rot_ready.at(m.turn, m.k - 2))
                    p.tensor_tensor(rn[:, m.b, HEADS:], ss[:, m.b, HEADS:], e.neg_half[:, 0:HEADS], ALU.pow).then_inc(s.norm_ready.sem, 1)
                    p.wait_ge(s.bias_ready.sem, s.bias_ready.at(m.turn, 4 * (m.k - 2)))
                    p.tensor_tensor(rn[:, m.b, 0:HEADS], ss[:, m.b, 0:HEADS], e.neg_half[:, 0:HEADS], ALU.pow)\
                     .then_inc(s.q_norm_ready.sem, 1)

                def first(new, after):
                    norms(new)

                def step(now, new, after):
                    p.wait_ge(s.shift_var.sem, s.shift_var.at(now.turn, now.k))
                    p.tensor_tensor(rstd2[:, now.b:now.b + 1], ve2[:, now.b:now.b + 1], e.neg_half[:, 0:1], ALU.pow)\
                     .then_inc(s.shift_rstd.sem, 1)
                    if new:
                        norms(new)
                    p.wait_ge(s.y_done.sem, s.y_done.at(now.turn, now.k - 2))
                    p.tensor_tensor(y1b[:, now.b, :], y1[:, now.b, now.odd, :], b2[:], ALU.add).then_inc(s.y1b_ready.sem, 1)

                layers(p, pool, lambda layer: None, first, step)

            @block.tensor
            def _(pe):
                pe.wait_ge(ffn.loaded, ffn.all)

                def y_transposed(m):
                    pe.wait_ge(s.ff_ready.sem, s.ff_ready.at(m.turn, FPAIRS * (m.k - 3) + 1))
                    pe.wait_ge(s.ys_ready.sem, s.ys_ready.at(m.turn, m.k))
                    for ch in range(DCH):
                        mm = pe.transpose(ps[:, m.bank, ch * P:(ch + 1) * P], ys[:, m.b, ch * P:(ch + 1) * P], e.ident[:])
                    mm.then_inc(s.yT_psum.sem, 1)

                def qkv(m, n, chunks=range(DCH)):
                    if n == 0:
                        pe.wait_ge(s.hT_ready.sem, s.hT_ready.at(m.turn, m.k))
                    if n == 2:
                        pe.wait_ge(s.y_done.sem, s.y_done.at(m.turn, m.k - 2))
                    for ch in chunks:
                        mm = pe.matmul(ps[:, m.bank + 1 + n, :], hT[:, m.b, m.odd, ch, 1 - ch:P + 1 - ch],
                                       wqkv[:, bass.ds(m.layer, 1), ch, n * INNER:(n + 1) * INNER].rearrange("p l n -> p (l n)"),
                                       start=ch == 0, stop=ch == DCH - 1)
                    if n > 0 and chunks[-1] == DCH - 1:
                        mm.then_inc((s.qk_psum if n == 1 else s.v_psum).sem, 1)

                def qk_transposed(m):
                    pe.wait_ge(s.rot_ready.sem, s.rot_ready.at(m.turn, m.k))
                    for n in range(2):
                        for j in range(4):
                            mm = pe.transpose(ps[:, m.bank + n, j * P:(j + 1) * P],
                                              work[:, m.b, 2 * n + j // 2, (j % 2) * P:(j % 2 + 1) * P], e.ident[:])
                    mm.then_inc(s.qkT_psum.sem, 1)

                def scores(m):
                    pe.wait_ge(s.v_ready.sem, s.v_ready.at(m.turn, m.k))
                    pe.wait_ge(s.qT_ready.sem, s.qT_ready.at(m.turn, m.k))
                    pe.wait_ge(s.kT_ready.sem, s.kT_ready.at(m.turn, m.k))
                    for j in range(4):
                        bank = ps[:, m.bank + j, :]
                        mask = (mask_odd[:].unsqueeze(1) if m.odd else mask_even[:, bass.ds(m.i, 1), :]).broadcast_to((P, 2, 2 * P))
                        pe.matmul(bank, e.ident_bf[:], mask, start=True, stop=False)
                        pe.matmul(bank, qT[:, m.b, j, :], kT[:, m.b, j, :, :, :].rearrange("p h w n -> p (h w n)"),
                                  start=False, stop=True).then_inc(s.scores_psum.sem, 1)

                def probs_transposed(m, banks):
                    for j in banks:
                        pe.wait_ge(s.probs_ready.sem, s.probs_ready.at(m.turn, 4 * (m.k - 1) + j + 1))
                        for n in range(4):
                            mm = pe.transpose(ps[:, m.bank + j, n * P:(n + 1) * P],
                                              work[:, m.b, 2 * j + n // 2, (n % 2) * P:(n % 2 + 1) * P], e.ident[:])
                        mm.then_inc(s.probsT_psum.sem, 1)

                def mixed(m):
                    pe.wait_ge(s.pT_act.sem, s.pT_act.at(m.turn, 2 * m.k))
                    pe.wait_ge(s.pT_dve.sem, s.pT_dve.at(m.turn, 2 * m.k))
                    for h in range(HEADS):
                        for c in range(2):
                            mm = pe.matmul(ps[:, m.bank, h * DH:(h + 1) * DH], pT[:, m.b, 2 * h + c, :],
                                           vv[:, m.b, c, h * DH:(h + 1) * DH], start=(h, c) == (0, 0), stop=c == 1,
                                           skip_group_check=True)
                    mm.then_inc(s.mixed_psum.sem, 1)

                def mix_transposed(m):
                    pe.wait_ge(s.mix_ready.sem, s.mix_ready.at(m.turn, m.k))
                    for j in range(4):
                        mm = pe.transpose(ps[:, m.bank + 1, j * P:(j + 1) * P], o[:, m.b, j * P:(j + 1) * P], e.ident[:])
                    mm.then_inc(s.mixT_psum.sem, 1)

                def attention_out(m):
                    pe.wait_ge(s.mixT_ready.sem, s.mixT_ready.at(m.turn, m.k))
                    for j in range(4):
                        mm = pe.matmul(ps[:, m.bank + 2, 0:D], oT[:, m.b, j, :],
                                       wo[:, bass.ds(m.layer, 1), j, :].rearrange("p l n -> p (l n)"), start=j == 0, stop=j == 3)
                    mm.then_inc(s.out_psum.sem, 1)

                def shifted(m):
                    pe.wait_ge(s.y1_ready.sem, s.y1_ready.at(m.turn, m.k))
                    pe.matmul(ps[:, m.bank + 3, 0:P], shift[:, 0, :], y1[:, m.b, m.odd, P:D], start=True, stop=False)
                    pe.matmul(ps[:, m.bank + 3, 0:P], shift[:, 1, :], y1[:, m.b, 1 - m.odd, P:D], start=False, stop=True)\
                      .then_inc(s.shift_psum.sem, 1)

                def h2_transposed(m):
                    pe.wait_ge(s.h2_ready.sem, s.h2_ready.at(m.turn, m.k))
                    for ch in range(DCH):
                        mm = pe.transpose(ps[:, m.bank, ch * P:(ch + 1) * P], h2[:, m.b, ch * P:(ch + 1) * P], e.ident[:])
                    mm.then_inc(s.h2T_psum.sem, 1)

                def ffn_up(m):
                    pe.wait_ge(w1_loaded, m.layer * 16 + 16)
                    pe.wait_ge(s.h2T_ready.sem, s.h2T_ready.at(m.turn, m.k))
                    for j in range(FCH):
                        for n in range(2):
                            at, to = n * HID + j * P, (2 * (j % 2) + n) * P
                            for ch in range(DCH):
                                mm = pe.matmul(ps[0:FW[j], m.bank + j // 2, to:to + P], w1[:, ch, at:at + FW[j]],
                                               h2T[:, ch, m.b, :], start=(j % 2, n, ch) == (0, 0, 0), stop=ch == DCH - 1,
                                               skip_group_check=True)
                        if j % 2:
                            mm.then_inc(s.hid_psum.sem, 1)

                def ffn_down(m, pair):
                    pe.wait_ge(s.ff_ready.sem, s.ff_ready.at(m.turn, FPAIRS * (m.k - 1) + pair + 1))
                    for j in (2 * pair, 2 * pair + 1):
                        mm = pe.matmul(ps[:, m.bank + 3, 0:D], ff[0:FW[j], j, :],
                                       w2[0:FW[j], bass.ds(m.layer, 1), j, :].rearrange("p l n -> p (l n)"),
                                       start=j == 0, stop=j == FCH - 1, skip_group_check=True)
                    if pair == FPAIRS - 1:
                        mm.then_inc(s.ffn_out.sem, 1)

                def first(new, after):
                    y_transposed(new)
                    for n in range(3):
                        qkv(new, n)
                    qk_transposed(new)
                    y_transposed(after)
                    scores(new)
                    probs_transposed(new, range(4))

                def step(now, new, after):
                    if new:
                        qkv(new, 0, (0,))
                    mixed(now)
                    if new:
                        qkv(new, 0, (1,))
                    mix_transposed(now)
                    if new:
                        qkv(new, 1, (0,))
                    attention_out(now)
                    if new:
                        qkv(new, 1, (1,))
                    shifted(now)
                    if new:
                        qkv(new, 2)
                    h2_transposed(now)
                    ffn_up(now)
                    if new:
                        qk_transposed(new)
                    if after:
                        y_transposed(after)
                    ffn_down(now, 0)
                    ffn_down(now, 1)
                    if new:
                        scores(new)
                        probs_transposed(new, (0,))
                    ffn_down(now, 2)
                    if new:
                        probs_transposed(new, (1, 2, 3))

                layers(pe, e.chain["pe"], lambda layer: None, first, step)

            @block.scalar
            def _(a):
                def start(layer):
                    at = layer * HALF
                    a.wait_ge(s.hT_ready.sem, s.hT_ready.at(at, 0))
                    a.wait_ge(s.v_psum.sem, s.v_psum.at(at, 0))
                    for b in range(BATCH):
                        z = nc.scalar.copy(hT[:, b, 0, 1, 0:1], zero[:])
                    act.link(z)
                    a.wait_ge(s.ff_ready.sem, s.ff_ready.at(at, 0))
                    act.link(nc.scalar.copy(cols[:], flat(all_cols[:, bass.ds(layer, 1), :])))
                    a.wait_ge(s.y1b_ready.sem, s.y1b_ready.at(at, 0))
                    act.link(nc.scalar.copy(b2[:], flat(all_b2[:, bass.ds(layer, 1), :])))

                def copy_hT(m):
                    a.wait_ge(s.yT_psum.sem, s.yT_psum.at(m.turn, m.k))
                    a.wait_ge(s.v_psum.sem, s.v_psum.at(m.turn, m.k - 2))
                    nc.scalar.copy(hT[:, m.b, m.odd, :, 1:P + 1], ps[:, m.bank, 0:D].rearrange("p (c n) -> p c n", c=DCH))
                    nc.scalar.copy(hT[:, m.b, 1 - m.odd, 1, 0:1], ps[:, m.bank, D - 1:D]).then_inc(s.hT_ready.sem, 1)

                def squares(m):
                    a.wait_ge(s.qk_psum.sem, s.qk_psum.at(m.turn, m.k))
                    a.wait_ge(s.mixed_psum.sem, s.mixed_psum.at(m.turn, m.k - 2))
                    nc.scalar.activation(flat(pT[:, m.b, 0:HEADS, :]), flat(ps[:, m.bank + 1:m.bank + 3, :]), ACT.Square)\
                      .then_inc(s.sq_ready.sem, 1)

                def copy_v(m):
                    a.wait_ge(s.v_psum.sem, s.v_psum.at(m.turn, m.k))
                    a.wait_ge(s.mixed_psum.sem, s.mixed_psum.at(m.turn, m.k - 2))
                    nc.scalar.copy(vv[:, m.b, m.odd, :], ps[:, m.bank + 3, :]).then_inc(s.v_ready.sem, 1)

                def copy_qT(m):
                    a.wait_ge(s.qkT_psum.sem, s.qkT_psum.at(m.turn, m.k))
                    a.wait_ge(s.scores_psum.sem, s.scores_psum.at(m.turn, 4 * (m.k - 2)))
                    nc.scalar.copy(flat(qT[:, m.b, :, :]), ps[:, m.bank, :]).then_inc(s.qT_ready.sem, 1)

                def probs(m):
                    for slot in range(HEADS):
                        if slot % 2 == 0:
                            a.wait_ge(s.bias_ready.sem, s.bias_ready.at(m.turn, 4 * (m.k - 1) + slot // 2 + 1))
                        ex = nc.scalar.activation(work[:, m.b, slot, :], ps[:, m.bank + slot // 2, (slot % 2) * 2 * P:(slot % 2 + 1) * 2 * P],
                                                  ACT.Exp, bias=bias[:, m.b, slot:slot + 1], scale=scale[:, m.b, slot:slot + 1],
                                                  accum_out=den[:, m.b, slot:slot + 1])
                        if slot % 2:
                            ex.then_inc(s.probs_ready.sem, 1)

                def copy_pT(m):
                    for j in range(2):
                        a.wait_ge(s.probsT_psum.sem, s.probsT_psum.at(m.turn, 4 * (m.k - 1) + j + 1))
                        nc.scalar.copy(flat(pT[:, m.b, 4 * j:4 * j + 4, :]), ps[:, m.bank + j, :]).then_inc(s.pT_act.sem, 1)

                def copy_oT(m):
                    a.wait_ge(s.mixT_psum.sem, s.mixT_psum.at(m.turn, m.k))
                    a.wait_ge(s.out_psum.sem, s.out_psum.at(m.turn, m.k - 2))
                    nc.scalar.copy(flat(oT[:, m.b, :, :]), ps[:, m.bank + 1, :]).then_inc(s.mixT_ready.sem, 1)

                def affine_h2T(m):
                    a.wait_ge(s.h2T_psum.sem, s.h2T_psum.at(m.turn, m.k))
                    a.wait_ge(s.hid_psum.sem, s.hid_psum.at(m.turn, FPAIRS * (m.k - 2)))
                    for ch in range(DCH):
                        cp = nc.scalar.activation(h2T[:, ch, m.b, :], ps[:, m.bank, ch * P:(ch + 1) * P], ACT.Identity,
                                                  scale=cols[:, ch:ch + 1], bias=cols[:, DCH + ch:DCH + ch + 1])
                    cp.then_inc(s.h2T_ready.sem, 1)

                def gates(m):
                    for j in range(FCH):
                        if j % 2 == 0:
                            a.wait_ge(s.hid_psum.sem, s.hid_psum.at(m.turn, FPAIRS * (m.k - 1) + j // 2 + 1))
                            a.wait_ge(s.ff_ready.sem, s.ff_ready.at(m.turn, FPAIRS * (m.k - 2) + j // 2 + 1))
                        col, of = 2 * DCH + FCH + j, (2 * (j % 2) + 1) * P
                        g = nc.scalar.activation(gate[0:FW[j], j, :], ps[0:FW[j], m.bank + j // 2, of:of + P],
                                                 ACT.Gelu, bias=cols[0:FW[j], col:col + 1])
                        if j % 2:
                            g.then_inc(s.gate_ready.sem, 1)

                def load_table(func):
                    act.link(nc.scalar.activation(unused[:], zero[:], func))

                def first(new, after):
                    copy_hT(new)
                    squares(new)
                    copy_v(new)
                    copy_qT(new)
                    copy_hT(after)
                    probs(new)

                def step(now, new, after):
                    copy_pT(now)
                    copy_oT(now)
                    load_table(ACT.Gelu)
                    if new:
                        squares(new)
                    affine_h2T(now)
                    if new:
                        copy_v(new)
                    gates(now)
                    if new:
                        copy_qT(new)
                    if after:
                        copy_hT(after)
                    if new:
                        load_table(ACT.Exp)
                        probs(new)

                layers(a, act, start, first, step)

            @block.vector
            def _(v):
                def start(layer):
                    v.wait_ge(rot_loaded, layer * 16 + 16)
                    for part in range(2):
                        for n in range(2):
                            last = v.tensor_tensor(rot[:, part, :, n, :], rot[:, part, :, n, :],
                                                   qk_scale[:, bass.ds(layer, 1), part, n, :].broadcast_to((P, TILES, DH)), ALU.mult)
                    dve.link(last)
                    v.wait_ge(s.shift_psum.sem, s.shift_psum.at(layer * HALF, 0))
                    v.wait_ge(s.y1b_ready.sem, s.y1b_ready.at(layer * HALF, 0))
                    for b in range(BATCH):
                        z = v.memset(y1[:, b, 1, :], 0.0)
                    dve.link(z)

                def take_y(m):
                    v.wait_ge(s.y_done.sem, s.y_done.at(m.turn, m.k - 16))
                    v.wait_ge(s.y1_ready.sem, s.y1_ready.at(m.turn, m.k - 2))
                    v.tensor_copy(ys[:, m.b, :], tile_of(y, m.t, m.b)).then_inc(s.ys_ready.sem, 1)

                def rotary_parts(m):
                    qk = ps[:, m.bank + 1:m.bank + 3, :].rearrange("p n (h x) -> p n h x", x=DH)
                    w = [work[:, m.b, 4 * n:4 * n + 4, :].rearrange("p a f -> p (a f)").rearrange("p (n h x) -> p n h x", n=2, x=DH)
                         for n in range(2)]
                    table = [rot[:, part, bass.ds(m.t, 1), :, :].rearrange("p t n x -> p (t n) x").unsqueeze(2)
                             .broadcast_to((P, 2, HEADS, DH)) for part in range(2)]
                    return qk, w, table

                def norms(m):
                    v.wait_ge(s.sq_ready.sem, s.sq_ready.at(m.turn, m.k))
                    v.wait_ge(s.q_norm_ready.sem, s.q_norm_ready.at(m.turn, m.k - 2))
                    dve.link(v.tensor_reduce(ss[:, m.b, :], flat(pT[:, m.b, 0:HEADS, :]).rearrange("p (h x) -> p h x", x=DH), AX.X, ALU.add))
                    v.tensor_scalar(ss[:, m.b, :], ss[:, m.b, :], 1e-24, None, ALU.max).then_inc(s.ss_ready.sem, 1)

                def rotate_cos(m):
                    qk, w, table = rotary_parts(m)
                    v.wait_ge(s.sq_ready.sem, s.sq_ready.at(m.turn, m.k))
                    v.wait_ge(s.probsT_psum.sem, s.probsT_psum.at(m.turn, 4 * (m.k - 2)))
                    v.tensor_tensor(w[0], qk, table[0], ALU.mult)

                def rotate_sin(m):
                    qk, w, table = rotary_parts(m)
                    hx = DH // 2
                    v.tensor_tensor(w[1][:, :, :, 0:hx], qk[:, :, :, hx:DH], table[1][:, :, :, 0:hx], ALU.mult)
                    dve.link(v.tensor_tensor(w[1][:, :, :, hx:DH], qk[:, :, :, 0:hx], table[1][:, :, :, hx:DH], ALU.mult))

                def rotate_sum(m):
                    _, w, _ = rotary_parts(m)
                    dve.link(v.tensor_tensor(w[0], w[0], w[1], ALU.add))

                def scale_k(m):
                    kr = work[:, m.b, 2:4, :].rearrange("p a f -> p (a f)").rearrange("p (h x) -> p h x", x=DH)
                    v.wait_ge(s.norm_ready.sem, s.norm_ready.at(m.turn, m.k))
                    v.tensor_tensor(kr, kr, rn[:, m.b, HEADS:].unsqueeze(2).broadcast_to((P, HEADS, DH)), ALU.mult)\
                     .then_inc(s.rot_ready.sem, 1)

                def copy_kT(m):
                    v.wait_ge(s.qkT_psum.sem, s.qkT_psum.at(m.turn, m.k))
                    v.wait_ge(s.scores_psum.sem, s.scores_psum.at(m.turn, 4 * (m.k - 2)))
                    for n in range(2):
                        own = slice(n * DH, (n + 1) * DH)
                        cp = v.tensor_copy(kT[own, m.b, :, n, m.odd, :], ps[own, m.bank + 1, :].rearrange("p (j n) -> p j n", j=4))
                    cp.then_inc(s.kT_ready.sem, 1)

                def maxima(m):
                    v.wait_ge(s.q_norm_ready.sem, s.q_norm_ready.at(m.turn, m.k))
                    v.wait_ge(s.probs_ready.sem, s.probs_ready.at(m.turn, 4 * (m.k - 2)))
                    v.tensor_scalar(scale[:, m.b, :], rn[:, m.b, 0:HEADS], float(DH) ** 0.5, None, ALU.mult)
                    for j in range(4):
                        v.wait_ge(s.scores_psum.sem, s.scores_psum.at(m.turn, 4 * (m.k - 1) + j + 1))
                        heads = slice(2 * j, 2 * j + 2)
                        dve.link(v.tensor_reduce(top[:, m.b, heads], ps[:, m.bank + j, :].rearrange("p (n x) -> p n x", n=2), AX.X, ALU.max))
                        v.scalar_tensor_tensor(bias[:, m.b, heads], top[:, m.b, heads], -1.0, scale[:, m.b, heads],
                                               ALU.mult, ALU.mult).then_inc(s.bias_ready.sem, 1)

                def copy_pT(m):
                    for j in range(2, 4):
                        v.wait_ge(s.probsT_psum.sem, s.probsT_psum.at(m.turn, 4 * (m.k - 1) + j + 1))
                        v.tensor_copy(flat(pT[:, m.b, 4 * j:4 * j + 4, :]), ps[:, m.bank + j, :]).then_inc(s.pT_dve.sem, 1)

                def mix(m):
                    v.wait_ge(s.probs_ready.sem, s.probs_ready.at(m.turn, 4 * m.k))
                    dve.link(v.reciprocal(rden[:, m.b, :], den[:, m.b, :]))
                    v.wait_ge(s.mixed_psum.sem, s.mixed_psum.at(m.turn, m.k))
                    v.wait_ge(s.mixT_psum.sem, s.mixT_psum.at(m.turn, m.k - 2))
                    v.tensor_tensor(o[:, m.b, :].rearrange("p (h x) -> p h x", x=DH), ps[:, m.bank, :].rearrange("p (h x) -> p h x", x=DH),
                                    rden[:, m.b, :].unsqueeze(2).broadcast_to((P, HEADS, DH)), ALU.mult).then_inc(s.mix_ready.sem, 1)

                def add_attention(m):
                    v.wait_ge(s.out_psum.sem, s.out_psum.at(m.turn, m.k))
                    v.wait_ge(s.shift_psum.sem, s.shift_psum.at(m.turn, m.k - 2))
                    v.wait_ge(s.y1b_ready.sem, s.y1b_ready.at(m.turn, m.k - 2))
                    v.tensor_tensor(y1[:, m.b, m.odd, :], ps[:, m.bank + 2, 0:D], ys[:, m.b, :], ALU.add).then_inc(s.y1_ready.sem, 1)

                def shifted_stats(m):
                    v.wait_ge(s.y1_ready.sem, s.y1_ready.at(m.turn, m.k))
                    v.bn_stats(bn2[:, m.b, 0, :], y1[:, m.b, m.odd, 0:P])
                    v.wait_ge(s.shift_psum.sem, s.shift_psum.at(m.turn, m.k))
                    dve.link(v.bn_stats(bn2[:, m.b, 1, :], ps[:, m.bank + 3, 0:P]))
                    dve.link(v.bn_aggr(mv2[:, m.b, :], flat(bn2[:, m.b, :, :])))
                    v.tensor_scalar(ve2[:, m.b:m.b + 1], mv2[:, m.b, 1:2], EPS, None, ALU.add).then_inc(s.shift_var.sem, 1)

                def normalise_h2(m):
                    v.wait_ge(s.shift_rstd.sem, s.shift_rstd.at(m.turn, m.k))
                    v.wait_ge(s.h2T_psum.sem, s.h2T_psum.at(m.turn, m.k - 2))
                    v.tensor_scalar(h2[:, m.b, 0:P], y1[:, m.b, m.odd, 0:P], mv2[:, m.b, 0:1], rstd2[:, m.b:m.b + 1], ALU.subtract, ALU.mult)
                    v.tensor_scalar(h2[:, m.b, P:D], ps[:, m.bank + 3, 0:P], mv2[:, m.b, 0:1], rstd2[:, m.b:m.b + 1], ALU.subtract, ALU.mult)\
                     .then_inc(s.h2_ready.sem, 1)

                def gated(m, pair):
                    v.wait_ge(s.gate_ready.sem, s.gate_ready.at(m.turn, FPAIRS * (m.k - 1) + pair + 1))
                    if pair == 0:
                        v.wait_ge(s.ffn_out.sem, s.ffn_out.at(m.turn, m.k - 1))
                    for j in (2 * pair, 2 * pair + 1):
                        col, of = 2 * DCH + j, 2 * (j % 2) * P
                        ins = v.scalar_tensor_tensor(ff[0:FW[j], j, :], ps[0:FW[j], m.bank + pair, of:of + P], cols[0:FW[j], col:col + 1],
                                                     gate[0:FW[j], j, :], ALU.add, ALU.mult)
                    ins.then_inc(s.ff_ready.sem, 1)

                def add_ffn(m):
                    v.wait_ge(s.ffn_out.sem, s.ffn_out.at(m.turn, m.k))
                    v.wait_ge(s.y1b_ready.sem, s.y1b_ready.at(m.turn, m.k))
                    v.tensor_tensor(tile_of(y, m.t, m.b), ps[:, m.bank + 3, 0:D], y1b[:, m.b, :], ALU.add).then_inc(s.y_done.sem, 1)

                def first(new, after):
                    take_y(new)
                    take_y(after)
                    norms(new)
                    rotate_cos(new)
                    rotate_sin(new)
                    rotate_sum(new)
                    scale_k(new)
                    copy_kT(new)
                    maxima(new)

                def step(now, new, after):
                    copy_pT(now)
                    mix(now)
                    add_attention(now)
                    shifted_stats(now)
                    normalise_h2(now)
                    if new:
                        rotate_cos(new)
                        norms(new)
                        rotate_sin(new)
                        rotate_sum(new)
                    gated(now, 0)
                    if new:
                        scale_k(new)
                    gated(now, 1)
                    if after:
                        take_y(after)
                    gated(now, 2)
                    if new:
                        copy_kT(new)
                        maxima(new)
                    add_ffn(now)

                layers(v, dve, start, first, step)
        end(turns, *four, s.scores_psum, s.probs_ready, s.probsT_psum, s.bias_ready, s.pT_act, s.pT_dve, s.hid_psum, s.gate_ready, s.ff_ready)

        for n in (s.ln_var, s.ln_rstd):
            n.each(2)
        with nc.Block() as block:
            @block.vector
            def _(v):
                with v.Fori(0, TILES) as it:
                    dve.begin(v)
                    for b in range(BATCH):
                        dve.link(v.tensor_tensor(tile_of(e.x, it, b), tile_of(e.x, it, b), tile_of(y, it, b), ALU.add))
                        stats_dve(e, v, it, b)

            @block.gpsimd
            def _(p):
                with p.Fori(0, TILES) as it:
                    for b in range(BATCH):
                        stats_pool(e, p, it, b)
        for n in (s.ln_var, s.ln_rstd):
            n.close(TILES)


def load(e, sp, *pairs):
    for to, of in pairs:
        sp.dma_start(to[:], e.dram[of]).then_inc(e.loaded, 16)
        e.loads += 16


def add_to_x(e, v, it, b, out):
    e.chain["dve"].link(v.tensor_tensor(tile_of(e.x, it, b), out, tile_of(e.x, it, b), ALU.add))
    stats_dve(e, v, it, b)


def l1_xattn(e, *following):
    nc, s, ps = e.nc, e.s, e.ps
    dve = e.chain["dve"]
    with ExitStack() as ctx:
        sb = memory(e, ctx, "l1_xattn")
        first_mask = sb("first_mask", [P, CTX])
        mask = sb("causal", [P, TILES, CTX], BF16)
        a = sb("a", [P, BATCH, CTX])
        den = sb("a_den", [P, BATCH])
        rec = sb("a_rec", [P, BATCH])
        nmax = sb("nmax", [P, BATCH])
        aT = sb("aT", [P, P])
        two = (s.c_ready, s.cT_psum, s.cT_ready, s.scores_psum, s.max_ready, s.probs_ready, s.mix_psum, s.mix_ready, s.ln_var, s.ln_rstd)
        begin(2, *two)
        begin(1, s.probsT_psum, s.probsT_ready, s.mask_ready)
        with nc.Block() as block:
            @block.sync
            def _(sp):
                load(e, sp, (first_mask, "causal"))
                load_ahead(e, sp, *following)

            @block.tensor
            def _(pe):
                pe.wait_ge(s.mask_ready.sem, s.mask_ready.at(0))

                def transposes(it):
                    for b in range(BATCH):
                        transpose_c(e, pe, it, b, b)

                def scores(it):
                    for b in range(BATCH):
                        pe.wait_ge(s.cT_ready.sem, s.cT_ready.at(it, b + 1))
                        pe.wait_ge(s.probs_ready.sem, s.probs_ready.before(it, b + 1))
                        pe.matmul(ps[2 + b][:, 0:CTX], e.ident_bf[:], flat(mask[:, bass.ds(it, 1), :]), start=True, stop=False)
                        for ch in range(DCH):
                            mm = pe.matmul(ps[2 + b][:, 0:CTX], e.cT[:, b, ch, :], e.ctxT[:, ch, b, :], start=False, stop=ch == DCH - 1)
                        mm.then_inc(s.scores_psum.sem, 1)

                def probs_transposed(it):
                    pe.wait_ge(s.probs_ready.sem, s.probs_ready.at(it, 2))
                    pe.wait_ge(s.probsT_ready.sem, s.probsT_ready.before(it))
                    pe.transpose(ps[4][:, 0:P], flat(a[:]), e.ident[:]).then_inc(s.probsT_psum.sem, 1)

                def mix(it):
                    pe.wait_ge(s.probsT_ready.sem, s.probsT_ready.at(it))
                    for b in range(BATCH):
                        own = slice(b * CTX, (b + 1) * CTX)
                        pe.wait_ge(s.ln_var.sem, s.ln_var.before(it, b + 1))
                        pe.matmul(ps[6 + b][:, 0:D], aT[own, :], e.ctx_tok[own, b, :], start=True, stop=True)\
                          .then_inc(s.mix_psum.sem, 1)

                def first(new, after):
                    transposes(new)
                    scores(new)
                    transposes(after)

                def step(now, new, after):
                    probs_transposed(now)
                    if new is not None:
                        scores(new)
                    mix(now)
                    if after is not None:
                        transposes(after)

                turns_of_tiles(pe, e.chain["pe"], first, step)

            @block.scalar
            def _(act_):
                def copy(it):
                    for b in range(BATCH):
                        copy_cT(e, act_, it, b, b, s.scores_psum)

                def exp(it):
                    for b in range(BATCH):
                        act_.wait_ge(s.max_ready.sem, s.max_ready.at(it, b + 1))
                        act_.wait_ge(s.probsT_psum.sem, s.probsT_psum.before(it))
                        act_.wait_ge(s.mix_ready.sem, s.mix_ready.before(it, b + 1))
                        nc.scalar.activation(a[:, b, :], ps[2 + b][:, 0:CTX], ACT.Exp, bias=nmax[:, b:b + 1],
                                             accum_out=den[:, b:b + 1]).then_inc(s.probs_ready.sem, 1)

                def copy_aT(it):
                    act_.wait_ge(s.probsT_psum.sem, s.probsT_psum.at(it))
                    act_.wait_ge(s.mix_psum.sem, s.mix_psum.before(it, 2))
                    nc.scalar.copy(aT[:], ps[4][:, 0:P]).then_inc(s.probsT_ready.sem, 1)

                def first(new, after):
                    copy(new)
                    exp(new)
                    copy(after)

                def step(now, new, after):
                    copy_aT(now)
                    if new is not None:
                        exp(new)
                    if after is not None:
                        copy(after)

                turns_of_tiles(act_, e.chain["act"], first, step)

            @block.vector
            def _(v):
                dve.begin(v)
                dve.link(v.memset(mask[:], 0.0))
                v.wait_ge(e.loaded, e.loads)
                v.tensor_copy(mask[:, 0, :], first_mask[:]).then_inc(s.mask_ready.sem, 1)

                def normal(it):
                    for b in range(BATCH):
                        normalise(e, v, it, b)

                def maxima(it):
                    for b in range(BATCH):
                        v.wait_ge(s.scores_psum.sem, s.scores_psum.at(it, b + 1))
                        v.wait_ge(s.probs_ready.sem, s.probs_ready.before(it, b + 1))
                        v.tensor_reduce(nmax[:, b:b + 1], ps[2 + b][:, 0:CTX], AX.X, ALU.max, negate=True)\
                         .then_inc(s.max_ready.sem, 1)

                def reciprocals(it):
                    for b in range(BATCH):
                        v.wait_ge(s.probs_ready.sem, s.probs_ready.at(it, b + 1))
                        v.reciprocal(rec[:, b:b + 1], den[:, b:b + 1]).then_inc(s.mix_ready.sem, 1)

                def add(it):
                    for b in range(BATCH):
                        v.wait_ge(s.mix_ready.sem, s.mix_ready.at(it, b + 1))
                        v.wait_ge(s.mix_psum.sem, s.mix_psum.at(it, b + 1))
                        dve.link(v.scalar_tensor_tensor(tile_of(e.x, it, b), ps[6 + b][:, 0:D], rec[:, b:b + 1],
                                                        tile_of(e.x, it, b), ALU.mult, ALU.add))
                        stats_dve(e, v, it, b)

                def first(new, after):
                    normal(new)
                    normal(after)
                    maxima(new)

                def step(now, new, after):
                    reciprocals(now)
                    if new is not None:
                        maxima(new)
                    if after is not None:
                        normal(after)
                    add(now)

                turns_of_tiles(v, dve, first, step)

            @block.gpsimd
            def _(p):
                with p.Fori(0, TILES) as it:
                    for b in range(BATCH):
                        stats_pool(e, p, it, b)
        end(TILES, *two, s.probsT_psum, s.probsT_ready)
        end(1, s.mask_ready)


EXPERTS = 8
MOE_HID = 512
MCH = MOE_HID // P
CAPACITY = -(-BATCH * SEQ * 5 // (EXPERTS * 4))
CHOICES = 2
ITEMS = ALL_TILES * CHOICES
WIDTH = 3
CAPACITY_TILES = -(-CAPACITY // P)
DROPPING_TILES = EXPERTS * CAPACITY_TILES
KEEPING_TILES = (BATCH * SEQ * CHOICES + EXPERTS * (P - 1)) // P
assert DROPPING_TILES % WIDTH == 0 and KEEPING_TILES % WIDTH == 0 and CAPACITY_TILES == WIDTH
MAX_TILES = max(DROPPING_TILES, KEEPING_TILES)


def expert_constants():
    rows = [np.arange(MAX_TILES + 1) * P, np.arange(P), np.arange(ITEMS) // CHOICES, np.arange(EXPERTS) * CAPACITY_TILES * P]
    at = np.cumsum([0] + [len(r) for r in rows])
    return np.concatenate(rows), [slice(int(a), int(b)) for a, b in zip(at[:-1], at[1:])]


class Moe(Ahead):

    def __init__(self, e, ctx, stage, router, *weights):
        sb = memory(e, ctx, stage + "_in")
        self.router = sb("router", [P, DCH, EXPERTS])
        self.number = sb("expert_number", [P, EXPERTS])
        self.const = sb("constants", [P, len(expert_constants()[0])])
        self.p_col = sb("p_col", [P, 1])
        self.tri32 = sb("tri32", [P, P])
        self.weights = [sb(n, shape) for n, shape, _ in weights]
        super().__init__(e, stage, [(self.router, router), (self.number, "expert_number"), (self.const, "expert_constants"),
                                    (self.p_col, "p_col"), (self.tri32, "tri")] + [(w, of) for w, (_, _, of) in zip(self.weights, weights)])


def route(e, ctx, stage, given, gates_are_softmax):
    nc, s, ps = e.nc, e.s, e.ps
    dve = e.chain["dve"]
    sb = memory(e, ctx, stage)
    E8 = EXPERTS
    every = (P, ALL_TILES, E8)
    chosen = sb("chosen", every, BF16)
    hots = sb("hots", [P, ALL_TILES, CHOICES, E8])
    comb = sb("comb", every)
    c_all = sb("c_all", [P, ALL_TILES, D])
    number = sb("expert_number", [P, E8])
    values = sb("values", [P, CHOICES, ALL_TILES, E8])
    equal = sb("equal", every)
    top = sb("top", [P, CHOICES, ALL_TILES])
    index = sb("index", [P, ALL_TILES])
    den = sb("gate_den", [P, ALL_TILES])
    pair = sb("pair_weights", [P, CHOICES, ALL_TILES])
    two = (s.c_ready, s.cT_psum, s.cT_ready, s.logits_psum, s.routed)
    begin(2, *two)
    with nc.Block() as block:
        @block.tensor
        def _(pe):
            pe.wait_ge(given.loaded, given.all)

            def logits(m):
                pe.wait_ge(s.cT_ready.sem, s.cT_ready.at(m.it, m.k))
                pe.wait_ge(s.routed.sem, s.routed.before(m.it, m.k))
                for ch in range(DCH):
                    mm = pe.matmul(ps[2 + m.b][:, 0:E8], e.cT[:, m.b, ch, :], given.router[:, ch, :], start=ch == 0, stop=ch == DCH - 1)
                mm.then_inc(s.logits_psum.sem, 1)

            def first(new, after):
                transpose_c(e, pe, new.it, new.b, new.b)
                transpose_c(e, pe, after.it, after.b, after.b)

            def step(now, new, after):
                logits(now)
                if after:
                    transpose_c(e, pe, after.it, after.b, after.b)

            tiles(pe, e.chain["pe"], first, step)

        @block.scalar
        def _(act_):
            def copy(m):
                copy_cT(e, act_, m.it, m.b, m.b, s.logits_psum)

            def first(new, after):
                copy(new)
                copy(after)

            def step(now, new, after):
                if after:
                    copy(after)

            tiles(act_, e.chain["act"], first, step)

        @block.vector
        def _(v):
            def keep_c(m):
                k = m.it + m.b * TILES
                v.tensor_scalar(tile_of(c_all, m.it, m.b), tile_of(e.x, m.it, m.b), flat(e.mean_var[:, bass.ds(k, 1), 0:1]),
                                e.rstd[:, bass.ds(k, 1)], ALU.subtract, ALU.mult)

            def copy_logits(m):
                v.wait_ge(s.logits_psum.sem, s.logits_psum.at(m.it, m.k))
                v.tensor_copy(tile_of(values[:, 0, :, :], m.it, m.b), ps[2 + m.b][:, 0:E8]).then_inc(s.routed.sem, 1)

            def first(new, after):
                normalise(e, v, new.it, new.b)
                normalise(e, v, after.it, after.b)

            def step(now, new, after):
                keep_c(now)
                if after:
                    normalise(e, v, after.it, after.b)
                copy_logits(now)

            tiles(v, dve, first, step)
    end(TILES, *two)

    begin(1, s.max_ready, s.probs_ready)
    by_expert = lambda a: a.unsqueeze(2).broadcast_to(every)
    numbers = number[:].unsqueeze(1).broadcast_to(every)
    with nc.Block() as block:
        @block.scalar
        def _(act_):
            act_.wait_ge(s.max_ready.sem, s.max_ready.at(0))
            of = values[:, 0, :, :] if gates_are_softmax else pair[:, 1, :]
            nc.scalar.activation(of, of, ACT.Exp).then_inc(s.probs_ready.sem, 1)

        @block.vector
        def _(v):
            dve.begin(v)
            dve.link(v.tensor_scalar(number[:], given.number[:], -float(E8), None, ALU.add))
            if gates_are_softmax:
                dve.link(v.tensor_reduce(top[:, 0, :], values[:, 0, :, :], AX.X, ALU.max))
                v.tensor_tensor(values[:, 0, :, :], values[:, 0, :, :], by_expert(top[:, 0, :]), ALU.subtract).then_inc(s.max_ready.sem, 1)
                v.wait_ge(s.probs_ready.sem, s.probs_ready.at(0))
                dve.link(v.tensor_reduce(den[:], values[:, 0, :, :], AX.X, ALU.add))
                dve.link(v.reciprocal(den[:], den[:]))
                dve.link(v.tensor_tensor(values[:, 0, :, :], values[:, 0, :, :], by_expert(den[:]), ALU.mult))
            for c in range(CHOICES):
                dve.link(v.tensor_reduce(top[:, c, :], values[:, c, :, :], AX.X, ALU.max))
                dve.link(v.tensor_tensor(equal[:], values[:, c, :, :], by_expert(top[:, c, :]), ALU.is_equal))
                dve.link(v.tensor_tensor(equal[:], equal[:], numbers, ALU.mult))
                dve.link(v.tensor_reduce(index[:], equal[:], AX.X, ALU.min))
                dve.link(v.tensor_tensor(hots[:, :, c, :], numbers, by_expert(index[:]), ALU.is_equal))
                if c == 0:
                    dve.link(v.scalar_tensor_tensor(values[:, 1, :, :], hots[:, :, 0, :], MASKED, values[:, 0, :, :], ALU.mult, ALU.add))
            dve.link(v.tensor_tensor(chosen[:], hots[:, :, 0, :], hots[:, :, 1, :], ALU.add))
            if gates_are_softmax:
                v.tensor_tensor(comb[:], values[:, 0, :, :], chosen[:], ALU.mult)
            else:
                v.tensor_tensor(pair[:, 1, :], top[:, 1, :], top[:, 0, :], ALU.subtract).then_inc(s.max_ready.sem, 1)
                v.wait_ge(s.probs_ready.sem, s.probs_ready.at(0))
                dve.link(v.tensor_scalar(den[:], pair[:, 1, :], 1.0, None, ALU.add))
                dve.link(v.reciprocal(pair[:, 0, :], den[:]))
                dve.link(v.tensor_tensor(pair[:, 1, :], pair[:, 1, :], pair[:, 0, :], ALU.mult))
                dve.link(v.tensor_tensor(comb[:], hots[:, :, 0, :], by_expert(pair[:, 0, :]), ALU.mult))
                dve.link(v.tensor_tensor(equal[:], hots[:, :, 1, :], by_expert(pair[:, 1, :]), ALU.mult))
                v.tensor_tensor(comb[:], comb[:], equal[:], ALU.add)
    end(1, s.max_ready, s.probs_ready)
    return chosen, hots, comb, c_all


class Slots:

    def __init__(self, turn, j):
        self.turn, self.j, self.k = turn, j, j + 1


def experts(e, ctx, stage, given, routed, n_tiles, dropping, up_weight, down_weight, with_stats):
    nc, s, ps = e.nc, e.s, e.ps
    dve = e.chain["dve"]
    sb = memory(e, ctx, stage)
    E8, turns = EXPERTS, n_tiles // WIDTH
    chosen, hots, comb, c_all = routed
    c_rows = nc.dram_tensor(f"{stage}_c_rows", (ALL_TILES * P, D), F32).ap()
    y_rows = nc.dram_tensor(f"{stage}_y_rows", (n_tiles * P, D), F32).ap()
    values, (of_p, to_p, of_item, of_base) = expert_constants()
    const, p_col, tri32 = given.const, given.p_col, given.tri32
    tri = sb("tri", [P, P], BF16)
    ones_bf = sb("ones_bf", [P, P], BF16)
    scan = sb("scan", [P, 2, ALL_TILES, E8])
    rank = sb("rank", [P, ALL_TILES, E8])
    weight = sb("weight", [P, ALL_TILES])
    prod = sb("prod", [P, ALL_TILES, CHOICES, E8])
    weights = sb("weights", [P, ITEMS])
    slot = sb("slot", [P, ITEMS])
    above = sb("above", [P, ITEMS, n_tiles + 1])
    in_tile = sb("in_tile", [P, ITEMS, n_tiles])
    high = sb("high", [P, ITEMS])
    low = sb("low", [P, ITEMS])
    in_row = sb("in_row", [P, ITEMS, P], BF16)
    place = sb("place", [P, ITEMS, 2, n_tiles], BF16)
    token_f = sb("token_f", [P, n_tiles])
    token = sb("token", [P, n_tiles], U32)
    back = sb("back", [P, ITEMS], U32)
    rows = sb("rows", [P, max(n_tiles, ITEMS), D])
    row = sb("row", [P, WIDTH, D])
    rowT = sb("rowT", [P, WIDTH, DCH, P])
    upT = sb("upT", [P, WIDTH, MCH, P])
    y = sb("y", [P, WIDTH, D])
    if not dropping:
        per = DCH * MOE_HID // D
        up_w = c_all[:, 0:WIDTH * per, :].rearrange("p (j a) d -> p j (a d)", j=WIDTH)
        filled = sb("filled", [P, E8, ALL_TILES])
        ends = sb("ends", [P, 2, E8])
        base = sb("base", [P, E8])
        past = sb("past", [P, n_tiles, E8])
        expert_f = sb("expert_f", [P, n_tiles])
        expert_of = sb("expert_of", [P, n_tiles], I32)
    n8 = ALL_TILES * E8
    c_kept = e.dma_sem(f"{stage}_c_kept")
    gathered = [e.dma_sem(f"{stage}_gathered{g}") for g in range(3)]
    returned = [e.dma_sem(f"{stage}_returned{g}") for g in range(4)]
    cuts = [0, 1, turns * 9 // 16, turns - 1]
    until = [WIDTH * (c + 1) for c in cuts]
    until[0] = 0
    begin(1, s.sums_psum, s.placed, s.prep_psum)
    with nc.Block() as block:
        @block.sync
        def _(sp):
            sp.dma_start(c_rows.rearrange("(t p) d -> p t d", p=P), c_all[:]).then_inc(c_kept, 16)

        @block.tensor
        def _(pe):
            pe.wait_ge(s.placed.sem, s.placed.at(0, 1))
            pe.matmul(ps[0][:, 0:n8], tri[:], flat(chosen[:]), start=True, stop=True)
            pe.matmul(ps[1][:, 0:n8], ones_bf[:], flat(chosen[:]), start=True, stop=True).then_inc(s.sums_psum.sem, 1)
            pe.wait_ge(s.placed.sem, s.placed.at(0, 2))
            for i in range(ITEMS):
                mm = pe.matmul(ps[2][:, 0:2 * n_tiles], in_row[:, i, :], place[:, i, :, :].rearrange("p c n -> p (c n)"),
                               start=i == 0, stop=i == ITEMS - 1)
            mm.then_inc(s.prep_psum.sem, 1)

        @block.vector
        def _(v):
            dve.begin(v)
            v.wait_ge(given.loaded, given.all)
            v.memset(ones_bf[:], 1.0)
            v.tensor_copy(tri[:], tri32[:]).then_inc(s.placed.sem, 1)
            v.wait_ge(s.sums_psum.sem, s.sums_psum.at(0))
            dve.link(v.tensor_copy(flat(scan[:, 0, :, :]), ps[1][:, 0:n8]))
            step, at = 1, 0
            while step < ALL_TILES:
                v.tensor_copy(scan[:, 1 - at, 0:step, :], scan[:, at, 0:step, :])
                dve.link(v.tensor_tensor(scan[:, 1 - at, step:, :], scan[:, at, step:, :], scan[:, at, 0:ALL_TILES - step, :], ALU.add))
                step, at = 2 * step, 1 - at
            count = scan[:, at, ALL_TILES - 1, :]
            dve.link(v.tensor_tensor(flat(rank[:]), flat(scan[:, at, :, :]), ps[1][:, 0:n8], ALU.subtract))
            dve.link(v.tensor_tensor(flat(rank[:]), ps[0][:, 0:n8], flat(rank[:]), ALU.add))
            by_item = lambda a: a.unsqueeze(2).broadcast_to((P, ALL_TILES, CHOICES, E8))
            if dropping:
                dve.link(v.scalar_tensor_tensor(comb[:], rank[:], float(CAPACITY), comb[:], ALU.is_le, ALU.mult))
                dve.link(v.tensor_reduce(weight[:], comb[:], AX.X, ALU.add))
                dve.link(v.tensor_scalar(weight[:], weight[:], 1e-6, None, ALU.add))
                dve.link(v.reciprocal(weight[:], weight[:]))
                dve.link(v.tensor_tensor(comb[:], comb[:], weight[:].unsqueeze(2).broadcast_to((P, ALL_TILES, E8)), ALU.mult))
                dve.link(v.tensor_tensor(scan[:, 0, :, :], rank[:], const[:, of_base].unsqueeze(1).broadcast_to((P, ALL_TILES, E8)), ALU.add))
                dve.link(v.scalar_tensor_tensor(rank[:], rank[:], float(CAPACITY), scan[:, 0, :, :], ALU.is_le, ALU.mult))
            else:
                dve.link(v.tensor_tensor(filled[:], count.unsqueeze(2).broadcast_to((P, E8, ALL_TILES)),
                                         const[:, of_p][:, 0:ALL_TILES].unsqueeze(1).broadcast_to((P, E8, ALL_TILES)), ALU.is_gt))
                dve.link(v.tensor_reduce(base[:], filled[:], AX.X, ALU.add))
                dve.link(v.tensor_copy(ends[:, 0, :], base[:]))
                step, at = 1, 0
                while step < E8:
                    v.tensor_copy(ends[:, 1 - at, 0:step], ends[:, at, 0:step])
                    dve.link(v.tensor_tensor(ends[:, 1 - at, step:], ends[:, at, step:], ends[:, at, 0:E8 - step], ALU.add))
                    step, at = 2 * step, 1 - at
                dve.link(v.tensor_tensor(base[:], ends[:, at, :], base[:], ALU.subtract))
                dve.link(v.tensor_scalar(base[:], base[:], float(P), None, ALU.mult))
                dve.link(v.tensor_tensor(rank[:], rank[:], base[:].unsqueeze(1).broadcast_to((P, ALL_TILES, E8)), ALU.add))
                dve.link(v.tensor_scalar(ends[:, 1 - at, :], ends[:, at, :], float(P), None, ALU.mult))
                dve.link(v.tensor_tensor(past[:], const[:, of_p][:, 0:n_tiles].unsqueeze(2).broadcast_to((P, n_tiles, E8)),
                                         ends[:, 1 - at, :].unsqueeze(1).broadcast_to((P, n_tiles, E8)), ALU.is_ge))
                dve.link(v.tensor_reduce(expert_f[:], past[:], AX.X, ALU.add))
                v.tensor_scalar(expert_of[:], expert_f[:], float(E8 - 1), None, ALU.min)
            dve.link(v.tensor_tensor(prod[:], hots[:], by_item(rank[:]), ALU.mult))
            dve.link(v.tensor_reduce(slot[:].rearrange("p (t c) -> p t c", c=CHOICES), prod[:], AX.X, ALU.add))
            dve.link(v.tensor_tensor(prod[:], hots[:], by_item(comb[:]), ALU.mult))
            v.tensor_reduce(weights[:].rearrange("p (t c) -> p t c", c=CHOICES), prod[:], AX.X, ALU.add)
            dve.link(v.tensor_tensor(above[:], slot[:].unsqueeze(2).broadcast_to((P, ITEMS, n_tiles + 1)),
                                     const[:, of_p][:, 0:n_tiles + 1].unsqueeze(1).broadcast_to((P, ITEMS, n_tiles + 1)), ALU.is_gt))
            v.tensor_tensor(in_tile[:], above[:, :, 0:n_tiles], above[:, :, 1:], ALU.subtract)
            dve.link(v.tensor_reduce(high[:], above[:], AX.X, ALU.add))
            dve.link(v.tensor_scalar(high[:], high[:], -float(P), float(P - 1), ALU.mult, ALU.add))
            dve.link(v.tensor_tensor(low[:], slot[:], high[:], ALU.add))
            v.tensor_tensor(in_row[:], low[:].unsqueeze(2).broadcast_to((P, ITEMS, P)),
                            const[:, to_p].unsqueeze(1).broadcast_to((P, ITEMS, P)), ALU.is_equal)
            v.tensor_scalar(place[:, :, 0, :], in_tile[:], p_col[:], None, ALU.mult)
            v.tensor_tensor(place[:, :, 1, :], in_tile[:], const[:, of_item].unsqueeze(2).broadcast_to((P, ITEMS, n_tiles)), ALU.mult)\
             .then_inc(s.placed.sem, 1)
            v.tensor_scalar(back[:], slot[:], -1.0, 0.0, ALU.add, ALU.max)
            v.wait_ge(s.prep_psum.sem, s.prep_psum.at(0))
            dve.link(v.tensor_copy(token_f[:], ps[2][:, 0:n_tiles]))
            v.scalar_tensor_tensor(token[:], ps[2][:, n_tiles:2 * n_tiles], float(P), token_f[:], ALU.mult, ALU.add)
    end(1, s.sums_psum, s.prep_psum)
    s.placed.base += 2

    three = (s.row_copied, s.rowT_psum, s.rowT_ready, s.up_psum, s.upT_ready, s.down_psum, s.y_copied)\
        + (() if dropping else (s.up_w_ready,))
    begin(WIDTH, *three)
    stored = (s.y_stored0, s.y_stored1, s.y_stored2)
    begin(16, *stored)

    def expert(pe, m):
        if dropping:
            return m.turn
        return pe.value_load(expert_of[0:1, bass.ds(m.turn * WIDTH + m.j, 1)], min_val=0, max_val=E8 - 1)

    with nc.Block() as block:
        @block.gpsimd
        def _(p):
            p.wait_ge(c_kept, 16)
            for g in range(3):
                for t in range(until[g], until[g + 1]):
                    p.indirect_dma_start(rows[:, t, :], None, c_rows, bass.IndirectOffsetOnAxis(ap=token[:, t:t + 1], axis=0))\
                     .then_inc(gathered[g], 16)

        @block.sync
        def _(sp):
            with sp.Fori(0, turns) as turn:
                for j in range(WIDTH):
                    sp.wait_ge(s.y_copied.sem, s.y_copied.at(turn, j + 1))
                    sp.dma_start(y_rows.rearrange("(t p) d -> p t d", p=P)[:, bass.ds(turn * WIDTH + j, 1), :].rearrange("p t d -> p (t d)"),
                                 y[:, j, :]).then_inc(stored[j].sem, 16)

        @block.tensor
        def _(pe):
            def row_transposed(m):
                pe.wait_ge(s.row_copied.sem, s.row_copied.at(m.turn, m.k))
                pe.wait_ge(s.rowT_ready.sem, s.rowT_ready.at(m.turn, m.k - 1))
                for ch in range(DCH):
                    mm = pe.transpose(ps[6][:, ch * P:(ch + 1) * P], row[:, m.j, ch * P:(ch + 1) * P], e.ident[:])
                mm.then_inc(s.rowT_psum.sem, 1)

            def up_product(m):
                pe.wait_ge(s.upT_ready.sem, s.upT_ready.at(m.turn, m.k - WIDTH))
                pe.wait_ge(s.rowT_ready.sem, s.rowT_ready.at(m.turn, m.k))
                if not dropping:
                    pe.wait_ge(s.up_w_ready.sem, s.up_w_ready.at(m.turn, m.k))
                for f in range(MCH):
                    for ch in range(DCH):
                        at = ch * MOE_HID + f * P
                        w = up_weight[:, ch, f * P:(f + 1) * P] if dropping else up_w[:, m.j, at:at + P]
                        mm = pe.matmul(ps[m.j][:, f * P:(f + 1) * P], w, rowT[:, m.j, ch, :], start=(f, ch) == (0, 0), stop=ch == DCH - 1,
                                       skip_group_check=True)
                mm.then_inc(s.up_psum.sem, 1)

            def down_product(m):
                x = expert(pe, m)
                pe.wait_ge(s.y_copied.sem, s.y_copied.at(m.turn, m.k - WIDTH))
                pe.wait_ge(s.upT_ready.sem, s.upT_ready.at(m.turn, m.k))
                for f in range(MCH):
                    mm = pe.matmul(ps[3 + m.j][:, 0:D], upT[:, m.j, f, :], down_weight(x, f), start=f == 0, stop=f == MCH - 1)
                mm.then_inc(s.down_psum.sem, 1)

            def first(new, after):
                row_transposed(new)
                row_transposed(after)
                up_product(new)

            def step(now, new, after):
                if new:
                    up_product(new)
                if after:
                    row_transposed(after)
                down_product(now)

            pipeline(pe, e.chain["pe"], turns, WIDTH, Slots, first, step)

        @block.scalar
        def _(act_):
            def copy_rowT(m):
                act_.wait_ge(s.rowT_psum.sem, s.rowT_psum.at(m.turn, m.k))
                act_.wait_ge(s.up_psum.sem, s.up_psum.at(m.turn, m.k - WIDTH))
                nc.scalar.copy(flat(rowT[:, m.j, :, :]), ps[6][:, 0:D]).then_inc(s.rowT_ready.sem, 1)

            def silu(m):
                act_.wait_ge(s.up_psum.sem, s.up_psum.at(m.turn, m.k))
                act_.wait_ge(s.down_psum.sem, s.down_psum.at(m.turn, m.k - WIDTH))
                nc.scalar.activation(flat(upT[:, m.j, :, :]), ps[m.j], ACT.Silu).then_inc(s.upT_ready.sem, 1)

            def copy_y(m):
                act_.wait_ge(s.down_psum.sem, s.down_psum.at(m.turn, m.k))
                act_.wait_ge(stored[m.j].sem, stored[m.j].at(m.turn, 0))
                nc.scalar.copy(y[:, m.j, :], ps[3 + m.j][:, 0:D]).then_inc(s.y_copied.sem, 1)

            def first(new, after):
                copy_rowT(new)
                copy_rowT(after)
                silu(new)

            def step(now, new, after):
                if new:
                    silu(new)
                if after:
                    copy_rowT(after)
                copy_y(now)

            pipeline(act_, e.chain["act"], turns, WIDTH, Slots, first, step)

        @block.vector
        def _(v):
            def copy_row(m):
                v.wait_ge(s.rowT_psum.sem, s.rowT_psum.at(m.turn, m.k - WIDTH))
                v.tensor_copy(row[:, m.j, :], flat(rows[:, bass.ds(m.turn * WIDTH + m.j, 1), :])).then_inc(s.row_copied.sem, 1)

            def copy_weights(m):
                if not dropping:
                    x = v.value_load(expert_of[0:1, bass.ds(m.turn * WIDTH + m.j, 1)], min_val=0, max_val=E8 - 1)
                    v.wait_ge(s.up_psum.sem, s.up_psum.at(m.turn, m.k - WIDTH))
                    v.tensor_copy(up_w[:, m.j, :], up_weight(x)).then_inc(s.up_w_ready.sem, 1)

            def first(new, after):
                copy_weights(new)
                copy_weights(after)
                copy_row(new)
                copy_row(after)

            def step(now, new, after):
                if after:
                    copy_row(after)
                    copy_weights(after)

            def wait_rows(g):
                v.wait_ge(gathered[g], 16 * (until[g + 1] - until[g]))

            pipeline(v, dve, turns, WIDTH, Slots, first, step, cuts, wait_rows)
    end(turns, *three, *stored)

    if with_stats:
        begin(2, s.ln_var, s.ln_rstd)
    per = TILES // len(returned)
    with nc.Block() as block:
        @block.gpsimd
        def _(p):
            for one in stored:
                p.wait_ge(one.sem, one.base)
            for g in range(len(returned)):
                for t in range(g * per, (g + 1) * per):
                    for b in range(BATCH):
                        for c in range(CHOICES):
                            i = (t + b * TILES) * CHOICES + c
                            p.indirect_dma_start(rows[:, i, :], None, y_rows, bass.IndirectOffsetOnAxis(ap=back[:, i:i + 1], axis=0))\
                             .then_inc(returned[g], 16)
            if with_stats:
                with p.Fori(0, TILES) as it:
                    for b in range(BATCH):
                        stats_pool(e, p, it, b)

        @block.vector
        def _(v):
            for g in range(len(returned)):
                v.wait_ge(returned[g], 16 * per * BATCH * CHOICES)
                with v.Fori(g * per, (g + 1) * per) as it:
                    dve.begin(v)
                    for b in range(BATCH):
                        for c in range(CHOICES):
                            i = (it + b * TILES) * CHOICES + c
                            dve.link(v.scalar_tensor_tensor(tile_of(e.x, it, b), flat(rows[:, bass.ds(i, 1), :]), weights[:, bass.ds(i, 1)],
                                                            tile_of(e.x, it, b), ALU.mult, ALU.add))
                        if with_stats:
                            stats_dve(e, v, it, b)
    if with_stats:
        end(TILES, s.ln_var, s.ln_rstd)


def l1_ffn_ahead(e, ctx):
    return Moe(e, ctx, "l1_ffn", "L1_router", ("gate", [P, DCH, MOE_HID], "L1_gate"), ("down", [P, MCH, EXPERTS, D], "L1_down"))


def l1_ffn(e, given):
    w_gate, w_down = given.weights
    with ExitStack() as ctx:
        routed = route(e, ctx, "l1_route", given, True)
        experts(e, ctx, "l1_experts", given, routed, DROPPING_TILES, True, w_gate, lambda x, f: flat(w_down[:, f, bass.ds(x, 1), :]), True)


PARTS = 3
XH, XD = 16, 16


class Xattn(Ahead):

    def __init__(self, e, ctx, name, biased, before=None):
        sb = memory(e, ctx, name + "in")
        names = ("wk", "wv", "wq", "wo")
        self.own_head = before.own_head if before else sb("own_head", [P, XH // 2])
        self.matrices = before.matrices if before else [sb(n, [P, DCH, D]) for n in names]
        self.wk, self.wv, self.wq, self.wo = self.matrices
        given = [(self.own_head, "own_head")] + [(w, name + n) for w, n in zip(self.matrices, names)]
        if biased:
            self.bq = sb("bq", [P, DCH])
            self.bk = sb("bk", [P, DCH])
            self.bv = sb("bv", [P, D])
            self.bo = sb("bo", [P, D])
            given += [(self.bq, name + "bq"), (self.bk, name + "bk"), (self.bv, name + "bv"), (self.bo, name + "bo")]
        else:
            self.slopes = sb("slopes", [BATCH * XH, 1])
            self.key_pos = sb("key_pos", [BATCH * XH, CTX], I32)
            self.query_pos = sb("query_pos", [ALL_TILES, P], I32)
            self.mask_i = sb("mask_i", [P, ALL_TILES, CTX], I32)
            given += [(self.slopes, "slopes"), (self.key_pos, "key_pos"), (self.query_pos, "query_pos"), (self.mask_i, "mask_if1")]
        super().__init__(e, name + "xattn", given)


def cross_attention(e, name, biased, sink, given, *following):
    nc, s, ps = e.nc, e.s, e.ps
    dve = e.chain["dve"]
    with ExitStack() as ctx:
        sb = memory(e, ctx, name)
        HALF_XH = XH // 2
        wq, wk, wv, wo, own_head = given.wq, given.wk, given.wv, given.wo, given.own_head
        keysT = sb("keysT", [P, DCH, BATCH, CTX])
        keys = sb("keys", [P, DCH, BATCH, HALF_XH, CTX])
        qT = sb("qT", [P, BATCH, DCH, P])
        V1 = sb("V1", [P, BATCH, HALF_XH, 2, XD + 1])
        MIX = XH * (XD + 1)
        probs = sb("probs", [P, BATCH, XH, CTX])
        probsT = sb("probsT", [P, BATCH, HALF_XH, P])
        top = sb("top", [P, BATCH, XH])
        den = sb("den", [P, BATCH, XH])
        rec = sb("rec", [P, BATCH, XH])
        o = sb("o", [P, BATCH, D])
        oT = sb("oT", [P, BATCH, DCH, P])
        if biased:
            bq, bk, bv, bo = given.bq, given.bk, given.bv, given.bo
        else:
            ROWS = PARTS * PARTS + PARTS
            BH = BATCH * XH
            slopes, key_pos, query_pos, mask_i = given.slopes, given.key_pos, given.query_pos, given.mask_i
            pos_f = sb("pos_f", [BH, P])
            rest = sb("rest", [BH, P])
            slope_f = sb("slope_f", [BH, CTX])
            query_parts = sb("query_parts", [ALL_TILES, PARTS, P], BF16)
            slope_parts = sb("slope_parts", [BH, PARTS, CTX], BF16)
            key_parts = sb("key_parts", [BH, PARTS, CTX], BF16)
            query_rows = sb("query_rows", [ROWS, ALL_TILES, P], BF16)
            key_rows = sb("key_rows", [ROWS, BATCH, XH, CTX], BF16)
            mask = sb("mask", [P, ALL_TILES, CTX], BF16)
            of_query = nc.dram_tensor("query_parts", (PARTS, ALL_TILES, P), BF16).ap()
            of_slope = nc.dram_tensor("slope_parts", (PARTS, BH, CTX), BF16).ap()
            of_key = nc.dram_tensor("key_parts", (PARTS, BH, CTX), BF16).ap()
            parts_stored, rows_loaded = e.dma_sem("parts_stored"), e.dma_sem("rows_loaded")
        begin(1, s.prep_psum, s.prep_ready, s.ones_set)
        with nc.Block() as block:
            @block.sync
            def _(sp):
                load_ahead(e, sp, *following)
                if not biased:
                    sp.wait_ge(s.prep_ready.sem, s.prep_ready.at(0))
                    for to, of in ((of_query, query_parts), (of_slope, slope_parts), (of_key, key_parts)):
                        sp.dma_start(to.rearrange("i r n -> r i n"), of[:]).then_inc(parts_stored, 16)
                    sp.wait_ge(s.ones_set.sem, s.ones_set.at(0))
                    sp.wait_ge(parts_stored, 3 * 16)
                    for j in range(PARTS):
                        own = slice(PARTS * j, PARTS * (j + 1))
                        sp.dma_start(query_rows[own].rearrange("i t p -> i (t p)"), of_query.rearrange("i t p -> i (t p)"))\
                          .then_inc(rows_loaded, 16)
                        sp.dma_start(key_rows[own].rearrange("i b h n -> i (b h n)"),
                                     of_slope[j:j + 1].rearrange("i r n -> i (r n)").broadcast_to((PARTS, BH * CTX))).then_inc(rows_loaded, 16)
                    sp.dma_start(key_rows[PARTS * PARTS:ROWS].rearrange("i b h n -> i (b h n)"), of_key.rearrange("i r n -> i (r n)"))\
                      .then_inc(rows_loaded, 16)

            @block.gpsimd
            def _(p):
                if not biased:
                    p.memset(query_rows[:], 1.0).then_inc(s.ones_set.sem, 1)

            @block.tensor
            def _(pe):
                pe.wait_ge(given.loaded, given.all)
                for half in range(2):
                    for ch in range(DCH):
                        pe.matmul(ps[0][:, half * P:(half + 1) * P], wk[:, ch, half * P:(half + 1) * P],
                                  e.ctxT[:, ch, :, :], start=(half, ch) == (0, 0), stop=ch == DCH - 1, skip_group_check=True)
                for b in range(BATCH):
                    for ch in range(DCH):
                        mm = pe.matmul(ps[4][:, b * D:(b + 1) * D], e.ctxT2[:, ch, b, :, :], wv[:, ch, :],
                                       start=(b, ch) == (0, 0), stop=ch == DCH - 1, skip_group_check=True)
                mm.then_inc(s.prep_psum.sem, 1)

            @block.vector
            def _(v):
                dve.begin(v)
                if not biased:
                    def in_parts(parts, of, left):
                        for i in range(PARTS):
                            dve.link(v.tensor_copy(parts[:, i, :], of))
                            if i < PARTS - 1:
                                dve.link(v.tensor_tensor(left, of, parts[:, i, :], ALU.subtract))
                                of = left

                    v.wait_ge(given.loaded, given.all)
                    dve.link(v.tensor_copy(pos_f[0:ALL_TILES, :], query_pos[:]))
                    in_parts(query_parts, pos_f[0:ALL_TILES, :], rest[0:ALL_TILES, :])
                    dve.link(v.tensor_scalar(slope_f[:], slopes[:].broadcast_to((BH, CTX)), -1.0, None, ALU.mult))
                    in_parts(slope_parts, slope_f[:], rest[:, 0:CTX])
                    dve.link(v.tensor_copy(pos_f[:, 0:CTX], key_pos[:]))
                    dve.link(v.tensor_scalar(pos_f[:, 0:CTX], pos_f[:, 0:CTX], slopes[:, 0:1], None, ALU.mult))
                    in_parts(key_parts, pos_f[:, 0:CTX], rest[:, 0:CTX])
                dve.link(v.memset(V1[:], 0.0))
                for half in range(2):
                    ones = v.memset(V1[half * CTX:(half + 1) * CTX, :, :, half, XD:], 1.0)
                ones.then_inc(s.prep_ready.sem, 1)
                v.wait_ge(s.prep_ready.sem, s.prep_ready.at(0))
                v.wait_ge(given.loaded, given.all)
                if not biased:
                    v.tensor_scalar(mask[:], mask_i[:], 0.0, MASKED, ALU.is_equal, ALU.mult)
                v.wait_ge(s.prep_psum.sem, s.prep_psum.at(0))
                kp = ps[0][:, 0:D].rearrange("p (a n) -> p a n", n=P)
                kt = keysT[:].rearrange("p a b n -> p a (b n)")
                if biased:
                    dve.link(v.tensor_tensor(kt, kp, bk[:].unsqueeze(2).broadcast_to((P, DCH, P)), ALU.add))
                else:
                    dve.link(v.tensor_copy(kt, kp))
                for half in range(2):
                    for b in range(BATCH):
                        v.tensor_tensor(keys[:, half, b, :, :], keysT[:, half, b, :].unsqueeze(1).broadcast_to((P, HALF_XH, CTX)),
                                        own_head[:].unsqueeze(2).broadcast_to((P, HALF_XH, CTX)), ALU.mult)
                for b in range(BATCH):
                    for half in range(2):
                        r = slice(half * CTX, (half + 1) * CTX)
                        of = ps[4][r, b * D:(b + 1) * D].rearrange("p (h two x) -> p h two x", two=2, x=XD)[:, :, half, :]
                        to = V1[r, b, :, half, 0:XD]
                        if biased:
                            v.tensor_tensor(to, of, bv[r, :].rearrange("p (h two x) -> p h two x", two=2, x=XD)[:, :, half, :], ALU.add)
                        else:
                            v.tensor_copy(to, of)
        end(1, s.prep_psum, s.prep_ready)
        if not biased:
            end(1, s.ones_set)

        two = (s.c_ready, s.cT_psum, s.cT_ready, s.scores_psum, s.max_ready, s.probs_ready, s.probsT_psum, s.probsT_ready,
               s.mix_psum, s.mix_ready, s.mixT_psum, s.mixT_ready, s.out_psum, s.ln_var, s.ln_rstd,
               s.q_psum, s.q_ready) + ((s.bias_added,) if biased else ())
        begin(2, *two)

        BANKS = 4
        with nc.Block() as block:
            @block.tensor
            def _(pe):
                if not biased:
                    pe.wait_ge(rows_loaded, (2 * PARTS + 1) * 16)

                def transposed(m):
                    pe.wait_ge(s.q_ready.sem, s.q_ready.before(m.it, m.k))
                    transpose_c(e, pe, m.it, m.b, BANKS * m.b)

                def queries(m):
                    pe.wait_ge(s.cT_ready.sem, s.cT_ready.at(m.it, m.k))
                    for half in range(2):
                        for ch in range(DCH):
                            mm = pe.matmul(ps[BANKS * m.b][:, D + half * P:D + (half + 1) * P], wq[:, ch, half * P:(half + 1) * P], e.cT[:, m.b, ch, :],
                                           start=(half, ch) == (0, 0), stop=ch == DCH - 1, skip_group_check=True)
                    mm.then_inc(s.q_psum.sem, 1)

                def scores(m):
                    pe.wait_ge(s.q_ready.sem, s.q_ready.at(m.it, m.k))
                    pe.wait_ge(s.probsT_ready.sem, s.probsT_ready.before(m.it, m.k))
                    for half in range(2):
                        bank = ps[BANKS * m.b + 2 + half]
                        mm = pe.matmul(bank, qT[:, m.b, half, :], keys[:, half, m.b, :, :].rearrange("p h n -> p (h n)"), start=True, stop=biased)
                        if not biased:
                            tile = bass.ds(m.it + m.b * TILES, 1)
                            pe.matmul(bank, e.ident_bf[:], mask[:, tile, :].broadcast_to((P, HALF_XH, CTX)), start=False, stop=False)
                            mm = pe.matmul(bank, flat(query_rows[:, tile, :]),
                                           key_rows[:, m.b, half * HALF_XH:(half + 1) * HALF_XH, :].rearrange("p h n -> p (h n)"),
                                           start=False, stop=True)
                    mm.then_inc(s.scores_psum.sem, 1)

                def probs_transposed(m):
                    pe.wait_ge(s.probs_ready.sem, s.probs_ready.at(m.it, m.k))
                    for j in range(XH // 2):
                        mm = pe.transpose(ps[BANKS * m.b + 2 + j // 4][:, (j % 4) * P:(j % 4 + 1) * P],
                                          probs[:, m.b, 2 * j:2 * j + 2, :].rearrange("p h n -> p (h n)"), e.ident[:])
                    mm.then_inc(s.probsT_psum.sem, 1)

                def mix(m):
                    pe.wait_ge(s.probsT_ready.sem, s.probsT_ready.at(m.it, m.k))
                    pe.wait_ge(s.ln_var.sem, s.ln_var.before(m.it, m.k))
                    for j in range(XH // 2):
                        mm = pe.matmul(ps[BANKS * m.b + 1][:, j * 2 * (XD + 1):(j + 1) * 2 * (XD + 1)], probsT[:, m.b, j, :], flat(V1[:, m.b, j, :, :]),
                                       start=j == 0, stop=True, skip_group_check=True)
                    mm.then_inc(s.mix_psum.sem, 1)

                def mix_transposed(m):
                    pe.wait_ge(s.mix_ready.sem, s.mix_ready.at(m.it, m.k))
                    for ch in range(DCH):
                        mm = pe.transpose(ps[BANKS * m.b + 1][:, ch * P:(ch + 1) * P], o[:, m.b, ch * P:(ch + 1) * P], e.ident[:])
                    mm.then_inc(s.mixT_psum.sem, 1)

                def projected(m):
                    pe.wait_ge(s.mixT_ready.sem, s.mixT_ready.at(m.it, m.k))
                    bank = ps[BANKS * m.b + 1][:, D:2 * D]
                    for ch in range(DCH):
                        mm = pe.matmul(bank, oT[:, m.b, ch, :], wo[:, ch, :], start=ch == 0, stop=ch == DCH - 1)
                    mm.then_inc(s.out_psum.sem, 1)

                def first(one, two, three):
                    transposed(one)
                    transposed(two)
                    queries(one)
                    queries(two)
                    scores(one)
                    transposed(three)
                    scores(two)
                    probs_transposed(one)
                    queries(three)
                    mix(one)

                def step(one, two, three, four):
                    if three:
                        scores(three)
                    mix_transposed(one)
                    if four:
                        transposed(four)
                    if two:
                        probs_transposed(two)
                    projected(one)
                    if four:
                        queries(four)
                    if two:
                        mix(two)

                tiles(pe, e.chain["pe"], first, step, depth=4)

            @block.scalar
            def _(act_):
                def exp(m):
                    act_.wait_ge(s.max_ready.sem, s.max_ready.at(m.it, m.k))
                    nc.scalar.activation(flat(probs[:, m.b, :, :]), flat(probs[:, m.b, :, :]), ACT.Exp, scale=float(XD) ** -0.5)\
                      .then_inc(s.probs_ready.sem, 1)

                def copy_probsT(m):
                    act_.wait_ge(s.probsT_psum.sem, s.probsT_psum.at(m.it, m.k))
                    act_.wait_ge(s.mix_psum.sem, s.mix_psum.before(m.it, m.k))
                    nc.scalar.copy(flat(probsT[:, m.b, :, :]), flat(e.psum[:, BANKS * m.b + 2:BANKS * m.b + 4, :])).then_inc(s.probsT_ready.sem, 1)

                def copy_oT(m):
                    act_.wait_ge(s.mixT_psum.sem, s.mixT_psum.at(m.it, m.k))
                    act_.wait_ge(s.out_psum.sem, s.out_psum.before(m.it, m.k))
                    nc.scalar.copy(flat(oT[:, m.b, :, :]), ps[BANKS * m.b + 1][:, 0:D]).then_inc(s.mixT_ready.sem, 1)

                def copy_qT(m):
                    act_.wait_ge(s.q_psum.sem, s.q_psum.at(m.it, m.k))
                    act_.wait_ge(s.scores_psum.sem, s.scores_psum.before(m.it, m.k))
                    of = ps[BANKS * m.b][:, D:2 * D]
                    if biased:
                        nc.scalar.activation(qT[:, m.b, 0, :], of[:, 0:P], ACT.Identity, bias=bq[:, 0:1])
                        nc.scalar.activation(qT[:, m.b, 1, :], of[:, P:D], ACT.Identity, bias=bq[:, 1:2]).then_inc(s.q_ready.sem, 1)
                    else:
                        nc.scalar.copy(flat(qT[:, m.b, :, :]), of).then_inc(s.q_ready.sem, 1)

                def copy_c(m):
                    copy_cT(e, act_, m.it, m.b, BANKS * m.b, s.q_psum)

                def first(one, two, three):
                    copy_c(one)
                    copy_c(two)
                    copy_qT(one)
                    copy_qT(two)
                    copy_c(three)
                    exp(one)
                    copy_probsT(one)
                    copy_qT(three)
                    exp(two)

                def step(one, two, three, four):
                    copy_oT(one)
                    if four:
                        copy_c(four)
                    if two:
                        copy_probsT(two)
                    if four:
                        copy_qT(four)
                    if three:
                        exp(three)

                tiles(act_, e.chain["act"], first, step, depth=4)

            @block.vector
            def _(v):
                def scores_of(m):
                    return e.psum[:, BANKS * m.b + 2:BANKS * m.b + 4, :].rearrange("p a (h n) -> p (a h) n", n=CTX)

                def maxima(m):
                    v.wait_ge(s.scores_psum.sem, s.scores_psum.at(m.it, m.k))
                    dve.link(v.tensor_reduce(top[:, m.b, :], scores_of(m), AX.X, ALU.max))

                def subtract(m):
                    v.wait_ge(s.probsT_psum.sem, s.probsT_psum.before(m.it, m.k))
                    v.tensor_tensor(probs[:, m.b, :, :], scores_of(m), top[:, m.b, :].unsqueeze(2).broadcast_to((P, XH, CTX)), ALU.subtract)\
                     .then_inc(s.max_ready.sem, 1)

                def weighted(m):
                    mixed = ps[BANKS * m.b + 1][:, 0:MIX].rearrange("p (h x) -> p h x", x=XD + 1)
                    v.wait_ge(s.mix_psum.sem, s.mix_psum.at(m.it, m.k))
                    of = mixed[:, :, XD]
                    if sink:
                        dve.link(v.tensor_scalar(den[:, m.b, :], of, 1.0, None, ALU.add))
                        of = den[:, m.b, :]
                    dve.link(v.reciprocal(rec[:, m.b, :], of))
                    v.wait_ge(s.mixT_psum.sem, s.mixT_psum.before(m.it, m.k))
                    v.tensor_tensor(o[:, m.b, :].rearrange("p (h x) -> p h x", x=XD), mixed[:, :, 0:XD],
                                    rec[:, m.b, :].unsqueeze(2).broadcast_to((P, XH, XD)), ALU.mult).then_inc(s.mix_ready.sem, 1)

                def normal(m):
                    normalise(e, v, m.it, m.b)

                def softmax(m):
                    maxima(m)
                    subtract(m)

                def add(m):
                    v.wait_ge(s.out_psum.sem, s.out_psum.at(m.it, m.k))
                    if biased:
                        v.wait_ge(s.bias_added.sem, s.bias_added.at(m.it, m.k))
                    add_to_x(e, v, m.it, m.b, ps[BANKS * m.b + 1][:, D:2 * D])

                def first(one, two, three):
                    normal(one)
                    normal(two)
                    softmax(one)
                    normal(three)
                    softmax(two)

                def step(one, two, three, four):
                    weighted(one)
                    if four:
                        normal(four)
                    if three:
                        softmax(three)
                    add(one)

                tiles(v, e.chain["dve"], first, step, depth=4)

            @block.gpsimd
            def _(p):
                with p.Fori(0, TILES) as it:
                    if biased:
                        for b in range(BATCH):
                            p.wait_ge(s.c_ready.sem, s.c_ready.at(it, b + 1))
                            p.tensor_tensor(tile_of(e.x, it, b), tile_of(e.x, it, b), bo[:], ALU.add).then_inc(s.bias_added.sem, 1)
                    for b in range(BATCH):
                        stats_pool(e, p, it, b)
        end(TILES, *two)


def l2_xattn(e, given, *following):
    cross_attention(e, "L2_", True, False, given, *following)


def l3_xattn(e, given):
    cross_attention(e, "L3_", False, True, given)


QI = 704
QCH = -(-QI // P)
QW = [min(P, QI - j * P) for j in range(QCH)]
QMAX = 127.0
MAGIC = 1.5 * 2.0 ** 23


class L2Ffn(Ahead):

    def __init__(self, e, ctx):
        sb = memory(e, ctx, "l2_ffn_in")
        self.w_gu = sb("w_gu", [P, 2 * QCH, D])
        self.w_d = sb("w_d", [P, DCH, QI])
        self.clips = sb("clips", [P, 2])
        super().__init__(e, "l2_ffn", ((self.w_gu, "L2_gu"), (self.w_d, "L2_d"), (self.clips, "L2_clips")))


def l2_ffn(e, ffn, *following):
    nc, s, ps = e.nc, e.s, e.ps
    dve = e.chain["dve"]
    w_gu, w_d, clips = ffn.w_gu, ffn.w_d, ffn.clips
    LOW, HIGH = MAGIC - QMAX - 1.0, MAGIC + QMAX
    with ExitStack() as ctx:
        sb = memory(e, ctx, "l2_ffn")
        magic = sb("magic", [P, 1])
        sig = sb("sig", [P, 2])
        gu_scale = sb("gu_scale", [P, 2 * QCH])
        d_scale = sb("d_scale", [P, DCH])
        d_row = sb("d_row", [P, D])
        w_guT = sb("w_guT", [P, DCH, 2, QI], BF16)
        w_dT = sb("w_dT", [P, QCH, D], BF16)
        amax = sb("amax", [P, ALL_TILES])
        one = sb("one_max", [P, 1])
        allmax = sb("allmax", [P, 1])
        xs = sb("xs", [P, 2])
        hmax = sb("hmax", [P, TILES])
        c_all = sb("c_all", [P, ALL_TILES, D])
        with ExitStack() as inner:
            sbi = memory(e, inner, "l2_ffn_weights")
            t_gu = sbi("t_gu", [P, 2 * QCH, D])
            t_d = sbi("t_d", [P, DCH, QI])
            q_gu = sbi("q_gu", [P, 2 * QCH, D], BF16)
            q_d = sbi("q_d", [P, DCH, QI], BF16)
            inv = sbi("inv", [P, 2 * QCH + DCH])
            diag = sbi("diag", [P, DCH, P])
            begin(1, s.probs_ready, s.ones_set, s.inv_ready)
            begin(2, s.scaled, s.clipped)
            with nc.Block() as block:
                @block.sync
                def _(sp):
                    load_ahead(e, sp, *following)

                @block.scalar
                def _(act_):
                    act_.wait_ge(ffn.loaded, ffn.all)
                    nc.scalar.activation(sig[:], clips[:], ACT.Exp, scale=-1.0).then_inc(s.probs_ready.sem, 1)
                    act_.wait_ge(s.inv_ready.sem, s.inv_ready.at(0))
                    act_.wait_ge(s.ones_set.sem, s.ones_set.at(0))
                    for j in range(2 * QCH):
                        sc = nc.scalar.activation(t_gu[:, j, :], w_gu[:, j, :], ACT.Identity, scale=inv[:, j:j + 1], bias=magic[:, 0:1])
                    sc.then_inc(s.scaled.sem, 1)
                    for ch in range(DCH):
                        sc = nc.scalar.activation(t_d[:, ch, :], w_d[:, ch, :], ACT.Identity, scale=inv[:, 2 * QCH + ch:2 * QCH + ch + 1],
                                                  bias=magic[:, 0:1])
                    sc.then_inc(s.scaled.sem, 1)

                @block.vector
                def _(v):
                    dve.begin(v)
                    dve.link(v.memset(inv[:], 1.0))
                    v.wait_ge(ffn.loaded, ffn.all)
                    v.tensor_reduce(gu_scale[:], w_gu[:], AX.X, ALU.max, apply_absolute_value=True)
                    dve.link(v.tensor_reduce(d_scale[:], w_d[:], AX.X, ALU.max, apply_absolute_value=True))
                    v.tensor_scalar(gu_scale[:], gu_scale[:], 1.0 / QMAX, None, ALU.mult)
                    dve.link(v.tensor_scalar(d_scale[:], d_scale[:], 1.0 / QMAX, None, ALU.mult))
                    for n in range(2):
                        v.reciprocal(inv[:, n * QCH:n * QCH + QCH - 1], gu_scale[:, n * QCH:n * QCH + QCH - 1])
                        last = slice(n * QCH + QCH - 1, (n + 1) * QCH)
                        v.reciprocal(inv[0:QW[-1], last], gu_scale[0:QW[-1], last])
                    v.reciprocal(inv[:, 2 * QCH:], d_scale[:]).then_inc(s.inv_ready.sem, 1)
                    with v.Fori(0, TILES) as it:
                        dve.begin(v)
                        for b in range(BATCH):
                            k = it + b * TILES
                            c = v.tensor_scalar(tile_of(c_all, it, b), tile_of(e.x, it, b), flat(e.mean_var[:, bass.ds(k, 1), 0:1]),
                                                e.rstd[:, bass.ds(k, 1)], ALU.subtract, ALU.mult)
                        dve.link(c)
                        for b in range(BATCH):
                            v.tensor_reduce(amax[:, bass.ds(it + b * TILES, 1)], tile_of(c_all, it, b), AX.X, ALU.max, apply_absolute_value=True)
                    dve.begin(v)
                    for n, t in enumerate((t_gu, t_d)):
                        v.wait_ge(s.scaled.sem, s.scaled.at(0, n + 1))
                        v.tensor_scalar(t[:], t[:], LOW, HIGH, ALU.max, ALU.min).then_inc(s.clipped.sem, 1)
                    for ch in range(DCH):
                        v.tensor_scalar(diag[:, ch, :], e.ident[:], d_scale[:, ch:ch + 1], None, ALU.mult)
                    v.wait_ge(s.probs_ready.sem, s.probs_ready.at(0))
                    dve.link(v.tensor_scalar(sig[:], sig[:], 1.0, None, ALU.add))
                    dve.link(v.reciprocal(sig[:], sig[:]))
                    v.tensor_scalar(sig[:], sig[:], 1.0 / QMAX, None, ALU.mult)

                @block.gpsimd
                def _(p):
                    p.memset(magic[:], MAGIC).then_inc(s.ones_set.sem, 1)
                    for n, (q, t) in enumerate(((q_gu, t_gu), (q_d, t_d))):
                        p.wait_ge(s.clipped.sem, s.clipped.at(0, n + 1))
                        p.tensor_scalar(q[:], t[:], -MAGIC, None, ALU.add)
            end(1, s.probs_ready, s.ones_set, s.inv_ready, s.scaled, s.clipped)
            begin(8, s.prep_psum, s.prep_ready)
            begin(1, s.max_ready, s.allreduce)
            with nc.Block() as block:
                @block.tensor
                def _(pe):
                    for n in range(2):
                        for ch in range(DCH):
                            for j in range(QCH):
                                bank = ps[2 * (2 * n + ch) + j // 4]
                                mm = pe.matmul(bank[:, (j % 4) * P:(j % 4) * P + QW[j]], q_gu[0:QW[j], n * QCH + j, ch * P:(ch + 1) * P],
                                               e.ident_bf[0:QW[j], 0:QW[j]], start=j % 4 == 0, stop=True, skip_group_check=True)
                            mm.then_inc(s.prep_psum.sem, 1)
                    pe.wait_ge(s.prep_ready.sem, s.prep_ready.at(0, 4))
                    for j in range(QCH):
                        for ch in range(DCH):
                            mm = pe.matmul(ps[j // 2][0:QW[j], (j % 2) * D + ch * P:(j % 2) * D + (ch + 1) * P], q_d[:, ch, j * P:j * P + QW[j]],
                                           e.ident_bf[:], start=(j % 2, ch) == (0, 0), stop=True, skip_group_check=True)
                    mm.then_inc(s.prep_psum.sem, 1)
                    for ch in range(DCH):
                        mm = pe.matmul(ps[4][:, ch * P:(ch + 1) * P], e.ones[:], diag[:, ch, :], start=ch == 0, stop=True, skip_group_check=True)
                    mm.then_inc(s.prep_psum.sem, 1)

                @block.vector
                def _(v):
                    v.tensor_reduce(one[:], amax[:], AX.X, ALU.max).then_inc(s.max_ready.sem, 1)
                    for n in range(2):
                        for ch in range(DCH):
                            k = 2 * n + ch
                            v.wait_ge(s.prep_psum.sem, s.prep_psum.at(0, k + 1))
                            v.tensor_copy(w_guT[:, ch, n, :], e.psum[:, 2 * k:2 * k + 2, :].rearrange("p a n -> p (a n)")[:, 0:QI])\
                             .then_inc(s.prep_ready.sem, 1)
                    v.wait_ge(s.prep_psum.sem, s.prep_psum.at(0, 5))
                    for j in range(QCH):
                        v.tensor_copy(w_dT[0:QW[j], j, :], ps[j // 2][0:QW[j], (j % 2) * D:(j % 2 + 1) * D])
                    v.wait_ge(s.prep_psum.sem, s.prep_psum.at(0, 6))
                    v.tensor_copy(d_row[:], ps[4][:, 0:D])

                @block.gpsimd
                def _(p):
                    p.wait_ge(s.max_ready.sem, s.max_ready.at(0))
                    p.partition_all_reduce(allmax[:], one[:], P, bass.bass_isa.ReduceOp.max).then_inc(s.allreduce.sem, 1)
            s.prep_psum.base += 6
            s.prep_ready.base += 4
            end(1, s.max_ready, s.allreduce)

        h = sb("h", [P, QCH, ALL_TILES, P])
        gsc = sb("gsc", [P, 2, QCH])
        x_magic = w_gu[:, 0:2 * BATCH, :].rearrange("p (n b) d -> p n b d", b=BATCH)
        xq = sb("xq", [P, 2, BATCH, D], BF16)
        xqT = sb("xqT", [P, 2, BATCH, DCH, P], BF16)
        gate = w_gu[:, 2 * BATCH:2 * BATCH + QCH, :]
        with nc.Block() as block:
            @block.vector
            def _(v):
                dve.begin(v)
                dve.link(v.tensor_scalar(xs[:, 0:1], allmax[:], sig[:, 0:1], None, ALU.mult))
                v.reciprocal(xs[:, 1:2], xs[:, 0:1])
                v.tensor_scalar(flat(gsc[:]), gu_scale[:], xs[:, 0:1], None, ALU.mult)

            @block.gpsimd
            def _(p):
                p.memset(h[:, QCH - 1, :, :], 0.0)

        class Pair:

            def __init__(self, at, n):
                self.it, self.slot, self.turn, self.k = at * 2 + n, n, at, n + 1

            def of(self, buf):
                return buf.rearrange("p (b t) n -> p b t n", b=BATCH)[:, :, bass.ds(self.it, 1), :].rearrange("p b t n -> p b (t n)")

        def pairs(engine, order, first, step):
            pipeline(engine, order, TILES // 2, 2, Pair, first, step)

        two = (s.scaled, s.clipped, s.c_ready, s.cT_psum, s.cT_ready, s.h_max)
        begin(2, *two)
        begin(2 * QCH, s.hidden_psum, s.gate_done, s.hidden_ready)
        with nc.Block() as block:
            @block.tensor
            def _(pe):
                def transposes(m):
                    pe.wait_ge(s.c_ready.sem, s.c_ready.at(m.turn, m.k))
                    pe.wait_ge(s.cT_ready.sem, s.cT_ready.before(m.turn, m.k))
                    for b in range(BATCH):
                        for ch in range(DCH):
                            mm = pe.matmul(ps[m.slot][:, (b * DCH + ch) * P:(b * DCH + ch + 1) * P], xq[:, m.slot, b, ch * P:(ch + 1) * P],
                                           e.ident_bf[:], start=(b, ch) == (0, 0), stop=True, skip_group_check=True)
                    mm.then_inc(s.cT_psum.sem, 1)

                def hidden(m):
                    pe.wait_ge(s.cT_ready.sem, s.cT_ready.at(m.turn, m.k))
                    for j in range(QCH):
                        pe.wait_ge(s.hidden_ready.sem, s.hidden_ready.at(m.turn, QCH * (m.k - 2) + j + 1))
                        for n in range(2):
                            for ch in range(DCH):
                                mm = pe.matmul(ps[2 + j][0:QW[j], n * 2 * P:(n + 1) * 2 * P], w_guT[:, ch, n, j * P:j * P + QW[j]],
                                               xqT[:, m.slot, :, ch, :], start=(n, ch) == (0, 0), stop=ch == DCH - 1, skip_group_check=True)
                        mm.then_inc(s.hidden_psum.sem, 1)

                def first(new, after):
                    transposes(new)

                def step(now, new, after):
                    if new:
                        transposes(new)
                    hidden(now)

                pairs(pe, e.chain["pe"], first, step)

            @block.scalar
            def _(act_):
                def scale(m):
                    act_.wait_ge(s.c_ready.sem, s.c_ready.before(m.turn, m.k))
                    nc.scalar.activation(x_magic[:, m.slot, :, :], m.of(c_all[:]), ACT.Identity, scale=xs[:, 1:2], bias=magic[:, 0:1])\
                      .then_inc(s.scaled.sem, 1)

                def copy(m):
                    act_.wait_ge(s.cT_psum.sem, s.cT_psum.at(m.turn, m.k))
                    act_.wait_ge(s.hidden_psum.sem, s.hidden_psum.before(m.turn, QCH * m.k))
                    nc.scalar.copy(xqT[:, m.slot, :, :, :].rearrange("p b c n -> p (b c n)"), ps[m.slot]).then_inc(s.cT_ready.sem, 1)

                def gates(m):
                    for j in range(QCH):
                        act_.wait_ge(s.hidden_psum.sem, s.hidden_psum.at(m.turn, QCH * (m.k - 1) + j + 1))
                        act_.wait_ge(s.hidden_ready.sem, s.hidden_ready.at(m.turn, QCH * (m.k - 2) + j + 1))
                        nc.scalar.activation(gate[0:QW[j], j, :], ps[2 + j][0:QW[j], 0:2 * P], ACT.Silu, scale=gsc[0:QW[j], 0, j:j + 1])\
                          .then_inc(s.gate_done.sem, 1)

                def first(new, after):
                    scale(new)
                    scale(after)
                    copy(new)

                def step(now, new, after):
                    if after:
                        scale(after)
                    if new:
                        copy(new)
                    gates(now)

                pairs(act_, e.chain["act"], first, step)

            @block.vector
            def _(v):
                def clip(m):
                    v.wait_ge(s.scaled.sem, s.scaled.at(m.turn, m.k))
                    v.tensor_scalar(x_magic[:, m.slot, :, :], x_magic[:, m.slot, :, :], LOW, HIGH, ALU.max, ALU.min).then_inc(s.clipped.sem, 1)

                def product(m):
                    for j in range(QCH):
                        r = slice(0, QW[j])
                        v.wait_ge(s.gate_done.sem, s.gate_done.at(m.turn, QCH * (m.k - 1) + j + 1))
                        v.scalar_tensor_tensor(m.of(h[r, j, :, :]), ps[2 + j][r, 2 * P:4 * P].rearrange("p (b n) -> p b n", b=BATCH),
                                               gsc[r, 1, j:j + 1], gate[r, j, :].rearrange("p (b n) -> p b n", b=BATCH), ALU.mult, ALU.mult)\
                         .then_inc(s.hidden_ready.sem, 1)

                def largest(m):
                    v.wait_ge(s.hidden_ready.sem, s.hidden_ready.at(m.turn, QCH * m.k))
                    of = h[:].rearrange("p j (b t) n -> p j b t n", b=BATCH)[:, :, :, bass.ds(m.it, 1), :].rearrange("p j b t n -> p j b (t n)")
                    v.tensor_reduce(hmax[:, bass.ds(m.it, 1)], of, AX.XYZ, ALU.max, apply_absolute_value=True).then_inc(s.h_max.sem, 1)

                def first(new, after):
                    clip(new)
                    clip(after)

                def step(now, new, after):
                    if after:
                        clip(after)
                    product(now)
                    largest(now)

                pairs(v, dve, first, step)

            @block.gpsimd
            def _(p):
                def rounded(m):
                    p.wait_ge(s.clipped.sem, s.clipped.at(m.turn, m.k))
                    p.wait_ge(s.cT_psum.sem, s.cT_psum.before(m.turn, m.k))
                    p.tensor_tensor(xq[:, m.slot, :, :], x_magic[:, m.slot, :, :], magic[:].unsqueeze(2).broadcast_to((P, BATCH, D)), ALU.subtract).then_inc(s.c_ready.sem, 1)

                def first(new, after):
                    rounded(new)
                    rounded(after)

                def step(now, new, after):
                    if after:
                        rounded(after)

                pairs(p, e.chain["pool"], first, step)
        end(TILES // 2, *two, s.hidden_psum, s.gate_done, s.hidden_ready)

        begin(1, s.max_ready, s.allreduce)
        with nc.Block() as block:
            @block.vector
            def _(v):
                dve.begin(v)
                v.tensor_reduce(one[:], hmax[:], AX.X, ALU.max).then_inc(s.max_ready.sem, 1)
                v.wait_ge(s.allreduce.sem, s.allreduce.at(0))
                dve.link(v.tensor_scalar(xs[:, 0:1], allmax[:], sig[:, 1:2], None, ALU.mult))
                v.reciprocal(xs[:, 1:2], xs[:, 0:1])
                v.tensor_scalar(d_row[:], d_row[:], xs[:, 0:1], None, ALU.mult)

            @block.gpsimd
            def _(p):
                p.wait_ge(s.max_ready.sem, s.max_ready.at(0))
                p.partition_all_reduce(allmax[:], one[:], P, bass.bass_isa.ReduceOp.max).then_inc(s.allreduce.sem, 1)
        end(1, s.max_ready, s.allreduce)

        h_magic = w_gu[:, 0:QCH, :].rearrange("p j d -> p (j d)").rearrange("p (b j n) -> p b j n", b=BATCH, n=P)
        hq = sb("hq", [P, BATCH, QCH, P], BF16)
        out = sb("q_out", [P, BATCH, D])
        two = (s.scaled, s.clipped, s.hidden_ready, s.out_psum, s.ln_var, s.ln_rstd)
        begin(2, *two)
        with nc.Block() as block:
            @block.scalar
            def _(act_):
                def scale(m):
                    act_.wait_ge(s.hidden_ready.sem, s.hidden_ready.before(m.it, m.k))
                    nc.scalar.activation(h_magic[:, m.b, :, :], h[:, :, bass.ds(m.it + m.b * TILES, 1), :].rearrange("p j t n -> p j (t n)"),
                                         ACT.Identity, scale=xs[:, 1:2], bias=magic[:, 0:1]).then_inc(s.scaled.sem, 1)

                def first(new, after):
                    scale(new)
                    scale(after)

                def step(now, new, after):
                    if after:
                        scale(after)

                tiles(act_, e.chain["act"], first, step)

            @block.tensor
            def _(pe):
                def down(m):
                    pe.wait_ge(s.hidden_ready.sem, s.hidden_ready.at(m.it, m.k))
                    pe.wait_ge(s.ln_var.sem, s.ln_var.before(m.it, m.k))
                    for j in range(QCH):
                        mm = pe.matmul(ps[m.b][:, 0:D], hq[0:QW[j], m.b, j, :], w_dT[0:QW[j], j, :], start=j == 0, stop=j == QCH - 1)
                    mm.then_inc(s.out_psum.sem, 1)

                def first(new, after):
                    down(new)

                def step(now, new, after):
                    if new:
                        down(new)

                tiles(pe, e.chain["pe"], first, step)

            @block.vector
            def _(v):
                def clip(m):
                    v.wait_ge(s.scaled.sem, s.scaled.at(m.it, m.k))
                    v.tensor_scalar(h_magic[:, m.b, :, :], h_magic[:, m.b, :, :], LOW, HIGH, ALU.max, ALU.min).then_inc(s.clipped.sem, 1)

                def add(m):
                    v.wait_ge(s.out_psum.sem, s.out_psum.at(m.it, m.k))
                    dve.link(v.tensor_tensor(out[:, m.b, :], ps[m.b][:, 0:D], d_row[:], ALU.mult))
                    add_to_x(e, v, m.it, m.b, out[:, m.b, :])

                def first(new, after):
                    clip(new)
                    clip(after)

                def step(now, new, after):
                    if after:
                        clip(after)
                    add(now)

                tiles(v, dve, first, step)

            @block.gpsimd
            def _(p):
                def rounded(m):
                    p.wait_ge(s.clipped.sem, s.clipped.at(m.it, m.k))
                    p.wait_ge(s.out_psum.sem, s.out_psum.before(m.it, m.k))
                    p.tensor_tensor(hq[:, m.b, :, :], h_magic[:, m.b, :, :], magic[:].unsqueeze(2).broadcast_to((P, QCH, P)), ALU.subtract).then_inc(s.hidden_ready.sem, 1)

                def first(new, after):
                    rounded(new)
                    rounded(after)

                def step(now, new, after):
                    if after:
                        rounded(after)
                    stats_pool(e, p, now.it, now.b)

                tiles(p, e.chain["pool"], first, step)
        end(TILES, *two)


def l3_ffn_ahead(e, ctx):
    return Moe(e, ctx, "l3_ffn", "L3_gate", ("w1", [P, EXPERTS, DCH, MOE_HID], "L3_w1"), ("w2", [P, EXPERTS, MCH, D], "L3_w2"))


def l3_ffn(e, given):
    w1, w2 = given.weights
    with ExitStack() as ctx:
        routed = route(e, ctx, "l3_route", given, False)
        experts(e, ctx, "l3_experts", given, routed, KEEPING_TILES, False, lambda x: w1[:, bass.ds(x, 1), :, :].rearrange("p x c n -> p (x c n)"),
                lambda x, f: w2[:, bass.ds(x, 1), f, :].rearrange("p x n -> p (x n)"), False)


def finish(e):
    with e.nc.Block() as block:
        @block.sync
        def _(sp):
            sp.dma_start(e.out, e.x[:]).then_inc(e.stored, 16)
            sp.wait_ge(e.stored, 16)


def rotary():
    one = np.float32
    half = np.arange(0, DH, 2, dtype=one)
    t = np.arange(SEQ, dtype=one)
    freqs = t[:, None] * (one(1.0) / one(10000.0) ** (half / one(DH)))[None]
    base = (half + one(0.4 * DH)) / one(1.4 * DH)
    scale = base[None] ** ((t - SEQ // 2) / one(P // 2))[:, None]
    cos, sin = np.cos(freqs), np.sin(freqs)
    both = lambda w: np.stack([w * scale, w / scale], 1)
    c, n = both(cos), both(sin)
    parts = np.stack([np.concatenate([c, c], -1), np.concatenate([-n, n], -1)])
    return parts.reshape(2, TILES, P, 2, DH).transpose(2, 0, 1, 3, 4).astype(one)


def laid_out(inp):
    f = {k: np.asarray(v) for k, v in inp.items()}
    rows = lambda w: w.reshape(-1, P, w.shape[-1]).transpose(1, 0, 2)
    ctx = f["ctx_1024"]
    a = {}
    a["x"] = f["x"].reshape(ALL_TILES, P, D).transpose(1, 0, 2)
    a["ident"] = np.eye(P, dtype=np.float32)
    a["ctxT"] = ctx.transpose(2, 0, 1).reshape(DCH, P, BATCH, CTX).transpose(1, 0, 2, 3)
    a["ctx_tok"] = np.concatenate([ctx, ctx], 1).transpose(1, 0, 2)
    a["L0_W_l"] = rows(f["L0_xattn_W_l"].T)
    a["L0_w3"] = rows(np.stack([f["L0_xattn_w_cq"], f["L0_xattn_w_c"], f["L0_xattn_w_q"]], 1))
    a["L0_b3"] = np.tile(np.stack([f["L0_xattn_b_cq"], f["L0_xattn_b_c"], f["L0_xattn_b_q"]])[None], (P, 1))
    a["L0_b_l"] = f["L0_xattn_b_l"][None]
    every = lambda w: np.tile(w[None], (P,) + (1,) * w.ndim)
    per_layer = lambda w: np.stack([rows(w[l]) for l in range(LAYERS)], 1)
    padded = lambda w: np.pad(w, [(0, FCH * P - HID)] + [(0, 0)] * (w.ndim - 1))
    swap = lambda w: np.concatenate([w[..., DH // 2:], w[..., :DH // 2]], -1)
    a["L0_wqkv"] = per_layer(f["L0_ffn_wqkv"])
    a["L0_wo"] = per_layer(f["L0_ffn_wo"])
    a["L0_w1"] = per_layer(f["L0_ffn_w1"]).transpose(1, 0, 2, 3)
    a["L0_w2"] = per_layer(np.stack([padded(w) for w in f["L0_ffn_w2"]]))
    columns = lambda l: np.concatenate([f["L0_ffn_ln_g"][l], f["L0_ffn_ln_b"][l], padded(f["L0_ffn_b1"][l, :HID]),
                                        padded(f["L0_ffn_b1"][l, HID:])]).reshape(-1, P).T
    a["L0_cols"] = np.stack([columns(l) for l in range(LAYERS)], 1)
    a["L0_b2"] = every(f["L0_ffn_b2"])
    scales = np.stack([f["L0_ffn_q_scale"], f["L0_ffn_k_scale"]], 1)
    a["L0_qk_scale"] = every(np.stack([scales, swap(scales)], 1))
    a["rotary"] = rotary()
    a["shift"] = np.stack([np.eye(P, k=1), np.eye(P, k=1 - P)], 1).astype(np.float32)
    q, k = np.arange(P)[:, None], np.arange(P)[None]
    own, before, none = np.where(k <= q, 0, MASKED), np.where(k >= q, 0, MASKED), np.full((P, P), MASKED)
    a["mask"] = np.stack([np.concatenate(m, 1) for m in ((own, none), (own, before), (before, own))], 1).astype(np.float32)
    a["ctxT2"] = np.stack([a["ctxT"], a["ctxT"]], 3)
    a["causal"] = np.where(np.arange(CTX)[None] <= np.arange(P)[:, None], 0, MASKED).astype(np.float32)
    a["tri"] = np.triu(np.ones((P, P), np.float32))
    a["expert_constants"] = every(expert_constants()[0].astype(np.float32))
    a["p_col"] = np.arange(P, dtype=np.float32)[:, None]
    a["expert_number"] = every(np.arange(EXPERTS, dtype=np.float32))
    a["L1_router"] = rows(f["L1_ffn_w_router"].T)
    a["L1_gate"] = rows(f["L1_ffn_w_gate"].T)
    a["L1_down"] = f["L1_ffn_w_down"].transpose(2, 0, 1).reshape(MCH, P, EXPERTS, D).transpose(1, 0, 2, 3)
    for n, (q, k, v, o) in (("L2_", [f["L2_xattn_w_" + c] for c in "qkvo"]), ("L3_", [f["L3_xattn_W_" + c] for c in "qkvo"])):
        for c, w in zip("qkvo", (q, k, v, o)):
            a[n + "w" + c] = rows(w.T)
    a["own_head"] = (np.arange(P)[:, None] // XD == np.arange(XH // 2)[None]).astype(np.float32)
    a["L2_bq"] = f["L2_xattn_b_q"].reshape(DCH, P).T
    a["L2_bk"] = f["L2_xattn_b_k"].reshape(DCH, P).T
    a["L2_bv"] = every(f["L2_xattn_b_v"])
    a["L2_bo"] = every(f["L2_xattn_b_o"])
    to_chunks = lambda w: np.pad(w, [(0, QCH * P - QI), (0, 0)]).reshape(QCH, P, D).transpose(1, 0, 2)
    a["L2_gu"] = np.concatenate([to_chunks(f["L2_ffn_w_gate"]), to_chunks(f["L2_ffn_w_up"])], 1)
    a["L2_d"] = rows(f["L2_ffn_w_down"])
    a["L2_clips"] = every(np.concatenate([f["L2_ffn_clip_x"], f["L2_ffn_clip_down"]]))
    ratio = 2.0 ** (-8.0 / XH)
    slopes = np.asarray([ratio ** i for i in range(1, XH + 1)], np.float32) * np.float32(XD ** 0.5)
    a["slopes"] = np.tile(slopes, BATCH)[:, None]
    kp, qp = f["itok_BxS2_1_8191"], f["itok_BxS_8_8191"].reshape(ALL_TILES, P)
    a["key_pos"], a["query_pos"] = np.repeat(kp, XH, 0), qp
    a["mask_if1"] = f["mask_BxSxS2_if1"].reshape(ALL_TILES, P, CTX).transpose(1, 0, 2)
    a["L3_gate"] = rows(f["L3_ffn_gate_w"])
    a["L3_w1"] = f["L3_ffn_w1"].reshape(EXPERTS, DCH, P, MOE_HID).transpose(2, 0, 1, 3)
    a["L3_w2"] = f["L3_ffn_w2"].reshape(EXPERTS, MCH, P, D).transpose(2, 0, 1, 3)
    return {k: np.ascontiguousarray(v) for k, v in a.items()}


def kernel(**inputs):
    import concourse.bacc as bacc
    from concourse.bass_utils import run_bass_kernel_spmd as run

    arrays = laid_out(inputs)
    nc = bacc.Bacc("TRN2", target_bir_lowering=False, num_devices=1)
    dram = {k: nc.dram_tensor(f"in_{k}", v.shape, mybir.dt.from_np(v.dtype), kind="ExternalInput").ap()
            for k, v in arrays.items()}
    out = nc.dram_tensor("out_x", (P, ALL_TILES, D), F32, kind="ExternalOutput").ap()
    build(nc, dram, out)
    r = run(nc, [{f"in_{k}": v for k, v in arrays.items()}], core_ids=[0])
    return r.results[0]["out_x"].transpose(1, 0, 2).reshape(BATCH, SEQ, D)
```
